# Optimizing a Trainium2 kernel written in Bass

```python
import numpy as np
import jax
import jax.numpy as jnp

def _softmax(x, axis=-1):
    return jax.nn.softmax(x, axis=axis)

def _gelu(x):
    return jax.nn.gelu(x, approximate=True)

def _silu(x):
    return jax.nn.silu(x)

def _sigmoid(x):
    return jax.nn.sigmoid(x)

def _layernorm(x, axis=-1, eps=1e-05):
    m = jnp.mean(x, axis=axis, keepdims=True)
    v = jnp.var(x, axis=axis, keepdims=True)
    return (x - m) / jnp.sqrt(v + eps)

def _scatter_add(tgt, idx, src, axis=0):
    return tgt.at[idx].add(src)

def _segment_sum(src, seg, n):
    return jax.ops.segment_sum(src, seg, n)
kernel_name = 'mk_perceiver_d4_seqx_r4_02ad7a'

def setup_inputs(seed: int=0):
    np.random.seed(seed)
    _w = jnp.asarray

    def _rec_inputs():
        import jax
        import jax.numpy as jnp
        _rk = jax.random.key(seed)
        x = -0.0002928 + 1 * jax.random.normal(jax.random.fold_in(_rk, 1), (16, 64, 256), jnp.float32)
        _lenS = 64 - jax.random.randint(jax.random.fold_in(_rk, 7), (16,), 0, max(1, 64 // 4) + 1, jnp.int32)
        _lenS2 = 256 - jax.random.randint(jax.random.fold_in(_rk, 8), (16,), 0, max(1, 256 // 4) + 1, jnp.int32)
        _ctx_1024P = jax.random.normal(jax.random.fold_in(_rk, 11), (16, 16, 256), jnp.float32)
        _ctx_1024c = jax.random.dirichlet(jax.random.fold_in(_rk, 511), 0.3 * jnp.ones((16,), jnp.float32), (16, 256))
        _ctx_1024t = jnp.einsum('bsk,bkd->bsd', _ctx_1024c, _ctx_1024P)
        _ctx_1024t = _ctx_1024t * jax.lax.rsqrt(jnp.mean(jnp.square(_ctx_1024t)) + 1e-12) * 0.953939
        ctx_1024 = -1.39393e-06 + 0.999914 * (_ctx_1024t + 0.3 * jax.random.normal(jax.random.fold_in(_rk, 611), (16, 256, 256), jnp.float32))
        _validS = jnp.arange(64)[None, :] < _lenS[:, None]
        _validS2 = jnp.arange(256)[None, :] < _lenS2[:, None]
        _causal = jnp.tril(jnp.ones((64, 64), dtype=bool))
        mask_BxS2_bf1 = jnp.ones((16, 256), dtype=bool)
        mask_BxS2_bk0 = jnp.logical_not(jnp.broadcast_to(_validS2[:, :], (16, 256)))
        return (x, ctx_1024, mask_BxS2_bf1, mask_BxS2_bk0)
    x, ctx_1024, mask_BxS2_bf1, mask_BxS2_bk0 = _rec_inputs()

    def _L0_xattn_setup():
        import jax, jax.numpy as jnp
        import numpy as np
        B, N, HID, HEADS, TOPK = (2, 512, 256, 16, 64)
        DHEAD = HID // HEADS

        def _split_heads(x):
            b, n, _ = x.shape
            return x.reshape(b, n, HEADS, DHEAD).transpose(0, 2, 1, 3)
        key = jax.random.key(seed)
        ks = jax.random.split(key, 12)
        s = 1.0 / np.sqrt(HID)
        inp = {'q': jax.random.normal(ks[0], (B, N, HID), jnp.float32), 'k': jax.random.normal(ks[1], (B, N, HID), jnp.float32), 'v': jax.random.normal(ks[2], (B, N, HID), jnp.float32), 'mask': jnp.ones((B, N), jnp.bool_), 'topk': TOPK, 'wq_w': jax.random.normal(ks[3], (HID, HID), jnp.float32) * s, 'wq_b': jnp.zeros((HID,), jnp.float32), 'wk_w': jax.random.normal(ks[4], (HID, HID), jnp.float32) * s, 'wk_b': jnp.zeros((HID,), jnp.float32), 'wv_w': jax.random.normal(ks[5], (HID, HID), jnp.float32) * s, 'wv_b': jnp.zeros((HID,), jnp.float32), 'wo_w': jax.random.normal(ks[6], (HID, HID), jnp.float32) * s, 'wo_b': jnp.zeros((HID,), jnp.float32)}
        return inp
    _L0_xattn_all = _L0_xattn_setup()
    _L0_xattn_in = {k: v for k, v in _L0_xattn_all.items() if k in ('wq_w', 'wq_b', 'wk_w', 'wk_b', 'wv_w', 'wv_b', 'wo_w', 'wo_b')}
    del _L0_xattn_all

    def _L0_attn_setup():
        import jax, jax.numpy as jnp
        import numpy as np
        N_HEADS = 16
        SEG = 64
        EPS = 1e-06

        def _sigma(x):
            return jax.nn.elu(x) + 1.0

        def _infini_attention(x, W_q, W_k, W_v, W_o, beta_param):
            B, T, D = x.shape
            H = N_HEADS
            dk = D // H
            assert T % SEG == 0
            S = T // SEG

            def proj(W):
                y = (x @ W.T).reshape(B, T, H, dk).transpose(0, 2, 1, 3)
                return y.reshape(B, H, S, SEG, dk).transpose(2, 0, 1, 3, 4)
            Qs, Ks, Vs = (proj(W_q), proj(W_k), proj(W_v))
            beta = jax.nn.sigmoid(beta_param).reshape(1, H, 1, 1)
            causal = jnp.triu(jnp.ones((SEG, SEG), dtype=bool), k=1)
            inv_sqrt_dk = 1.0 / jnp.sqrt(jnp.asarray(dk, x.dtype))
            M0 = jnp.zeros((B, H, dk, dk), dtype=x.dtype)
            z0 = jnp.zeros((B, H, dk), dtype=x.dtype)

            def step(carry, qkv):
                M, z = carry
                q, k, v = qkv
                sq = _sigma(q)
                denom_q = jnp.sum(sq * z[:, :, None, :], axis=-1, keepdims=True) + EPS
                A_mem = jnp.matmul(sq, M) / denom_q
                scores = jnp.matmul(q, jnp.swapaxes(k, -2, -1)) * inv_sqrt_dk
                scores = jnp.where(causal, -jnp.inf, scores)
                A_dot = jnp.matmul(jax.nn.softmax(scores, axis=-1), v)
                A_s = beta * A_mem + (1.0 - beta) * A_dot
                sk = _sigma(k)
                denom_k = jnp.sum(sk * z[:, :, None, :], axis=-1, keepdims=True) + EPS
                V_prev = jnp.matmul(sk, M) / denom_k
                M_new = M + jnp.einsum('bhtk,bhtv->bhkv', sk, v - V_prev)
                z_new = z + jnp.sum(sk, axis=-2)
                return ((M_new, z_new), A_s)
            (M, z), outs = jax.lax.scan(step, (M0, z0), (Qs, Ks, Vs))
            out = outs.transpose(1, 3, 0, 2, 4).reshape(B, S * SEG, H, dk)
            out = outs.transpose(1, 2, 0, 3, 4).reshape(B, H, T, dk)
            out = out.transpose(0, 2, 1, 3).reshape(B, T, D)
            out = out @ W_o.T
            return (out, M.mean(0), z.mean(0))

        def _reference_tuple_inner(x, W_q, W_k, W_v, W_o, beta_param):
            return _infini_attention(x, W_q, W_k, W_v, W_o, beta_param)
        key = jax.random.key(seed)
        kx, kq, kk, kv, ko = jax.random.split(key, 5)
        B, T, D = (4, 1024, 256)
        scale = D ** (-0.5)
        return {'x': jax.random.normal(kx, (B, T, D), dtype=jnp.float32), 'W_q': jax.random.normal(kq, (D, D), dtype=jnp.float32) * scale, 'W_k': jax.random.normal(kk, (D, D), dtype=jnp.float32) * scale, 'W_v': jax.random.normal(kv, (D, D), dtype=jnp.float32) * scale, 'W_o': jax.random.normal(ko, (D, D), dtype=jnp.float32) * scale, 'beta_param': jnp.zeros((N_HEADS,), dtype=jnp.float32)}
    _L0_attn_all = _L0_attn_setup()
    _L0_attn_in = {k: v for k, v in _L0_attn_all.items() if k in ('W_q', 'W_k', 'W_v', 'W_o', 'beta_param')}
    del _L0_attn_all

    def _L0_ffn_setup():
        import jax, jax.numpy as jnp
        import numpy as np
        import math
        DIM = 256
        NUM_HEADS = 16
        SHARED_HEADS = 1
        ROUTED_HEADS = 3
        HEAD_DIM = DIM // NUM_HEADS
        B, N = (2, 512)
        key = jax.random.key(seed)
        ks = jax.random.split(key, 16)
        s = 1.0 / math.sqrt(DIM)
        inp = {'x': jax.random.normal(ks[0], (B, N, DIM), dtype=jnp.float32), 'Wq': jax.random.uniform(ks[1], (DIM, DIM), minval=-s, maxval=s), 'bq': jax.random.uniform(ks[2], (DIM,), minval=-s, maxval=s), 'Wk': jax.random.uniform(ks[3], (DIM, DIM), minval=-s, maxval=s), 'bk': jax.random.uniform(ks[4], (DIM,), minval=-s, maxval=s), 'Wv': jax.random.uniform(ks[5], (DIM, DIM), minval=-s, maxval=s), 'bv': jax.random.uniform(ks[6], (DIM,), minval=-s, maxval=s), 'Wp': jax.random.uniform(ks[7], (DIM, DIM), minval=-s, maxval=s), 'bp': jax.random.uniform(ks[8], (DIM,), minval=-s, maxval=s), 'Wr': jax.random.uniform(ks[9], (NUM_HEADS - SHARED_HEADS, DIM), minval=-s, maxval=s), 'br': jax.random.uniform(ks[10], (NUM_HEADS - SHARED_HEADS,), minval=-s, maxval=s), 'Ws': jax.random.uniform(ks[11], (2, DIM), minval=-s, maxval=s), 'bs': jax.random.uniform(ks[12], (2,), minval=-s, maxval=s), 'temperature': jnp.full((NUM_HEADS, 1, 1), float(np.log(np.expm1(1.0 / 0.24))), dtype=jnp.float32), 'query_embedding': 0.02 * jax.random.normal(ks[13], (NUM_HEADS, 1, HEAD_DIM), dtype=jnp.float32)}
        return inp
    _L0_ffn_all = _L0_ffn_setup()
    _L0_ffn_in = {k: v for k, v in _L0_ffn_all.items() if k in ('Wq', 'bq', 'Wk', 'bk', 'Wv', 'bv', 'Wp', 'bp', 'Wr', 'br', 'Ws', 'bs', 'temperature', 'query_embedding')}
    del _L0_ffn_all

    def _L1_xattn_setup():
        import jax, jax.numpy as jnp
        import numpy as np
        DIM = 256
        NUM_HEADS = 16
        DIM_HEAD = 64
        INNER = NUM_HEADS * DIM_HEAD
        SCALE = DIM_HEAD ** (-0.5)

        def _layernorm(x, gamma, beta, eps=1e-05):
            mu = jnp.mean(x, axis=-1, keepdims=True)
            var = jnp.mean(jnp.square(x - mu), axis=-1, keepdims=True)
            return (x - mu) * jax.lax.rsqrt(var + eps) * gamma + beta
        key = jax.random.key(seed)
        ks = jax.random.split(key, 8)
        B, SQ, SK = (2, 512, 1024)
        x = jax.random.normal(ks[0], (B, SQ, DIM), dtype=jnp.float32)
        context = jax.random.normal(ks[1], (B, SK, DIM), dtype=jnp.float32)
        ln_gamma = jnp.ones((DIM,), jnp.float32)
        ln_beta = jnp.zeros((DIM,), jnp.float32)
        w_q = jax.random.normal(ks[2], (DIM, INNER), dtype=jnp.float32) / np.sqrt(DIM)
        w_kv = jax.random.normal(ks[3], (DIM, 2 * INNER), dtype=jnp.float32) / np.sqrt(DIM)
        w_out = jax.random.normal(ks[4], (INNER, DIM), dtype=jnp.float32) / np.sqrt(INNER)
        b_out = jnp.zeros((DIM,), jnp.float32)
        gate = jnp.array([0.5], jnp.float32)
        return {'x': x, 'context': context, 'ln_gamma': ln_gamma, 'ln_beta': ln_beta, 'w_q': w_q, 'w_kv': w_kv, 'w_out': w_out, 'b_out': b_out, 'gate': gate}
    _L1_xattn_all = _L1_xattn_setup()
    _L1_xattn_in = {k: v for k, v in _L1_xattn_all.items() if k in ('ln_gamma', 'ln_beta', 'w_q', 'w_kv', 'w_out', 'b_out', 'gate')}
    del _L1_xattn_all

    def _L1_attn_setup():
        import jax, jax.numpy as jnp
        import numpy as np
        from jax import lax
        D_MODEL = 256
        D_IN = 256
        N_STATE = 16
        DT_RANK = 64
        D_FFN = 1024
        BATCH, SEQ = (2, 512)

        def _ln(x, g, b, eps=1e-05):
            m = x.mean(-1, keepdims=True)
            v = ((x - m) ** 2).mean(-1, keepdims=True)
            return (x - m) / jnp.sqrt(v + eps) * g + b

        def _mamba(x, in_proj_w, conv_w, conv_b, x_proj_w, dt_proj_w, dt_proj_b, A_log, Dp, out_proj_w):
            B, L, _ = x.shape
            xz = x @ in_proj_w.T
            x_in, z = jnp.split(xz, 2, axis=-1)
            x_prev = jnp.pad(x_in, ((0, 0), (1, 0), (0, 0)))[:, :L]
            x_c = jax.nn.silu(x_prev * conv_w[:, 0] + x_in * conv_w[:, 1] + conv_b)
            x_dbl = x_c @ x_proj_w.T
            dt, Bm, Cm = jnp.split(x_dbl, [DT_RANK, DT_RANK + N_STATE], axis=-1)
            delta = jax.nn.softplus(dt @ dt_proj_w.T + dt_proj_b)
            A = -jnp.exp(A_log)
            deltaA = jnp.exp(delta[..., None] * A)
            dBu = delta[..., None] * Bm[:, :, None, :] * x_c[..., None]

            def step(h, t):
                dA_t, dBu_t, C_t = t
                h = dA_t * h + dBu_t
                y = jnp.einsum('bdn,bn->bd', h, C_t)
                return (h, y)
            h0 = jnp.zeros((B, D_IN, N_STATE), x.dtype)
            _, ys = lax.scan(step, h0, (deltaA.transpose(1, 0, 2, 3), dBu.transpose(1, 0, 2, 3), Cm.transpose(1, 0, 2)))
            y = ys.transpose(1, 0, 2)
            y = (y + x_c * Dp) * jax.nn.silu(z)
            return y @ out_proj_w.T
        key = jax.random.key(seed)
        ks = jax.random.split(key, 12)
        r = lambda i, shape, s=0.02: jax.random.normal(ks[i], shape, jnp.float32) * s
        ones = lambda n: jnp.ones((n,), jnp.float32)
        zeros = lambda n: jnp.zeros((n,), jnp.float32)
        A_log = jnp.log(jnp.tile(jnp.arange(1, N_STATE + 1, dtype=jnp.float32), (D_IN, 1)))
        return {'src': jax.random.normal(ks[0], (BATCH, SEQ, D_MODEL), jnp.float32), 'in_proj_w': r(1, (2 * D_IN, D_MODEL)), 'conv_w': r(2, (D_IN, 2), 0.5), 'conv_b': zeros(D_IN), 'x_proj_w': r(3, (DT_RANK + 2 * N_STATE, D_IN)), 'dt_proj_w': r(4, (D_IN, DT_RANK), 0.1), 'dt_proj_b': r(5, (D_IN,), 0.1), 'A_log': A_log, 'Dp': ones(D_IN), 'out_proj_w': r(6, (D_MODEL, D_IN)), 'mnorm_g': ones(D_MODEL), 'mnorm_b': zeros(D_MODEL), 'n1_g': ones(D_MODEL), 'n1_b': zeros(D_MODEL), 'n2_g': ones(D_MODEL), 'n2_b': zeros(D_MODEL), 'n3_g': ones(D_MODEL), 'n3_b': zeros(D_MODEL), 'ffn_w1': r(7, (D_FFN, D_MODEL)), 'ffn_w2': r(8, (D_MODEL, D_FFN)), 'fe_w': r(9, (D_MODEL, D_MODEL)), 'fe_b': zeros(D_MODEL)}
    _L1_attn_all = _L1_attn_setup()
    _L1_attn_in = {k: v for k, v in _L1_attn_all.items() if k in ('in_proj_w', 'conv_w', 'conv_b', 'x_proj_w', 'dt_proj_w', 'dt_proj_b', 'A_log', 'Dp', 'out_proj_w', 'mnorm_g', 'mnorm_b', 'n1_g', 'n1_b', 'n2_g', 'n2_b', 'n3_g', 'n3_b', 'ffn_w1', 'ffn_w2', 'fe_w', 'fe_b')}
    del _L1_attn_all

    def _L1_ffn_setup():
        import jax, jax.numpy as jnp
        import numpy as np
        QB = 127.0
        EPS = 1e-05

        def _ste(x, q):
            return x + jax.lax.stop_gradient(q - x)

        def bitlinear(x, W, b):
            w_scale = jnp.clip(jnp.mean(jnp.abs(W)), EPS, None)
            Wq = _ste(W, jnp.clip(jnp.round(W / w_scale), -1.0, 1.0) * w_scale)
            x_scale = jnp.clip(jnp.max(jnp.abs(x), axis=-1, keepdims=True), EPS, None)
            xq = _ste(x, jnp.clip(jnp.round(x * (QB / x_scale)), -QB - 1.0, QB) * (x_scale / QB))
            return jnp.einsum('bnd,hd->bnh', xq, Wq) + b
        key = jax.random.key(seed)
        k0, k1, k2 = jax.random.split(key, 3)
        B, N, D = (8, 1024, 256)
        H = int(D * 4.0)
        x = jax.random.normal(k0, (B, N, D), dtype=jnp.float32)
        W1 = jax.random.normal(k1, (H, D), dtype=jnp.float32) * 0.02
        b1 = jnp.zeros((H,), dtype=jnp.float32)
        W2 = jax.random.normal(k2, (D, H), dtype=jnp.float32) * 0.02
        b2 = jnp.zeros((D,), dtype=jnp.float32)
        return {'x': x, 'W1': W1, 'b1': b1, 'W2': W2, 'b2': b2}
    _L1_ffn_all = _L1_ffn_setup()
    _L1_ffn_in = {k: v for k, v in _L1_ffn_all.items() if k in ('W1', 'b1', 'W2', 'b2')}
    del _L1_ffn_all

    def _L2_xattn_setup():
        import jax, jax.numpy as jnp
        import numpy as np
        D_MODEL = 256
        NUM_HEADS = 16
        D_K = D_MODEL // NUM_HEADS
        key = jax.random.key(seed)
        ks = jax.random.split(key, 11)
        B, T = (4, 512)
        s = 1.0 / np.sqrt(D_MODEL)
        inp = {'query': jax.random.normal(ks[0], (B, T, D_MODEL), jnp.float32), 'key': jax.random.normal(ks[1], (B, T, D_MODEL), jnp.float32), 'value': jax.random.normal(ks[2], (B, T, D_MODEL), jnp.float32), 'Wq': jax.random.normal(ks[3], (D_MODEL, D_MODEL), jnp.float32) * s, 'bq': jnp.zeros((D_MODEL,), jnp.float32), 'Wk': jax.random.normal(ks[4], (D_MODEL, D_MODEL), jnp.float32) * s, 'bk': jnp.zeros((D_MODEL,), jnp.float32), 'Wv': jax.random.normal(ks[5], (D_MODEL, D_MODEL), jnp.float32) * s, 'bv': jnp.zeros((D_MODEL,), jnp.float32), 'Wo': jax.random.normal(ks[6], (D_MODEL, D_MODEL), jnp.float32) * s, 'bo': jnp.zeros((D_MODEL,), jnp.float32)}
        return inp
    _L2_xattn_all = _L2_xattn_setup()
    _L2_xattn_in = {k: v for k, v in _L2_xattn_all.items() if k in ('Wq', 'bq', 'Wk', 'bk', 'Wv', 'bv', 'Wo', 'bo')}
    del _L2_xattn_all

    def _L2_attn_setup():
        import jax, jax.numpy as jnp
        import numpy as np
        CHUNK = 32
        H = 4

        def silu(x):
            return x * jax.nn.sigmoid(x)

        def l2norm(x):
            return x * jax.lax.rsqrt(jnp.sum(x * x, -1, keepdims=True) + 1e-06)

        def dwconv_causal(x_cl, w):
            k = w.shape[1]
            xp = jnp.pad(x_cl, ((0, 0), (0, 0), (k - 1, 0)))
            return jax.lax.conv_general_dilated(xp, w[:, None, :], (1,), 'VALID', dimension_numbers=('NCH', 'OIH', 'NCH'), feature_group_count=x_cl.shape[1])

        def short_conv_silu(x_bld, w):
            y = dwconv_causal(jnp.swapaxes(x_bld, 1, 2), w)
            return silu(jnp.swapaxes(y, 1, 2))

        def delta_rule_chunkwise(q, k, v, beta, chunk=CHUNK):
            b, h, L, dk = q.shape
            dv = v.shape[-1]
            pad = -L % chunk
            if pad:
                q, k, v = (jnp.pad(t, ((0, 0), (0, 0), (0, pad), (0, 0))) for t in (q, k, v))
                beta = jnp.pad(beta, ((0, 0), (0, 0), (0, pad)))
            n = (L + pad) // chunk
            q = l2norm(q)
            k = l2norm(k)
            v = v * beta[..., None]
            kb = k * beta[..., None]
            ch = lambda x: x.reshape(b, h, n, chunk, x.shape[-1])
            qc, kc, vc, kbc = map(ch, (q, k, v, kb))
            idx = jnp.arange(chunk)
            strict_lower = (idx[:, None] > idx[None, :]).astype(q.dtype)
            incl_lower = (idx[:, None] >= idx[None, :]).astype(q.dtype)
            attn = -jnp.einsum('bhncd,bhned->bhnce', kbc, kc) * strict_lower
            for i in range(1, chunk):
                upd = jnp.einsum('...j,...ji->...i', attn[..., i, :], attn[..., :, :i])
                attn = attn.at[..., i, :i].add(upd)
            attn = attn + jnp.eye(chunk, dtype=q.dtype)
            u = attn @ vc
            w = attn @ kbc
            xs = tuple((jnp.moveaxis(t, 2, 0) for t in (qc, kc, u, w)))
            S0 = jnp.zeros((b, h, dk, dv), q.dtype)

            def step(S, x):
                qi, ki, ui, wi = x
                a_loc = jnp.einsum('bhcd,bhed->bhce', qi, ki) * incl_lower
                ui = ui - wi @ S
                oi = qi @ S + a_loc @ ui
                S = S + jnp.einsum('bhcd,bhcv->bhdv', ki, ui)
                return (S, oi)
            S, o = jax.lax.scan(step, S0, xs)
            o = jnp.moveaxis(o, 0, 2).reshape(b, h, n * chunk, dv)[:, :, :L]
            return (o, S)

        def multiscale_conv(v, ms_w3, ms_w15, ms_w31, kernel_mix_w, channel_mixer_w):
            b, l, h, d = v.shape
            x = jnp.swapaxes(v.reshape(b, l, h * d), 1, 2)
            outs = [dwconv_causal(x, w) for w in (ms_w3, ms_w15, ms_w31)]
            y = jnp.concatenate(outs, axis=1)
            y = y.reshape(b, h, 3 * d, l).transpose(0, 3, 1, 2)
            y = y @ kernel_mix_w
            y = (y.reshape(b, l, h * d) @ channel_mixer_w).reshape(b, l, h, d)
            return y

        def _forward(hidden_states, Wq, Wk, Wv, Wb, conv_q_w, conv_k_w, conv_v_w, ms_w3, ms_w15, ms_w31, kernel_mix_w, channel_mixer_w, fusion_w1, fusion_b1, fusion_w2, fusion_b2, o_norm_w, Wo):
            b, L, D = hidden_states.shape
            h = H
            dk = Wq.shape[1] // h
            dv = Wv.shape[1] // h
            q = short_conv_silu(hidden_states @ Wq, conv_q_w).reshape(b, L, h, dk)
            k = short_conv_silu(hidden_states @ Wk, conv_k_w).reshape(b, L, h, dk)
            v = short_conv_silu(hidden_states @ Wv, conv_v_w).reshape(b, L, h, dv)
            v_direct = v
            beta = jax.nn.sigmoid(hidden_states @ Wb)
            tr = lambda x: jnp.swapaxes(x, 1, 2)
            delta_out, _S = delta_rule_chunkwise(tr(q), tr(k), tr(v), tr(beta))
            delta_out = jnp.swapaxes(delta_out, 1, 2)
            ms_out = multiscale_conv(v_direct, ms_w3, ms_w15, ms_w31, kernel_mix_w, channel_mixer_w)
            bn = lambda x: jnp.mean(jnp.abs(x), -1)
            gate_features = jnp.concatenate([hidden_states, bn(ms_out), bn(delta_out), bn(v_direct)], -1)
            hdn = jax.nn.gelu(gate_features @ fusion_w1 + fusion_b1, approximate=False)
            logits = (hdn @ fusion_w2 + fusion_b2).reshape(b, L, h, 3)
            wts = jax.nn.softmax(logits, -1)
            o = wts[..., 0:1] * ms_out + wts[..., 1:2] * delta_out + wts[..., 2:3] * v_direct
            o = o * jax.lax.rsqrt(jnp.mean(o * o, -1, keepdims=True) + 1e-05) * o_norm_w
            return o.reshape(b, L, h * dv) @ Wo
        B, L, D = (4, 512, 256)
        h, d = (H, D // H)
        key = jax.random.key(seed)
        ks = jax.random.split(key, 20)
        nrm = lambda k, shp, s: jax.random.normal(k, shp, dtype=jnp.float32) * s
        inp = {'hidden_states': nrm(ks[0], (B, L, D), 1.0), 'Wq': nrm(ks[1], (D, D), D ** (-0.5)), 'Wk': nrm(ks[2], (D, D), D ** (-0.5)), 'Wv': nrm(ks[3], (D, D), D ** (-0.5)), 'Wb': nrm(ks[4], (D, h), D ** (-0.5)), 'conv_q_w': nrm(ks[5], (D, 4), 0.3), 'conv_k_w': nrm(ks[6], (D, 4), 0.3), 'conv_v_w': nrm(ks[7], (D, 4), 0.3), 'ms_w3': nrm(ks[8], (D, 3), 0.02), 'ms_w15': nrm(ks[9], (D, 15), 0.02), 'ms_w31': nrm(ks[10], (D, 31), 0.02), 'kernel_mix_w': nrm(ks[11], (3 * d, d), (3 * d) ** (-0.5)), 'channel_mixer_w': nrm(ks[12], (D, D), D ** (-0.5)), 'fusion_w1': nrm(ks[13], (D + 3 * h, 2 * D), (D + 3 * h) ** (-0.5)), 'fusion_b1': jnp.zeros((2 * D,), jnp.float32), 'fusion_w2': nrm(ks[14], (2 * D, 3 * h), (2 * D) ** (-0.5)), 'fusion_b2': jnp.concatenate([jnp.zeros((2 * h,), jnp.float32), jnp.ones((h,), jnp.float32)]), 'o_norm_w': jnp.ones((d,), jnp.float32), 'Wo': nrm(ks[15], (D, D), D ** (-0.5))}
        return inp
    _L2_attn_all = _L2_attn_setup()
    _L2_attn_in = {k: v for k, v in _L2_attn_all.items() if k in ('Wq', 'Wk', 'Wv', 'Wb', 'conv_q_w', 'conv_k_w', 'conv_v_w', 'ms_w3', 'ms_w15', 'ms_w31', 'kernel_mix_w', 'channel_mixer_w', 'fusion_w1', 'fusion_b1', 'fusion_w2', 'fusion_b2', 'o_norm_w', 'Wo')}
    del _L2_attn_all

    def _L2_ffn_setup():
        import jax, jax.numpy as jnp
        import numpy as np
        IN_DIM, OUT_DIM, N_PROTO, RANK = (256, 256, 32, 16)
        key = jax.random.key(seed)
        ks = jax.random.split(key, 5)
        x = jax.random.normal(ks[0], (2, 1024, IN_DIM), dtype=jnp.float32)
        prototypes = jax.random.normal(ks[1], (N_PROTO, IN_DIM), dtype=jnp.float32) * 0.02
        B = jax.random.normal(ks[2], (N_PROTO, RANK, IN_DIM), dtype=jnp.float32) * 0.02
        A = jax.random.normal(ks[3], (N_PROTO, OUT_DIM, RANK), dtype=jnp.float32) * 0.02
        bias = jnp.zeros((N_PROTO, OUT_DIM), dtype=jnp.float32)
        temp = jnp.asarray(1.0, dtype=jnp.float32)
        return {'x': x, 'prototypes': prototypes, 'B': B, 'A': A, 'bias': bias, 'temp': temp}
    _L2_ffn_all = _L2_ffn_setup()
    _L2_ffn_in = {k: v for k, v in _L2_ffn_all.items() if k in ('prototypes', 'B', 'A', 'bias', 'temp')}
    del _L2_ffn_all

    def _L3_xattn_setup():
        import jax, jax.numpy as jnp
        import numpy as np
        NUM_HEADS, NUM_KV, HEAD_DIM, WIDTH = (4, 1, 64, 256)
        MASK_FILL = -2.3819763e+38

        def _apply_rope(x, positions, max_wavelength=10000.0):
            d = x.shape[-1]
            freq_exp = 2.0 / d * jnp.arange(d // 2, dtype=jnp.float32)
            timescale = max_wavelength ** freq_exp
            radians = positions[..., None].astype(jnp.float32) / timescale
            radians = radians[..., None, :]
            sin, cos = (jnp.sin(radians), jnp.cos(radians))
            x1, x2 = jnp.split(x, 2, axis=-1)
            out = jnp.concatenate([x1 * cos - x2 * sin, x2 * cos + x1 * sin], axis=-1)
            return out.astype(x.dtype)

        def _rmsnorm(x, scale):
            var = jnp.mean(jnp.square(x.astype(jnp.float32)), axis=-1, keepdims=True)
            normed = x * jax.lax.rsqrt(var + 1e-06)
            return (normed * (1 + scale)).astype(x.dtype)
        key = jax.random.key(seed)
        ks = jax.random.split(key, 7)
        B, T, S = (8, 128, 512)
        return {'x': jax.random.normal(ks[0], (B, T, WIDTH), jnp.float32), 'mem_seq': jax.random.normal(ks[1], (B, S, WIDTH), jnp.float32), 'mem_mask': jax.random.randint(ks[2], (B, S), 0, 2).astype(bool), 'rms_scale': jax.random.normal(ks[3], (WIDTH,), jnp.float32) * 0.02, 'q_w': jax.random.normal(ks[4], (NUM_HEADS, WIDTH, HEAD_DIM), jnp.float32) / np.sqrt(WIDTH), 'kv_w': jax.random.normal(ks[5], (2, NUM_KV, WIDTH, HEAD_DIM), jnp.float32) / np.sqrt(WIDTH), 'out_w': jax.random.normal(ks[6], (NUM_HEADS, HEAD_DIM, WIDTH), jnp.float32) / np.sqrt(NUM_HEADS * HEAD_DIM)}
    _L3_xattn_all = _L3_xattn_setup()
    _L3_xattn_in = {k: v for k, v in _L3_xattn_all.items() if k in ('rms_scale', 'q_w', 'kv_w', 'out_w')}
    del _L3_xattn_all

    def _L3_attn_setup():
        import jax, jax.numpy as jnp
        import numpy as np
        BATCH, L, D_MODEL = (2, 256, 256)
        D_STATE, D_CONV, EXPAND = (16, 4, 2)
        D_INNER = EXPAND * D_MODEL
        DT_RANK = max(1, -(-D_MODEL // 16))

        def _forward(x, W_in, conv_w, conv_b, W_x, W_dt, b_dt, A_log, D, W_out):
            xv = x @ W_in
            xc = jnp.transpose(xv, (0, 2, 1))
            xc = jax.lax.conv_general_dilated(xc, conv_w, window_strides=(1,), padding=[(D_CONV - 1, 0)], dimension_numbers=('NCH', 'OIH', 'NCH'), feature_group_count=D_INNER)
            xv = jnp.transpose(xc, (0, 2, 1)) + conv_b
            xv = jax.nn.silu(xv)
            ssm = xv @ W_x
            dt_raw = ssm[..., :DT_RANK]
            Bp = ssm[..., DT_RANK:DT_RANK + D_STATE]
            Cp = ssm[..., DT_RANK + D_STATE:]
            delta = jax.nn.softplus(dt_raw @ W_dt + b_dt)
            A = -jnp.exp(A_log)
            dA = jnp.exp(delta[..., None] * A)
            dBx = delta[..., None] * Bp[:, :, None, :] * xv[..., None]

            def comb(c1, c2):
                a1, b1 = c1
                a2, b2 = c2
                return (a1 * a2, a2 * b1 + b2)
            _, h = jax.lax.associative_scan(comb, (dA, dBx), axis=1)
            y = jnp.einsum('bldn,bln->bld', h, Cp)
            y = y + xv * D
            return y @ W_out
        key = jax.random.key(seed)
        ks = jax.random.split(key, 10)
        s = 0.02
        x = jax.random.normal(ks[0], (BATCH, L, D_MODEL), jnp.float32)
        W_in = jax.random.normal(ks[1], (D_MODEL, D_INNER), jnp.float32) * s
        conv_w = jax.random.normal(ks[2], (D_INNER, 1, D_CONV), jnp.float32) * s
        conv_b = jax.random.normal(ks[3], (D_INNER,), jnp.float32) * s
        W_x = jax.random.normal(ks[4], (D_INNER, DT_RANK + 2 * D_STATE), jnp.float32) * s
        W_dt = jax.random.normal(ks[5], (DT_RANK, D_INNER), jnp.float32) * s
        b_dt = jax.random.normal(ks[6], (D_INNER,), jnp.float32) * s
        A_log = jnp.log(jnp.broadcast_to(jnp.arange(1, D_STATE + 1, dtype=jnp.float32), (D_INNER, D_STATE)))
        D = jnp.ones((D_INNER,), jnp.float32)
        W_out = jax.random.normal(ks[7], (D_INNER, D_MODEL), jnp.float32) * s
        return {'x': x, 'W_in': W_in, 'conv_w': conv_w, 'conv_b': conv_b, 'W_x': W_x, 'W_dt': W_dt, 'b_dt': b_dt, 'A_log': A_log, 'D': D, 'W_out': W_out}
    _L3_attn_all = _L3_attn_setup()
    _L3_attn_in = {k: v for k, v in _L3_attn_all.items() if k in ('W_in', 'conv_w', 'conv_b', 'W_x', 'W_dt', 'b_dt', 'A_log', 'D', 'W_out')}
    del _L3_attn_all

    def _L3_ffn_setup():
        import jax, jax.numpy as jnp
        import numpy as np
        EPS = 1e-08

        def _ternary_linear(x, w):
            alpha = jnp.mean(jnp.abs(w))
            w_t = jnp.sign(w) * (jnp.abs(w) > 0.5 * alpha).astype(w.dtype)
            w_q = w + jax.lax.stop_gradient(w_t - w)
            d = x.shape[-1]
            rms = jnp.sqrt(jnp.sum(x * x, axis=-1, keepdims=True)) / jnp.sqrt(jnp.asarray(d, x.dtype))
            x_norm = x / (rms + EPS)
            return jnp.einsum('bsd,fd->bsf', x_norm, w_q)
        key = jax.random.key(seed)
        k1, k2, k3 = jax.random.split(key, 3)
        d_model, d_ff = (256, 1024)
        B, S = (4, 1024)
        x = jax.random.normal(k1, (B, S, d_model), dtype=jnp.float32)
        w_up = jax.random.normal(k2, (d_ff, d_model), dtype=jnp.float32) * 0.02
        w_down = jax.random.normal(k3, (d_model, d_ff), dtype=jnp.float32) * 0.02
        return {'x': x, 'w_up': w_up, 'w_down': w_down}
    _L3_ffn_all = _L3_ffn_setup()
    _L3_ffn_in = {k: v for k, v in _L3_ffn_all.items() if k in ('w_up', 'w_down')}
    del _L3_ffn_all
    return {'x': x, 'ctx_1024': ctx_1024, 'mask_BxS2_bf1': mask_BxS2_bf1, 'mask_BxS2_bk0': mask_BxS2_bk0, 'L0_xattn_wq_w': _L0_xattn_in['wq_w'], 'L0_xattn_wq_b': _L0_xattn_in['wq_b'], 'L0_xattn_wk_w': _L0_xattn_in['wk_w'], 'L0_xattn_wk_b': _L0_xattn_in['wk_b'], 'L0_xattn_wv_w': _L0_xattn_in['wv_w'], 'L0_xattn_wv_b': _L0_xattn_in['wv_b'], 'L0_xattn_wo_w': _L0_xattn_in['wo_w'], 'L0_xattn_wo_b': _L0_xattn_in['wo_b'], 'L0_attn_W_q': _L0_attn_in['W_q'], 'L0_attn_W_k': _L0_attn_in['W_k'], 'L0_attn_W_v': _L0_attn_in['W_v'], 'L0_attn_W_o': _L0_attn_in['W_o'], 'L0_attn_beta_param': _L0_attn_in['beta_param'], 'L0_ffn_Wq': _L0_ffn_in['Wq'], 'L0_ffn_bq': _L0_ffn_in['bq'], 'L0_ffn_Wk': _L0_ffn_in['Wk'], 'L0_ffn_bk': _L0_ffn_in['bk'], 'L0_ffn_Wv': _L0_ffn_in['Wv'], 'L0_ffn_bv': _L0_ffn_in['bv'], 'L0_ffn_Wp': _L0_ffn_in['Wp'], 'L0_ffn_bp': _L0_ffn_in['bp'], 'L0_ffn_Wr': _L0_ffn_in['Wr'], 'L0_ffn_br': _L0_ffn_in['br'], 'L0_ffn_Ws': _L0_ffn_in['Ws'], 'L0_ffn_bs': _L0_ffn_in['bs'], 'L0_ffn_temperature': _L0_ffn_in['temperature'], 'L0_ffn_query_embedding': _L0_ffn_in['query_embedding'], 'L1_xattn_ln_gamma': _L1_xattn_in['ln_gamma'], 'L1_xattn_ln_beta': _L1_xattn_in['ln_beta'], 'L1_xattn_w_q': _L1_xattn_in['w_q'], 'L1_xattn_w_kv': _L1_xattn_in['w_kv'], 'L1_xattn_w_out': _L1_xattn_in['w_out'], 'L1_xattn_b_out': _L1_xattn_in['b_out'], 'L1_xattn_gate': _L1_xattn_in['gate'], 'L1_attn_in_proj_w': _L1_attn_in['in_proj_w'], 'L1_attn_conv_w': _L1_attn_in['conv_w'], 'L1_attn_conv_b': _L1_attn_in['conv_b'], 'L1_attn_x_proj_w': _L1_attn_in['x_proj_w'], 'L1_attn_dt_proj_w': _L1_attn_in['dt_proj_w'], 'L1_attn_dt_proj_b': _L1_attn_in['dt_proj_b'], 'L1_attn_A_log': _L1_attn_in['A_log'], 'L1_attn_Dp': _L1_attn_in['Dp'], 'L1_attn_out_proj_w': _L1_attn_in['out_proj_w'], 'L1_attn_mnorm_g': _L1_attn_in['mnorm_g'], 'L1_attn_mnorm_b': _L1_attn_in['mnorm_b'], 'L1_attn_n1_g': _L1_attn_in['n1_g'], 'L1_attn_n1_b': _L1_attn_in['n1_b'], 'L1_attn_n2_g': _L1_attn_in['n2_g'], 'L1_attn_n2_b': _L1_attn_in['n2_b'], 'L1_attn_n3_g': _L1_attn_in['n3_g'], 'L1_attn_n3_b': _L1_attn_in['n3_b'], 'L1_attn_ffn_w1': _L1_attn_in['ffn_w1'], 'L1_attn_ffn_w2': _L1_attn_in['ffn_w2'], 'L1_attn_fe_w': _L1_attn_in['fe_w'], 'L1_attn_fe_b': _L1_attn_in['fe_b'], 'L1_ffn_W1': _L1_ffn_in['W1'], 'L1_ffn_b1': _L1_ffn_in['b1'], 'L1_ffn_W2': _L1_ffn_in['W2'], 'L1_ffn_b2': _L1_ffn_in['b2'], 'L2_xattn_Wq': _L2_xattn_in['Wq'], 'L2_xattn_bq': _L2_xattn_in['bq'], 'L2_xattn_Wk': _L2_xattn_in['Wk'], 'L2_xattn_bk': _L2_xattn_in['bk'], 'L2_xattn_Wv': _L2_xattn_in['Wv'], 'L2_xattn_bv': _L2_xattn_in['bv'], 'L2_xattn_Wo': _L2_xattn_in['Wo'], 'L2_xattn_bo': _L2_xattn_in['bo'], 'L2_attn_Wq': _L2_attn_in['Wq'], 'L2_attn_Wk': _L2_attn_in['Wk'], 'L2_attn_Wv': _L2_attn_in['Wv'], 'L2_attn_Wb': _L2_attn_in['Wb'], 'L2_attn_conv_q_w': _L2_attn_in['conv_q_w'], 'L2_attn_conv_k_w': _L2_attn_in['conv_k_w'], 'L2_attn_conv_v_w': _L2_attn_in['conv_v_w'], 'L2_attn_ms_w3': _L2_attn_in['ms_w3'], 'L2_attn_ms_w15': _L2_attn_in['ms_w15'], 'L2_attn_ms_w31': _L2_attn_in['ms_w31'], 'L2_attn_kernel_mix_w': _L2_attn_in['kernel_mix_w'], 'L2_attn_channel_mixer_w': _L2_attn_in['channel_mixer_w'], 'L2_attn_fusion_w1': _L2_attn_in['fusion_w1'], 'L2_attn_fusion_b1': _L2_attn_in['fusion_b1'], 'L2_attn_fusion_w2': _L2_attn_in['fusion_w2'], 'L2_attn_fusion_b2': _L2_attn_in['fusion_b2'], 'L2_attn_o_norm_w': _L2_attn_in['o_norm_w'], 'L2_attn_Wo': _L2_attn_in['Wo'], 'L2_ffn_prototypes': _L2_ffn_in['prototypes'], 'L2_ffn_B': _L2_ffn_in['B'], 'L2_ffn_A': _L2_ffn_in['A'], 'L2_ffn_bias': _L2_ffn_in['bias'], 'L2_ffn_temp': _L2_ffn_in['temp'], 'L3_xattn_rms_scale': _L3_xattn_in['rms_scale'], 'L3_xattn_q_w': _L3_xattn_in['q_w'], 'L3_xattn_kv_w': _L3_xattn_in['kv_w'], 'L3_xattn_out_w': _L3_xattn_in['out_w'], 'L3_attn_W_in': _L3_attn_in['W_in'], 'L3_attn_conv_w': _L3_attn_in['conv_w'], 'L3_attn_conv_b': _L3_attn_in['conv_b'], 'L3_attn_W_x': _L3_attn_in['W_x'], 'L3_attn_W_dt': _L3_attn_in['W_dt'], 'L3_attn_b_dt': _L3_attn_in['b_dt'], 'L3_attn_A_log': _L3_attn_in['A_log'], 'L3_attn_D': _L3_attn_in['D'], 'L3_attn_W_out': _L3_attn_in['W_out'], 'L3_ffn_w_up': _L3_ffn_in['w_up'], 'L3_ffn_w_down': _L3_ffn_in['w_down']}

def reference(x, ctx_1024, mask_BxS2_bf1, mask_BxS2_bk0, L0_xattn_wq_w, L0_xattn_wq_b, L0_xattn_wk_w, L0_xattn_wk_b, L0_xattn_wv_w, L0_xattn_wv_b, L0_xattn_wo_w, L0_xattn_wo_b, L0_attn_W_q, L0_attn_W_k, L0_attn_W_v, L0_attn_W_o, L0_attn_beta_param, L0_ffn_Wq, L0_ffn_bq, L0_ffn_Wk, L0_ffn_bk, L0_ffn_Wv, L0_ffn_bv, L0_ffn_Wp, L0_ffn_bp, L0_ffn_Wr, L0_ffn_br, L0_ffn_Ws, L0_ffn_bs, L0_ffn_temperature, L0_ffn_query_embedding, L1_xattn_ln_gamma, L1_xattn_ln_beta, L1_xattn_w_q, L1_xattn_w_kv, L1_xattn_w_out, L1_xattn_b_out, L1_xattn_gate, L1_attn_in_proj_w, L1_attn_conv_w, L1_attn_conv_b, L1_attn_x_proj_w, L1_attn_dt_proj_w, L1_attn_dt_proj_b, L1_attn_A_log, L1_attn_Dp, L1_attn_out_proj_w, L1_attn_mnorm_g, L1_attn_mnorm_b, L1_attn_n1_g, L1_attn_n1_b, L1_attn_n2_g, L1_attn_n2_b, L1_attn_n3_g, L1_attn_n3_b, L1_attn_ffn_w1, L1_attn_ffn_w2, L1_attn_fe_w, L1_attn_fe_b, L1_ffn_W1, L1_ffn_b1, L1_ffn_W2, L1_ffn_b2, L2_xattn_Wq, L2_xattn_bq, L2_xattn_Wk, L2_xattn_bk, L2_xattn_Wv, L2_xattn_bv, L2_xattn_Wo, L2_xattn_bo, L2_attn_Wq, L2_attn_Wk, L2_attn_Wv, L2_attn_Wb, L2_attn_conv_q_w, L2_attn_conv_k_w, L2_attn_conv_v_w, L2_attn_ms_w3, L2_attn_ms_w15, L2_attn_ms_w31, L2_attn_kernel_mix_w, L2_attn_channel_mixer_w, L2_attn_fusion_w1, L2_attn_fusion_b1, L2_attn_fusion_w2, L2_attn_fusion_b2, L2_attn_o_norm_w, L2_attn_Wo, L2_ffn_prototypes, L2_ffn_B, L2_ffn_A, L2_ffn_bias, L2_ffn_temp, L3_xattn_rms_scale, L3_xattn_q_w, L3_xattn_kv_w, L3_xattn_out_w, L3_attn_W_in, L3_attn_conv_w, L3_attn_conv_b, L3_attn_W_x, L3_attn_W_dt, L3_attn_b_dt, L3_attn_A_log, L3_attn_D, L3_attn_W_out, L3_ffn_w_up, L3_ffn_w_down):
    import jax
    import jax.numpy as jnp

    def _L0_xattn_ref(q, k, v, mask, topk, wq_w, wq_b, wk_w, wk_b, wv_w, wv_b, wo_w, wo_b):
        import jax, jax.numpy as jnp
        import numpy as np
        B, N, HID, HEADS, TOPK = (2, 512, 256, 16, 64)
        DHEAD = HID // HEADS

        def _split_heads(x):
            b, n, _ = x.shape
            return x.reshape(b, n, HEADS, DHEAD).transpose(0, 2, 1, 3)
        qh = _split_heads(q @ wq_w.T + wq_b)
        kh = _split_heads(k @ wk_w.T + wk_b)
        vh = _split_heads(v @ wv_w.T + wv_b)
        scores = jnp.einsum('bhqd,bhkd->bhqk', qh, kh) / np.sqrt(DHEAD)
        neg = jnp.finfo(scores.dtype).min
        scores = jnp.where(mask[:, None, None, :], scores, neg)
        if topk and 0 < topk < scores.shape[-1]:
            vals, idx = jax.lax.top_k(scores, topk)
            b, h, nq, _ = scores.shape
            bI = jnp.arange(b)[:, None, None, None]
            hI = jnp.arange(h)[None, :, None, None]
            qI = jnp.arange(nq)[None, None, :, None]
            scores = jnp.full_like(scores, neg).at[bI, hI, qI, idx].set(vals)
        probs = jax.nn.softmax(scores, axis=-1)
        ctx = jnp.einsum('bhqk,bhkd->bhqd', probs, vh)
        ctx = ctx.transpose(0, 2, 1, 3).reshape(q.shape[0], q.shape[1], HID)
        return ctx @ wo_w.T + wo_b

    def _L0_attn_ref(x, W_q, W_k, W_v, W_o, beta_param):
        import jax, jax.numpy as jnp
        import numpy as np
        N_HEADS = 16
        SEG = 64
        EPS = 1e-06

        def _sigma(x):
            return jax.nn.elu(x) + 1.0

        def _infini_attention(x, W_q, W_k, W_v, W_o, beta_param):
            B, T, D = x.shape
            H = N_HEADS
            dk = D // H
            assert T % SEG == 0
            S = T // SEG

            def proj(W):
                y = (x @ W.T).reshape(B, T, H, dk).transpose(0, 2, 1, 3)
                return y.reshape(B, H, S, SEG, dk).transpose(2, 0, 1, 3, 4)
            Qs, Ks, Vs = (proj(W_q), proj(W_k), proj(W_v))
            beta = jax.nn.sigmoid(beta_param).reshape(1, H, 1, 1)
            causal = jnp.triu(jnp.ones((SEG, SEG), dtype=bool), k=1)
            inv_sqrt_dk = 1.0 / jnp.sqrt(jnp.asarray(dk, x.dtype))
            M0 = jnp.zeros((B, H, dk, dk), dtype=x.dtype)
            z0 = jnp.zeros((B, H, dk), dtype=x.dtype)

            def step(carry, qkv):
                M, z = carry
                q, k, v = qkv
                sq = _sigma(q)
                denom_q = jnp.sum(sq * z[:, :, None, :], axis=-1, keepdims=True) + EPS
                A_mem = jnp.matmul(sq, M) / denom_q
                scores = jnp.matmul(q, jnp.swapaxes(k, -2, -1)) * inv_sqrt_dk
                scores = jnp.where(causal, -jnp.inf, scores)
                A_dot = jnp.matmul(jax.nn.softmax(scores, axis=-1), v)
                A_s = beta * A_mem + (1.0 - beta) * A_dot
                sk = _sigma(k)
                denom_k = jnp.sum(sk * z[:, :, None, :], axis=-1, keepdims=True) + EPS
                V_prev = jnp.matmul(sk, M) / denom_k
                M_new = M + jnp.einsum('bhtk,bhtv->bhkv', sk, v - V_prev)
                z_new = z + jnp.sum(sk, axis=-2)
                return ((M_new, z_new), A_s)
            (M, z), outs = jax.lax.scan(step, (M0, z0), (Qs, Ks, Vs))
            out = outs.transpose(1, 3, 0, 2, 4).reshape(B, S * SEG, H, dk)
            out = outs.transpose(1, 2, 0, 3, 4).reshape(B, H, T, dk)
            out = out.transpose(0, 2, 1, 3).reshape(B, T, D)
            out = out @ W_o.T
            return (out, M.mean(0), z.mean(0))

        def _reference_tuple_inner(x, W_q, W_k, W_v, W_o, beta_param):
            return _infini_attention(x, W_q, W_k, W_v, W_o, beta_param)
        return _reference_tuple_inner(x, W_q, W_k, W_v, W_o, beta_param)[0]

    def _L0_ffn_ref(x, Wq, bq, Wk, bk, Wv, bv, Wp, bp, Wr, br, Ws, bs, temperature, query_embedding):
        import jax, jax.numpy as jnp
        import numpy as np
        import math
        DIM = 256
        NUM_HEADS = 16
        SHARED_HEADS = 1
        ROUTED_HEADS = 3
        HEAD_DIM = DIM // NUM_HEADS
        B, N = (2, 512)
        Bsz, Nn, C = x.shape
        H, hd = (NUM_HEADS, HEAD_DIM)

        def heads(W, b):
            y = x @ W.T + b
            return y.reshape(Bsz, Nn, H, hd).transpose(0, 2, 1, 3)
        q = heads(Wq, bq)
        k = heads(Wk, bk)
        v = heads(Wv, bv)
        q_norm = q / jnp.linalg.norm(q, axis=-1, keepdims=True)
        q_scaled = (q_norm + query_embedding[None]) * jax.nn.softplus(temperature)[None]
        attn = jnp.einsum('bhqd,bhkd->bhqk', q_scaled, k) / math.sqrt(hd)
        attn = jax.nn.softmax(attn, axis=-1)
        h = jnp.einsum('bhqk,bhkd->bhqd', attn, v)
        h = h.transpose(0, 2, 1, 3).reshape(Bsz, Nn, C)
        gates = jax.nn.softmax(h @ Wr.T + br, axis=-1)
        _, idx = jax.lax.top_k(gates, ROUTED_HEADS)
        mask = jax.nn.one_hot(idx, H - SHARED_HEADS, dtype=gates.dtype).sum(axis=-2)
        routed_gates = gates * mask * ROUTED_HEADS
        sw = jax.nn.softmax(h @ Ws.T + bs, axis=-1)
        shared_gates = sw * SHARED_HEADS
        weight_0 = sw * 2.0
        shared_gates = weight_0[..., 0:1] * shared_gates
        routed_gates = weight_0[..., 1:2] * routed_gates
        masked_gates = jnp.concatenate([shared_gates, routed_gates], axis=-1)
        out = h * masked_gates.sum(axis=-1, keepdims=True)
        return out @ Wp.T + bp

    def _L1_xattn_ref(x, context, ln_gamma, ln_beta, w_q, w_kv, w_out, b_out, gate):
        import jax, jax.numpy as jnp
        import numpy as np
        DIM = 256
        NUM_HEADS = 16
        DIM_HEAD = 64
        INNER = NUM_HEADS * DIM_HEAD
        SCALE = DIM_HEAD ** (-0.5)

        def _layernorm(x, gamma, beta, eps=1e-05):
            mu = jnp.mean(x, axis=-1, keepdims=True)
            var = jnp.mean(jnp.square(x - mu), axis=-1, keepdims=True)
            return (x - mu) * jax.lax.rsqrt(var + eps) * gamma + beta
        B, SQ, _ = x.shape
        SK = context.shape[1]
        xn = _layernorm(x, ln_gamma, ln_beta)
        q = (xn @ w_q).reshape(B, SQ, NUM_HEADS, DIM_HEAD)
        kv = context @ w_kv
        k, v = jnp.split(kv, 2, axis=-1)
        k = k.reshape(B, SK, NUM_HEADS, DIM_HEAD)
        v = v.reshape(B, SK, NUM_HEADS, DIM_HEAD)
        scores = jnp.einsum('bqhd,bkhd->bhqk', q * SCALE, k)
        attn = jax.nn.softmax(scores, axis=-1)
        out = jnp.einsum('bhqk,bkhd->bqhd', attn, v).reshape(B, SQ, INNER)
        out = out @ w_out + b_out
        return out * jnp.tanh(gate[0])

    def _L1_attn_ref(src, in_proj_w, conv_w, conv_b, x_proj_w, dt_proj_w, dt_proj_b, A_log, Dp, out_proj_w, mnorm_g, mnorm_b, n1_g, n1_b, n2_g, n2_b, n3_g, n3_b, ffn_w1, ffn_w2, fe_w, fe_b):
        import jax, jax.numpy as jnp
        import numpy as np
        from jax import lax
        D_MODEL = 256
        D_IN = 256
        N_STATE = 16
        DT_RANK = 64
        D_FFN = 1024
        BATCH, SEQ = (2, 512)

        def _ln(x, g, b, eps=1e-05):
            m = x.mean(-1, keepdims=True)
            v = ((x - m) ** 2).mean(-1, keepdims=True)
            return (x - m) / jnp.sqrt(v + eps) * g + b

        def _mamba(x, in_proj_w, conv_w, conv_b, x_proj_w, dt_proj_w, dt_proj_b, A_log, Dp, out_proj_w):
            B, L, _ = x.shape
            xz = x @ in_proj_w.T
            x_in, z = jnp.split(xz, 2, axis=-1)
            x_prev = jnp.pad(x_in, ((0, 0), (1, 0), (0, 0)))[:, :L]
            x_c = jax.nn.silu(x_prev * conv_w[:, 0] + x_in * conv_w[:, 1] + conv_b)
            x_dbl = x_c @ x_proj_w.T
            dt, Bm, Cm = jnp.split(x_dbl, [DT_RANK, DT_RANK + N_STATE], axis=-1)
            delta = jax.nn.softplus(dt @ dt_proj_w.T + dt_proj_b)
            A = -jnp.exp(A_log)
            deltaA = jnp.exp(delta[..., None] * A)
            dBu = delta[..., None] * Bm[:, :, None, :] * x_c[..., None]

            def step(h, t):
                dA_t, dBu_t, C_t = t
                h = dA_t * h + dBu_t
                y = jnp.einsum('bdn,bn->bd', h, C_t)
                return (h, y)
            h0 = jnp.zeros((B, D_IN, N_STATE), x.dtype)
            _, ys = lax.scan(step, h0, (deltaA.transpose(1, 0, 2, 3), dBu.transpose(1, 0, 2, 3), Cm.transpose(1, 0, 2)))
            y = ys.transpose(1, 0, 2)
            y = (y + x_c * Dp) * jax.nn.silu(z)
            return y @ out_proj_w.T
        h = _mamba(_ln(src, n1_g, n1_b), in_proj_w, conv_w, conv_b, x_proj_w, dt_proj_w, dt_proj_b, A_log, Dp, out_proj_w)
        src = src + _ln(h, mnorm_g, mnorm_b)
        f = _ln(src, n2_g, n2_b) @ ffn_w1.T
        f = jnp.where(f >= 0, f, 0.01 * f) @ ffn_w2.T
        src = src + f
        src = src + (_ln(src, n3_g, n3_b) @ fe_w.T + fe_b)
        return src

    def _L1_ffn_ref(x, W1, b1, W2, b2):
        import jax, jax.numpy as jnp
        import numpy as np
        QB = 127.0
        EPS = 1e-05

        def _ste(x, q):
            return x + jax.lax.stop_gradient(q - x)

        def bitlinear(x, W, b):
            w_scale = jnp.clip(jnp.mean(jnp.abs(W)), EPS, None)
            Wq = _ste(W, jnp.clip(jnp.round(W / w_scale), -1.0, 1.0) * w_scale)
            x_scale = jnp.clip(jnp.max(jnp.abs(x), axis=-1, keepdims=True), EPS, None)
            xq = _ste(x, jnp.clip(jnp.round(x * (QB / x_scale)), -QB - 1.0, QB) * (x_scale / QB))
            return jnp.einsum('bnd,hd->bnh', xq, Wq) + b
        h = bitlinear(x, W1, b1)
        h = jax.nn.gelu(h, approximate=False)
        return bitlinear(h, W2, b2)

    def _L2_xattn_ref(query, key, value, Wq, bq, Wk, bk, Wv, bv, Wo, bo):
        import jax, jax.numpy as jnp
        import numpy as np
        D_MODEL = 256
        NUM_HEADS = 16
        D_K = D_MODEL // NUM_HEADS
        B, Tq, _ = query.shape
        Tk = key.shape[1]
        Q = (query @ Wq + bq).reshape(B, Tq, NUM_HEADS, D_K).transpose(0, 2, 1, 3)
        K = (key @ Wk + bk).reshape(B, Tk, NUM_HEADS, D_K).transpose(0, 2, 1, 3)
        V = (value @ Wv + bv).reshape(B, Tk, NUM_HEADS, D_K).transpose(0, 2, 1, 3)
        scores = jnp.einsum('bhtd,bhsd->bhts', Q, K) / jnp.sqrt(jnp.float32(D_K))
        attn = jax.nn.softmax(scores, axis=-1)
        ctx = jnp.einsum('bhts,bhsd->bhtd', attn, V)
        ctx = ctx.transpose(0, 2, 1, 3).reshape(B, Tq, D_MODEL)
        return ctx @ Wo + bo

    def _L2_attn_ref(hidden_states, Wq, Wk, Wv, Wb, conv_q_w, conv_k_w, conv_v_w, ms_w3, ms_w15, ms_w31, kernel_mix_w, channel_mixer_w, fusion_w1, fusion_b1, fusion_w2, fusion_b2, o_norm_w, Wo):
        import jax, jax.numpy as jnp
        import numpy as np
        CHUNK = 32
        H = 4

        def silu(x):
            return x * jax.nn.sigmoid(x)

        def l2norm(x):
            return x * jax.lax.rsqrt(jnp.sum(x * x, -1, keepdims=True) + 1e-06)

        def dwconv_causal(x_cl, w):
            k = w.shape[1]
            xp = jnp.pad(x_cl, ((0, 0), (0, 0), (k - 1, 0)))
            return jax.lax.conv_general_dilated(xp, w[:, None, :], (1,), 'VALID', dimension_numbers=('NCH', 'OIH', 'NCH'), feature_group_count=x_cl.shape[1])

        def short_conv_silu(x_bld, w):
            y = dwconv_causal(jnp.swapaxes(x_bld, 1, 2), w)
            return silu(jnp.swapaxes(y, 1, 2))

        def delta_rule_chunkwise(q, k, v, beta, chunk=CHUNK):
            b, h, L, dk = q.shape
            dv = v.shape[-1]
            pad = -L % chunk
            if pad:
                q, k, v = (jnp.pad(t, ((0, 0), (0, 0), (0, pad), (0, 0))) for t in (q, k, v))
                beta = jnp.pad(beta, ((0, 0), (0, 0), (0, pad)))
            n = (L + pad) // chunk
            q = l2norm(q)
            k = l2norm(k)
            v = v * beta[..., None]
            kb = k * beta[..., None]
            ch = lambda x: x.reshape(b, h, n, chunk, x.shape[-1])
            qc, kc, vc, kbc = map(ch, (q, k, v, kb))
            idx = jnp.arange(chunk)
            strict_lower = (idx[:, None] > idx[None, :]).astype(q.dtype)
            incl_lower = (idx[:, None] >= idx[None, :]).astype(q.dtype)
            attn = -jnp.einsum('bhncd,bhned->bhnce', kbc, kc) * strict_lower
            for i in range(1, chunk):
                upd = jnp.einsum('...j,...ji->...i', attn[..., i, :], attn[..., :, :i])
                attn = attn.at[..., i, :i].add(upd)
            attn = attn + jnp.eye(chunk, dtype=q.dtype)
            u = attn @ vc
            w = attn @ kbc
            xs = tuple((jnp.moveaxis(t, 2, 0) for t in (qc, kc, u, w)))
            S0 = jnp.zeros((b, h, dk, dv), q.dtype)

            def step(S, x):
                qi, ki, ui, wi = x
                a_loc = jnp.einsum('bhcd,bhed->bhce', qi, ki) * incl_lower
                ui = ui - wi @ S
                oi = qi @ S + a_loc @ ui
                S = S + jnp.einsum('bhcd,bhcv->bhdv', ki, ui)
                return (S, oi)
            S, o = jax.lax.scan(step, S0, xs)
            o = jnp.moveaxis(o, 0, 2).reshape(b, h, n * chunk, dv)[:, :, :L]
            return (o, S)

        def multiscale_conv(v, ms_w3, ms_w15, ms_w31, kernel_mix_w, channel_mixer_w):
            b, l, h, d = v.shape
            x = jnp.swapaxes(v.reshape(b, l, h * d), 1, 2)
            outs = [dwconv_causal(x, w) for w in (ms_w3, ms_w15, ms_w31)]
            y = jnp.concatenate(outs, axis=1)
            y = y.reshape(b, h, 3 * d, l).transpose(0, 3, 1, 2)
            y = y @ kernel_mix_w
            y = (y.reshape(b, l, h * d) @ channel_mixer_w).reshape(b, l, h, d)
            return y

        def _forward(hidden_states, Wq, Wk, Wv, Wb, conv_q_w, conv_k_w, conv_v_w, ms_w3, ms_w15, ms_w31, kernel_mix_w, channel_mixer_w, fusion_w1, fusion_b1, fusion_w2, fusion_b2, o_norm_w, Wo):
            b, L, D = hidden_states.shape
            h = H
            dk = Wq.shape[1] // h
            dv = Wv.shape[1] // h
            q = short_conv_silu(hidden_states @ Wq, conv_q_w).reshape(b, L, h, dk)
            k = short_conv_silu(hidden_states @ Wk, conv_k_w).reshape(b, L, h, dk)
            v = short_conv_silu(hidden_states @ Wv, conv_v_w).reshape(b, L, h, dv)
            v_direct = v
            beta = jax.nn.sigmoid(hidden_states @ Wb)
            tr = lambda x: jnp.swapaxes(x, 1, 2)
            delta_out, _S = delta_rule_chunkwise(tr(q), tr(k), tr(v), tr(beta))
            delta_out = jnp.swapaxes(delta_out, 1, 2)
            ms_out = multiscale_conv(v_direct, ms_w3, ms_w15, ms_w31, kernel_mix_w, channel_mixer_w)
            bn = lambda x: jnp.mean(jnp.abs(x), -1)
            gate_features = jnp.concatenate([hidden_states, bn(ms_out), bn(delta_out), bn(v_direct)], -1)
            hdn = jax.nn.gelu(gate_features @ fusion_w1 + fusion_b1, approximate=False)
            logits = (hdn @ fusion_w2 + fusion_b2).reshape(b, L, h, 3)
            wts = jax.nn.softmax(logits, -1)
            o = wts[..., 0:1] * ms_out + wts[..., 1:2] * delta_out + wts[..., 2:3] * v_direct
            o = o * jax.lax.rsqrt(jnp.mean(o * o, -1, keepdims=True) + 1e-05) * o_norm_w
            return o.reshape(b, L, h * dv) @ Wo
        return _forward(hidden_states, Wq, Wk, Wv, Wb, conv_q_w, conv_k_w, conv_v_w, ms_w3, ms_w15, ms_w31, kernel_mix_w, channel_mixer_w, fusion_w1, fusion_b1, fusion_w2, fusion_b2, o_norm_w, Wo)

    def _L2_ffn_ref(x, prototypes, B, A, bias, temp):
        import jax, jax.numpy as jnp
        import numpy as np
        IN_DIM, OUT_DIM, N_PROTO, RANK = (256, 256, 32, 16)
        lead = x.shape[:-1]
        xf = x.reshape(-1, IN_DIM)
        x2 = jnp.sum(xf * xf, axis=1, keepdims=True)
        p2 = jnp.sum(prototypes * prototypes, axis=1)
        d2 = x2 + p2[None, :] - 2.0 * (xf @ prototypes.T)
        dists = jnp.sqrt(jnp.maximum(d2, 0.0))
        t = jnp.maximum(jnp.abs(temp), 0.1)
        w = jax.nn.softmax(-dists / t, axis=1)
        topw, topi = jax.lax.top_k(w, 2)
        topw = topw / jnp.sum(topw, axis=1, keepdims=True)
        out = jnp.zeros((xf.shape[0], OUT_DIM), dtype=xf.dtype)
        for tslot in range(2):
            idx = topi[:, tslot]
            wt = topw[:, tslot:tslot + 1]
            h = jnp.einsum('nri,ni->nr', B[idx], xf)
            y = jnp.einsum('nor,nr->no', A[idx], h) + bias[idx]
            out = out + wt * y
        return out.reshape(*lead, OUT_DIM)

    def _L3_xattn_ref(x, mem_seq, mem_mask, rms_scale, q_w, kv_w, out_w):
        import jax, jax.numpy as jnp
        import numpy as np
        NUM_HEADS, NUM_KV, HEAD_DIM, WIDTH = (4, 1, 64, 256)
        MASK_FILL = -2.3819763e+38

        def _apply_rope(x, positions, max_wavelength=10000.0):
            d = x.shape[-1]
            freq_exp = 2.0 / d * jnp.arange(d // 2, dtype=jnp.float32)
            timescale = max_wavelength ** freq_exp
            radians = positions[..., None].astype(jnp.float32) / timescale
            radians = radians[..., None, :]
            sin, cos = (jnp.sin(radians), jnp.cos(radians))
            x1, x2 = jnp.split(x, 2, axis=-1)
            out = jnp.concatenate([x1 * cos - x2 * sin, x2 * cos + x1 * sin], axis=-1)
            return out.astype(x.dtype)

        def _rmsnorm(x, scale):
            var = jnp.mean(jnp.square(x.astype(jnp.float32)), axis=-1, keepdims=True)
            normed = x * jax.lax.rsqrt(var + 1e-06)
            return (normed * (1 + scale)).astype(x.dtype)
        B, S, _ = mem_seq.shape
        T = x.shape[1]
        G = NUM_HEADS // NUM_KV
        xn = _rmsnorm(x, rms_scale)
        mn = _rmsnorm(mem_seq, rms_scale)
        q = jnp.einsum('BTD,NDH->BTNH', xn, q_w)
        kv = jnp.einsum('BSD,cKDH->cBSKH', mn, kv_w)
        k, v = (kv[0], kv[1])
        q_pos = jnp.broadcast_to(jnp.arange(S, T + S), (B, T))
        k_pos = jnp.broadcast_to(jnp.arange(S), (B, S))
        q = _apply_rope(q, q_pos) * HEAD_DIM ** (-0.5)
        k = _apply_rope(k, k_pos)
        q = q.reshape(B, T, NUM_KV, G, HEAD_DIM)
        logits = jnp.einsum('BTKGH,BSKH->BKGTS', q, k, preferred_element_type=jnp.float32)
        masked = jnp.where(mem_mask[:, None, None, None, :], logits, MASK_FILL)
        probs = jax.nn.softmax(masked, axis=-1).astype(x.dtype)
        enc = jnp.einsum('BKGTS,BSKH->BTKGH', probs, v).reshape(B, T, NUM_HEADS, HEAD_DIM)
        return jnp.einsum('BTNH,NHD->BTD', enc, out_w)

    def _L3_attn_ref(x, W_in, conv_w, conv_b, W_x, W_dt, b_dt, A_log, D, W_out):
        import jax, jax.numpy as jnp
        import numpy as np
        BATCH, L, D_MODEL = (2, 256, 256)
        D_STATE, D_CONV, EXPAND = (16, 4, 2)
        D_INNER = EXPAND * D_MODEL
        DT_RANK = max(1, -(-D_MODEL // 16))

        def _forward(x, W_in, conv_w, conv_b, W_x, W_dt, b_dt, A_log, D, W_out):
            xv = x @ W_in
            xc = jnp.transpose(xv, (0, 2, 1))
            xc = jax.lax.conv_general_dilated(xc, conv_w, window_strides=(1,), padding=[(D_CONV - 1, 0)], dimension_numbers=('NCH', 'OIH', 'NCH'), feature_group_count=D_INNER)
            xv = jnp.transpose(xc, (0, 2, 1)) + conv_b
            xv = jax.nn.silu(xv)
            ssm = xv @ W_x
            dt_raw = ssm[..., :DT_RANK]
            Bp = ssm[..., DT_RANK:DT_RANK + D_STATE]
            Cp = ssm[..., DT_RANK + D_STATE:]
            delta = jax.nn.softplus(dt_raw @ W_dt + b_dt)
            A = -jnp.exp(A_log)
            dA = jnp.exp(delta[..., None] * A)
            dBx = delta[..., None] * Bp[:, :, None, :] * xv[..., None]

            def comb(c1, c2):
                a1, b1 = c1
                a2, b2 = c2
                return (a1 * a2, a2 * b1 + b2)
            _, h = jax.lax.associative_scan(comb, (dA, dBx), axis=1)
            y = jnp.einsum('bldn,bln->bld', h, Cp)
            y = y + xv * D
            return y @ W_out
        return _forward(x, W_in, conv_w, conv_b, W_x, W_dt, b_dt, A_log, D, W_out)

    def _L3_ffn_ref(x, w_up, w_down):
        import jax, jax.numpy as jnp
        import numpy as np
        EPS = 1e-08

        def _ternary_linear(x, w):
            alpha = jnp.mean(jnp.abs(w))
            w_t = jnp.sign(w) * (jnp.abs(w) > 0.5 * alpha).astype(w.dtype)
            w_q = w + jax.lax.stop_gradient(w_t - w)
            d = x.shape[-1]
            rms = jnp.sqrt(jnp.sum(x * x, axis=-1, keepdims=True)) / jnp.sqrt(jnp.asarray(d, x.dtype))
            x_norm = x / (rms + EPS)
            return jnp.einsum('bsd,fd->bsf', x_norm, w_q)
        h = jax.nn.gelu(_ternary_linear(x, w_up), approximate=False)
        return _ternary_linear(h, w_down)
    x = x + _L0_xattn_ref(_layernorm(x, axis=-1), ctx_1024, ctx_1024, mask_BxS2_bf1, 64, L0_xattn_wq_w, L0_xattn_wq_b, L0_xattn_wk_w, L0_xattn_wk_b, L0_xattn_wv_w, L0_xattn_wv_b, L0_xattn_wo_w, L0_xattn_wo_b)
    x = x + _L0_attn_ref(_layernorm(x, axis=-1), L0_attn_W_q, L0_attn_W_k, L0_attn_W_v, L0_attn_W_o, L0_attn_beta_param)
    x = x + _L0_ffn_ref(_layernorm(x, axis=-1), L0_ffn_Wq, L0_ffn_bq, L0_ffn_Wk, L0_ffn_bk, L0_ffn_Wv, L0_ffn_bv, L0_ffn_Wp, L0_ffn_bp, L0_ffn_Wr, L0_ffn_br, L0_ffn_Ws, L0_ffn_bs, L0_ffn_temperature, L0_ffn_query_embedding)
    x = x + _L1_xattn_ref(_layernorm(x, axis=-1), ctx_1024, L1_xattn_ln_gamma, L1_xattn_ln_beta, L1_xattn_w_q, L1_xattn_w_kv, L1_xattn_w_out, L1_xattn_b_out, L1_xattn_gate)
    x = x + _L1_attn_ref(_layernorm(x, axis=-1), L1_attn_in_proj_w, L1_attn_conv_w, L1_attn_conv_b, L1_attn_x_proj_w, L1_attn_dt_proj_w, L1_attn_dt_proj_b, L1_attn_A_log, L1_attn_Dp, L1_attn_out_proj_w, L1_attn_mnorm_g, L1_attn_mnorm_b, L1_attn_n1_g, L1_attn_n1_b, L1_attn_n2_g, L1_attn_n2_b, L1_attn_n3_g, L1_attn_n3_b, L1_attn_ffn_w1, L1_attn_ffn_w2, L1_attn_fe_w, L1_attn_fe_b)
    x = x + _L1_ffn_ref(_layernorm(x, axis=-1), L1_ffn_W1, L1_ffn_b1, L1_ffn_W2, L1_ffn_b2)
    x = x + _L2_xattn_ref(_layernorm(x, axis=-1), ctx_1024, ctx_1024, L2_xattn_Wq, L2_xattn_bq, L2_xattn_Wk, L2_xattn_bk, L2_xattn_Wv, L2_xattn_bv, L2_xattn_Wo, L2_xattn_bo)
    x = x + _L2_attn_ref(_layernorm(x, axis=-1), L2_attn_Wq, L2_attn_Wk, L2_attn_Wv, L2_attn_Wb, L2_attn_conv_q_w, L2_attn_conv_k_w, L2_attn_conv_v_w, L2_attn_ms_w3, L2_attn_ms_w15, L2_attn_ms_w31, L2_attn_kernel_mix_w, L2_attn_channel_mixer_w, L2_attn_fusion_w1, L2_attn_fusion_b1, L2_attn_fusion_w2, L2_attn_fusion_b2, L2_attn_o_norm_w, L2_attn_Wo)
    x = x + _L2_ffn_ref(_layernorm(x, axis=-1), L2_ffn_prototypes, L2_ffn_B, L2_ffn_A, L2_ffn_bias, L2_ffn_temp)
    x = x + _L3_xattn_ref(_layernorm(x, axis=-1), ctx_1024, mask_BxS2_bk0, L3_xattn_rms_scale, L3_xattn_q_w, L3_xattn_kv_w, L3_xattn_out_w)
    x = x + _L3_attn_ref(_layernorm(x, axis=-1), L3_attn_W_in, L3_attn_conv_w, L3_attn_conv_b, L3_attn_W_x, L3_attn_W_dt, L3_attn_b_dt, L3_attn_A_log, L3_attn_D, L3_attn_W_out)
    x = x + _L3_ffn_ref(_layernorm(x, axis=-1), L3_ffn_w_up, L3_ffn_w_down)
    return x

_drawn_inputs = setup_inputs


def setup_inputs(seed=0):
    import zlib

    import numpy as np

    out = dict(_drawn_inputs(seed))
    spreads = {'L0_xattn_wq_b': (0.0, 0.1),
     'L0_xattn_wk_b': (0.0, 0.8),
     'L0_xattn_wv_b': (0.0, 0.1),
     'L0_xattn_wo_b': (0.0, 0.1),
     'L0_attn_beta_param': (0.0, 0.563),
     'L0_ffn_temperature': (4.151041507720947, 0.6),
     'L1_xattn_ln_gamma': (1.0, 0.6),
     'L1_xattn_ln_beta': (0.0, 0.8),
     'L1_xattn_b_out': (0.0, 0.1),
     'L1_attn_conv_b': (0.0, 0.1),
     'L1_attn_Dp': (1.0, 0.2),
     'L1_attn_mnorm_g': (1.0, 0.2),
     'L1_attn_mnorm_b': (0.0, 0.1),
     'L1_attn_n1_g': (1.0, 0.2),
     'L1_attn_n1_b': (0.0, 0.1),
     'L1_attn_n2_g': (1.0, 0.6),
     'L1_attn_n2_b': (0.0, 0.8),
     'L1_attn_n3_g': (1.0, 0.596),
     'L1_attn_n3_b': (0.0, 0.568),
     'L1_attn_fe_b': (0.0, 0.1),
     'L1_ffn_b1': (0.0, 0.8),
     'L1_ffn_b2': (0.0, 0.1),
     'L2_xattn_bq': (0.0, 0.8),
     'L2_xattn_bk': (0.0, 0.8),
     'L2_xattn_bv': (0.0, 0.1),
     'L2_xattn_bo': (0.0, 0.1),
     'L2_attn_fusion_b1': (0.0, 0.8),
     'L2_attn_o_norm_w': (1.0, 0.2),
     'L2_ffn_bias': (0.0, 0.337),
     'L3_attn_D': (1.0, 0.6)}
    factors = {'L0_ffn_bq': 8.0,
     'L0_ffn_bk': 8.0,
     'L0_ffn_Wr': 8.0,
     'L0_ffn_br': 8.0,
     'L0_ffn_Ws': 8.0,
     'L0_ffn_bs': 8.0,
     'L0_ffn_query_embedding': 8.0,
     'L1_attn_x_proj_w': 8.0,
     'L1_attn_dt_proj_w': 8.0,
     'L1_attn_dt_proj_b': 8.0,
     'L1_attn_A_log': 8.0,
     'L1_ffn_W1': 2.948,
     'L2_attn_ms_w3': 6.309,
     'L2_attn_ms_w15': 3.046,
     'L2_ffn_B': 8.0,
     'L2_ffn_A': 8.0,
     'L3_xattn_rms_scale': 8.0,
     'L3_attn_W_in': 8.0,
     'L3_attn_conv_w': 8.0,
     'L3_attn_conv_b': 8.0,
     'L3_attn_W_x': 8.0,
     'L3_attn_W_dt': 8.0,
     'L3_attn_b_dt': 8.0,
     'L3_attn_A_log': 8.0,
     'L3_attn_W_out': 8.0}
    for name, (base, spread) in spreads.items():
        noise = np.random.default_rng([zlib.crc32(name.encode()), seed]).standard_normal(out[name].shape)
        drawn = base * np.exp(spread * noise) if base else spread * noise
        out[name] = jnp.asarray(drawn.astype(out[name].dtype))
    for name, factor in factors.items():
        out[name] = (out[name] * factor).astype(out[name].dtype)
    return out
```

```python
from contextlib import ExitStack

import numpy as np
import concourse.bass as bass
from concourse import mybir

F32 = mybir.dt.float32
BF16 = mybir.dt.bfloat16
U8 = mybir.dt.uint8
ALU = mybir.AluOpType
ACT = mybir.ActivationFunctionType
AX_X = mybir.AxisListType.X

P = 128
BATCH, SEQ, D = 16, 64, 256
TOKENS = BATCH * SEQ
TILES = TOKENS // P
PER_TILE = P // SEQ
CTX = 256
CTX_TILE = PER_TILE * CTX
CHUNKS = D // P
BANK = 512
LN_EPS = 1e-5
NEG = float(np.finfo(np.float32).min)
WMAX = 8500

LAYERS = [0, 1, 2, 3, 4, 5, 6, 7, 8, 9, 10, 11]


class Core:

    def __init__(self, nc, ctx, dram):
        self.nc, self.ctx, self.dram = nc, ctx, dram
        self.sems, self.used = {}, set()
        self.prefix = ""
        self.x = self.sb(ctx, "x_tok", [P, TILES, D])
        self.xn = self.sb(ctx, "xn_tok", [P, TILES, D])
        self.xnT = self.sb(ctx, "xn_feat", [P, CHUNKS, TOKENS])
        self.ctxT = self.sb(ctx, "ctx_feat", [P, CHUNKS, BATCH * CTX])
        self.ident = self.sb(ctx, "ident", [P, P])
        self.hmask16 = self.sb(ctx, "hmask16", [P, 8])
        self.fold = self.sb(ctx, "fold", [P, SEQ])
        self.hmask64 = self.sb(ctx, "hmask64", [P, 2])
        self.stats = self.sb(ctx, "ln_stats", [P, TILES, 6])
        self.meanvar = self.sb(ctx, "ln_meanvar", [P, TILES, 2])
        self.rstd = self.sb(ctx, "ln_rstd", [P, TILES])
        self.weights = [self.sb(ctx, f"weights{i}", [P, WMAX]) for i in range(2)]
        self.banks = ctx.enter_context(nc.psum_tensor("banks", [P, 8, BANK], F32))

    def sb(self, ctx, name, shape, dt=F32):
        return ctx.enter_context(self.nc.sbuf_tensor(f"{self.prefix}{name}", shape, dt))

    def sem(self, name):
        if name not in self.sems:
            self.sems[name] = self.ctx.enter_context(self.nc.semaphore(name))
        self.used.add(name)
        return self.sems[name]

    def clear(self):
        names = sorted(self.used)
        self.used = set()
        with self.nc.Block() as block:

            @block.sync
            def _(sp):
                for name in names:
                    sp.sem_clear(self.sems[name])


def linker(eng, sem, start=0):
    count = [start]

    def link(ins):
        count[0] += 1
        ins.then_inc(sem, 1)
        eng.wait_ge(sem, count[0])

    return link


def normalize(k, src=None, turn=True, scale=None, shift=None):
    src = k.x if src is None else src
    nc = k.nc
    with nc.Block() as block:

        @block.vector
        def _(dve):
            link = linker(dve, k.sem("dve_step"))
            for t in range(TILES):
                last = nc.vector.bn_stats(k.stats[:, t, :], src[:, t, :])
            link(last)
            for t in range(TILES):
                last = nc.vector.bn_aggr(k.meanvar[:, t, :], k.stats[:, t, :])
            link(last)
            nc.vector.tensor_scalar(k.rstd[:, :], k.meanvar[:, :, 1], LN_EPS, None, ALU.add).then_inc(k.sem("var_ready"), 1)
            dve.wait_ge(k.sem("std_ready"), 1)
            link(nc.vector.reciprocal(k.rstd[:, :], k.rstd[:, :]))
            for t in range(TILES):
                nc.vector.tensor_scalar(k.xn[:, t, :], src[:, t, :], k.meanvar[:, t, 0:1], k.rstd[:, t:t + 1],
                                        ALU.subtract, ALU.mult).then_inc(k.sem("xn_ready"), 1)

        @block.scalar
        def _(act):
            act.wait_ge(k.sem("var_ready"), 1)
            nc.scalar.activation(k.rstd[:, :], k.rstd[:, :], ACT.Sqrt).then_inc(k.sem("std_ready"), 1)
            for h in range(TILES // 4 if turn else 0):
                for c in range(CHUNKS):
                    act.wait_ge(k.sem("xnT_in_psum"), CHUNKS * h + c + 1)
                    out, raw = k.xnT[:, c, h * BANK:(h + 1) * BANK], k.banks[:, CHUNKS * h + c, :]
                    if scale is None:
                        nc.scalar.copy(out, raw)
                    else:
                        nc.scalar.activation(out, raw, ACT.Identity, bias=shift[:, c:c + 1], scale=scale[:, c:c + 1])

        @block.tensor
        def _(pe):
            for h in range(TILES // 4 if turn else 0):
                pe.wait_ge(k.sem("xn_ready"), 4 * (h + 1))
                for c in range(CHUNKS):
                    for t in range(4):
                        last = nc.tensor.transpose(k.banks[:, CHUNKS * h + c, t * P:(t + 1) * P],
                                                   k.xn[:, 4 * h + t, c * P:(c + 1) * P], k.ident[:, :])
                    last.then_inc(k.sem("xnT_in_psum"), 1)
    k.clear()


def project(k, jobs, src=None, chunks=CHUNKS, tokens=TOKENS):
    nc = k.nc
    src = k.xnT if src is None else src
    halves = [(j, h) for j in range(len(jobs)) for h in range(tokens // BANK)]
    with nc.Block() as block:

        @block.tensor
        def _(pe):
            for n, (j, h) in enumerate(halves):
                w, col, out, _, _ = jobs[j]
                m = out.shape[0]
                if n >= 4:
                    pe.wait_ge(k.sem("product_used"), n - 3)
                for c in range(chunks):
                    last = nc.tensor.matmul(k.banks[0:m, n % 4, :], w[:, c, col:col + m], src[:, c, h * BANK:(h + 1) * BANK],
                                            start=(c == 0), stop=(c == chunks - 1))
                last.then_inc(k.sem("product_ready"), 1)

        @block.scalar
        def _(act):
            for n, (j, h) in enumerate(halves):
                _, _, out, bias, func = jobs[j]
                m = out.shape[0]
                act.wait_ge(k.sem("product_ready"), n + 1)
                nc.scalar.activation(out[:, h * BANK:(h + 1) * BANK], k.banks[0:m, n % 4, :], func,
                                     bias=0.0 if bias is None else bias).then_inc(k.sem("product_used"), 1)
    k.clear()


def softplus(k, x, e, low):
    nc = k.nc
    with nc.Block() as block:

        @block.scalar
        def _(act):
            nc.scalar.activation(e, x, ACT.Abs).then_inc(k.sem("abs_ready"), 1)
            act.wait_ge(k.sem("abs_ready"), 1)
            nc.scalar.activation(e, e, ACT.Exp, scale=-1.0).then_inc(k.sem("exp_ready"), 1)
            act.wait_ge(k.sem("low_ready"), 1)
            nc.scalar.activation(e, e, ACT.Ln, bias=1.0).then_inc(k.sem("log_ready"), 1)

        @block.vector
        def _(dve):
            link = linker(dve, k.sem("dve_step"))
            dve.wait_ge(k.sem("exp_ready"), 1)
            link(nc.vector.tensor_scalar(low, e, 1.0, 1.0, ALU.add, ALU.subtract))
            nc.vector.tensor_tensor(low, e, low, ALU.subtract).then_inc(k.sem("low_ready"), 1)
            dve.wait_ge(k.sem("low_ready"), 1)
            dve.wait_ge(k.sem("log_ready"), 1)
            link(nc.vector.tensor_tensor(low, low, e, ALU.add))
            nc.vector.scalar_tensor_tensor(x, x, 0.0, low, ALU.max, ALU.add)
    k.clear()




class Attention:

    SLOTS = 4

    def __init__(self, k, ctx, keys, qchunks, kchunks, vfeat, head, pairs, scale, unroll, jobs, copied=False, topk=False, gated=False,
                 split=False):
        self.keys, self.qchunks, self.kchunks, self.head, self.scale = keys, qchunks, kchunks, head, scale
        self.vfeat, self.copied, self.topk, self.unroll, self.split = vfeat, copied, topk, unroll, split
        self.per_seq = len(pairs)
        self.per_tile = PER_TILE * self.per_seq
        self.seqs = 1 if split else PER_TILE
        self.per_unit = self.seqs * self.per_seq
        self.units = unroll * PER_TILE // self.seqs
        self.groups = [(j, b, (j * PER_TILE + b) // self.seqs, b % self.seqs, g)
                       for j in range(unroll) for b in range(PER_TILE) for g in pairs]
        self.kparts = (keys + P - 1) // P
        self.krows = min(keys, P)
        self.rows = 2 * head
        self.exp_lag = 1 if topk else 0
        self.turn_lag, self.out_lag, self.fold_lag = (3, 4, 5) if topk else (2, 3, 4)
        n = len(self.groups)
        self.first = [(kind, 0, i, h) for kind, i, h in jobs]
        self.at = [[] for _ in range(n + self.fold_lag + 3)]
        early = [job for job in jobs if job[0] != "v"]
        late = [job for job in jobs if job[0] == "v"]
        for u in range(1, self.units):
            for m, (kind, i, h) in enumerate(early):
                if kind != "q" or not split:
                    self.at[self.per_unit * (u - 1) + m * self.per_unit // len(early)].append((kind, u, i, h))
                elif u % PER_TILE == 0:
                    self.at[self.per_unit * (u - 1) - 1].append((kind, u // PER_TILE, i, h))
            for m, (kind, i, h) in enumerate(late):
                self.at[self.per_unit * (u - 1) + self.out_lag + m * self.per_unit // len(late)].append((kind, u, i, h))
        for j in range(unroll):
            done = self.per_tile * (j + 1) - 1 + self.fold_lag
            if gated:
                self.at[done].append(("g", j, 0, 0))
            self.at[done + 1].append(("o", j, 0, 0))
        self.order = self.first + [job for step in self.at for job in step]
        self.steps = len(self.at)
        self.place = {job: (s, i, m) for s in range(self.steps) for i in range(self.SLOTS) for m, job in enumerate(self.slot(s, i))}
        self.nk = sum(kind == "k" for kind, _, _ in jobs)
        self.nv = sum(kind == "v" for kind, _, _ in jobs)
        bufs = min(2, self.units)
        self.q_heads = k.sb(ctx, "q_heads", [P, bufs, qchunks, self.seqs, P // head * SEQ])
        self.kT = k.sb(ctx, "kT", [P, bufs, kchunks, self.seqs * keys]) if kchunks else None
        self.v = k.sb(ctx, "v", [P, bufs, self.seqs * self.kparts, vfeat])
        self.moving = k.sb(ctx, "unit_rows", [P, bufs, CHUNKS, self.seqs * keys])
        self.probs = k.sb(ctx, "probs", [P, 2, 4, keys])
        self.probsT = k.sb(ctx, "probsT", [P, 2, self.kparts, BANK])
        self.own = k.sb(ctx, "own_out", [P, 2, 4 * self.rows])
        self.factor = k.sb(ctx, "own_factor", [P, n, 4, 2])
        self.oT = k.sb(ctx, "oT", [P, min(2, unroll), qchunks, P])
        self.rowmax = k.sb(ctx, "rowmax", [P, n, 4])
        self.rowsum = k.sb(ctx, "rowsum", [P, n, 4])
        self.sum = k.sb(ctx, "branch", [P, D])
        self.keys_of = None
        self.oT_scale = self.oT_bias = None

    def score(self, k, g):
        flat = k.banks[:, 2 * (g % 2):2 * (g % 2) + 2, :].rearrange("p b n -> p (b n)")
        return flat[:, 0:4 * self.keys].rearrange("p (i n) -> p i n", i=4)

    def turned(self, k):
        return k.banks[:, 4:4 + self.kparts, :]

    def products(self, k, g):
        return k.banks[:, 6, 0:len(self.groups[g][4]) * self.rows]

    def folded(self, k, g):
        return k.banks[:, 6, 0:len(self.groups[g][4]) * self.rows // P * SEQ]

    def bank_of(self, n):
        if n < len(self.first):
            return 7 if n % 4 == 0 else n % 4
        s, i, m = self.place[self.order[n]]
        return 5 if i == 0 and m == 0 else 4 if i == 3 and m == 1 else 7

    def bank(self, k, kind, j, i, h):
        return k.banks[:, self.bank_of(self.order.index((kind, j, i, h))), :]

    def wait_job(self, k, eng, kind, j, i, h):
        eng.wait_ge(k.sem("job_ready"), self.order.index((kind, j, i, h)) + 1)

    def wait_read(self, k, eng, n):
        kind = self.order[n][0]
        count = sum(1 for job in self.order[:n + 1] if job[0] == kind)
        eng.wait_ge(k.sem({"q": "queries_ready", "k": "keys_ready", "v": "values_ready", "g": "gates_read", "o": "branch_read"}[kind]), count)

    def wait_bank(self, k, eng, kind, j, i, h):
        n = self.order.index((kind, j, i, h))
        before = [m for m in range(n) if self.bank_of(m) == self.bank_of(n)]
        if before:
            self.wait_read(k, eng, before[-1])
        if n >= len(self.first) and self.bank_of(n) != 7:
            s, i, _ = self.place[self.order[n]]
            turned = min(s - self.turn_lag + (i > 1), len(self.groups))
            if turned > 0:
                eng.wait_ge(k.sem("probsT_ready"), turned)

    def wait_turned_banks(self, k, eng, s):
        for bank in (4, 5):
            before = [n for n in range(len(self.first), len(self.order))
                      if self.bank_of(n) == bank and self.place[self.order[n]][0:2] in ((s - 1, 3), (s, 0))]
            if before:
                self.wait_read(k, eng, before[-1])

    def slot(self, s, i):
        jobs = self.at[s]
        return jobs[len(jobs) * i // self.SLOTS:len(jobs) * (i + 1) // self.SLOTS]

    def wait_unit(self, k, eng, sem, u):
        if u >= 2:
            eng.wait_ge(k.sem(sem), self.per_unit * (u - 1))


def attend_pe(k, a, pe, job):
    nc, n = k.nc, len(a.groups)

    def run(jobs):
        for one in jobs:
            a.wait_bank(k, pe, *one)
            job(pe, *one).then_inc(k.sem("job_ready"), 1)

    run(a.first)
    for s in range(a.steps):
        run(a.slot(s, 0))
        g = s - a.fold_lag
        if 0 <= g < n:
            pe.wait_ge(k.sem("own_ready"), g + 1)
            w = len(a.groups[g][4]) * a.rows // P
            for c in range(w):
                last = nc.tensor.matmul(a.folded(k, g)[:, c * SEQ:(c + 1) * SEQ], a.own[:, g % 2, c * P:(c + 1) * P], k.fold[:, :],
                                        start=True, stop=True)
            last.then_inc(k.sem("folded_ready"), 1)
        run(a.slot(s, 1))
        g = s - a.turn_lag
        if 0 <= g < n:
            pairs = a.groups[g][4]
            pe.wait_ge(k.sem("picked_ready" if a.topk else "exp_ready"), g + 1)
            if g >= 1:
                pe.wait_ge(k.sem("probsT_ready"), g)
            a.wait_turned_banks(k, pe, s)
            for part in range(a.kparts):
                for i in range(len(pairs)):
                    last = nc.tensor.transpose(a.turned(k)[0:a.krows, part, i * P:(i + 1) * P],
                                               a.probs[:, g % 2, i, part * P:part * P + a.krows], k.ident[:, :])
            last.then_inc(k.sem("probs_turned"), 1)
        run(a.slot(s, 2))
        if s < n:
            j, b, u, ub, pairs = a.groups[s]
            if s == 0:
                for m in range(max(0, len(a.first) - 4), len(a.first)):
                    a.wait_read(k, pe, m)
            if s % a.per_unit == 0:
                pe.wait_ge(k.sem("q_heads_ready"), (u + 1) * a.qchunks * a.seqs)
                if a.nk:
                    pe.wait_ge(k.sem("keys_ready"), (u + 1) * a.nk)
            if s >= 2:
                pe.wait_ge(k.sem("scores_copied" if a.copied else "exp_ready"), s - 1)
            for i, (qc, kc, vc, row) in enumerate(pairs):
                head = row // a.head
                keys = a.keys_of(j, kc, b) if a.keys_of else a.kT[:, u % 2, kc, ub * a.keys:(ub + 1) * a.keys]
                last = nc.tensor.matmul(a.score(k, s)[:, i, :], a.q_heads[:, u % 2, qc, ub, head * SEQ:(head + 2) * SEQ], keys,
                                        start=True, stop=True)
            last.then_inc(k.sem("scores_ready"), 1)
        run(a.slot(s, 3))
        g = s - a.out_lag
        if 0 <= g < n:
            j, b, u, ub, pairs = a.groups[g]
            if g % a.per_unit == 0:
                pe.wait_ge(k.sem("values_ready"), (u + 1) * a.nv)
            pe.wait_ge(k.sem("probsT_ready"), g + 1)
            if g >= 1:
                pe.wait_ge(k.sem("oT_chunks"), g)
            for i, (_, _, vc, row) in enumerate(pairs):
                for part in range(a.kparts):
                    last = nc.tensor.matmul(a.products(k, g)[:, i * a.rows:(i + 1) * a.rows],
                                            a.probsT[0:a.krows, g % 2, part, i * P:(i + 1) * P],
                                            a.v[0:a.krows, u % 2, ub * a.kparts + part, vc * P + row:vc * P + row + a.rows],
                                            start=(part == 0), stop=(part == a.kparts - 1))
            last.then_inc(k.sem("out_ready"), 1)


def attend_act(k, a, act, job):
    nc, n = k.nc, len(a.groups)

    def run(jobs):
        for one in jobs:
            job(act, *one)

    run(a.first)
    for s in range(a.steps):
        run(a.slot(s, 0))
        g = s - a.fold_lag
        if 0 <= g < n:
            j, b, _, _, pairs = a.groups[g]
            act.wait_ge(k.sem("folded_ready"), g + 1)
            if j >= 2 and g % a.per_tile == 0:
                act.wait_ge(k.sem("branch_read"), j - 1)
            w, c0 = len(pairs) * a.rows // P, pairs[0][0]
            out, src = a.oT[:, j % 2, c0:c0 + w, b * SEQ:(b + 1) * SEQ], a.folded(k, g).rearrange("p (c q) -> p c q", q=SEQ)
            if a.oT_scale is None and a.oT_bias is None:
                nc.scalar.copy(out, src).then_inc(k.sem("oT_chunks"), 1)
            else:
                nc.scalar.activation(out, src, ACT.Identity, scale=1.0 if a.oT_scale is None else a.oT_scale[:, c0:c0 + 1],
                                     bias=0.0 if a.oT_bias is None else a.oT_bias[:, c0:c0 + 1]).then_inc(k.sem("oT_chunks"), 1)
        run(a.slot(s, 1))
        g = s - a.turn_lag
        if 0 <= g < n:
            act.wait_ge(k.sem("probs_turned"), g + 1)
            if g >= 2:
                act.wait_ge(k.sem("out_ready"), g - 1)
            w = len(a.groups[g][4]) * P
            nc.scalar.copy(a.probsT[0:a.krows, g % 2, :, 0:w], a.turned(k)[0:a.krows, :, 0:w]).then_inc(k.sem("probsT_ready"), 1)
        run(a.slot(s, 2))
        if a.topk and s < n:
            act.wait_ge(k.sem("scores_ready"), s + 1)
            if s >= 2:
                act.wait_ge(k.sem("outside_ready"), s - 1)
            nc.scalar.copy(a.masked[:, s % 2, :, :], a.score(k, s)).then_inc(k.sem("scores_copied"), 1)
        g = s - a.exp_lag
        if 0 <= g < n:
            act.wait_ge(k.sem("rowmax_ready"), g + 1)
            if g >= 2:
                act.wait_ge(k.sem("probs_turned"), g - 1)
            for i in range(len(a.groups[g][4])):
                src = a.masked[:, g % 2, i, :] if a.topk else a.probs[:, g % 2, i, :] if a.copied else a.score(k, g)[:, i, :]
                last = nc.scalar.activation(a.probs[:, g % 2, i, :], src, ACT.Exp, bias=a.rowmax[:, g, i:i + 1], scale=a.scale,
                                            accum_out=None if a.topk else a.rowsum[:, g, i:i + 1])
            last.then_inc(k.sem("exp_ready"), 1)
        run(a.slot(s, 3))


def attend_dve(k, a, dve, link, job, mask=None):
    nc, n = k.nc, len(a.groups)

    def run(jobs):
        for one in jobs:
            job(dve, *one)

    run(a.first)
    for s in range(a.steps):
        for i in range(3):
            run(a.slot(s, i))
        g = s - a.exp_lag
        if 0 <= g < n:
            j, b, _, _, pairs = a.groups[g]
            w = len(pairs)
            if a.topk:
                mask(dve, g)
            else:
                dve.wait_ge(k.sem("scores_ready"), g + 1)
                if mask is not None:
                    if g >= 2:
                        dve.wait_ge(k.sem("probs_turned"), g - 1)
                    mask(dve, g, j, b, w)
                else:
                    link(nc.vector.reduce_max(a.rowmax[:, g, 0:w], a.score(k, g)[:, 0:w, :], AX_X))
                nc.vector.tensor_scalar(a.rowmax[:, g, 0:w], a.rowmax[:, g, 0:w], -a.scale, None,
                                        ALU.mult).then_inc(k.sem("rowmax_ready"), 1)
        g = s - 2
        if a.topk and 0 <= g < n:
            mask.pick(dve, g)
        run(a.slot(s, 3))
        g = s - a.out_lag
        if 0 <= g < n:
            w = len(a.groups[g][4])
            dve.wait_ge(k.sem("picked_ready" if a.topk else "exp_ready"), g + 1)
            link(nc.vector.reciprocal(a.rowsum[:, g, 0:w], a.rowsum[:, g, 0:w]))
            link(nc.vector.tensor_tensor(a.factor[:, g, 0:w, :], a.rowsum[:, g, 0:w].unsqueeze(2).broadcast_to([P, w, 2]),
                                         k.hmask64[:, :].unsqueeze(1).broadcast_to([P, w, 2]), ALU.mult))
            dve.wait_ge(k.sem("out_ready"), g + 1)
            if g >= 2:
                dve.wait_ge(k.sem("folded_ready"), g - 1)
            nc.vector.tensor_tensor(a.own[:, g % 2, 0:w * a.rows].rearrange("p (i h d) -> p i h d", i=w, h=2),
                                    a.products(k, g).rearrange("p (i h d) -> p i h d", i=w, h=2),
                                    a.factor[:, g, 0:w, :].unsqueeze(3).broadcast_to([P, w, 2, a.head]),
                                    ALU.mult).then_inc(k.sem("own_ready"), 1)


def mask_queries(k, a, pool, u, q_of):
    nc = k.nc
    m = k.hmask16 if a.head == 16 else k.hmask64
    n = P // a.head
    a.wait_unit(k, pool, "scores_ready", u)
    for c in range(a.qchunks):
        for b in range(a.seqs):
            nc.gpsimd.tensor_tensor(a.q_heads[:, u % 2, c, b, :].rearrange("p (h q) -> p h q", q=SEQ),
                                    q_of(c, b).unsqueeze(1).broadcast_to([P, n, SEQ]),
                                    m[:, :].unsqueeze(2).broadcast_to([P, n, SEQ]), ALU.mult).then_inc(k.sem("q_heads_ready"), 1)


def copy_rows(k, a, pool, u, src):
    if u >= 2:
        a.wait_job(k, pool, *[job for job in a.order if job[0] == "v" and job[1] == u - 2][-1])
    k.nc.gpsimd.tensor_copy(a.moving[:, u % 2, :, :], src).then_inc(k.sem("rows_copied"), 1)


def context_jobs(kchunks, vfeat, seqs=PER_TILE, queries=0):
    per = BANK // (seqs * CTX)
    jobs = [("q", c, 0) for c in range(0, queries, 4)] + [("k", c, 0) for c in range(0, kchunks, per)]
    rows = seqs * CTX // P
    if vfeat >= BANK:
        return jobs + [("v", j, n) for j in range(rows) for n in range(vfeat // BANK)]
    return jobs + [("v", j, 0) for j in range(0, rows, BANK // vfeat)]


def projections(k, a, w, t, ctx_keys, x_moving=None, gates=None):
    nc = k.nc

    def job(pe, kind, j, i, h):
        bank = a.bank(k, kind, j, i, h)
        if kind == "q":
            for m in range(4):
                for c in range(CHUNKS):
                    last = nc.tensor.matmul(bank[:, m * P:(m + 1) * P], w["wq"][:, c, (i + m) * P:(i + m + 1) * P], x_moving(j, c),
                                            start=(c == 0), stop=(c == CHUNKS - 1))
        elif kind == "k":
            n = a.seqs * CTX
            for m in range(BANK // n):
                for c in range(CHUNKS):
                    last = nc.tensor.matmul(bank[:, m * n:(m + 1) * n], w["wk"][:, c, (i + m) * P:(i + m + 1) * P], ctx_keys(j, c),
                                            start=(c == 0), stop=(c == CHUNKS - 1))
        elif kind == "v":
            pe.wait_ge(k.sem("rows_copied"), j + 1)
            if a.keys == CTX:
                width = min(a.vfeat, BANK)
                for m in range(BANK // width):
                    for c in range(CHUNKS):
                        last = nc.tensor.matmul(bank[:, m * width:(m + 1) * width], a.moving[:, j % 2, c, (i + m) * P:(i + m + 1) * P],
                                                w["wv"][:, c, h * BANK:h * BANK + width], start=(c == 0), stop=(c == CHUNKS - 1))
            else:
                for b in range(PER_TILE):
                    for c in range(CHUNKS):
                        last = nc.tensor.matmul(bank[0:SEQ, b * D:(b + 1) * D], a.moving[:, j % 2, c, b * SEQ:(b + 1) * SEQ],
                                                w["wv"][:, c, :], start=(c == 0), stop=(c == CHUNKS - 1))
        elif kind == "g":
            pe.wait_ge(k.sem("oT_chunks"), a.per_tile * (j + 1))
            for c in range(CHUNKS):
                last = nc.tensor.matmul(bank[:, 0:17], a.oT[:, j % 2, c, :], w["wgate"][:, c, :], start=(c == 0), stop=(c == CHUNKS - 1))
        else:
            pe.wait_ge(k.sem("oT_chunks"), a.per_tile * (j + 1))
            for c in range(a.qchunks):
                last = nc.tensor.matmul(bank[:, 0:D], a.oT[:, j % 2, c, :], w["wo"][:, c, :], start=(c == 0), stop=(c == a.qchunks - 1))
        return last

    return job


def values_out(k, a, eng, copy, j, i, h):
    a.wait_job(k, eng, "v", j, i, h)
    a.wait_unit(k, eng, "out_ready", j)
    if a.keys == CTX:
        width = min(a.vfeat, BANK)
        rows, out = P, a.v[:, j % 2, i:i + BANK // width, h * BANK:h * BANK + width]
    else:
        width, rows = D, SEQ
        out = a.v[0:SEQ, j % 2, :, :]
    copy(out, a.bank(k, "v", j, i, h)[0:rows, :].rearrange("p (i w) -> p i w", w=width)).then_inc(k.sem("values_ready"), 1)


def act_jobs(k, a, bk, gate=None, values=False):
    nc = k.nc

    def job(act, kind, j, i, h):
        if kind == "q":
            a.wait_job(k, act, kind, j, i, h)
            if j >= 1:
                act.wait_ge(k.sem("q_heads_ready"), j * PER_TILE * a.qchunks)
            nc.scalar.copy(a.q_tile[:, i:i + 4, :], a.bank(k, kind, j, i, h).rearrange("p (i n) -> p i n", i=4)).then_inc(k.sem("queries_ready"), 1)
        elif kind == "k":
            a.wait_job(k, act, kind, j, i, h)
            a.wait_unit(k, act, "scores_ready", j)
            n = a.seqs * CTX
            nc.scalar.activation(a.kT[:, j % 2, i:i + BANK // n, :], a.bank(k, kind, j, i, h).rearrange("p (i n) -> p i n", n=n), ACT.Identity,
                                 bias=0.0 if bk is None else bk[:, i:i + 1]).then_inc(k.sem("keys_ready"), 1)
        elif kind == "v" and values:
            values_out(k, a, act, nc.scalar.copy, j, i, h)
        elif kind == "g":
            gate(act, j)

    return job


def dve_jobs(k, a, link, t, bo=None, factor=None, gate=None, factor_of=None, values=True):
    nc = k.nc

    def job(dve, kind, j, i, h):
        if kind == "v" and values:
            values_out(k, a, dve, nc.vector.tensor_copy, j, i, h)
        elif kind == "g":
            gate(dve, j)
        elif kind == "o":
            if factor_of:
                factor_of(dve, j)
            a.wait_job(k, dve, kind, j, i, h)
            dst = k.x[:, t * a.unroll + j, :]
            src = a.bank(k, kind, j, i, h)[:, 0:D]
            if bo is not None:
                nc.vector.tensor_tensor(a.sum[:, :], src, bo, ALU.add).then_inc(k.sem("branch_read"), 1)
                dve.wait_ge(k.sem("branch_read"), j + 1)
                src = a.sum[:, :]
            if factor is not None:
                last = nc.vector.scalar_tensor_tensor(dst, src, factor, dst, ALU.mult, ALU.add)
            else:
                last = nc.vector.tensor_tensor(dst, src, dst, ALU.add)
            if bo is None:
                last.then_inc(k.sem("branch_read"), 1)

    return job


def pairs16():
    return [[(fc, fc, fc, 32 * j) for j in range(4)] for fc in range(CHUNKS)]


def pairs64(qchunks, shared):
    n = min(4, qchunks)
    return [[(c, 0 if shared else c, 0 if shared else c, 0) for c in range(g, g + n)] for g in range(0, qchunks, n)]


def load_mask(k, mask8, name):
    with k.nc.Block() as block:

        @block.sync
        def _(sp):
            sp.dma_start(mask8[:, :], k.dram[name]).then_inc(k.sem("mask_loaded"), 16)
            sp.wait_ge(k.sem("mask_loaded"), 16)
    k.clear()


def context_attention(k, w, topk):
    nc = k.nc
    unroll = 4
    with ExitStack() as ctx:
        a = Attention(k, ctx, CTX, CHUNKS, CHUNKS, D, 16, pairs16(), 0.25, unroll, context_jobs(CHUNKS, D), copied=topk, topk=topk)
        a.oT_bias = w["bv"]
        qT = k.xn[:, :, :].rearrange("p t d -> p (t d)").rearrange("p (c n) -> p c n", c=CHUNKS)
        if topk:
            low = k.sb(ctx, "key_low", [P, PER_TILE, CTX])
            mask8 = k.sb(ctx, "key_mask", [P, BATCH * CTX], U8)
            work = k.sb(ctx, "topk_work", [P, 2, 4, CTX])
            best = k.sb(ctx, "topk_best", [P, 4, 8])
            allout = k.sb(ctx, "all_masked", [P, 2, 4])
            a.masked = k.sb(ctx, "masked_scores", [P, 2, 4, CTX])
            load_mask(k, mask8, "mask_xattn")
        project(k, [(w["wq"], c * P, qT[:, c, :], w["bq"][:, c:c + 1], ACT.Identity) for c in range(CHUNKS)])
        with nc.Fori(0, TILES // unroll) as t:

            def ctx_cols(j):
                return bass.ds((t * unroll + j) * CTX_TILE, CTX_TILE)

            def best_keys(dve, g):
                sc = a.masked[:, g % 2]
                dve.wait_ge(k.sem("masked_ready"), g + 1)
                if g >= 2:
                    dve.wait_ge(k.sem("picked_ready"), g - 1)

                def step(ins):
                    best_keys.done += 1
                    ins.then_inc(k.sem("topk_step"), 1)

                def settled(back):
                    dve.wait_ge(k.sem("topk_step"), best_keys.done - back)

                for r in range(8):
                    src = work[:, g % 2] if r else sc
                    for i in range(4):
                        if g or r:
                            settled(3)
                        step(nc.vector.max(best[:, i, :], src[:, i, :]))
                    if r == 0:
                        settled(0)
                        nc.vector.tensor_scalar(allout[:, g % 2, :], best[:, :, 0], NEG, -1.0, ALU.is_equal, ALU.mult)
                        nc.vector.tensor_scalar(a.rowmax[:, g, :], best[:, :, 0], -a.scale, None, ALU.mult).then_inc(k.sem("rowmax_ready"), 1)
                    for i in range(4):
                        settled(3)
                        step(nc.vector.match_replace(work[:, g % 2, i, :], best[:, i, :], src[:, i, :], NEG))

            def pick(dve, g):
                dve.wait_ge(k.sem("outside_ready"), g + 1)
                dve.wait_ge(k.sem("exp_ready"), g + 1)
                for i in range(4):
                    last = nc.vector.scalar_tensor_tensor(a.probs[:, g % 2, i, :], work[:, g % 2, i, :], allout[:, g % 2, i:i + 1],
                                                          a.probs[:, g % 2, i, :], ALU.is_gt, ALU.mult, accum_out=a.rowsum[:, g, i:i + 1])
                last.then_inc(k.sem("picked_ready"), 1)

            best_keys.pick = pick

            with nc.Block() as block:

                @block.gpsimd
                def _(pool):
                    def tile(j):
                        copy_rows(k, a, pool, j, k.ctxT[:, :, ctx_cols(j)])
                        mask_queries(k, a, pool, j, lambda c, b: qT[:, c, bass.ds((t * unroll + j) * P + b * SEQ, SEQ)])
                    if not topk:
                        for j in range(unroll):
                            tile(j)
                        return
                    tile(0)
                    for s in range(len(a.groups) + 1):
                        if s < len(a.groups):
                            j, b = a.groups[s][0:2]
                            if s % CHUNKS == 0:
                                seq = s // CHUNKS
                                nc.gpsimd.tensor_copy(low[:, b, :], mask8[:, bass.ds((t * unroll * PER_TILE + seq) * CTX, CTX)]
                                                      ).then_inc(k.sem("low_step"), 1)
                                pool.wait_ge(k.sem("low_step"), 2 * seq + 1)
                                nc.gpsimd.tensor_scalar(low[:, b, :], low[:, b, :], -NEG, NEG, ALU.mult, ALU.add).then_inc(k.sem("low_step"), 1)
                                pool.wait_ge(k.sem("low_step"), 2 * seq + 2)
                            sc = a.masked[:, s % 2, :, :]
                            pool.wait_ge(k.sem("scores_copied"), s + 1)
                            nc.gpsimd.tensor_tensor(sc, sc, low[:, b, :].unsqueeze(1).broadcast_to([P, 4, CTX]),
                                                    ALU.add).then_inc(k.sem("masked_ready"), 1)
                            if s % a.per_tile == 1 and j + 1 < unroll:
                                tile(j + 1)
                        if s >= 1:
                            g = s - 1
                            pool.wait_ge(k.sem("topk_step"), 64 * (g + 1))
                            pool.wait_ge(k.sem("exp_ready"), g + 1)
                            nc.gpsimd.tensor_tensor(work[:, g % 2], a.masked[:, g % 2], work[:, g % 2],
                                                    ALU.subtract).then_inc(k.sem("outside_ready"), 1)

                @block.tensor
                def _(pe):
                    attend_pe(k, a, pe, projections(k, a, w, t, lambda j, c: k.ctxT[:, c, ctx_cols(j)]))

                @block.scalar
                def _(act):
                    attend_act(k, a, act, act_jobs(k, a, w["bk"], values=topk))

                @block.vector
                def _(dve):
                    link = linker(dve, k.sem("dve_step"))
                    best_keys.done = 0
                    attend_dve(k, a, dve, link, dve_jobs(k, a, link, t, w["bo"], values=not topk), best_keys if topk else None)
            k.clear()


def layer0_xattn(k, w):
    context_attention(k, w, True)


def layer6_xattn(k, w):
    context_attention(k, w, False)


BUILDERS = {0: layer0_xattn, 6: layer6_xattn}


def self_attention(k, w, a, qT, kT, mask=None, gates=None, factor_of=None, factor=None, bo=None):
    nc = k.nc
    unroll = a.unroll
    with nc.Fori(0, TILES // unroll) as t:

        def keys_of(j, c, b):
            return kT[:, c, bass.ds((t * unroll + j) * P + b * SEQ, SEQ)]

        a.keys_of = keys_of
        with nc.Block() as block:

            @block.gpsimd
            def _(pool):
                for j in range(unroll):
                    copy_rows(k, a, pool, j, k.xnT[:, :, bass.ds((t * unroll + j) * P, P)])
                    mask_queries(k, a, pool, j, lambda c, b: qT[:, c, bass.ds((t * unroll + j) * P + b * SEQ, SEQ)])

            @block.tensor
            def _(pe):
                attend_pe(k, a, pe, projections(k, a, w, t, None))

            @block.scalar
            def _(act):
                attend_act(k, a, act, act_jobs(k, a, None, gate=gates and gates[0]))

            @block.vector
            def _(dve):
                link = linker(dve, k.sem("dve_step"))
                jobs = dve_jobs(k, a, link, t, bo=bo, factor=factor,
                                gate=gates and (lambda dve, j: gates[1](dve, link, j)),
                                factor_of=factor_of and (lambda dve, j: factor_of(dve, link, j)))
                attend_dve(k, a, dve, link, jobs, mask and mask(link))
        k.clear()


def layer1_attn(k, w):
    nc = k.nc
    with ExitStack() as ctx:
        a = Attention(k, ctx, SEQ, CHUNKS, 0, D, 16, pairs16(), 0.25, 4, [("v", 0, 0)], copied=True)
        qT = k.sb(ctx, "qT", [P, CHUNKS, TOKENS])
        kT = k.sb(ctx, "kT_all", [P, CHUNKS, TOKENS])
        a.oT_scale = share = k.sb(ctx, "dot_share", [P, CHUNKS])
        project(k, [(w[n], c * P, o[:, c, :], None, ACT.Identity) for n, o in (("wq", qT), ("wk", kT)) for c in range(CHUNKS)])
        with nc.Block() as block:

            @block.scalar
            def _(act):
                nc.scalar.activation(share[:, :], w["beta"], ACT.Sigmoid, scale=-1.0)
        k.clear()

        def mask(link):
            def causal(dve, g, j, b, n):
                pr = a.probs[:, g % 2, 0:n, :]
                nc.vector.tensor_tensor(pr, a.score(k, g)[:, 0:n, :], w["causal"].unsqueeze(1).broadcast_to([P, n, SEQ]),
                                        ALU.add).then_inc(k.sem("scores_copied"), 1)
                dve.wait_ge(k.sem("scores_copied"), g + 1)
                link(nc.vector.reduce_max(a.rowmax[:, g, 0:n], pr, AX_X))
            return causal

        self_attention(k, w, a, qT, kT, mask)


def layer2_ffn(k, w):
    nc = k.nc
    with ExitStack() as ctx:
        a = Attention(k, ctx, SEQ, CHUNKS, 0, D, 16, pairs16(), 0.25, 4, [("v", 0, 0)], gated=True)
        qT = k.sb(ctx, "qT", [P, CHUNKS, TOKENS])
        kT = k.sb(ctx, "kT_all", [P, CHUNKS, TOKENS])
        sq = k.sb(ctx, "q_squares", [P, CHUNKS, TOKENS])
        a.oT_bias = w["bv"]
        heat = k.sb(ctx, "heat", [P, 2, CHUNKS])
        softplus(k, w["temp"], heat[:, 0, :], heat[:, 1, :])
        gate = k.sb(ctx, "gates", [P, 17])
        best = k.sb(ctx, "gates_best", [P, 8])
        cols = k.sb(ctx, "gate_cols", [P, 10])
        factor = k.sb(ctx, "gate_factor", [P, 1])
        project(k, [(w[n], c * P, o[:, c, :], w[bn][:, c:c + 1], ACT.Identity)
                    for n, bn, o in (("wq", "bq", qT), ("wk", "bk", kT)) for c in range(CHUNKS)])
        parts = [(c, h) for c in range(CHUNKS) for h in range(TOKENS // BANK)]
        with nc.Block() as block:

            @block.scalar
            def _(act):
                for c in range(CHUNKS):
                    nc.scalar.activation(sq[:, c, :], qT[:, c, :], ACT.Square).then_inc(k.sem("squares_ready"), 1)
                for n, (c, h) in enumerate(parts):
                    act.wait_ge(k.sem("norm_in_psum"), n + 1)
                    nc.scalar.activation(sq[:, c, h * BANK:(h + 1) * BANK], k.banks[:, n, :], ACT.Sqrt).then_inc(k.sem("norm_ready"), 1)

            @block.tensor
            def _(pe):
                pe.wait_ge(k.sem("squares_ready"), CHUNKS)
                for n, (c, h) in enumerate(parts):
                    nc.tensor.matmul(k.banks[:, n, :], w["same16"], sq[:, c, h * BANK:(h + 1) * BANK],
                                     start=True, stop=True).then_inc(k.sem("norm_in_psum"), 1)

            @block.vector
            def _(dve):
                link = linker(dve, k.sem("dve_step"))
                dve.wait_ge(k.sem("norm_ready"), len(parts))
                link(nc.vector.reciprocal(sq[:, :, :], sq[:, :, :]))
                link(nc.vector.tensor_tensor(qT[:, :, :], qT[:, :, :], sq[:, :, :], ALU.mult))
                for c in range(CHUNKS):
                    nc.vector.tensor_scalar(qT[:, c, :], qT[:, c, :], w["qe"][:, c:c + 1], w["temp"][:, c:c + 1], ALU.add, ALU.mult)
        k.clear()

        def gate_act(act, j):
            act.wait_ge(k.sem("gate_max_ready"), j + 1)
            nc.scalar.activation(gate[:, 0:15], gate[:, 0:15], ACT.Exp, bias=cols[:, 0:1], accum_out=cols[:, 2:3])
            nc.scalar.activation(gate[:, 15:17], gate[:, 15:17], ACT.Exp, bias=cols[:, 1:2],
                                 accum_out=cols[:, 3:4]).then_inc(k.sem("gate_exp_ready"), 1)

        def gate_dve(dve, link, j):
            a.wait_job(k, dve, "g", j, 0, 0)
            nc.vector.tensor_tensor(gate[:, :], k.banks[:, 7, 0:17], w["bgate"], ALU.add).then_inc(k.sem("gates_read"), 1)
            dve.wait_ge(k.sem("gates_read"), j + 1)
            nc.vector.reduce_max(cols[:, 0:1], gate[:, 0:15], AX_X)
            link(nc.vector.reduce_max(cols[:, 1:2], gate[:, 15:17], AX_X))
            nc.vector.tensor_scalar(cols[:, 0:2], cols[:, 0:2], -1.0, None, ALU.mult).then_inc(k.sem("gate_max_ready"), 1)

        def gate_factor(dve, link, j):
            dve.wait_ge(k.sem("gate_exp_ready"), j + 1)
            link(nc.vector.reciprocal(cols[:, 2:4], cols[:, 2:4]))
            link(nc.vector.max(best[:, :], gate[:, 0:15]))
            link(nc.vector.reduce_sum(cols[:, 4:5], best[:, 0:3], AX_X))
            link(nc.vector.tensor_tensor(cols[:, 4:5], cols[:, 4:5], cols[:, 2:3], ALU.mult))
            link(nc.vector.tensor_scalar(cols[:, 5:7], gate[:, 15:17], cols[:, 3:4], None, ALU.mult))
            link(nc.vector.reduce_sum(cols[:, 7:8], cols[:, 5:7], AX_X))
            link(nc.vector.scalar_tensor_tensor(cols[:, 7:8], cols[:, 7:8], 2.0, cols[:, 5:6], ALU.mult, ALU.mult))
            link(nc.vector.scalar_tensor_tensor(cols[:, 8:9], cols[:, 4:5], 6.0, cols[:, 6:7], ALU.mult, ALU.mult))
            link(nc.vector.tensor_tensor(factor[:, :], cols[:, 7:8], cols[:, 8:9], ALU.add))

        self_attention(k, w, a, qT, kT, gates=(gate_act, gate_dve), factor_of=gate_factor, factor=factor[:, 0:1])
        with nc.Block() as block:

            @block.vector
            def _(dve):
                nc.vector.tensor_tensor(k.x[:, :, :], k.x[:, :, :], w["bo"].unsqueeze(1).broadcast_to([P, TILES, D]), ALU.add)


def layer3_xattn(k, w):
    nc = k.nc
    inner = 1024
    unroll = 4
    normalize(k, src=k.xn, scale=w["gamma"], shift=w["beta"])
    with ExitStack() as ctx:
        a = Attention(k, ctx, CTX, inner // P, inner // P, inner, 64, pairs64(inner // P, False), 0.125, unroll,
                      context_jobs(inner // P, inner, seqs=1, queries=inner // P), split=True)
        a.q_tile = k.sb(ctx, "q_tile", [P, inner // P, P])
        opening = k.sb(ctx, "gate_tanh", [P, 1])
        with nc.Block() as block:

            @block.scalar
            def _(act):
                nc.scalar.activation(opening[:, :], w["gate"], ACT.Tanh)
        with nc.Fori(0, TILES // unroll) as t:

            def ctx_cols(u):
                return bass.ds((t * a.units + u) * CTX, CTX)

            with nc.Block() as block:

                @block.gpsimd
                def _(pool):
                    for u in range(a.units):
                        copy_rows(k, a, pool, u, k.ctxT[:, :, ctx_cols(u)])
                        pool.wait_ge(k.sem("queries_ready"), 2 * (u // PER_TILE + 1))
                        mask_queries(k, a, pool, u, lambda c, b: a.q_tile[:, c, (u % PER_TILE) * SEQ:(u % PER_TILE + 1) * SEQ])

                @block.tensor
                def _(pe):
                    attend_pe(k, a, pe, projections(k, a, w, t, lambda u, c: k.ctxT[:, c, ctx_cols(u)],
                                                    lambda j, c: k.xnT[:, c, bass.ds((t * unroll + j) * P, P)]))

                @block.scalar
                def _(act):
                    attend_act(k, a, act, act_jobs(k, a, None))

                @block.vector
                def _(dve):
                    link = linker(dve, k.sem("dve_step"))
                    attend_dve(k, a, dve, link, dve_jobs(k, a, link, t, w["bo"], factor=opening[:, 0:1]))
            k.clear()


BUILDERS |= {1: layer1_attn, 2: layer2_ffn, 3: layer3_xattn}


def layout_attention(g, out):
    a = "L0_attn_"
    later = (np.arange(SEQ)[None, :] > (np.arange(P) % SEQ)[:, None]) * np.float32(NEG)
    out[1] = dict(wq=_mat(g[a + "W_q"].T), wk=_mat(g[a + "W_k"].T), wv=_mat(g[a + "W_v"].T), wo=_mat(g[a + "W_o"].T),
                  beta=_col(np.repeat(g[a + "beta_param"], 16)), causal=later.astype(np.float32))
    a = "L0_ffn_"
    same = (np.arange(P)[:, None] // 16 == np.arange(P)[None, :] // 16).astype(np.float32)
    out[2] = dict(wq=_mat(g[a + "Wq"].T), wk=_mat(g[a + "Wk"].T), wv=_mat(g[a + "Wv"].T), wo=_mat(g[a + "Wp"].T),
                  bq=_col(g[a + "bq"]), bk=_col(g[a + "bk"]), bv=_col(g[a + "bv"]), bo=_row(g[a + "bp"]),
                  temp=_col(np.repeat(g[a + "temperature"].reshape(-1), 16)), qe=_col(g[a + "query_embedding"].reshape(-1)),
                  wgate=_mat(np.concatenate([g[a + "Wr"], g[a + "Ws"]]).T),
                  bgate=_row(np.concatenate([g[a + "br"], g[a + "bs"]])), same16=same)
    a = "L1_xattn_"
    kv = g[a + "w_kv"]
    out[3] = dict(wq=_mat(g[a + "w_q"]), wk=_mat(kv[:, :1024]), wv=_mat(kv[:, 1024:]), wo=_mat(g[a + "w_out"]),
                  gamma=_col(g[a + "ln_gamma"]), beta=_col(g[a + "ln_beta"]), bo=_row(g[a + "b_out"]), gate=_row(g[a + "gate"]))


def rms_inverse(k, ones, src, squares, inv, chunks, scale_rows):
    nc = k.nc
    with nc.Block() as block:

        @block.gpsimd
        def _(pool):
            for n in range(chunks):
                if n >= 2:
                    pool.wait_ge(k.sem("sumsq_ready"), n - 1)
                cols = src[:, :, n * BANK:(n + 1) * BANK]
                nc.gpsimd.tensor_tensor(squares[:, n % 2, :, :], cols, cols, ALU.mult).then_inc(k.sem("squares_ready"), 1)

        @block.scalar
        def _(act):
            for n in range(chunks):
                act.wait_ge(k.sem("sumsq_ready"), n + 1)
                nc.scalar.activation(inv[:, n * BANK:(n + 1) * BANK], k.banks[:, n % 4, :], ACT.Sqrt, bias=scale_rows["eps"],
                                     scale=1.0 / D).then_inc(k.sem("rms_ready"), 1)

        @block.tensor
        def _(pe):
            for n in range(chunks):
                pe.wait_ge(k.sem("squares_ready"), n + 1)
                if n >= 4:
                    pe.wait_ge(k.sem("rms_ready"), n - 3)
                for c in range(CHUNKS):
                    last = nc.tensor.matmul(k.banks[:, n % 4, :], ones, squares[:, n % 2, c, :], start=(c == 0), stop=(c == CHUNKS - 1))
                last.then_inc(k.sem("sumsq_ready"), 1)

        @block.vector
        def _(dve):
            for n in range(chunks):
                cols = slice(n * BANK, (n + 1) * BANK)
                dve.wait_ge(k.sem("rms_ready"), n + 1)
                nc.vector.reciprocal(inv[:, cols], inv[:, cols]).then_inc(k.sem("inverse_ready"), 1)
                dve.wait_ge(k.sem("inverse_ready"), n + 1)
                for c in range(CHUNKS):
                    nc.vector.scalar_tensor_tensor(src[:, c, cols], src[:, c, cols], scale_rows["gain"][:, c:c + 1], inv[:, cols],
                                                   ALU.mult, ALU.mult)
    k.clear()


def rotate(k, straight, swapped, cos, sin, batch, n):
    nc = k.nc
    with nc.Block() as block:

        @block.gpsimd
        def _(pool):
            for c in range(straight.shape[1]):
                v = swapped[:, c, :].rearrange("p (b q) -> p b q", q=n)
                nc.gpsimd.tensor_tensor(v, v, sin.unsqueeze(1).broadcast_to([P, batch, n]), ALU.mult).then_inc(k.sem("sine_ready"), 1)

        @block.vector
        def _(dve):
            for c in range(straight.shape[1]):
                v = straight[:, c, :].rearrange("p (b q) -> p b q", q=n)
                nc.vector.tensor_tensor(v, v, cos.unsqueeze(1).broadcast_to([P, batch, n]), ALU.mult).then_inc(k.sem("cosine_ready"), 1)
            for c in range(straight.shape[1]):
                dve.wait_ge(k.sem("cosine_ready"), c + 1)
                dve.wait_ge(k.sem("sine_ready"), c + 1)
                nc.vector.tensor_tensor(straight[:, c, :], straight[:, c, :], swapped[:, c, :], ALU.add)
    k.clear()


def layer9_xattn(k, w):
    nc = k.nc
    keys_all = BATCH * CTX
    unroll = 4
    with ExitStack() as ctx:
        a = Attention(k, ctx, CTX, CHUNKS, 0, P, 64, pairs64(CHUNKS, True), 0.125, unroll, context_jobs(0, P), copied=True)
        qT = k.xn[:, :, :].rearrange("p t d -> p (t d)").rearrange("p (c n) -> p c n", c=CHUNKS)
        kT = k.sb(ctx, "kT_all", [P, 1, keys_all])
        low = k.sb(ctx, "key_low", [P, 2, CTX_TILE])
        mask8 = k.sb(ctx, "key_mask", [P, keys_all], U8)
        gain = k.sb(ctx, "rms_gain", [P, CHUNKS])
        eps = k.sb(ctx, "rms_eps", [P, 1])
        with nc.Block() as block:

            @block.sync
            def _(sp):
                sp.dma_start(mask8[:, :], k.dram["mask_last"]).then_inc(k.sem("mask_loaded"), 16)
                sp.wait_ge(k.sem("mask_loaded"), 16)

            @block.vector
            def _(dve):
                nc.vector.memset(eps[:, :], 1e-6)
                nc.vector.tensor_scalar(gain[:, :], w["rms"], 1.0, None, ALU.add)
        k.clear()
        with ExitStack() as early:
            swapped = k.sb(early, "k_swapped", [P, 1, keys_all])
            squares = swapped[:, 0, 0:2 * CHUNKS * BANK].rearrange("p (i c n) -> p i c n", i=2, c=CHUNKS)
            inv = kT[:, 0, :]
            rows = dict(eps=eps[:, 0:1], gain=gain)
            rms_inverse(k, w["ones"], k.ctxT, squares, inv, keys_all // BANK, rows)
            rms_inverse(k, w["ones"], k.xnT, squares, inv, TOKENS // BANK, rows)
            qswap = swapped[:, 0, 0:CHUNKS * TOKENS].rearrange("p (c n) -> p c n", c=CHUNKS)
            project(k, [(w[n], c * P, o[:, c, :], None, ACT.Identity) for n, o in (("wq", qT), ("wqs", qswap)) for c in range(CHUNKS)])
            rotate(k, qT, qswap, w["cosq"], w["sinq"], BATCH, SEQ)
            project(k, [(w["wk"], 0, kT[:, 0, :], None, ACT.Identity), (w["wk"], P, swapped[:, 0, :], None, ACT.Identity)],
                    src=k.ctxT, tokens=keys_all)
            rotate(k, kT, swapped, w["cosk"], w["sink"], BATCH, CTX)
        with nc.Fori(0, TILES // unroll) as t:

            def cols(j, b=0):
                return bass.ds((t * unroll + j) * CTX_TILE + b * CTX, CTX)

            def mask(link):
                def hide(dve, g, j, b, n):
                    pr = a.probs[:, g % 2, 0:n, :]
                    dve.wait_ge(k.sem("low_ready"), 2 * j + 2)
                    nc.vector.tensor_tensor(pr, a.score(k, g)[:, 0:n, :],
                                            low[:, j % 2, b * CTX:(b + 1) * CTX].unsqueeze(1).broadcast_to([P, n, CTX]),
                                            ALU.add).then_inc(k.sem("scores_copied"), 1)
                    dve.wait_ge(k.sem("scores_copied"), g + 1)
                    link(nc.vector.reduce_max(a.rowmax[:, g, 0:n], pr, AX_X))
                return hide

            a.keys_of = lambda j, c, b: kT[:, 0, cols(j, b)]
            with nc.Block() as block:

                @block.gpsimd
                def _(pool):
                    for j in range(unroll):
                        tile = bass.ds((t * unroll + j) * CTX_TILE, CTX_TILE)
                        copy_rows(k, a, pool, j, k.ctxT[:, :, tile])
                        mask_queries(k, a, pool, j, lambda c, b: qT[:, c, bass.ds((t * unroll + j) * P + b * SEQ, SEQ)])
                        if j >= 2:
                            pool.wait_ge(k.sem("scores_copied"), a.per_tile * (j - 1))
                        nc.gpsimd.tensor_copy(low[:, j % 2, :], mask8[:, tile]).then_inc(k.sem("low_ready"), 1)
                        pool.wait_ge(k.sem("low_ready"), 2 * j + 1)
                        nc.gpsimd.tensor_scalar(low[:, j % 2, :], low[:, j % 2, :], -NEG, NEG, ALU.mult, ALU.add).then_inc(k.sem("low_ready"), 1)

                @block.tensor
                def _(pe):
                    attend_pe(k, a, pe, projections(k, a, w, t, None))

                @block.scalar
                def _(act):
                    attend_act(k, a, act, act_jobs(k, a, None))

                @block.vector
                def _(dve):
                    link = linker(dve, k.sem("dve_step"))
                    attend_dve(k, a, dve, link, dve_jobs(k, a, link, t), mask(link))
            k.clear()


HIDDEN = 1024
ROUND = 1.5 * 2.0 ** 23
QB = 127.0


def two_layers(k, dt, prepare_x, hidden_act, prepare_h, finish, w1, w2, buf, extra=None):
    nc = k.nc
    xq, xqT, hq, hqT, ident, turned = buf
    nh = HIDDEN // P
    with nc.Fori(0, TILES) as t:
        with nc.Block() as block:

            @block.tensor
            def _(pe):
                pe.wait_ge(k.sem("xq_ready"), 1)
                for c in range(CHUNKS):
                    last = nc.tensor.transpose(turned[:, c * P:(c + 1) * P], xq[:, c * P:(c + 1) * P], ident)
                last.then_inc(k.sem("xq_turned"), 1)
                pe.wait_ge(k.sem("xqT_ready"), 1)
                for h in range(HIDDEN // BANK):
                    for c in range(CHUNKS):
                        last = nc.tensor.matmul(k.banks[:, 2 + h, :], xqT[:, c, :], w1[:, c, h * BANK:(h + 1) * BANK],
                                                start=(c == 0), stop=(c == CHUNKS - 1))
                    last.then_inc(k.sem("hidden_ready"), 1)
                pe.wait_ge(k.sem("hq_ready"), 1)
                for c in range(nh):
                    last = nc.tensor.transpose(turned[:, c * P:(c + 1) * P], hq[:, c * P:(c + 1) * P], ident)
                last.then_inc(k.sem("hq_turned"), 1)
                pe.wait_ge(k.sem("hqT_ready"), 1)
                for c in range(nh):
                    last = nc.tensor.matmul(k.banks[:, 4, 0:D], hqT[:, c, :], w2[:, c, :], start=(c == 0), stop=(c == nh - 1))
                last.then_inc(k.sem("branch_ready"), 1)

            @block.scalar
            def _(act):
                link = linker(act, k.sem("act_step"))
                prepare_x[0](act, link, t)
                act.wait_ge(k.sem("xq_turned"), 1)
                nc.scalar.copy(xqT[:, :, :], turned[:, 0:D].rearrange("p (c n) -> p c n", n=P)).then_inc(k.sem("xqT_ready"), 1)
                hidden_act(act, link)
                prepare_h[0](act, link)
                act.wait_ge(k.sem("hq_turned"), 1)
                nc.scalar.copy(hqT[:, :, :], turned[:, 0:HIDDEN].rearrange("p (c n) -> p c n", n=P)).then_inc(k.sem("hqT_ready"), 1)

            @block.vector
            def _(dve):
                link = linker(dve, k.sem("dve_step"))
                prepare_x[1](dve, link, t)
                prepare_h[1](dve, link)
                dve.wait_ge(k.sem("branch_ready"), 1)
                finish(dve, link, t)
        k.clear()


def abs_totals(k, dve, link, flat, work, tot):
    nc = k.nc
    for i in range(2):
        nc.vector.tensor_reduce(work[:, 32 * i:32 * i + 32], flat[i].rearrange("p (a b) -> p a b", a=32), AX_X, ALU.add,
                                apply_absolute_value=True).then_inc(k.sem("runs_ready"), 1)
    dve.wait_ge(k.sem("runs_ready"), 2)
    nc.vector.tensor_reduce(tot[:, :], work[:, 0:64].rearrange("p (i a) -> p i a", i=2), AX_X, ALU.add).then_inc(k.sem("abs_ready"), 1)


def layer5_ffn(k, w):
    nc = k.nc
    nh = HIDDEN // P
    with ExitStack() as ctx:
        w1 = k.sb(ctx, "w1_int", [P, CHUNKS, HIDDEN], BF16)
        w2 = k.sb(ctx, "w2_int", [P, nh, D], BF16)
        xq = k.sb(ctx, "xq", [P, D], BF16)
        xqT = k.sb(ctx, "xqT", [P, CHUNKS, P], BF16)
        hq = k.sb(ctx, "hq", [P, HIDDEN], BF16)
        hqT = k.sb(ctx, "hqT", [P, nh, P], BF16)
        ident = k.sb(ctx, "ident16", [P, P], BF16)
        work = k.sb(ctx, "quant_work", [P, HIDDEN * 2])
        hid = k.sb(ctx, "hidden", [P, HIDDEN])
        tot = k.sb(ctx, "abs_total", [P, 2])
        ws = k.sb(ctx, "w_scales", [P, 6])
        sc = k.sb(ctx, "row_scales", [P, 8])
        turned = k.banks[:, 0, :].bitcast(BF16)
        flat = [w["w1"].rearrange("p a b -> p (a b)"), w["w2"].rearrange("p a b -> p (a b)")]
        outs = [w1[:, :, :].rearrange("p a b -> p (a b)"), w2[:, :, :].rearrange("p a b -> p (a b)")]
        with nc.Block() as block:

            @block.scalar
            def _(act):
                nc.scalar.copy(ident[:, :], k.ident[:, :])

            @block.tensor
            def _(pe):
                pe.wait_ge(k.sem("abs_ready"), 1)
                nc.tensor.matmul(k.banks[:, 1, 0:2], w["ones"], tot[:, :], start=True, stop=True).then_inc(k.sem("total_ready"), 1)

            @block.vector
            def _(dve):
                link = linker(dve, k.sem("dve_step"))
                abs_totals(k, dve, link, flat, work, tot)
                dve.wait_ge(k.sem("total_ready"), 1)
                link(nc.vector.tensor_scalar(ws[:, 0:2], k.banks[:, 1, 0:2], 1.0 / (HIDDEN * D), 1e-5, ALU.mult, ALU.max))
                link(nc.vector.reciprocal(ws[:, 2:4], ws[:, 0:2]))
                link(nc.vector.tensor_scalar(ws[:, 4:6], ws[:, 0:2], 1.0 / QB, None, ALU.mult))
                for i in range(2):
                    link(nc.vector.tensor_scalar(work[:, :], flat[i], ws[:, 2 + i:3 + i], ROUND, ALU.mult, ALU.add))
                    link(nc.vector.tensor_scalar(work[:, :], work[:, :], ROUND, 1.0, ALU.subtract, ALU.min))
                    link(nc.vector.tensor_scalar(outs[i], work[:, :], -1.0, None, ALU.max))
        k.clear()

        def quantize(dve, link, src, out, n, col, ready):
            link(nc.vector.tensor_reduce(sc[:, col:col + 1], src, AX_X, ALU.max, apply_absolute_value=True))
            link(nc.vector.tensor_scalar(sc[:, col:col + 1], sc[:, col:col + 1], 1e-5, None, ALU.max))
            link(nc.vector.reciprocal(sc[:, col + 1:col + 2], sc[:, col:col + 1]))
            link(nc.vector.tensor_scalar(sc[:, col + 1:col + 2], sc[:, col + 1:col + 2], QB, None, ALU.mult))
            link(nc.vector.tensor_scalar(work[:, 0:n], src, sc[:, col + 1:col + 2], ROUND, ALU.mult, ALU.add))
            link(nc.vector.tensor_scalar(work[:, 0:n], work[:, 0:n], ROUND, QB, ALU.subtract, ALU.min))
            nc.vector.tensor_scalar(out, work[:, 0:n], -QB - 1.0, None, ALU.max).then_inc(k.sem(ready), 1)

        def x_dve(dve, link, t):
            quantize(dve, link, k.xn[:, t, :], xq[:, :], D, 0, "xq_ready")
            link(nc.vector.tensor_tensor(sc[:, 2:3], sc[:, 0:1], ws[:, 4:5], ALU.mult))

        def h_dve(dve, link):
            dve.wait_ge(k.sem("hidden_ready"), 2)
            nc.vector.scalar_tensor_tensor(hid[:, :], k.banks[:, 2:4, :].rearrange("p h n -> p (h n)"), sc[:, 2:3], w["b1"],
                                           ALU.mult, ALU.add).then_inc(k.sem("pre_ready"), 1)
            dve.wait_ge(k.sem("gelu_ready"), 1)
            quantize(dve, link, hid[:, :], hq[:, :], HIDDEN, 4, "hq_ready")
            link(nc.vector.tensor_tensor(sc[:, 6:7], sc[:, 4:5], ws[:, 5:6], ALU.mult))

        def gelu(act, link):
            act.wait_ge(k.sem("pre_ready"), 1)
            nc.scalar.activation(hid[:, :], hid[:, :], ACT.Gelu).then_inc(k.sem("gelu_ready"), 1)

        def finish(dve, link, t):
            link(nc.vector.scalar_tensor_tensor(work[:, 0:D], k.banks[:, 4, 0:D], sc[:, 6:7], w["b2"], ALU.mult, ALU.add))
            link(nc.vector.tensor_tensor(k.x[:, t, :], k.x[:, t, :], work[:, 0:D], ALU.add))

        two_layers(k, BF16, (lambda *_: None, x_dve), gelu, (lambda *_: None, h_dve), finish, w1, w2,
                   (xq, xqT, hq, hqT, ident[:, :], turned))


def layer11_ffn(k, w):
    nc = k.nc
    nh = HIDDEN // P
    with ExitStack() as ctx:
        w1 = k.sb(ctx, "w1_tern", [P, CHUNKS, HIDDEN])
        w2 = k.sb(ctx, "w2_tern", [P, nh, D])
        xq = k.sb(ctx, "x_unit", [P, D])
        xqT = k.sb(ctx, "x_unitT", [P, CHUNKS, P])
        hq = k.sb(ctx, "h_unit", [P, HIDDEN])
        hqT = k.sb(ctx, "h_unitT", [P, nh, P])
        work = k.sb(ctx, "work", [P, HIDDEN * 2])
        hid = k.sb(ctx, "hidden", [P, HIDDEN])
        tot = k.sb(ctx, "abs_total", [P, 2])
        th = k.sb(ctx, "thresholds", [P, 4])
        sc = k.sb(ctx, "row_scales", [P, 4])
        flat = [w["w1"].rearrange("p a b -> p (a b)"), w["w2"].rearrange("p a b -> p (a b)")]
        outs = [w1[:, :, :].rearrange("p a b -> p (a b)"), w2[:, :, :].rearrange("p a b -> p (a b)")]
        with nc.Block() as block:


            @block.tensor
            def _(pe):
                pe.wait_ge(k.sem("abs_ready"), 1)
                nc.tensor.matmul(k.banks[:, 1, 0:2], w["ones"], tot[:, :], start=True, stop=True).then_inc(k.sem("total_ready"), 1)

            @block.vector
            def _(dve):
                link = linker(dve, k.sem("dve_step"))
                abs_totals(k, dve, link, flat, work, tot)
                dve.wait_ge(k.sem("total_ready"), 1)
                nc.vector.tensor_scalar(th[:, 0:2], k.banks[:, 1, 0:2], 0.5 / (HIDDEN * D), None, ALU.mult)
                link(nc.vector.tensor_scalar(th[:, 2:4], k.banks[:, 1, 0:2], -0.5 / (HIDDEN * D), None, ALU.mult))
                for i in range(2):
                    link(nc.vector.tensor_scalar(work[:, :], flat[i], th[:, 2 + i:3 + i], None, ALU.is_lt))
                    link(nc.vector.scalar_tensor_tensor(outs[i], flat[i], th[:, i:i + 1], work[:, :], ALU.is_gt, ALU.subtract))
        k.clear()

        def unit(dve, link, src, out, n, col, ready):
            link(nc.vector.tensor_scalar(sc[:, col:col + 1], sc[:, col:col + 1], 1e-8, None, ALU.add))
            link(nc.vector.reciprocal(sc[:, col:col + 1], sc[:, col:col + 1]))
            nc.vector.tensor_scalar(out, src, sc[:, col:col + 1], None, ALU.mult).then_inc(k.sem(ready), 1)

        def x_act(act, link, t):
            link(nc.scalar.activation(work[:, 0:D], k.xn[:, t, :], ACT.Square, accum_out=sc[:, 0:1]))
            nc.scalar.activation(sc[:, 0:1], sc[:, 0:1], ACT.Sqrt, scale=1.0 / D).then_inc(k.sem("x_rms"), 1)

        def x_dve(dve, link, t):
            dve.wait_ge(k.sem("x_rms"), 1)
            unit(dve, link, k.xn[:, t, :], xq[:, :], D, 0, "xq_ready")

        def gelu(act, link):
            act.wait_ge(k.sem("hidden_ready"), 2)
            link(nc.scalar.activation(hid[:, :], k.banks[:, 2:4, :].rearrange("p h n -> p (h n)"), ACT.Gelu))

        def h_act(act, link):
            link(nc.scalar.activation(work[:, HIDDEN:], hid[:, :], ACT.Square, accum_out=sc[:, 1:2]))
            nc.scalar.activation(sc[:, 1:2], sc[:, 1:2], ACT.Sqrt, scale=1.0 / HIDDEN).then_inc(k.sem("h_rms"), 1)

        def h_dve(dve, link):
            dve.wait_ge(k.sem("h_rms"), 1)
            unit(dve, link, hid[:, :], hq[:, :], HIDDEN, 1, "hq_ready")

        def finish(dve, link, t):
            link(nc.vector.tensor_tensor(k.x[:, t, :], k.x[:, t, :], k.banks[:, 4, 0:D], ALU.add))

        two_layers(k, F32, (x_act, x_dve), gelu, (h_act, h_dve), finish, w1, w2,
                   (xq, xqT, hq, hqT, k.ident[:, :], k.banks[:, 0:2, :].rearrange("p b n -> p (b n)")))


PROTOS, RANK = 32, 16


def layer8_ffn(k, w):
    nc = k.nc
    pr = PROTOS * RANK
    nr = pr // P
    with ExitStack() as ctx:
        rows = k.sb(ctx, "x_rows", [P, CHUNKS, P])
        psq = k.sb(ctx, "proto_squares", [P, CHUNKS, PROTOS])
        p2 = k.sb(ctx, "proto_norms", [P, PROTOS])
        temp = k.sb(ctx, "temp_inverse", [P, 2])
        dist = k.sb(ctx, "dist", [P, PROTOS])
        wt = k.sb(ctx, "proto_weights", [P, PROTOS])
        pick = k.sb(ctx, "picked_two", [P, 2, PROTOS])
        best = k.sb(ctx, "best8", [P, 8])
        where = k.sb(ctx, "best8_at", [P, 8], mybir.dt.uint32)
        wheref = k.sb(ctx, "best8_at_float", [P, 8])
        cols = k.sb(ctx, "columns", [P, 8])
        junk = k.sb(ctx, "x_squares", [P, D])
        low = k.sb(ctx, "low_rank", [P, pr])
        lowT = k.sb(ctx, "low_rankT", [P, nr, P])
        wtT = k.sb(ctx, "proto_weightsT", [PROTOS, P])
        with nc.Block() as block:

            @block.scalar
            def _(act):
                nc.scalar.activation(psq[:, :, :], w["protos"], ACT.Square).then_inc(k.sem("squares_ready"), 1)
                nc.scalar.activation(temp[:, 0:1], w["temp"], ACT.Abs).then_inc(k.sem("temp_ready"), 1)

            @block.tensor
            def _(pe):
                pe.wait_ge(k.sem("squares_ready"), 1)
                for c in range(CHUNKS):
                    last = nc.tensor.matmul(k.banks[:, 0, 0:PROTOS], w["ones"], psq[:, c, :], start=(c == 0), stop=(c == CHUNKS - 1))
                last.then_inc(k.sem("norms_ready"), 1)

            @block.vector
            def _(dve):
                link = linker(dve, k.sem("dve_step"))
                dve.wait_ge(k.sem("temp_ready"), 1)
                link(nc.vector.tensor_scalar(temp[:, 0:1], temp[:, 0:1], 0.1, None, ALU.max))
                link(nc.vector.reciprocal(temp[:, 0:1], temp[:, 0:1]))
                nc.vector.tensor_scalar(temp[:, 1:2], temp[:, 0:1], -1.0, None, ALU.mult)
                dve.wait_ge(k.sem("norms_ready"), 1)
                nc.vector.tensor_copy(p2[:, :], k.banks[:, 0, 0:PROTOS])
        k.clear()
        with nc.Fori(0, TILES) as t:
            with nc.Block() as block:

                @block.tensor
                def _(pe):
                    pe.wait_ge(k.sem("rows_ready"), 1)
                    for c in range(CHUNKS):
                        last = nc.tensor.matmul(k.banks[:, 0, 0:PROTOS], rows[:, c, :], w["protos"][:, c, :],
                                                start=(c == 0), stop=(c == CHUNKS - 1))
                    last.then_inc(k.sem("cross_ready"), 1)
                    for c in range(CHUNKS):
                        last = nc.tensor.matmul(k.banks[:, 1, :], rows[:, c, :], w["B"][:, c, :], start=(c == 0), stop=(c == CHUNKS - 1))
                    last.then_inc(k.sem("low_ready"), 1)
                    pe.wait_ge(k.sem("weights_ready"), 1)
                    nc.tensor.transpose(k.banks[0:PROTOS, 3, 0:P], wt[:, :], k.ident[:, :])
                    pe.wait_ge(k.sem("weighted_ready"), 1)
                    for c in range(nr):
                        last = nc.tensor.transpose(k.banks[:, 2, c * P:(c + 1) * P], low[:, c * P:(c + 1) * P], k.ident[:, :])
                    last.then_inc(k.sem("turned"), 1)
                    pe.wait_ge(k.sem("turned_ready"), 2)
                    for c in range(nr):
                        nc.tensor.matmul(k.banks[:, 4, 0:D], lowT[:, c, :], w["A"][:, c, :], start=(c == 0), stop=False)
                    nc.tensor.matmul(k.banks[:, 4, 0:D], wtT[:, :], w["bias"][0:PROTOS, :], start=False,
                                     stop=True).then_inc(k.sem("branch_ready"), 1)

                @block.scalar
                def _(act):
                    nc.scalar.copy(rows[:, :, :], k.xnT[:, :, bass.ds(t * P, P)]).then_inc(k.sem("rows_ready"), 1)
                    nc.scalar.activation(junk[:, :], k.xn[:, t, :], ACT.Square, accum_out=cols[:, 0:1]).then_inc(k.sem("x2_ready"), 1)
                    act.wait_ge(k.sem("d2_ready"), 1)
                    nc.scalar.activation(dist[:, :], dist[:, :], ACT.Sqrt).then_inc(k.sem("dist_ready"), 1)
                    act.wait_ge(k.sem("shift_ready"), 1)
                    nc.scalar.activation(wt[:, :], dist[:, :], ACT.Exp, scale=temp[:, 1:2], bias=cols[:, 1:2],
                                         accum_out=cols[:, 2:3]).then_inc(k.sem("exp_ready"), 1)
                    act.wait_ge(k.sem("turned"), 1)
                    nc.scalar.copy(lowT[:, :, :], k.banks[:, 2, :].rearrange("p (c n) -> p c n", n=P)).then_inc(k.sem("turned_ready"), 1)
                    nc.scalar.copy(wtT[:, :], k.banks[0:PROTOS, 3, 0:P]).then_inc(k.sem("turned_ready"), 1)

                @block.vector
                def _(dve):
                    link = linker(dve, k.sem("dve_step"))
                    dve.wait_ge(k.sem("cross_ready"), 1)
                    dve.wait_ge(k.sem("x2_ready"), 1)
                    link(nc.vector.scalar_tensor_tensor(dist[:, :], k.banks[:, 0, 0:PROTOS], -2.0, p2[:, :], ALU.mult, ALU.add))
                    nc.vector.tensor_scalar(dist[:, :], dist[:, :], cols[:, 0:1], 0.0, ALU.add, ALU.max).then_inc(k.sem("d2_ready"), 1)
                    dve.wait_ge(k.sem("dist_ready"), 1)
                    link(nc.vector.tensor_reduce(cols[:, 1:2], dist[:, :], AX_X, ALU.min))
                    nc.vector.tensor_tensor(cols[:, 1:2], cols[:, 1:2], temp[:, 0:1], ALU.mult).then_inc(k.sem("shift_ready"), 1)
                    dve.wait_ge(k.sem("exp_ready"), 1)
                    link(nc.vector.reciprocal(cols[:, 2:3], cols[:, 2:3]))
                    link(nc.vector.tensor_scalar(wt[:, :], wt[:, :], cols[:, 2:3], None, ALU.mult))
                    link(nc.vector.max(best[:, :], wt[:, :]))
                    link(nc.vector.max_index(where[:, :], best[:, :], wt[:, :]))
                    link(nc.vector.tensor_copy(wheref[:, :], where[:, :]))
                    for i in range(2):
                        link(nc.vector.tensor_scalar(pick[:, i, :], w["iota"], wheref[:, i:i + 1], None, ALU.is_equal))
                    link(nc.vector.tensor_tensor(pick[:, 0, :], pick[:, 0, :], pick[:, 1, :], ALU.add))
                    link(nc.vector.tensor_tensor(wt[:, :], wt[:, :], pick[:, 0, :], ALU.mult))
                    link(nc.vector.reduce_sum(cols[:, 3:4], best[:, 0:2], AX_X))
                    link(nc.vector.reciprocal(cols[:, 3:4], cols[:, 3:4]))
                    nc.vector.tensor_scalar(wt[:, :], wt[:, :], cols[:, 3:4], None, ALU.mult).then_inc(k.sem("weights_ready"), 1)
                    dve.wait_ge(k.sem("weights_ready"), 1)
                    dve.wait_ge(k.sem("low_ready"), 1)
                    nc.vector.tensor_tensor(low[:, :].rearrange("p (a r) -> p a r", r=RANK),
                                            k.banks[:, 1, :].rearrange("p (a r) -> p a r", r=RANK),
                                            wt[:, :].unsqueeze(2).broadcast_to([P, PROTOS, RANK]), ALU.mult).then_inc(k.sem("weighted_ready"), 1)
                    dve.wait_ge(k.sem("branch_ready"), 1)
                    nc.vector.tensor_tensor(k.x[:, t, :], k.x[:, t, :], k.banks[:, 4, 0:D], ALU.add)
            k.clear()


BUILDERS |= {5: layer5_ffn, 8: layer8_ffn, 9: layer9_xattn, 11: layer11_ffn}


def layout_blocks(g, out):
    ones = np.ones((P, P), np.float32)
    a = "L1_ffn_"
    out[5] = dict(w1=_mat(g[a + "W1"].T), w2=_mat(g[a + "W2"].T), b1=_row(g[a + "b1"]), b2=_row(g[a + "b2"]), ones=ones)
    a = "L3_ffn_"
    out[11] = dict(w1=_mat(g[a + "w_up"].T), w2=_mat(g[a + "w_down"].T), ones=ones)
    a = "L2_ffn_"
    out[8] = dict(protos=_mat(g[a + "prototypes"].T), B=_mat(g[a + "B"].reshape(-1, D).T),
                  A=_mat(g[a + "A"].transpose(0, 2, 1).reshape(-1, D)), bias=g[a + "bias"],
                  temp=_row(g[a + "temp"].reshape(1)), iota=_row(np.arange(PROTOS, dtype=np.float32)), ones=ones)
    a = "L3_xattn_"
    hd = 64
    q = g[a + "q_w"].transpose(1, 0, 2)
    kv = g[a + "kv_w"][:, 0]
    swap = np.concatenate([np.arange(hd // 2, hd), np.arange(hd // 2)])
    timescale = np.float32(10000.0) ** (np.float32(2.0 / hd) * np.arange(hd // 2, dtype=np.float32))

    def table(fn, positions, signed):
        radians = positions.astype(np.float32)[:, None] / timescale
        t = fn(radians).T.astype(np.float32)
        both = np.concatenate([-t if signed else t, t])
        return np.ascontiguousarray(np.concatenate([both, both]))

    qpos, kpos = np.arange(CTX, CTX + SEQ), np.arange(CTX)
    out[9] = dict(wq=_mat(q.reshape(D, -1)), wqs=_mat(q[:, :, swap].reshape(D, -1)),
                  wk=_mat(np.concatenate([kv[0], kv[0], kv[0][:, swap], kv[0][:, swap]], 1)),
                  wv=_mat(np.concatenate([kv[1], kv[1]], 1)), wo=_mat(g[a + "out_w"].reshape(-1, D)), rms=_col(g[a + "rms_scale"]),
                  cosq=table(np.cos, qpos, False), sinq=table(np.sin, qpos, True),
                  cosk=table(np.cos, kpos, False), sink=table(np.sin, kpos, True), ones=ones)



STATES = 16


def token_product(k, src, w, chunks, evacuate):
    nc = k.nc
    with nc.Block() as block:

        @block.tensor
        def _(pe):
            for t in range(TILES):
                if t >= 2:
                    pe.wait_ge(k.sem("tile_used"), t - 1)
                for c in range(chunks):
                    last = nc.tensor.matmul(k.banks[:, t % 2, 0:D], src[:, c, t * P:(t + 1) * P], w[:, c, :],
                                            start=(c == 0), stop=(c == chunks - 1))
                last.then_inc(k.sem("tile_ready"), 1)

        @block.vector
        def _(dve):
            link = linker(dve, k.sem("dve_step"))
            for t in range(TILES):
                dve.wait_ge(k.sem("tile_ready"), t + 1)
                evacuate(dve, link, t, k.banks[:, t % 2, 0:D])
    k.clear()


def short_conv(k, x, out, taps, bias, chunks, tmp):
    nc = k.nc
    ntaps = taps.shape[2]
    with nc.Block() as block:

        @block.vector
        def _(dve):
            for c in range(chunks):
                if bias is None:
                    nc.vector.tensor_scalar(tmp[:, c, :], x[:, c, :], taps[:, c, ntaps - 1:ntaps], None,
                                            ALU.mult).then_inc(k.sem("taps_done"), 1)
                else:
                    nc.vector.tensor_scalar(tmp[:, c, :], x[:, c, :], taps[:, c, ntaps - 1:ntaps], bias[:, c:c + 1],
                                            ALU.mult, ALU.add).then_inc(k.sem("taps_done"), 1)
            for j in range(ntaps - 1):
                back = ntaps - 1 - j
                for c in range(chunks):
                    dve.wait_ge(k.sem("taps_done"), chunks * j + c + 1)
                    o = tmp[:, c, :].rearrange("p (b s) -> p b s", s=SEQ)
                    v = x[:, c, :].rearrange("p (b s) -> p b s", s=SEQ)
                    nc.vector.scalar_tensor_tensor(o[:, :, back:], v[:, :, :SEQ - back], taps[:, c, j:j + 1], o[:, :, back:],
                                                   ALU.mult, ALU.add).then_inc(k.sem("taps_done"), 1)

        @block.scalar
        def _(act):
            for c in range(chunks):
                act.wait_ge(k.sem("taps_done"), chunks * (ntaps - 1) + c + 1)
                nc.scalar.activation(out[:, c, :], tmp[:, c, :], ACT.Silu)
    k.clear()


def selective_scan(k, ctx, chunks, u, delta, bc, a_log, skip, y):
    nc = k.nc
    NB = 4
    neg_a = k.sb(ctx, "neg_a", [P, chunks, STATES])
    decay = k.sb(ctx, "decay", [P, NB, BANK])
    drive = k.sb(ctx, "drive", [P, BANK])
    state = k.sb(ctx, "state", [P, BANK])
    part = k.sb(ctx, "state_out", [P, 2, BANK])
    du = k.sb(ctx, "delta_u", [P, chunks, TOKENS])
    with nc.Block() as block:

        @block.scalar
        def _(act):
            nc.scalar.activation(neg_a[:, :, :], a_log, ACT.Exp).then_inc(k.sem("a_ready"), 1)

        @block.vector
        def _(dve):
            nc.vector.tensor_tensor(du[:, :, :], delta, u, ALU.mult)
            dve.wait_ge(k.sem("a_ready"), 1)
            nc.vector.tensor_scalar(neg_a[:, :, :], neg_a[:, :, :], -1.0, None, ALU.mult)
    k.clear()
    units = [(n, c) for n in range(STATES) for c in range(chunks)]
    with nc.Fori(0, TOKENS // BANK) as h:
        cols = bass.ds(h * BANK, BANK)
        with nc.Block() as block:

            @block.tensor
            def _(pe):
                def spread(n):
                    if n >= 2:
                        pe.wait_ge(k.sem("parts_ready"), chunks * (n - 1))
                    for i in range(2):
                        row = STATES * i + n
                        last = nc.tensor.matmul(k.banks[:, 4 + 2 * (n % 2) + i, :], k.ident[0:2 * STATES, row:row + 1].broadcast_to([2 * STATES, P]),
                                                bc[:, cols], start=True, stop=True)
                    last.then_inc(k.sem("rows_spread"), 1)

                spread(0)
                spread(1)
                for i, (n, c) in enumerate(units):
                    pe.wait_ge(k.sem("parts_ready"), i + 1)
                    nc.tensor.matmul(k.banks[:, c, :], k.ident[:, :], part[:, i % 2, :], start=(n == 0),
                                     stop=(n == STATES - 1)).then_inc(k.sem("parts_used"), 1)
                    if c == chunks - 1 and n + 2 < STATES:
                        spread(n + 2)

            @block.scalar
            def _(act):
                for i, (n, c) in enumerate(units):
                    if i >= NB:
                        act.wait_ge(k.sem("scanned"), i - NB + 1)
                    nc.scalar.activation(decay[:, i % NB, :], delta[:, c, cols], ACT.Exp,
                                         scale=neg_a[:, c, n:n + 1]).then_inc(k.sem("decay_ready"), 1)

            @block.gpsimd
            def _(pool):
                for i in range(len(units)):
                    pool.wait_ge(k.sem("decay_ready"), i + 1)
                    nc.gpsimd.memset(decay[:, i % NB, 0:BANK:SEQ], 0.0).then_inc(k.sem("decay_cut"), 1)

            @block.vector
            def _(dve):
                link = linker(dve, k.sem("dve_step"))
                for i, (n, c) in enumerate(units):
                    if c == 0:
                        dve.wait_ge(k.sem("rows_spread"), n + 1)
                    link(nc.vector.tensor_tensor(drive[:, :], du[:, c, cols], k.banks[:, 4 + 2 * (n % 2), :], ALU.mult))
                    dve.wait_ge(k.sem("decay_cut"), i + 1)
                    nc.vector.tensor_tensor_scan(state[:, :], decay[:, i % NB, :], drive[:, :], 0.0, ALU.mult,
                                                 ALU.add).then_inc(k.sem("scanned"), 1)
                    dve.wait_ge(k.sem("scanned"), i + 1)
                    if i >= 2:
                        dve.wait_ge(k.sem("parts_used"), i - 1)
                    nc.vector.tensor_tensor(part[:, i % 2, :], state[:, :], k.banks[:, 5 + 2 * (n % 2), :],
                                            ALU.mult).then_inc(k.sem("parts_ready"), 1)
                dve.wait_ge(k.sem("parts_used"), len(units))
                for c in range(chunks):
                    nc.vector.scalar_tensor_tensor(y[:, c, cols], u[:, c, cols], skip[:, c:c + 1], k.banks[:, c, :], ALU.mult, ALU.add)
        k.clear()


def layer10_attn(k, w):
    nc = k.nc
    chunks = 4
    with ExitStack() as ctx:
        u = k.sb(ctx, "u", [P, chunks, TOKENS])
        delta = k.sb(ctx, "delta", [P, chunks, TOKENS])
        dt = k.sb(ctx, "dt_low", [STATES, 1, TOKENS])
        bc = k.sb(ctx, "bc", [2 * STATES, TOKENS])
        project(k, [(w["win"], c * P, u[:, c, :], None, ACT.Identity) for c in range(chunks)])
        short_conv(k, u, u, w["taps"], w["cbias"], chunks, delta)
        project(k, [(w["wdt_low"], 0, dt[:, 0, :], None, ACT.Identity), (w["wbc"], 0, bc[:, :], None, ACT.Identity)], src=u, chunks=chunks)
        project(k, [(w["wdt"], c * P, delta[:, c, :], w["dtb"][:, c:c + 1], ACT.Identity) for c in range(chunks)], src=dt, chunks=1)
        with ExitStack() as room:
            e, low = (k.sb(room, n, [P, chunks, TOKENS])[:, :, :] for n in ("softplus_e", "softplus_low"))
            softplus(k, delta[:, :, :], e, low)
        selective_scan(k, ctx, chunks, u[:, :, :], delta[:, :, :], bc, w["a_log"], w["skip"], u)

        def finish(dve, link, t, psum):
            nc.vector.tensor_tensor(k.x[:, t, :], k.x[:, t, :], psum, ALU.add).then_inc(k.sem("tile_used"), 1)

        token_product(k, u, w["wout"], chunks, finish)


def layer4_attn(k, w):
    nc = k.nc
    with ExitStack() as ctx:
        s = k.sb(ctx, "inner_stream", [P, TILES, D])
        with nc.Block() as block:

            @block.gpsimd
            def _(pool):
                nc.gpsimd.tensor_copy(s[:, :, :], k.xn[:, :, :])
        normalize(k, src=k.xn, scale=w["n1g"], shift=w["n1b"])
        with ExitStack() as inner:
            u = k.sb(inner, "u", [P, CHUNKS, TOKENS])
            z = k.sb(inner, "z", [P, CHUNKS, TOKENS])
            delta = k.sb(inner, "delta", [P, CHUNKS, TOKENS])
            dt = k.sb(inner, "dt_low", [64, 1, TOKENS])
            bc = k.sb(inner, "bc", [2 * STATES, TOKENS])
            hs = k.sb(inner, "mixed", [P, D])
            st = k.sb(inner, "mixed_stats", [P, 6])
            mv = k.sb(inner, "mixed_meanvar", [P, 2])
            project(k, [(w["win"], c * P, u[:, c, :], None, ACT.Identity) for c in range(CHUNKS)]
                    + [(w["win"], D + c * P, z[:, c, :], None, ACT.Silu) for c in range(CHUNKS)])
            short_conv(k, u, u, w["taps"], w["cbias"], CHUNKS, delta)
            project(k, [(w["wdt_low"], 0, dt[:, 0, :], None, ACT.Identity), (w["wbc"], 0, bc[:, :], None, ACT.Identity)], src=u)
            project(k, [(w["wdt"], c * P, delta[:, c, :], w["dtb"][:, c:c + 1], ACT.Identity) for c in range(CHUNKS)], src=dt, chunks=1)
            with ExitStack() as room:
                e, low = (k.sb(room, n, [P, CHUNKS, TOKENS])[:, :, :] for n in ("softplus_e", "softplus_low"))
                softplus(k, delta[:, :, :], e, low)
            selective_scan(k, inner, CHUNKS, u[:, :, :], delta[:, :, :], bc, w["a_log"], w["skip"], u)
            with nc.Block() as block:

                @block.vector
                def _(dve):
                    nc.vector.tensor_tensor(u[:, :, :], u[:, :, :], z[:, :, :], ALU.mult)
            h_tok = k.xn

            def keep(dve, link, t, psum):
                nc.vector.tensor_copy(h_tok[:, t, :], psum).then_inc(k.sem("tile_used"), 1)

            token_product(k, u, w["wout"], CHUNKS, keep)
        normalize(k, src=k.xn, turn=False)
        with nc.Block() as block:

            @block.vector
            def _(dve):
                link = linker(dve, k.sem("dve_step"))
                for op, row in ((ALU.mult, w["mg"]), (ALU.add, w["mb"])):
                    link(nc.vector.tensor_tensor(k.xn[:, :, :], k.xn[:, :, :], row.unsqueeze(1).broadcast_to([P, TILES, D]), op))
                nc.vector.tensor_tensor(s[:, :, :], s[:, :, :], k.xn[:, :, :], ALU.add)
        k.clear()
        normalize(k, src=s, scale=w["n2g"], shift=w["n2b"])
        hidden = k.sb(ctx, "leaky_hidden", [P, HIDDEN // P, TOKENS])
        project(k, [(w["w1"], c * P, hidden[:, c, :], None, ACT.Identity) for c in range(HIDDEN // P)])
        with nc.Block() as block:

            @block.vector
            def _(dve):
                for c in range(HIDDEN // P):
                    nc.vector.scalar_tensor_tensor(hidden[:, c, :], hidden[:, c, :], 0.01, hidden[:, c, :], ALU.mult, ALU.max)

        def add_s(dve, link, t, psum):
            nc.vector.tensor_tensor(s[:, t, :], s[:, t, :], psum, ALU.add).then_inc(k.sem("tile_used"), 1)

        token_product(k, hidden, w["w2"], HIDDEN // P, add_s)
        normalize(k, src=s, scale=w["n3g"], shift=w["n3b"])

        def last(dve, link, t, psum):
            nc.vector.tensor_tensor(s[:, t, :], s[:, t, :], psum, ALU.add).then_inc(k.sem("tile_used"), 1)
            dve.wait_ge(k.sem("tile_used"), t + 1)
            link(nc.vector.tensor_tensor(s[:, t, :], s[:, t, :], w["feb"], ALU.add))
            nc.vector.tensor_tensor(k.x[:, t, :], k.x[:, t, :], s[:, t, :], ALU.add)

        token_product(k, k.xnT, w["fe"], CHUNKS, last)


BUILDERS |= {4: layer4_attn, 10: layer10_attn}


def layout_scans(g, out):
    a = "L1_attn_"
    xp = g[a + "x_proj_w"].T
    out[4] = dict(win=_mat(g[a + "in_proj_w"].T), taps=g[a + "conv_w"].reshape(-1, P, 2).transpose(1, 0, 2), cbias=_col(g[a + "conv_b"]),
                  wdt_low=_mat(xp[:, :64]), wbc=_mat(xp[:, 64:]), wdt=g[a + "dt_proj_w"].T[:, None, :], dtb=_col(g[a + "dt_proj_b"]),
                  a_log=g[a + "A_log"].reshape(-1, P, STATES).transpose(1, 0, 2), skip=_col(g[a + "Dp"]), wout=_mat(g[a + "out_proj_w"].T),
                  n1g=_col(g[a + "n1_g"]), n1b=_col(g[a + "n1_b"]), n2g=_col(g[a + "n2_g"]), n2b=_col(g[a + "n2_b"]),
                  n3g=_col(g[a + "n3_g"]), n3b=_col(g[a + "n3_b"]), mg=_row(g[a + "mnorm_g"]), mb=_row(g[a + "mnorm_b"]),
                  w1=_mat(g[a + "ffn_w1"].T), w2=_mat(g[a + "ffn_w2"].T), fe=_mat(g[a + "fe_w"].T), feb=_row(g[a + "fe_b"]))
    a = "L3_attn_"
    wx = g[a + "W_x"]
    out[10] = dict(win=_mat(g[a + "W_in"]), taps=g[a + "conv_w"].reshape(-1, P, 4).transpose(1, 0, 2), cbias=_col(g[a + "conv_b"]),
                   wdt_low=_mat(wx[:, :16]), wbc=_mat(wx[:, 16:]), wdt=g[a + "W_dt"][:, None, :], dtb=_col(g[a + "b_dt"]),
                   a_log=g[a + "A_log"].reshape(-1, P, STATES).transpose(1, 0, 2), skip=_col(g[a + "D"]), wout=_mat(g[a + "W_out"]))



DH = 4
HD = D // DH
DCHUNK = 32
LEVELS = 5


def unit_heads(k, x, sq, same64):
    nc = k.nc
    parts = [(c, h) for c in range(CHUNKS) for h in range(TOKENS // BANK)]
    with nc.Block() as block:

        @block.scalar
        def _(act):
            nc.scalar.activation(sq[:, :, :], x[:, :, :], ACT.Square).then_inc(k.sem("squares_ready"), 1)
            act.wait_ge(k.sem("sums_ready"), 1)
            nc.scalar.activation(sq[:, :, :], sq[:, :, :], ACT.Sqrt).then_inc(k.sem("norm_ready"), 1)

        @block.tensor
        def _(pe):
            pe.wait_ge(k.sem("squares_ready"), 1)
            for n, (c, h) in enumerate(parts):
                last = nc.tensor.matmul(k.banks[:, n, :], same64, sq[:, c, h * BANK:(h + 1) * BANK], start=True, stop=True)
            last.then_inc(k.sem("sums_in_psum"), 1)

        @block.vector
        def _(dve):
            link = linker(dve, k.sem("dve_step"))
            dve.wait_ge(k.sem("sums_in_psum"), 1)
            nc.vector.tensor_scalar(sq[:, :, :].rearrange("p c n -> p (c n)"), k.banks[:, 0:4, :].rearrange("p b n -> p (b n)"),
                                    1e-6, None, ALU.add).then_inc(k.sem("sums_ready"), 1)
            dve.wait_ge(k.sem("norm_ready"), 1)
            link(nc.vector.reciprocal(sq[:, :, :], sq[:, :, :]))
            nc.vector.tensor_tensor(x[:, :, :], x[:, :, :], sq[:, :, :], ALU.mult)
    k.clear()


def layer7_attn(k, w):
    nc = k.nc
    with ExitStack() as ctx:
        q, kk, v, kb, vb = (k.sb(ctx, "delta_" + n, [P, CHUNKS, TOKENS]) for n in ("q", "k", "v", "kb", "vb"))
        mixed = k.xn[:, :, :].rearrange("p t d -> p (t d)").rearrange("p (c n) -> p c n", c=CHUNKS)
        with ExitStack() as inner:
            cat = k.sb(inner, "conv_cat", [P, 6, TOKENS])
            project(k, [(w[n], c * P, o[:, c, :], None, f) for n, o, f in
                        (("wq", q, ACT.Identity), ("wk", kk, ACT.Identity), ("wv", v, ACT.Identity), ("wb", vb, ACT.Sigmoid))
                        for c in range(CHUNKS)])
            for x, taps in ((q, w["tq"]), (kk, w["tk"]), (v, w["tv"])):
                short_conv(k, x, x, taps, None, CHUNKS, cat)
            unit_heads(k, q, cat[:, 0:CHUNKS, :], w["same64"])
            unit_heads(k, kk, cat[:, 0:CHUNKS, :], w["same64"])
            with nc.Block() as block:

                @block.gpsimd
                def _(pool):
                    nc.gpsimd.tensor_tensor(kb[:, :, :], kk[:, :, :], vb[:, :, :], ALU.mult).then_inc(k.sem("kb_ready"), 1)
                    pool.wait_ge(k.sem("kb_ready"), 1)
                    nc.gpsimd.tensor_tensor(vb[:, :, :], v[:, :, :], vb[:, :, :], ALU.mult)

                @block.vector
                def _(dve):
                    for j in range(31):
                        for s, taps in enumerate((w["t31"], w["t15"], w["t3"])):
                            if j >= taps.shape[2]:
                                continue
                            n = taps.shape[2]
                            for c in range(CHUNKS):
                                o = cat[:, 2 * (2 - s) + c, :].rearrange("p (b s) -> p b s", s=SEQ)
                                x = v[:, c, :].rearrange("p (b s) -> p b s", s=SEQ)
                                tap = taps[:, c, n - 1 - j:n - j]
                                done = k.sem(f"conv{s}{c}")
                                if j == 0:
                                    nc.vector.tensor_scalar(o, x, tap, None, ALU.mult).then_inc(done, 1)
                                else:
                                    dve.wait_ge(done, j)
                                    nc.vector.scalar_tensor_tensor(o[:, :, j:], x[:, :, :SEQ - j], tap, o[:, :, j:], ALU.mult,
                                                                   ALU.add).then_inc(done, 1)
            k.clear()
            with nc.Block() as block:

                @block.tensor
                def _(pe):
                    for c in range(CHUNKS):
                        for h in range(TOKENS // BANK):
                            for g in range(3):
                                last = nc.tensor.matmul(k.banks[:, 2 * c + h, :], w["mix"][:, 3 * c + g, :], cat[:, 3 * c + g, h * BANK:(h + 1) * BANK],
                                                        start=(g == 0), stop=(g == 2))
                            last.then_inc(k.sem("mix_ready"), 1)

                @block.scalar
                def _(act):
                    for n in range(4):
                        act.wait_ge(k.sem("mix_ready"), n + 1)
                        nc.scalar.copy(mixed[:, n // 2, (n % 2) * BANK:(n % 2 + 1) * BANK], k.banks[:, n, :])
            k.clear()
        delta_tiles(k, ctx, w, (q, kk, kb, vb, v, mixed))


def delta_tiles(k, ctx, w, sources):
    nc = k.nc
    here = k.sb(ctx, "tile_feat", [P, 6, CHUNKS, P])
    tok = k.sb(ctx, "tile_tok", [P, 5, DH, HD])
    gram = k.sb(ctx, "gramT", [P, DH, P])
    level = k.sb(ctx, "gramT_level", [P, 2, DH, P])
    local = k.sb(ctx, "localT", [P, DH, P])
    T, TT, U = (k.sb(ctx, n, [P, DH, P]) for n in ("inverse", "inverseT", "level_product"))
    two = k.sb(ctx, "by_sequence", [P, 3, DH, PER_TILE, HD])
    qT2, wT2 = gram, T
    u = k.sb(ctx, "delta_u", [P, DH, HD])
    S = k.sb(ctx, "delta_state", [P, DH, HD])
    dl = k.sb(ctx, "delta_out", [P, DH, HD])
    ms = k.sb(ctx, "conv_out", [P, DH, HD])
    F = k.sb(ctx, "head_means", [P, 12])
    FT = k.sb(ctx, "head_meansT", [12, P])
    hdn = k.sb(ctx, "gate_hidden", [P, 4, P])
    lg = k.sb(ctx, "gate_logits", [P, DH, 3])
    gm = k.sb(ctx, "gate_col", [P, DH])
    o = k.sb(ctx, "mix_out", [P, DH, HD])
    o2 = k.sb(ctx, "mix_work", [P, DH, HD])
    oT = k.sb(ctx, "mix_outT", [P, CHUNKS, P])
    Q, K_, KB, VB, V_, MIX = range(6)
    B = k.banks

    def heads(bank, width):
        return B[:, bank, 0:DH * width].rearrange("p (h n) -> p h n", h=DH)

    with nc.Fori(0, TILES) as t:
        cols = bass.ds(t * P, P)
        with nc.Block() as block:

            @block.gpsimd
            def _(pool):
                for i in (V_, MIX):
                    nc.gpsimd.tensor_copy(here[:, i, :, :], sources[i][:, :, cols]).then_inc(k.sem("late_copied"), 1)
                pool.wait_ge(k.sem("gram_copied"), 2)
                for s in range(LEVELS):
                    if s >= 2:
                        pool.wait_ge(k.sem("product_ready"), s - 1)
                    if s == 2:
                        pool.wait_ge(k.sem("TT_ready"), 1)
                    nc.gpsimd.tensor_tensor(level[:, s % 2, :, :], gram[:, :, :], w["levels"][:, s, :].unsqueeze(1).broadcast_to([P, DH, P]),
                                            ALU.mult).then_inc(k.sem("level_ready"), 1)
                    if s == 1:
                        pool.wait_ge(k.sem("tok_ready"), 2)
                        for j, (src, ind) in enumerate(((Q, "second"), (KB, "second"), (K_, "first"))):
                            for b in range(PER_TILE):
                                nc.gpsimd.tensor_scalar(two[:, j, :, b, :], tok[:, src, :, :], w[ind][:, b:b + 1], None,
                                                        ALU.mult).then_inc(k.sem("two_ready"), 1)

            @block.tensor
            def _(pe):
                pe.wait_ge(k.sem("copied"), 4)
                for i in range(4):
                    for c in range(CHUNKS):
                        last = nc.tensor.transpose(B[:, i // 2, ((i % 2) * 2 + c) * P:((i % 2) * 2 + c + 1) * P], here[:, i, c, :], k.ident[:, :])
                last.then_inc(k.sem("turned"), 1)
                for bank, rhs, ready in ((3, KB, "gram_in_psum"), (4, Q, "local_in_psum")):
                    for h in range(DH):
                        part = slice(HD * (h % 2), HD * (h % 2) + HD)
                        last = nc.tensor.matmul(B[:, bank + 2 * (h % 2), h // 2 * P:(h // 2 + 1) * P], here[part, K_, h // 2, :], here[part, rhs, h // 2, :],
                                                start=True, stop=True)
                        if h >= DH - 2:
                            last.then_inc(k.sem(ready), 1)
                pe.wait_ge(k.sem("late_copied"), 2)
                for c in range(CHUNKS):
                    last = nc.tensor.transpose(B[:, 2, c * P:(c + 1) * P], here[:, V_, c, :], k.ident[:, :])
                last.then_inc(k.sem("v_turned"), 1)
                for s in range(LEVELS):
                    pe.wait_ge(k.sem("level_ready"), s + 1)
                    if s:
                        pe.wait_ge(k.sem("T_ready"), s)
                    for h in range(DH):
                        last = nc.tensor.matmul(B[:, 5, h * P:(h + 1) * P], level[:, s % 2, h, :], T[:, h, :] if s else k.ident[:, :],
                                                start=True, stop=True)
                    last.then_inc(k.sem("product_ready"), 1)
                    if s == 0:
                        continue
                    pe.wait_ge(k.sem("U_ready"), s)
                    pe.wait_ge(k.sem("TT_ready"), s)
                    for h in range(DH):
                        last = nc.tensor.matmul(B[:, 7, h * P:(h + 1) * P], U[:, h, :], TT[:, h, :], start=True, stop=True)
                    last.then_inc(k.sem("stepT_ready"), 1)
                    if s < LEVELS - 1:
                        pe.wait_ge(k.sem("local_ready"), 2)
                        for h in range(DH):
                            last = nc.tensor.matmul(B[:, 6, h * P:(h + 1) * P], TT[:, h, :], U[:, h, :], start=True, stop=True)
                        last.then_inc(k.sem("step_ready"), 1)
                pe.wait_ge(k.sem("tok_ready"), 3)
                pe.wait_ge(k.sem("two_ready"), 6)
                for h in range(DH):
                    last = nc.tensor.transpose(B[:, 2, h * P:(h + 1) * P], two[:, 0, h, :, :].rearrange("p b n -> p (b n)"), k.ident[:, :])
                last.then_inc(k.sem("q_turned"), 1)
                pe.wait_ge(k.sem("TT_ready"), LEVELS)
                for h in range(DH):
                    last = nc.tensor.matmul(B[:, 0, h * HD:(h + 1) * HD], TT[:, h, :], tok[:, VB, h, :], start=True, stop=True)
                last.then_inc(k.sem("u_in_psum"), 1)
                for h in range(DH):
                    last = nc.tensor.matmul(B[:, 1, h * P:(h + 1) * P], two[:, 1, h, :, :].rearrange("p b n -> p (b n)"), TT[:, h, :],
                                            start=True, stop=True)
                last.then_inc(k.sem("w_in_psum"), 1)
                pe.wait_ge(k.sem("u_copied"), 1)
                for h in range(DH):
                    last = nc.tensor.matmul(B[:, 3, h * HD:(h + 1) * HD], two[:, 2, h, :, :].rearrange("p b n -> p (b n)"), u[:, h, :],
                                            start=True, stop=True)
                last.then_inc(k.sem("state_in_psum"), 1)
                for c in range(CHUNKS):
                    last = nc.tensor.matmul(B[:, 7, 0:D], here[:, MIX, c, :], w["mixer"][:, c, :], start=(c == 0), stop=(c == CHUNKS - 1))
                last.then_inc(k.sem("conv_in_psum"), 1)
                pe.wait_ge(k.sem("state_copied"), 1)
                pe.wait_ge(k.sem("by_seq_copied"), 2)
                for h in range(DH):
                    last = nc.tensor.matmul(B[:, 5, h * HD:(h + 1) * HD], wT2[:, h, :], S[:, h, :], start=True, stop=True)
                last.then_inc(k.sem("ws_in_psum"), 1)
                pe.wait_ge(k.sem("u_final"), 1)
                for h in range(DH):
                    nc.tensor.matmul(B[:, 6, h * HD:(h + 1) * HD], qT2[:, h, :], S[:, h, :], start=True, stop=False)
                    last = nc.tensor.matmul(B[:, 6, h * HD:(h + 1) * HD], local[:, h, :], u[:, h, :], start=False, stop=True)
                last.then_inc(k.sem("delta_in_psum"), 1)
                pe.wait_ge(k.sem("means_ready"), 1)
                nc.tensor.transpose(B[0:12, 4, 0:P], F[:, :], k.ident[:, :]).then_inc(k.sem("means_turned"), 1)
                pe.wait_ge(k.sem("meansT_ready"), 1)
                for m in range(4):
                    for c in range(CHUNKS):
                        nc.tensor.matmul(B[:, 5, m * P:(m + 1) * P], w["f1"][:, c, m * P:(m + 1) * P], k.xnT[:, c, cols],
                                         start=(c == 0), stop=False)
                    last = nc.tensor.matmul(B[:, 5, m * P:(m + 1) * P], w["f1m"][:, m * P:(m + 1) * P], FT[:, :], start=False, stop=True)
                last.then_inc(k.sem("gate_in_psum"), 1)
                pe.wait_ge(k.sem("gate_hidden_ready"), 4)
                for m in range(4):
                    last = nc.tensor.matmul(B[:, 3, 0:12], hdn[:, m, :], w["f2"][:, m, :], start=(m == 0), stop=(m == 3))
                last.then_inc(k.sem("logits_in_psum"), 1)
                pe.wait_ge(k.sem("out_ready"), 1)
                for c in range(CHUNKS):
                    last = nc.tensor.transpose(B[:, 6, c * P:(c + 1) * P], o[:, 2 * c:2 * c + 2, :].rearrange("p h n -> p (h n)"), k.ident[:, :])
                last.then_inc(k.sem("out_turned"), 1)
                pe.wait_ge(k.sem("outT_ready"), 1)
                for c in range(CHUNKS):
                    last = nc.tensor.matmul(B[:, 0, 0:D], oT[:, c, :], w["wo"][:, c, :], start=(c == 0), stop=(c == CHUNKS - 1))
                last.then_inc(k.sem("branch_ready"), 1)

            @block.scalar
            def _(act):
                for i in range(4):
                    nc.scalar.copy(here[:, i, :, :], sources[i][:, :, cols]).then_inc(k.sem("copied"), 1)
                act.wait_ge(k.sem("gram_in_psum"), 2)
                for r in range(2):
                    nc.scalar.copy(gram[:, r::2, :], B[:, 3 + 2 * r, 0:2 * P].rearrange("p (h n) -> p h n", h=2)).then_inc(k.sem("gram_copied"), 1)
                for i in range(2):
                    nc.scalar.copy(tok[:, 2 * i:2 * i + 2, :, :].rearrange("p a h n -> p (a h n)"), B[:, i, :]).then_inc(k.sem("tok_ready"), 1)
                act.wait_ge(k.sem("v_turned"), 1)
                nc.scalar.copy(tok[:, V_, :, :], heads(2, HD)).then_inc(k.sem("tok_ready"), 1)
                for s in range(1, LEVELS):
                    act.wait_ge(k.sem("product_ready"), s + 1)
                    nc.scalar.copy(U[:, :, :], heads(5, P)).then_inc(k.sem("U_ready"), 1)
                act.wait_ge(k.sem("q_turned"), 1)
                nc.scalar.copy(qT2[:, :, :], heads(2, P)).then_inc(k.sem("by_seq_copied"), 1)
                act.wait_ge(k.sem("w_in_psum"), 1)
                nc.scalar.copy(wT2[:, :, :], heads(1, P)).then_inc(k.sem("by_seq_copied"), 1)
                act.wait_ge(k.sem("state_in_psum"), 1)
                nc.scalar.copy(S[:, :, :], heads(3, HD)).then_inc(k.sem("state_copied"), 1)
                act.wait_ge(k.sem("conv_in_psum"), 1)
                nc.scalar.copy(ms[:, :, :], heads(7, HD)).then_inc(k.sem("conv_ready"), 1)
                act.wait_ge(k.sem("means_turned"), 1)
                nc.scalar.copy(FT[:, :], B[0:12, 4, 0:P]).then_inc(k.sem("meansT_ready"), 1)
                act.wait_ge(k.sem("gate_in_psum"), 1)
                for m in range(4):
                    nc.scalar.activation(hdn[:, m, :], B[:, 5, m * P:(m + 1) * P], ACT.Gelu,
                                         bias=w["f1b"][:, m:m + 1]).then_inc(k.sem("gate_hidden_ready"), 1)
                act.wait_ge(k.sem("shifted"), 1)
                nc.scalar.activation(lg[:, :, :], lg[:, :, :], ACT.Exp).then_inc(k.sem("gate_exp"), 1)
                act.wait_ge(k.sem("mean_square"), 1)
                nc.scalar.activation(gm[:, :], gm[:, :], ACT.Sqrt).then_inc(k.sem("root"), 1)
                act.wait_ge(k.sem("out_turned"), 1)
                nc.scalar.copy(oT[:, :, :], B[:, 6, 0:D].rearrange("p (c n) -> p c n", n=P)).then_inc(k.sem("outT_ready"), 1)

            @block.vector
            def _(dve):
                link = linker(dve, k.sem("dve_step"))
                eye = k.ident[:, :].unsqueeze(1).broadcast_to([P, DH, P])
                dve.wait_ge(k.sem("level_ready"), 1)
                nc.vector.tensor_tensor(TT[:, :, :], eye, level[:, 0, :, :], ALU.subtract).then_inc(k.sem("TT_ready"), 1)
                dve.wait_ge(k.sem("product_ready"), 1)
                nc.vector.tensor_tensor(T[:, :, :], eye, heads(5, P), ALU.subtract).then_inc(k.sem("T_ready"), 1)
                dve.wait_ge(k.sem("local_in_psum"), 2)
                for r in range(2):
                    nc.vector.tensor_tensor(local[:, r::2, :], B[:, 4 + 2 * r, 0:2 * P].rearrange("p (h n) -> p h n", h=2),
                                            w["inclusive"].unsqueeze(1).broadcast_to([P, 2, P]), ALU.mult).then_inc(k.sem("local_ready"), 1)
                for s in range(1, LEVELS):
                    if s < LEVELS - 1:
                        dve.wait_ge(k.sem("step_ready"), s)
                        dve.wait_ge(k.sem("T_ready"), s)
                        nc.vector.tensor_tensor(T[:, :, :], T[:, :, :], heads(6, P), ALU.subtract).then_inc(k.sem("T_ready"), 1)
                    dve.wait_ge(k.sem("stepT_ready"), s)
                    dve.wait_ge(k.sem("TT_ready"), s)
                    nc.vector.tensor_tensor(TT[:, :, :], TT[:, :, :], heads(7, P), ALU.subtract).then_inc(k.sem("TT_ready"), 1)
                dve.wait_ge(k.sem("u_in_psum"), 1)
                nc.vector.tensor_copy(u[:, :, :], heads(0, HD)).then_inc(k.sem("u_copied"), 1)
                dve.wait_ge(k.sem("u_copied"), 1)
                dve.wait_ge(k.sem("ws_in_psum"), 1)
                nc.vector.tensor_tensor(u[:, :, :], u[:, :, :], heads(5, HD), ALU.subtract).then_inc(k.sem("u_final"), 1)
                dve.wait_ge(k.sem("delta_in_psum"), 1)
                link(nc.vector.tensor_copy(dl[:, :, :], heads(6, HD)))
                dve.wait_ge(k.sem("conv_ready"), 1)
                dve.wait_ge(k.sem("tok_ready"), 3)
                for i, src in enumerate((ms, dl, tok[:, V_, :, :])):
                    last = nc.vector.tensor_reduce(F[:, 4 * i:4 * i + 4], src[:, :, :], AX_X, ALU.add, apply_absolute_value=True)
                link(last)
                nc.vector.tensor_scalar(F[:, :], F[:, :], 1.0 / HD, None, ALU.mult).then_inc(k.sem("means_ready"), 1)
                dve.wait_ge(k.sem("logits_in_psum"), 1)
                link(nc.vector.tensor_tensor(lg[:, :, :].rearrange("p h n -> p (h n)"), B[:, 3, 0:12], w["f2b"], ALU.add))
                link(nc.vector.reduce_max(gm[:, :], lg[:, :, :], AX_X))
                nc.vector.tensor_tensor(lg[:, :, :], lg[:, :, :], gm[:, :].unsqueeze(2).broadcast_to([P, DH, 3]),
                                        ALU.subtract).then_inc(k.sem("shifted"), 1)
                dve.wait_ge(k.sem("gate_exp"), 1)
                link(nc.vector.reduce_sum(gm[:, :], lg[:, :, :], AX_X))
                link(nc.vector.reciprocal(gm[:, :], gm[:, :]))
                link(nc.vector.tensor_tensor(lg[:, :, :], lg[:, :, :], gm[:, :].unsqueeze(2).broadcast_to([P, DH, 3]), ALU.mult))

                def part(i):
                    return lg[:, :, i:i + 1].broadcast_to([P, DH, HD])

                link(nc.vector.tensor_tensor(o[:, :, :], ms[:, :, :], part(0), ALU.mult))
                link(nc.vector.tensor_tensor(dl[:, :, :], dl[:, :, :], part(1), ALU.mult))
                link(nc.vector.tensor_tensor(o[:, :, :], o[:, :, :], dl[:, :, :], ALU.add))
                link(nc.vector.tensor_tensor(dl[:, :, :], tok[:, V_, :, :], part(2), ALU.mult))
                link(nc.vector.tensor_tensor(o[:, :, :], o[:, :, :], dl[:, :, :], ALU.add))
                link(nc.vector.tensor_tensor(o2[:, :, :], o[:, :, :], o[:, :, :], ALU.mult))
                link(nc.vector.reduce_sum(gm[:, :], o2[:, :, :], AX_X))
                nc.vector.tensor_scalar(gm[:, :], gm[:, :], 1.0 / HD, 1e-5, ALU.mult, ALU.add).then_inc(k.sem("mean_square"), 1)
                dve.wait_ge(k.sem("root"), 1)
                link(nc.vector.reciprocal(gm[:, :], gm[:, :]))
                link(nc.vector.tensor_tensor(o[:, :, :], o[:, :, :], gm[:, :].unsqueeze(2).broadcast_to([P, DH, HD]), ALU.mult))
                nc.vector.tensor_tensor(o[:, :, :], o[:, :, :], w["onorm"].unsqueeze(1).broadcast_to([P, DH, HD]),
                                        ALU.mult).then_inc(k.sem("out_ready"), 1)
                dve.wait_ge(k.sem("branch_ready"), 1)
                nc.vector.tensor_tensor(k.x[:, t, :], k.x[:, t, :], B[:, 0, 0:D], ALU.add)
        k.clear()


BUILDERS |= {7: layer7_attn}


def layout_delta(g, out):
    a = "L2_attn_"
    i = np.arange(P)
    same = i[:, None] // DCHUNK == i[None, :] // DCHUNK
    levels = []
    for s in range(LEVELS):
        r = 2 ** s
        levels.append((i[None, :] > i[:, None]) & (i[:, None] // (2 * r) == i[None, :] // (2 * r)) & (i[:, None] // r != i[None, :] // r))
    levels = np.stack(levels, 1).astype(np.float32)
    inclusive = ((i[None, :] >= i[:, None]) & same).astype(np.float32)
    seqs, second = i // SEQ, (i % SEQ) // DCHUNK
    ind = {n: np.stack([((seqs == b) & (second == s)) for b in range(PER_TILE)], 1).astype(np.float32) for n, s in (("first", 0), ("second", 1))}
    mix = np.zeros((6, P, P), np.float32)
    km = g[a + "kernel_mix_w"]
    for h in range(DH):
        for r0 in range(0, 192, 64):
            row = 192 * h + r0
            mix[row // P, row % P:row % P + 64, HD * (h % 2):HD * (h % 2) + HD] = km[r0:r0 + 64]

    def taps(n):
        wt = g[a + n]
        return wt.reshape(-1, P, wt.shape[1]).transpose(1, 0, 2)

    f1 = g[a + "fusion_w1"]
    out[7] = dict(wq=_mat(g[a + "Wq"]), wk=_mat(g[a + "Wk"]), wv=_mat(g[a + "Wv"]), wb=_mat(np.repeat(g[a + "Wb"], HD, axis=1)),
                  tq=taps("conv_q_w"), tk=taps("conv_k_w"), tv=taps("conv_v_w"), t3=taps("ms_w3"), t15=taps("ms_w15"), t31=taps("ms_w31"),
                  mix=mix.transpose(1, 0, 2), mixer=_mat(g[a + "channel_mixer_w"]), f1=_mat(f1[:D]), f1m=f1[D:], f1b=_col(g[a + "fusion_b1"]),
                  f2=_mat(g[a + "fusion_w2"]), f2b=_row(g[a + "fusion_b2"]), onorm=_row(g[a + "o_norm_w"]), wo=_mat(g[a + "Wo"]),
                  same64=(i[:, None] // HD == i[None, :] // HD).astype(np.float32), levels=levels, inclusive=inclusive, **ind)


def build(nc, dram, places, layers):
    with ExitStack() as ctx:
        k = Core(nc, ctx, dram)
        loaded = ctx.enter_context(nc.semaphore("weights_loaded"))
        first = ctx.enter_context(nc.semaphore("first_loads"))
        stored = ctx.enter_context(nc.semaphore("out_stored"))
        with nc.Block() as block:

            @block.sync
            def _(sp):
                sp.dma_start(k.x[:, :, :], dram["x"].rearrange("(t c) s d -> (c s) t d", c=PER_TILE)).then_inc(first, 16)
                sp.dma_start(k.ident[:, :], dram["ident"]).then_inc(first, 16)
                sp.dma_start(k.hmask16[:, :], dram["hmask16"]).then_inc(first, 16)
                sp.dma_start(k.hmask64[:, :], dram["hmask64"]).then_inc(first, 16)
                sp.dma_start(k.ctxT[:, :, :], dram["ctxT"].rearrange("(c p) n -> p c n", p=P)).then_inc(first, 16)
                n = dram[f"w{layers[0]}"].shape[1]
                sp.dma_start(k.weights[0][:, 0:n], dram[f"w{layers[0]}"]).then_inc(loaded, 16)
                sp.dma_start(k.fold[:, :], dram["fold"]).then_inc(first, 16)
                sp.wait_ge(first, 6 * 16)
        for i, layer in enumerate(layers):
            with nc.Block() as block:

                @block.sync
                def _(sp):
                    sp.wait_ge(loaded, 16 * (i + 1))
                    if i + 1 < len(layers):
                        n = dram[f"w{layers[i + 1]}"].shape[1]
                        sp.dma_start(k.weights[(i + 1) % 2][:, 0:n], dram[f"w{layers[i + 1]}"]).then_inc(loaded, 16)
            w = {}
            for name, (at, shape) in places[layer].items():
                size = int(np.prod(shape[1:]))
                v = k.weights[i % 2][0:shape[0], at:at + size]
                if len(shape) == 3:
                    v = v.rearrange("p (a b) -> p a b", a=shape[1])
                w[name] = v
            k.prefix = f"sub{layer}_"
            normalize(k)
            BUILDERS[layer](k, w)
        with nc.Block() as block:

            @block.sync
            def _(sp):
                sp.dma_start(dram["out"].rearrange("(t c) s d -> (c s) t d", c=PER_TILE), k.x[:, :, :]).then_inc(stored, 16)
                sp.wait_ge(stored, 16)


def _mat(w):
    w = np.asarray(w)
    return np.ascontiguousarray(w.reshape(-1, P, w.shape[1]).transpose(1, 0, 2)) if w.shape[0] >= P else w[:, None, :]


def _col(v):
    return np.ascontiguousarray(np.asarray(v).reshape(-1, P).T)


def _row(v):
    v = np.asarray(v).reshape(1, -1)
    return np.broadcast_to(v, (P, v.shape[1]))


def layout(inp):
    g = {n: np.asarray(v) for n, v in inp.items()}
    out = {}
    a = "L0_xattn_"
    out[0] = dict(wq=_mat(g[a + "wq_w"].T), wk=_mat(g[a + "wk_w"].T), wv=_mat(g[a + "wv_w"].T), wo=_mat(g[a + "wo_w"].T),
                  bq=_col(g[a + "wq_b"]), bk=_col(g[a + "wk_b"]), bv=_col(g[a + "wv_b"]), bo=_row(g[a + "wo_b"]))
    a = "L2_xattn_"
    out[6] = dict(wq=_mat(g[a + "Wq"]), wk=_mat(g[a + "Wk"]), wv=_mat(g[a + "Wv"]), wo=_mat(g[a + "Wo"]),
                  bq=_col(g[a + "bq"]), bk=_col(g[a + "bk"]), bv=_col(g[a + "bv"]), bo=_row(g[a + "bo"]))
    more_layout(g, out)
    return out


def more_layout(g, out):
    layout_attention(g, out)
    layout_blocks(g, out)
    layout_scans(g, out)
    layout_delta(g, out)


def kernel(**inputs):
    import concourse.bacc as bacc
    from concourse.bass_utils import run_bass_kernel_spmd

    arrays = {}
    arrays["x"] = np.ascontiguousarray(inputs["x"])
    arrays["ctxT"] = np.ascontiguousarray(np.asarray(inputs["ctx_1024"]).reshape(BATCH * CTX, D).T)
    arrays["ident"] = np.eye(P, dtype=np.float32)
    arrays["hmask16"] = (np.arange(P)[:, None] // 16 == np.arange(8)[None, :]).astype(np.float32)
    arrays["fold"] = (np.arange(P)[:, None] % SEQ == np.arange(SEQ)[None, :]).astype(np.float32)
    arrays["hmask64"] = (np.arange(P)[:, None] // 64 == np.arange(2)[None, :]).astype(np.float32)
    for name, src in (("mask_xattn", "mask_BxS2_bf1"), ("mask_last", "mask_BxS2_bk0")):
        m = np.asarray(inputs[src]).reshape(1, BATCH * CTX)
        arrays[name] = np.ascontiguousarray(np.broadcast_to(m, (P, BATCH * CTX)))
    places = {}
    for layer, pieces in layout(inputs).items():
        if layer not in LAYERS:
            continue
        at, place, flat = 0, {}, []
        for name, piece in pieces.items():
            rows = piece.shape[0]
            size = int(np.prod(piece.shape[1:]))
            block = np.zeros((P, size), piece.dtype)
            block[:rows] = piece.reshape(rows, size)
            flat.append(block)
            place[name] = (at, piece.shape)
            at += size
        assert at <= WMAX, (layer, at)
        arrays[f"w{layer}"] = np.ascontiguousarray(np.concatenate(flat, axis=1))
        places[layer] = place

    nc = bacc.Bacc("TRN2", target_bir_lowering=False, num_devices=1)
    dram = {name: nc.dram_tensor(f"in_{name}", a.shape, mybir.dt.from_np(a.dtype), kind="ExternalInput").ap()
            for name, a in arrays.items()}
    dram["out"] = nc.dram_tensor("out_x", (BATCH, SEQ, D), F32, kind="ExternalOutput").ap()
    build(nc, dram, places, LAYERS)
    r = run_bass_kernel_spmd(nc, [{f"in_{n}": a for n, a in arrays.items()}], core_ids=[0])
    return r.results[0]["out_x"]
```

```python
from contextlib import ExitStack
from itertools import zip_longest

import numpy as np
import concourse.bass as bass
from concourse import mybir

F32 = mybir.dt.float32
BF16 = mybir.dt.bfloat16
U8 = mybir.dt.uint8
ALU = mybir.AluOpType
ACT = mybir.ActivationFunctionType
AX_X = mybir.AxisListType.X

P = 128
BATCH, SEQ, D = 16, 64, 256
TOKENS = BATCH * SEQ
TILES = TOKENS // P
PER_TILE = P // SEQ
CTX = 256
CTX_TILE = PER_TILE * CTX
CHUNKS = D // P
BANK = 512
LN_EPS = 1e-5
NEG = float(np.finfo(np.float32).min)
WMAX = 8500

LAYERS = [0, 1, 2, 3, 4, 5, 6, 7, 8, 9, 10, 11]


class Core:

    def __init__(self, nc, ctx, dram):
        self.nc, self.ctx, self.dram = nc, ctx, dram
        self.sems, self.used = {}, set()
        self.prefix = ""
        self.x = self.sb(ctx, "x_tok", [P, TILES, D])
        self.xn = self.sb(ctx, "xn_tok", [P, TILES, D])
        self.xnT = self.sb(ctx, "xn_feat", [P, CHUNKS, TOKENS])
        self.ctxT = self.sb(ctx, "ctx_feat", [P, CHUNKS, BATCH * CTX])
        self.ident = self.sb(ctx, "ident", [P, P])
        self.hmask16 = self.sb(ctx, "hmask16", [P, 8])
        self.fold = self.sb(ctx, "fold", [P, SEQ])
        self.hmask64 = self.sb(ctx, "hmask64", [P, 2])
        self.stats = self.sb(ctx, "ln_stats", [P, TILES, 6])
        self.meanvar = self.sb(ctx, "ln_meanvar", [P, TILES, 2])
        self.rstd = self.sb(ctx, "ln_rstd", [P, TILES])
        self.weights = [self.sb(ctx, f"weights{i}", [P, WMAX]) for i in range(2)]
        self.banks = ctx.enter_context(nc.psum_tensor("banks", [P, 8, BANK], F32))

    def sb(self, ctx, name, shape, dt=F32):
        return ctx.enter_context(self.nc.sbuf_tensor(f"{self.prefix}{name}", shape, dt))

    def sem(self, name):
        if name not in self.sems:
            self.sems[name] = self.ctx.enter_context(self.nc.semaphore(name))
        self.used.add(name)
        return self.sems[name]

    def clear(self):
        names = sorted(self.used)
        self.used = set()
        with self.nc.Block() as block:

            @block.sync
            def _(sp):
                for name in names:
                    sp.sem_clear(self.sems[name])


def linker(eng, sem, start=0):
    count = [start]

    def link(ins):
        count[0] += 1
        ins.then_inc(sem, 1)
        eng.wait_ge(sem, count[0])

    return link


def normalize(k, src=None, turn=True, scale=None, shift=None):
    src = k.x if src is None else src
    nc = k.nc
    with nc.Block() as block:

        @block.vector
        def _(dve):
            link = linker(dve, k.sem("dve_step"))
            for t in range(TILES):
                last = nc.vector.bn_stats(k.stats[:, t, :], src[:, t, :])
            link(last)
            for t in range(TILES):
                last = nc.vector.bn_aggr(k.meanvar[:, t, :], k.stats[:, t, :])
            link(last)
            nc.vector.tensor_scalar(k.rstd[:, :], k.meanvar[:, :, 1], LN_EPS, None, ALU.add).then_inc(k.sem("var_ready"), 1)
            dve.wait_ge(k.sem("std_ready"), 1)
            link(nc.vector.reciprocal(k.rstd[:, :], k.rstd[:, :]))
            for t in range(TILES):
                nc.vector.tensor_scalar(k.xn[:, t, :], src[:, t, :], k.meanvar[:, t, 0:1], k.rstd[:, t:t + 1],
                                        ALU.subtract, ALU.mult).then_inc(k.sem("xn_ready"), 1)

        @block.scalar
        def _(act):
            act.wait_ge(k.sem("var_ready"), 1)
            nc.scalar.activation(k.rstd[:, :], k.rstd[:, :], ACT.Sqrt).then_inc(k.sem("std_ready"), 1)
            for h in range(TILES // 4 if turn else 0):
                for c in range(CHUNKS):
                    act.wait_ge(k.sem("xnT_in_psum"), CHUNKS * h + c + 1)
                    out, raw = k.xnT[:, c, h * BANK:(h + 1) * BANK], k.banks[:, CHUNKS * h + c, :]
                    if scale is None:
                        nc.scalar.copy(out, raw)
                    else:
                        nc.scalar.activation(out, raw, ACT.Identity, bias=shift[:, c:c + 1], scale=scale[:, c:c + 1])

        @block.tensor
        def _(pe):
            for h in range(TILES // 4 if turn else 0):
                pe.wait_ge(k.sem("xn_ready"), 4 * (h + 1))
                for c in range(CHUNKS):
                    for t in range(4):
                        last = nc.tensor.transpose(k.banks[:, CHUNKS * h + c, t * P:(t + 1) * P],
                                                   k.xn[:, 4 * h + t, c * P:(c + 1) * P], k.ident[:, :])
                    last.then_inc(k.sem("xnT_in_psum"), 1)
    k.clear()


def project(k, jobs, src=None, chunks=CHUNKS, tokens=TOKENS):
    nc = k.nc
    src = k.xnT if src is None else src
    halves = [(j, h) for j in range(len(jobs)) for h in range(tokens // BANK)]
    with nc.Block() as block:

        @block.tensor
        def _(pe):
            for n, (j, h) in enumerate(halves):
                w, col, out, _, _ = jobs[j]
                m = out.shape[0]
                if n >= 4:
                    pe.wait_ge(k.sem("product_used"), n - 3)
                for c in range(chunks):
                    last = nc.tensor.matmul(k.banks[0:m, n % 4, :], w[:, c, col:col + m], src[:, c, h * BANK:(h + 1) * BANK],
                                            start=(c == 0), stop=(c == chunks - 1))
                last.then_inc(k.sem("product_ready"), 1)

        @block.scalar
        def _(act):
            for n, (j, h) in enumerate(halves):
                _, _, out, bias, func = jobs[j]
                m = out.shape[0]
                act.wait_ge(k.sem("product_ready"), n + 1)
                nc.scalar.activation(out[:, h * BANK:(h + 1) * BANK], k.banks[0:m, n % 4, :], func,
                                     bias=0.0 if bias is None else bias).then_inc(k.sem("product_used"), 1)
    k.clear()


def softplus(k, x, e, low):
    nc = k.nc
    with nc.Block() as block:

        @block.scalar
        def _(act):
            nc.scalar.activation(e, x, ACT.Abs).then_inc(k.sem("abs_ready"), 1)
            act.wait_ge(k.sem("abs_ready"), 1)
            nc.scalar.activation(e, e, ACT.Exp, scale=-1.0).then_inc(k.sem("exp_ready"), 1)
            act.wait_ge(k.sem("low_ready"), 1)
            nc.scalar.activation(e, e, ACT.Ln, bias=1.0).then_inc(k.sem("log_ready"), 1)

        @block.vector
        def _(dve):
            link = linker(dve, k.sem("dve_step"))
            dve.wait_ge(k.sem("exp_ready"), 1)
            link(nc.vector.tensor_scalar(low, e, 1.0, 1.0, ALU.add, ALU.subtract))
            nc.vector.tensor_tensor(low, e, low, ALU.subtract).then_inc(k.sem("low_ready"), 1)
            dve.wait_ge(k.sem("low_ready"), 1)
            dve.wait_ge(k.sem("log_ready"), 1)
            link(nc.vector.tensor_tensor(low, low, e, ALU.add))
            nc.vector.scalar_tensor_tensor(x, x, 0.0, low, ALU.max, ALU.add)
    k.clear()




class Attention:

    SLOTS = 4

    def __init__(self, k, ctx, keys, qchunks, kchunks, vfeat, head, pairs, scale, unroll, jobs, copied=False, topk=False, gated=False,
                 split=False):
        self.keys, self.qchunks, self.kchunks, self.head, self.scale = keys, qchunks, kchunks, head, scale
        self.vfeat, self.copied, self.topk, self.unroll, self.split = vfeat, copied, topk, unroll, split
        self.per_seq = len(pairs)
        self.per_tile = PER_TILE * self.per_seq
        self.seqs = 1 if split else PER_TILE
        self.per_unit = self.seqs * self.per_seq
        self.units = unroll * PER_TILE // self.seqs
        self.groups = [(j, b, (j * PER_TILE + b) // self.seqs, b % self.seqs, g)
                       for j in range(unroll) for b in range(PER_TILE) for g in pairs]
        self.kparts = (keys + P - 1) // P
        self.krows = min(keys, P)
        self.rows = 2 * head
        self.exp_lag = 1 if topk else 0
        self.turn_lag, self.out_lag, self.fold_lag = (3, 4, 5) if topk else (2, 3, 4)
        n = len(self.groups)
        self.first = [(kind, 0, i, h) for kind, i, h in jobs]
        self.at = [[] for _ in range(n + self.fold_lag + 3)]
        early = [job for job in jobs if job[0] != "v"]
        late = [job for job in jobs if job[0] == "v"]
        for u in range(1, self.units):
            for m, (kind, i, h) in enumerate(early):
                if kind != "q" or not split:
                    self.at[self.per_unit * (u - 1) + m * self.per_unit // len(early)].append((kind, u, i, h))
                elif u % PER_TILE == 0:
                    self.at[self.per_unit * (u - 1) - 1].append((kind, u // PER_TILE, i, h))
            for m, (kind, i, h) in enumerate(late):
                self.at[self.per_unit * (u - 1) + self.out_lag + m * self.per_unit // len(late)].append((kind, u, i, h))
        for j in range(unroll):
            done = self.per_tile * (j + 1) - 1 + self.fold_lag
            if gated:
                self.at[done].append(("g", j, 0, 0))
            self.at[done + 1].append(("o", j, 0, 0))
        self.order = self.first + [job for step in self.at for job in step]
        self.steps = len(self.at)
        self.place = {job: (s, i, m) for s in range(self.steps) for i in range(self.SLOTS) for m, job in enumerate(self.slot(s, i))}
        self.nk = sum(kind == "k" for kind, _, _ in jobs)
        self.nv = sum(kind == "v" for kind, _, _ in jobs)
        bufs = min(2, self.units)
        self.q_heads = k.sb(ctx, "q_heads", [P, bufs, qchunks, self.seqs, P // head * SEQ])
        self.kT = k.sb(ctx, "kT", [P, bufs, kchunks, self.seqs * keys]) if kchunks else None
        self.v = k.sb(ctx, "v", [P, bufs, self.seqs * self.kparts, vfeat])
        self.moving = k.sb(ctx, "unit_rows", [P, bufs, CHUNKS, self.seqs * keys])
        self.probs = k.sb(ctx, "probs", [P, 2, 4, keys])
        self.probsT = k.sb(ctx, "probsT", [P, 2, self.kparts, BANK])
        self.own = k.sb(ctx, "own_out", [P, 2, 4 * self.rows])
        self.factor = k.sb(ctx, "own_factor", [P, n, 4, 2])
        self.oT = k.sb(ctx, "oT", [P, min(2, unroll), qchunks, P])
        self.rowmax = k.sb(ctx, "rowmax", [P, n, 4])
        self.rowsum = k.sb(ctx, "rowsum", [P, n, 4])
        self.sum = k.sb(ctx, "branch", [P, D])
        self.keys_of = None
        self.oT_scale = self.oT_bias = None

    def score(self, k, g):
        flat = k.banks[:, 2 * (g % 2):2 * (g % 2) + 2, :].rearrange("p b n -> p (b n)")
        return flat[:, 0:4 * self.keys].rearrange("p (i n) -> p i n", i=4)

    def turned(self, k):
        return k.banks[:, 4:4 + self.kparts, :]

    def products(self, k, g):
        return k.banks[:, 6, 0:len(self.groups[g][4]) * self.rows]

    def folded(self, k, g):
        return k.banks[:, 6, 0:len(self.groups[g][4]) * self.rows // P * SEQ]

    def bank_of(self, n):
        if n < len(self.first):
            return 7 if n % 4 == 0 else n % 4
        s, i, m = self.place[self.order[n]]
        return 5 if i == 0 and m == 0 else 4 if i == 3 and m == 1 else 7

    def bank(self, k, kind, j, i, h):
        return k.banks[:, self.bank_of(self.order.index((kind, j, i, h))), :]

    def wait_job(self, k, eng, kind, j, i, h):
        eng.wait_ge(k.sem("job_ready"), self.order.index((kind, j, i, h)) + 1)

    def wait_read(self, k, eng, n):
        kind = self.order[n][0]
        count = sum(1 for job in self.order[:n + 1] if job[0] == kind)
        eng.wait_ge(k.sem({"q": "queries_ready", "k": "keys_ready", "v": "values_ready", "g": "gates_read", "o": "branch_read"}[kind]), count)

    def wait_bank(self, k, eng, kind, j, i, h):
        n = self.order.index((kind, j, i, h))
        before = [m for m in range(n) if self.bank_of(m) == self.bank_of(n)]
        if before:
            self.wait_read(k, eng, before[-1])
        if n >= len(self.first) and self.bank_of(n) != 7:
            s, i, _ = self.place[self.order[n]]
            turned = min(s - self.turn_lag + (i > 1), len(self.groups))
            if turned > 0:
                eng.wait_ge(k.sem("probsT_ready"), turned)

    def wait_turned_banks(self, k, eng, s):
        for bank in (4, 5):
            before = [n for n in range(len(self.first), len(self.order))
                      if self.bank_of(n) == bank and self.place[self.order[n]][0:2] in ((s - 1, 3), (s, 0))]
            if before:
                self.wait_read(k, eng, before[-1])

    def slot(self, s, i):
        jobs = self.at[s]
        return jobs[len(jobs) * i // self.SLOTS:len(jobs) * (i + 1) // self.SLOTS]

    def wait_unit(self, k, eng, sem, u):
        if u >= 2:
            eng.wait_ge(k.sem(sem), self.per_unit * (u - 1))


def attend_pe(k, a, pe, job):
    nc, n = k.nc, len(a.groups)

    def run(jobs):
        for one in jobs:
            a.wait_bank(k, pe, *one)
            job(pe, *one).then_inc(k.sem("job_ready"), 1)

    run(a.first)
    for s in range(a.steps):
        run(a.slot(s, 0))
        g = s - a.fold_lag
        if 0 <= g < n:
            pe.wait_ge(k.sem("own_ready"), g + 1)
            w = len(a.groups[g][4]) * a.rows // P
            for c in range(w):
                last = nc.tensor.matmul(a.folded(k, g)[:, c * SEQ:(c + 1) * SEQ], a.own[:, g % 2, c * P:(c + 1) * P], k.fold[:, :],
                                        start=True, stop=True)
            last.then_inc(k.sem("folded_ready"), 1)
        run(a.slot(s, 1))
        g = s - a.turn_lag
        if 0 <= g < n:
            pairs = a.groups[g][4]
            pe.wait_ge(k.sem("picked_ready" if a.topk else "exp_ready"), g + 1)
            if g >= 1:
                pe.wait_ge(k.sem("probsT_ready"), g)
            a.wait_turned_banks(k, pe, s)
            for part in range(a.kparts):
                for i in range(len(pairs)):
                    last = nc.tensor.transpose(a.turned(k)[0:a.krows, part, i * P:(i + 1) * P],
                                               a.probs[:, g % 2, i, part * P:part * P + a.krows], k.ident[:, :])
            last.then_inc(k.sem("probs_turned"), 1)
        run(a.slot(s, 2))
        if s < n:
            j, b, u, ub, pairs = a.groups[s]
            if s == 0:
                for m in range(max(0, len(a.first) - 4), len(a.first)):
                    a.wait_read(k, pe, m)
            if s % a.per_unit == 0:
                pe.wait_ge(k.sem("q_heads_ready"), (u + 1) * a.qchunks * a.seqs)
                if a.nk:
                    pe.wait_ge(k.sem("keys_ready"), (u + 1) * a.nk)
            if s >= 2:
                pe.wait_ge(k.sem("scores_copied" if a.copied else "exp_ready"), s - 1)
            for i, (qc, kc, vc, row) in enumerate(pairs):
                head = row // a.head
                keys = a.keys_of(j, kc, b) if a.keys_of else a.kT[:, u % 2, kc, ub * a.keys:(ub + 1) * a.keys]
                last = nc.tensor.matmul(a.score(k, s)[:, i, :], a.q_heads[:, u % 2, qc, ub, head * SEQ:(head + 2) * SEQ], keys,
                                        start=True, stop=True)
            last.then_inc(k.sem("scores_ready"), 1)
        run(a.slot(s, 3))
        g = s - a.out_lag
        if 0 <= g < n:
            j, b, u, ub, pairs = a.groups[g]
            if g % a.per_unit == 0:
                pe.wait_ge(k.sem("values_ready"), (u + 1) * a.nv)
            pe.wait_ge(k.sem("probsT_ready"), g + 1)
            if g >= 1:
                pe.wait_ge(k.sem("oT_chunks"), g)
            for i, (_, _, vc, row) in enumerate(pairs):
                for part in range(a.kparts):
                    last = nc.tensor.matmul(a.products(k, g)[:, i * a.rows:(i + 1) * a.rows],
                                            a.probsT[0:a.krows, g % 2, part, i * P:(i + 1) * P],
                                            a.v[0:a.krows, u % 2, ub * a.kparts + part, vc * P + row:vc * P + row + a.rows],
                                            start=(part == 0), stop=(part == a.kparts - 1))
            last.then_inc(k.sem("out_ready"), 1)


def attend_act(k, a, act, job):
    nc, n = k.nc, len(a.groups)

    def run(jobs):
        for one in jobs:
            job(act, *one)

    run(a.first)
    for s in range(a.steps):
        run(a.slot(s, 0))
        g = s - a.fold_lag
        if 0 <= g < n:
            j, b, _, _, pairs = a.groups[g]
            act.wait_ge(k.sem("folded_ready"), g + 1)
            if j >= 2 and g % a.per_tile == 0:
                act.wait_ge(k.sem("branch_read"), j - 1)
            w, c0 = len(pairs) * a.rows // P, pairs[0][0]
            out, src = a.oT[:, j % 2, c0:c0 + w, b * SEQ:(b + 1) * SEQ], a.folded(k, g).rearrange("p (c q) -> p c q", q=SEQ)
            if a.oT_scale is None and a.oT_bias is None:
                nc.scalar.copy(out, src).then_inc(k.sem("oT_chunks"), 1)
            else:
                nc.scalar.activation(out, src, ACT.Identity, scale=1.0 if a.oT_scale is None else a.oT_scale[:, c0:c0 + 1],
                                     bias=0.0 if a.oT_bias is None else a.oT_bias[:, c0:c0 + 1]).then_inc(k.sem("oT_chunks"), 1)
        run(a.slot(s, 1))
        g = s - a.turn_lag
        if 0 <= g < n:
            act.wait_ge(k.sem("probs_turned"), g + 1)
            if g >= 2:
                act.wait_ge(k.sem("out_ready"), g - 1)
            w = len(a.groups[g][4]) * P
            nc.scalar.copy(a.probsT[0:a.krows, g % 2, :, 0:w], a.turned(k)[0:a.krows, :, 0:w]).then_inc(k.sem("probsT_ready"), 1)
        run(a.slot(s, 2))
        if a.topk and s < n:
            act.wait_ge(k.sem("scores_ready"), s + 1)
            if s >= 2:
                act.wait_ge(k.sem("outside_ready"), s - 1)
            nc.scalar.copy(a.masked[:, s % 2, :, :], a.score(k, s)).then_inc(k.sem("scores_copied"), 1)
        g = s - a.exp_lag
        if 0 <= g < n:
            act.wait_ge(k.sem("rowmax_ready"), g + 1)
            if g >= 2:
                act.wait_ge(k.sem("probs_turned"), g - 1)
            for i in range(len(a.groups[g][4])):
                src = a.masked[:, g % 2, i, :] if a.topk else a.probs[:, g % 2, i, :] if a.copied else a.score(k, g)[:, i, :]
                last = nc.scalar.activation(a.probs[:, g % 2, i, :], src, ACT.Exp, bias=a.rowmax[:, g, i:i + 1], scale=a.scale,
                                            accum_out=None if a.topk else a.rowsum[:, g, i:i + 1])
            last.then_inc(k.sem("exp_ready"), 1)
        run(a.slot(s, 3))


def attend_dve(k, a, dve, link, job, mask=None):
    nc, n = k.nc, len(a.groups)

    def run(jobs):
        for one in jobs:
            job(dve, *one)

    run(a.first)
    for s in range(a.steps):
        for i in range(3):
            run(a.slot(s, i))
        g = s - a.exp_lag
        if 0 <= g < n:
            j, b, _, _, pairs = a.groups[g]
            w = len(pairs)
            if a.topk:
                mask(dve, g)
            else:
                dve.wait_ge(k.sem("scores_ready"), g + 1)
                if mask is not None:
                    if g >= 2:
                        dve.wait_ge(k.sem("probs_turned"), g - 1)
                    mask(dve, g, j, b, w)
                else:
                    link(nc.vector.reduce_max(a.rowmax[:, g, 0:w], a.score(k, g)[:, 0:w, :], AX_X))
                nc.vector.tensor_scalar(a.rowmax[:, g, 0:w], a.rowmax[:, g, 0:w], -a.scale, None,
                                        ALU.mult).then_inc(k.sem("rowmax_ready"), 1)
        g = s - 2
        if a.topk and 0 <= g < n:
            mask.pick(dve, g)
        run(a.slot(s, 3))
        g = s - a.out_lag
        if 0 <= g < n:
            w = len(a.groups[g][4])
            dve.wait_ge(k.sem("picked_ready" if a.topk else "exp_ready"), g + 1)
            link(nc.vector.reciprocal(a.rowsum[:, g, 0:w], a.rowsum[:, g, 0:w]))
            link(nc.vector.tensor_tensor(a.factor[:, g, 0:w, :], a.rowsum[:, g, 0:w].unsqueeze(2).broadcast_to([P, w, 2]),
                                         k.hmask64[:, :].unsqueeze(1).broadcast_to([P, w, 2]), ALU.mult))
            dve.wait_ge(k.sem("out_ready"), g + 1)
            if g >= 2:
                dve.wait_ge(k.sem("folded_ready"), g - 1)
            nc.vector.tensor_tensor(a.own[:, g % 2, 0:w * a.rows].rearrange("p (i h d) -> p i h d", i=w, h=2),
                                    a.products(k, g).rearrange("p (i h d) -> p i h d", i=w, h=2),
                                    a.factor[:, g, 0:w, :].unsqueeze(3).broadcast_to([P, w, 2, a.head]),
                                    ALU.mult).then_inc(k.sem("own_ready"), 1)


def mask_queries(k, a, pool, u, q_of):
    nc = k.nc
    m = k.hmask16 if a.head == 16 else k.hmask64
    n = P // a.head
    a.wait_unit(k, pool, "scores_ready", u)
    for c in range(a.qchunks):
        for b in range(a.seqs):
            nc.gpsimd.tensor_tensor(a.q_heads[:, u % 2, c, b, :].rearrange("p (h q) -> p h q", q=SEQ),
                                    q_of(c, b).unsqueeze(1).broadcast_to([P, n, SEQ]),
                                    m[:, :].unsqueeze(2).broadcast_to([P, n, SEQ]), ALU.mult).then_inc(k.sem("q_heads_ready"), 1)


def copy_rows(k, a, pool, u, src):
    if u >= 2:
        a.wait_job(k, pool, *[job for job in a.order if job[0] == "v" and job[1] == u - 2][-1])
    k.nc.gpsimd.tensor_copy(a.moving[:, u % 2, :, :], src).then_inc(k.sem("rows_copied"), 1)


def context_jobs(kchunks, vfeat, seqs=PER_TILE, queries=0):
    per = BANK // (seqs * CTX)
    jobs = [("q", c, 0) for c in range(0, queries, 4)] + [("k", c, 0) for c in range(0, kchunks, per)]
    rows = seqs * CTX // P
    if vfeat >= BANK:
        return jobs + [("v", j, n) for j in range(rows) for n in range(vfeat // BANK)]
    return jobs + [("v", j, 0) for j in range(0, rows, BANK // vfeat)]


def projections(k, a, w, t, ctx_keys, x_moving=None, gates=None):
    nc = k.nc

    def job(pe, kind, j, i, h):
        bank = a.bank(k, kind, j, i, h)
        if kind == "q":
            for m in range(4):
                for c in range(CHUNKS):
                    last = nc.tensor.matmul(bank[:, m * P:(m + 1) * P], w["wq"][:, c, (i + m) * P:(i + m + 1) * P], x_moving(j, c),
                                            start=(c == 0), stop=(c == CHUNKS - 1))
        elif kind == "k":
            n = a.seqs * CTX
            for m in range(BANK // n):
                for c in range(CHUNKS):
                    last = nc.tensor.matmul(bank[:, m * n:(m + 1) * n], w["wk"][:, c, (i + m) * P:(i + m + 1) * P], ctx_keys(j, c),
                                            start=(c == 0), stop=(c == CHUNKS - 1))
        elif kind == "v":
            pe.wait_ge(k.sem("rows_copied"), j + 1)
            if a.keys == CTX:
                width = min(a.vfeat, BANK)
                for m in range(BANK // width):
                    for c in range(CHUNKS):
                        last = nc.tensor.matmul(bank[:, m * width:(m + 1) * width], a.moving[:, j % 2, c, (i + m) * P:(i + m + 1) * P],
                                                w["wv"][:, c, h * BANK:h * BANK + width], start=(c == 0), stop=(c == CHUNKS - 1))
            else:
                for b in range(PER_TILE):
                    for c in range(CHUNKS):
                        last = nc.tensor.matmul(bank[0:SEQ, b * D:(b + 1) * D], a.moving[:, j % 2, c, b * SEQ:(b + 1) * SEQ],
                                                w["wv"][:, c, :], start=(c == 0), stop=(c == CHUNKS - 1))
        elif kind == "g":
            pe.wait_ge(k.sem("oT_chunks"), a.per_tile * (j + 1))
            for c in range(CHUNKS):
                last = nc.tensor.matmul(bank[:, 0:17], a.oT[:, j % 2, c, :], w["wgate"][:, c, :], start=(c == 0), stop=(c == CHUNKS - 1))
        else:
            pe.wait_ge(k.sem("oT_chunks"), a.per_tile * (j + 1))
            for c in range(a.qchunks):
                last = nc.tensor.matmul(bank[:, 0:D], a.oT[:, j % 2, c, :], w["wo"][:, c, :], start=(c == 0), stop=(c == a.qchunks - 1))
        return last

    return job


def values_out(k, a, eng, copy, j, i, h):
    a.wait_job(k, eng, "v", j, i, h)
    a.wait_unit(k, eng, "out_ready", j)
    if a.keys == CTX:
        width = min(a.vfeat, BANK)
        rows, out = P, a.v[:, j % 2, i:i + BANK // width, h * BANK:h * BANK + width]
    else:
        width, rows = D, SEQ
        out = a.v[0:SEQ, j % 2, :, :]
    copy(out, a.bank(k, "v", j, i, h)[0:rows, :].rearrange("p (i w) -> p i w", w=width)).then_inc(k.sem("values_ready"), 1)


def act_jobs(k, a, bk, gate=None, values=False):
    nc = k.nc

    def job(act, kind, j, i, h):
        if kind == "q":
            a.wait_job(k, act, kind, j, i, h)
            if j >= 1:
                act.wait_ge(k.sem("q_heads_ready"), j * PER_TILE * a.qchunks)
            nc.scalar.copy(a.q_tile[:, i:i + 4, :], a.bank(k, kind, j, i, h).rearrange("p (i n) -> p i n", i=4)).then_inc(k.sem("queries_ready"), 1)
        elif kind == "k":
            a.wait_job(k, act, kind, j, i, h)
            a.wait_unit(k, act, "scores_ready", j)
            n = a.seqs * CTX
            nc.scalar.activation(a.kT[:, j % 2, i:i + BANK // n, :], a.bank(k, kind, j, i, h).rearrange("p (i n) -> p i n", n=n), ACT.Identity,
                                 bias=0.0 if bk is None else bk[:, i:i + 1]).then_inc(k.sem("keys_ready"), 1)
        elif kind == "v" and values:
            values_out(k, a, act, nc.scalar.copy, j, i, h)
        elif kind == "g":
            gate(act, j)

    return job


def dve_jobs(k, a, link, t, bo=None, factor=None, gate=None, factor_of=None, values=True):
    nc = k.nc

    def job(dve, kind, j, i, h):
        if kind == "v" and values:
            values_out(k, a, dve, nc.vector.tensor_copy, j, i, h)
        elif kind == "g":
            gate(dve, j)
        elif kind == "o":
            if factor_of:
                factor_of(dve, j)
            a.wait_job(k, dve, kind, j, i, h)
            dst = k.x[:, t * a.unroll + j, :]
            src = a.bank(k, kind, j, i, h)[:, 0:D]
            if bo is not None:
                nc.vector.tensor_tensor(a.sum[:, :], src, bo, ALU.add).then_inc(k.sem("branch_read"), 1)
                dve.wait_ge(k.sem("branch_read"), j + 1)
                src = a.sum[:, :]
            if factor is not None:
                last = nc.vector.scalar_tensor_tensor(dst, src, factor, dst, ALU.mult, ALU.add)
            else:
                last = nc.vector.tensor_tensor(dst, src, dst, ALU.add)
            if bo is None:
                last.then_inc(k.sem("branch_read"), 1)

    return job


def pairs16():
    return [[(fc, fc, fc, 32 * j) for j in range(4)] for fc in range(CHUNKS)]


def pairs64(qchunks, shared):
    n = min(4, qchunks)
    return [[(c, 0 if shared else c, 0 if shared else c, 0) for c in range(g, g + n)] for g in range(0, qchunks, n)]


def load_mask(k, mask8, name):
    with k.nc.Block() as block:

        @block.sync
        def _(sp):
            sp.dma_start(mask8[:, :], k.dram[name]).then_inc(k.sem("mask_loaded"), 16)
            sp.wait_ge(k.sem("mask_loaded"), 16)
    k.clear()


def context_attention(k, w, topk):
    nc = k.nc
    unroll = 4
    with ExitStack() as ctx:
        a = Attention(k, ctx, CTX, CHUNKS, CHUNKS, D, 16, pairs16(), 0.25, unroll, context_jobs(CHUNKS, D), copied=topk, topk=topk)
        a.oT_bias = w["bv"]
        qT = k.xn[:, :, :].rearrange("p t d -> p (t d)").rearrange("p (c n) -> p c n", c=CHUNKS)
        if topk:
            low = k.sb(ctx, "key_low", [P, PER_TILE, CTX])
            mask8 = k.sb(ctx, "key_mask", [P, BATCH * CTX], U8)
            work = k.sb(ctx, "topk_work", [P, 2, 4, CTX])
            best = k.sb(ctx, "topk_best", [P, 4, 8])
            allout = k.sb(ctx, "all_masked", [P, 2, 4])
            a.masked = k.sb(ctx, "masked_scores", [P, 2, 4, CTX])
            load_mask(k, mask8, "mask_xattn")
        project(k, [(w["wq"], c * P, qT[:, c, :], w["bq"][:, c:c + 1], ACT.Identity) for c in range(CHUNKS)])
        with nc.Fori(0, TILES // unroll) as t:

            def ctx_cols(j):
                return bass.ds((t * unroll + j) * CTX_TILE, CTX_TILE)

            def best_keys(dve, g):
                sc = a.masked[:, g % 2]
                dve.wait_ge(k.sem("masked_ready"), g + 1)
                if g >= 2:
                    dve.wait_ge(k.sem("picked_ready"), g - 1)

                def step(ins):
                    best_keys.done += 1
                    ins.then_inc(k.sem("topk_step"), 1)

                def settled(back):
                    dve.wait_ge(k.sem("topk_step"), best_keys.done - back)

                for r in range(8):
                    src = work[:, g % 2] if r else sc
                    for i in range(4):
                        if g or r:
                            settled(3)
                        step(nc.vector.max(best[:, i, :], src[:, i, :]))
                    if r == 0:
                        settled(0)
                        nc.vector.tensor_scalar(allout[:, g % 2, :], best[:, :, 0], NEG, -1.0, ALU.is_equal, ALU.mult)
                        nc.vector.tensor_scalar(a.rowmax[:, g, :], best[:, :, 0], -a.scale, None, ALU.mult).then_inc(k.sem("rowmax_ready"), 1)
                    for i in range(4):
                        settled(3)
                        step(nc.vector.match_replace(work[:, g % 2, i, :], best[:, i, :], src[:, i, :], NEG))

            def pick(dve, g):
                dve.wait_ge(k.sem("outside_ready"), g + 1)
                dve.wait_ge(k.sem("exp_ready"), g + 1)
                for i in range(4):
                    last = nc.vector.scalar_tensor_tensor(a.probs[:, g % 2, i, :], work[:, g % 2, i, :], allout[:, g % 2, i:i + 1],
                                                          a.probs[:, g % 2, i, :], ALU.is_gt, ALU.mult, accum_out=a.rowsum[:, g, i:i + 1])
                last.then_inc(k.sem("picked_ready"), 1)

            best_keys.pick = pick

            with nc.Block() as block:

                @block.gpsimd
                def _(pool):
                    def tile(j):
                        copy_rows(k, a, pool, j, k.ctxT[:, :, ctx_cols(j)])
                        mask_queries(k, a, pool, j, lambda c, b: qT[:, c, bass.ds((t * unroll + j) * P + b * SEQ, SEQ)])
                    if not topk:
                        for j in range(unroll):
                            tile(j)
                        return
                    tile(0)
                    for s in range(len(a.groups) + 1):
                        if s < len(a.groups):
                            j, b = a.groups[s][0:2]
                            if s % CHUNKS == 0:
                                seq = s // CHUNKS
                                nc.gpsimd.tensor_copy(low[:, b, :], mask8[:, bass.ds((t * unroll * PER_TILE + seq) * CTX, CTX)]
                                                      ).then_inc(k.sem("low_step"), 1)
                                pool.wait_ge(k.sem("low_step"), 2 * seq + 1)
                                nc.gpsimd.tensor_scalar(low[:, b, :], low[:, b, :], -NEG, NEG, ALU.mult, ALU.add).then_inc(k.sem("low_step"), 1)
                                pool.wait_ge(k.sem("low_step"), 2 * seq + 2)
                            sc = a.masked[:, s % 2, :, :]
                            pool.wait_ge(k.sem("scores_copied"), s + 1)
                            nc.gpsimd.tensor_tensor(sc, sc, low[:, b, :].unsqueeze(1).broadcast_to([P, 4, CTX]),
                                                    ALU.add).then_inc(k.sem("masked_ready"), 1)
                            if s % a.per_tile == 1 and j + 1 < unroll:
                                tile(j + 1)
                        if s >= 1:
                            g = s - 1
                            pool.wait_ge(k.sem("topk_step"), 64 * (g + 1))
                            pool.wait_ge(k.sem("exp_ready"), g + 1)
                            nc.gpsimd.tensor_tensor(work[:, g % 2], a.masked[:, g % 2], work[:, g % 2],
                                                    ALU.subtract).then_inc(k.sem("outside_ready"), 1)

                @block.tensor
                def _(pe):
                    attend_pe(k, a, pe, projections(k, a, w, t, lambda j, c: k.ctxT[:, c, ctx_cols(j)]))

                @block.scalar
                def _(act):
                    attend_act(k, a, act, act_jobs(k, a, w["bk"], values=topk))

                @block.vector
                def _(dve):
                    link = linker(dve, k.sem("dve_step"))
                    best_keys.done = 0
                    attend_dve(k, a, dve, link, dve_jobs(k, a, link, t, w["bo"], values=not topk), best_keys if topk else None)
            k.clear()


def layer0_xattn(k, w):
    context_attention(k, w, True)


def layer6_xattn(k, w):
    context_attention(k, w, False)


BUILDERS = {0: layer0_xattn, 6: layer6_xattn}


def self_attention(k, w, a, qT, kT, mask=None, gates=None, factor_of=None, factor=None, bo=None):
    nc = k.nc
    unroll = a.unroll
    with nc.Fori(0, TILES // unroll) as t:

        def keys_of(j, c, b):
            return kT[:, c, bass.ds((t * unroll + j) * P + b * SEQ, SEQ)]

        a.keys_of = keys_of
        with nc.Block() as block:

            @block.gpsimd
            def _(pool):
                for j in range(unroll):
                    copy_rows(k, a, pool, j, k.xnT[:, :, bass.ds((t * unroll + j) * P, P)])
                    mask_queries(k, a, pool, j, lambda c, b: qT[:, c, bass.ds((t * unroll + j) * P + b * SEQ, SEQ)])

            @block.tensor
            def _(pe):
                attend_pe(k, a, pe, projections(k, a, w, t, None))

            @block.scalar
            def _(act):
                attend_act(k, a, act, act_jobs(k, a, None, gate=gates and gates[0]))

            @block.vector
            def _(dve):
                link = linker(dve, k.sem("dve_step"))
                jobs = dve_jobs(k, a, link, t, bo=bo, factor=factor,
                                gate=gates and (lambda dve, j: gates[1](dve, link, j)),
                                factor_of=factor_of and (lambda dve, j: factor_of(dve, link, j)))
                attend_dve(k, a, dve, link, jobs, mask and mask(link))
        k.clear()


def layer1_attn(k, w):
    nc = k.nc
    with ExitStack() as ctx:
        a = Attention(k, ctx, SEQ, CHUNKS, 0, D, 16, pairs16(), 0.25, 4, [("v", 0, 0)], copied=True)
        qT = k.sb(ctx, "qT", [P, CHUNKS, TOKENS])
        kT = k.sb(ctx, "kT_all", [P, CHUNKS, TOKENS])
        a.oT_scale = share = k.sb(ctx, "dot_share", [P, CHUNKS])
        project(k, [(w[n], c * P, o[:, c, :], None, ACT.Identity) for n, o in (("wq", qT), ("wk", kT)) for c in range(CHUNKS)])
        with nc.Block() as block:

            @block.scalar
            def _(act):
                nc.scalar.activation(share[:, :], w["beta"], ACT.Sigmoid, scale=-1.0)
        k.clear()

        def mask(link):
            def causal(dve, g, j, b, n):
                pr = a.probs[:, g % 2, 0:n, :]
                nc.vector.tensor_tensor(pr, a.score(k, g)[:, 0:n, :], w["causal"].unsqueeze(1).broadcast_to([P, n, SEQ]),
                                        ALU.add).then_inc(k.sem("scores_copied"), 1)
                dve.wait_ge(k.sem("scores_copied"), g + 1)
                link(nc.vector.reduce_max(a.rowmax[:, g, 0:n], pr, AX_X))
            return causal

        self_attention(k, w, a, qT, kT, mask)


def layer2_ffn(k, w):
    nc = k.nc
    with ExitStack() as ctx:
        a = Attention(k, ctx, SEQ, CHUNKS, 0, D, 16, pairs16(), 0.25, 4, [("v", 0, 0)], gated=True)
        qT = k.sb(ctx, "qT", [P, CHUNKS, TOKENS])
        kT = k.sb(ctx, "kT_all", [P, CHUNKS, TOKENS])
        sq = k.sb(ctx, "q_squares", [P, CHUNKS, TOKENS])
        a.oT_bias = w["bv"]
        heat = k.sb(ctx, "heat", [P, 2, CHUNKS])
        softplus(k, w["temp"], heat[:, 0, :], heat[:, 1, :])
        gate = k.sb(ctx, "gates", [P, 17])
        best = k.sb(ctx, "gates_best", [P, 8])
        cols = k.sb(ctx, "gate_cols", [P, 10])
        factor = k.sb(ctx, "gate_factor", [P, 1])
        project(k, [(w[n], c * P, o[:, c, :], w[bn][:, c:c + 1], ACT.Identity)
                    for n, bn, o in (("wq", "bq", qT), ("wk", "bk", kT)) for c in range(CHUNKS)])
        parts = [(c, h) for c in range(CHUNKS) for h in range(TOKENS // BANK)]
        with nc.Block() as block:

            @block.scalar
            def _(act):
                for c in range(CHUNKS):
                    nc.scalar.activation(sq[:, c, :], qT[:, c, :], ACT.Square).then_inc(k.sem("squares_ready"), 1)
                for n, (c, h) in enumerate(parts):
                    act.wait_ge(k.sem("norm_in_psum"), n + 1)
                    nc.scalar.activation(sq[:, c, h * BANK:(h + 1) * BANK], k.banks[:, n, :], ACT.Sqrt).then_inc(k.sem("norm_ready"), 1)

            @block.tensor
            def _(pe):
                pe.wait_ge(k.sem("squares_ready"), CHUNKS)
                for n, (c, h) in enumerate(parts):
                    nc.tensor.matmul(k.banks[:, n, :], w["same16"], sq[:, c, h * BANK:(h + 1) * BANK],
                                     start=True, stop=True).then_inc(k.sem("norm_in_psum"), 1)

            @block.vector
            def _(dve):
                link = linker(dve, k.sem("dve_step"))
                dve.wait_ge(k.sem("norm_ready"), len(parts))
                link(nc.vector.reciprocal(sq[:, :, :], sq[:, :, :]))
                link(nc.vector.tensor_tensor(qT[:, :, :], qT[:, :, :], sq[:, :, :], ALU.mult))
                for c in range(CHUNKS):
                    nc.vector.tensor_scalar(qT[:, c, :], qT[:, c, :], w["qe"][:, c:c + 1], w["temp"][:, c:c + 1], ALU.add, ALU.mult)
        k.clear()

        def gate_act(act, j):
            act.wait_ge(k.sem("gate_max_ready"), j + 1)
            nc.scalar.activation(gate[:, 0:15], gate[:, 0:15], ACT.Exp, bias=cols[:, 0:1], accum_out=cols[:, 2:3])
            nc.scalar.activation(gate[:, 15:17], gate[:, 15:17], ACT.Exp, bias=cols[:, 1:2],
                                 accum_out=cols[:, 3:4]).then_inc(k.sem("gate_exp_ready"), 1)

        def gate_dve(dve, link, j):
            a.wait_job(k, dve, "g", j, 0, 0)
            nc.vector.tensor_tensor(gate[:, :], k.banks[:, 7, 0:17], w["bgate"], ALU.add).then_inc(k.sem("gates_read"), 1)
            dve.wait_ge(k.sem("gates_read"), j + 1)
            nc.vector.reduce_max(cols[:, 0:1], gate[:, 0:15], AX_X)
            link(nc.vector.reduce_max(cols[:, 1:2], gate[:, 15:17], AX_X))
            nc.vector.tensor_scalar(cols[:, 0:2], cols[:, 0:2], -1.0, None, ALU.mult).then_inc(k.sem("gate_max_ready"), 1)

        def gate_factor(dve, link, j):
            dve.wait_ge(k.sem("gate_exp_ready"), j + 1)
            link(nc.vector.reciprocal(cols[:, 2:4], cols[:, 2:4]))
            link(nc.vector.max(best[:, :], gate[:, 0:15]))
            link(nc.vector.reduce_sum(cols[:, 4:5], best[:, 0:3], AX_X))
            link(nc.vector.tensor_tensor(cols[:, 4:5], cols[:, 4:5], cols[:, 2:3], ALU.mult))
            link(nc.vector.tensor_scalar(cols[:, 5:7], gate[:, 15:17], cols[:, 3:4], None, ALU.mult))
            link(nc.vector.reduce_sum(cols[:, 7:8], cols[:, 5:7], AX_X))
            link(nc.vector.scalar_tensor_tensor(cols[:, 7:8], cols[:, 7:8], 2.0, cols[:, 5:6], ALU.mult, ALU.mult))
            link(nc.vector.scalar_tensor_tensor(cols[:, 8:9], cols[:, 4:5], 6.0, cols[:, 6:7], ALU.mult, ALU.mult))
            link(nc.vector.tensor_tensor(factor[:, :], cols[:, 7:8], cols[:, 8:9], ALU.add))

        self_attention(k, w, a, qT, kT, gates=(gate_act, gate_dve), factor_of=gate_factor, factor=factor[:, 0:1])
        with nc.Block() as block:

            @block.vector
            def _(dve):
                nc.vector.tensor_tensor(k.x[:, :, :], k.x[:, :, :], w["bo"].unsqueeze(1).broadcast_to([P, TILES, D]), ALU.add)


def layer3_xattn(k, w):
    nc = k.nc
    inner = 1024
    unroll = 4
    normalize(k, src=k.xn, scale=w["gamma"], shift=w["beta"])
    with ExitStack() as ctx:
        a = Attention(k, ctx, CTX, inner // P, inner // P, inner, 64, pairs64(inner // P, False), 0.125, unroll,
                      context_jobs(inner // P, inner, seqs=1, queries=inner // P), split=True)
        a.q_tile = k.sb(ctx, "q_tile", [P, inner // P, P])
        opening = k.sb(ctx, "gate_tanh", [P, 1])
        with nc.Block() as block:

            @block.scalar
            def _(act):
                nc.scalar.activation(opening[:, :], w["gate"], ACT.Tanh)
        with nc.Fori(0, TILES // unroll) as t:

            def ctx_cols(u):
                return bass.ds((t * a.units + u) * CTX, CTX)

            with nc.Block() as block:

                @block.gpsimd
                def _(pool):
                    for u in range(a.units):
                        copy_rows(k, a, pool, u, k.ctxT[:, :, ctx_cols(u)])
                        pool.wait_ge(k.sem("queries_ready"), 2 * (u // PER_TILE + 1))
                        mask_queries(k, a, pool, u, lambda c, b: a.q_tile[:, c, (u % PER_TILE) * SEQ:(u % PER_TILE + 1) * SEQ])

                @block.tensor
                def _(pe):
                    attend_pe(k, a, pe, projections(k, a, w, t, lambda u, c: k.ctxT[:, c, ctx_cols(u)],
                                                    lambda j, c: k.xnT[:, c, bass.ds((t * unroll + j) * P, P)]))

                @block.scalar
                def _(act):
                    attend_act(k, a, act, act_jobs(k, a, None))

                @block.vector
                def _(dve):
                    link = linker(dve, k.sem("dve_step"))
                    attend_dve(k, a, dve, link, dve_jobs(k, a, link, t, w["bo"], factor=opening[:, 0:1]))
            k.clear()


BUILDERS |= {1: layer1_attn, 2: layer2_ffn, 3: layer3_xattn}


def layout_attention(g, out):
    a = "L0_attn_"
    later = (np.arange(SEQ)[None, :] > (np.arange(P) % SEQ)[:, None]) * np.float32(NEG)
    out[1] = dict(wq=_mat(g[a + "W_q"].T), wk=_mat(g[a + "W_k"].T), wv=_mat(g[a + "W_v"].T), wo=_mat(g[a + "W_o"].T),
                  beta=_col(np.repeat(g[a + "beta_param"], 16)), causal=later.astype(np.float32))
    a = "L0_ffn_"
    same = (np.arange(P)[:, None] // 16 == np.arange(P)[None, :] // 16).astype(np.float32)
    out[2] = dict(wq=_mat(g[a + "Wq"].T), wk=_mat(g[a + "Wk"].T), wv=_mat(g[a + "Wv"].T), wo=_mat(g[a + "Wp"].T),
                  bq=_col(g[a + "bq"]), bk=_col(g[a + "bk"]), bv=_col(g[a + "bv"]), bo=_row(g[a + "bp"]),
                  temp=_col(np.repeat(g[a + "temperature"].reshape(-1), 16)), qe=_col(g[a + "query_embedding"].reshape(-1)),
                  wgate=_mat(np.concatenate([g[a + "Wr"], g[a + "Ws"]]).T),
                  bgate=_row(np.concatenate([g[a + "br"], g[a + "bs"]])), same16=same)
    a = "L1_xattn_"
    kv = g[a + "w_kv"]
    out[3] = dict(wq=_mat(g[a + "w_q"]), wk=_mat(kv[:, :1024]), wv=_mat(kv[:, 1024:]), wo=_mat(g[a + "w_out"]),
                  gamma=_col(g[a + "ln_gamma"]), beta=_col(g[a + "ln_beta"]), bo=_row(g[a + "b_out"]), gate=_row(g[a + "gate"]))


def rms_inverse(k, ones, src, squares, inv, chunks, scale_rows):
    nc = k.nc
    with nc.Block() as block:

        @block.gpsimd
        def _(pool):
            for n in range(chunks):
                if n >= 2:
                    pool.wait_ge(k.sem("sumsq_ready"), n - 1)
                cols = src[:, :, n * BANK:(n + 1) * BANK]
                nc.gpsimd.tensor_tensor(squares[:, n % 2, :, :], cols, cols, ALU.mult).then_inc(k.sem("squares_ready"), 1)

        @block.scalar
        def _(act):
            for n in range(chunks):
                act.wait_ge(k.sem("sumsq_ready"), n + 1)
                nc.scalar.activation(inv[:, n * BANK:(n + 1) * BANK], k.banks[:, n % 4, :], ACT.Sqrt, bias=scale_rows["eps"],
                                     scale=1.0 / D).then_inc(k.sem("rms_ready"), 1)

        @block.tensor
        def _(pe):
            for n in range(chunks):
                pe.wait_ge(k.sem("squares_ready"), n + 1)
                if n >= 4:
                    pe.wait_ge(k.sem("rms_ready"), n - 3)
                for c in range(CHUNKS):
                    last = nc.tensor.matmul(k.banks[:, n % 4, :], ones, squares[:, n % 2, c, :], start=(c == 0), stop=(c == CHUNKS - 1))
                last.then_inc(k.sem("sumsq_ready"), 1)

        @block.vector
        def _(dve):
            for n in range(chunks):
                cols = slice(n * BANK, (n + 1) * BANK)
                dve.wait_ge(k.sem("rms_ready"), n + 1)
                nc.vector.reciprocal(inv[:, cols], inv[:, cols]).then_inc(k.sem("inverse_ready"), 1)
                dve.wait_ge(k.sem("inverse_ready"), n + 1)
                for c in range(CHUNKS):
                    nc.vector.scalar_tensor_tensor(src[:, c, cols], src[:, c, cols], scale_rows["gain"][:, c:c + 1], inv[:, cols],
                                                   ALU.mult, ALU.mult)
    k.clear()


def rotate(k, straight, swapped, cos, sin, batch, n):
    nc = k.nc
    with nc.Block() as block:

        @block.gpsimd
        def _(pool):
            for c in range(straight.shape[1]):
                v = swapped[:, c, :].rearrange("p (b q) -> p b q", q=n)
                nc.gpsimd.tensor_tensor(v, v, sin.unsqueeze(1).broadcast_to([P, batch, n]), ALU.mult).then_inc(k.sem("sine_ready"), 1)

        @block.vector
        def _(dve):
            for c in range(straight.shape[1]):
                v = straight[:, c, :].rearrange("p (b q) -> p b q", q=n)
                nc.vector.tensor_tensor(v, v, cos.unsqueeze(1).broadcast_to([P, batch, n]), ALU.mult).then_inc(k.sem("cosine_ready"), 1)
            for c in range(straight.shape[1]):
                dve.wait_ge(k.sem("cosine_ready"), c + 1)
                dve.wait_ge(k.sem("sine_ready"), c + 1)
                nc.vector.tensor_tensor(straight[:, c, :], straight[:, c, :], swapped[:, c, :], ALU.add)
    k.clear()


def layer9_xattn(k, w):
    nc = k.nc
    keys_all = BATCH * CTX
    unroll = 4
    with ExitStack() as ctx:
        a = Attention(k, ctx, CTX, CHUNKS, 0, P, 64, pairs64(CHUNKS, True), 0.125, unroll, context_jobs(0, P), copied=True)
        qT = k.xn[:, :, :].rearrange("p t d -> p (t d)").rearrange("p (c n) -> p c n", c=CHUNKS)
        kT = k.sb(ctx, "kT_all", [P, 1, keys_all])
        low = k.sb(ctx, "key_low", [P, 2, CTX_TILE])
        mask8 = k.sb(ctx, "key_mask", [P, keys_all], U8)
        gain = k.sb(ctx, "rms_gain", [P, CHUNKS])
        eps = k.sb(ctx, "rms_eps", [P, 1])
        with nc.Block() as block:

            @block.sync
            def _(sp):
                sp.dma_start(mask8[:, :], k.dram["mask_last"]).then_inc(k.sem("mask_loaded"), 16)
                sp.wait_ge(k.sem("mask_loaded"), 16)

            @block.vector
            def _(dve):
                nc.vector.memset(eps[:, :], 1e-6)
                nc.vector.tensor_scalar(gain[:, :], w["rms"], 1.0, None, ALU.add)
        k.clear()
        with ExitStack() as early:
            swapped = k.sb(early, "k_swapped", [P, 1, keys_all])
            squares = swapped[:, 0, 0:2 * CHUNKS * BANK].rearrange("p (i c n) -> p i c n", i=2, c=CHUNKS)
            inv = kT[:, 0, :]
            rows = dict(eps=eps[:, 0:1], gain=gain)
            rms_inverse(k, w["ones"], k.ctxT, squares, inv, keys_all // BANK, rows)
            rms_inverse(k, w["ones"], k.xnT, squares, inv, TOKENS // BANK, rows)
            qswap = swapped[:, 0, 0:CHUNKS * TOKENS].rearrange("p (c n) -> p c n", c=CHUNKS)
            project(k, [(w[n], c * P, o[:, c, :], None, ACT.Identity) for n, o in (("wq", qT), ("wqs", qswap)) for c in range(CHUNKS)])
            rotate(k, qT, qswap, w["cosq"], w["sinq"], BATCH, SEQ)
            project(k, [(w["wk"], 0, kT[:, 0, :], None, ACT.Identity), (w["wk"], P, swapped[:, 0, :], None, ACT.Identity)],
                    src=k.ctxT, tokens=keys_all)
            rotate(k, kT, swapped, w["cosk"], w["sink"], BATCH, CTX)
        with nc.Fori(0, TILES // unroll) as t:

            def cols(j, b=0):
                return bass.ds((t * unroll + j) * CTX_TILE + b * CTX, CTX)

            def mask(link):
                def hide(dve, g, j, b, n):
                    pr = a.probs[:, g % 2, 0:n, :]
                    dve.wait_ge(k.sem("low_ready"), 2 * j + 2)
                    nc.vector.tensor_tensor(pr, a.score(k, g)[:, 0:n, :],
                                            low[:, j % 2, b * CTX:(b + 1) * CTX].unsqueeze(1).broadcast_to([P, n, CTX]),
                                            ALU.add).then_inc(k.sem("scores_copied"), 1)
                    dve.wait_ge(k.sem("scores_copied"), g + 1)
                    link(nc.vector.reduce_max(a.rowmax[:, g, 0:n], pr, AX_X))
                return hide

            a.keys_of = lambda j, c, b: kT[:, 0, cols(j, b)]
            with nc.Block() as block:

                @block.gpsimd
                def _(pool):
                    for j in range(unroll):
                        tile = bass.ds((t * unroll + j) * CTX_TILE, CTX_TILE)
                        copy_rows(k, a, pool, j, k.ctxT[:, :, tile])
                        mask_queries(k, a, pool, j, lambda c, b: qT[:, c, bass.ds((t * unroll + j) * P + b * SEQ, SEQ)])
                        if j >= 2:
                            pool.wait_ge(k.sem("scores_copied"), a.per_tile * (j - 1))
                        nc.gpsimd.tensor_copy(low[:, j % 2, :], mask8[:, tile]).then_inc(k.sem("low_ready"), 1)
                        pool.wait_ge(k.sem("low_ready"), 2 * j + 1)
                        nc.gpsimd.tensor_scalar(low[:, j % 2, :], low[:, j % 2, :], -NEG, NEG, ALU.mult, ALU.add).then_inc(k.sem("low_ready"), 1)

                @block.tensor
                def _(pe):
                    attend_pe(k, a, pe, projections(k, a, w, t, None))

                @block.scalar
                def _(act):
                    attend_act(k, a, act, act_jobs(k, a, None))

                @block.vector
                def _(dve):
                    link = linker(dve, k.sem("dve_step"))
                    attend_dve(k, a, dve, link, dve_jobs(k, a, link, t), mask(link))
            k.clear()


HIDDEN = 1024
ROUND = 1.5 * 2.0 ** 23
QB = 127.0


def two_layers(k, dt, prepare_x, hidden_act, prepare_h, finish, w1, w2, buf, extra=None):
    nc = k.nc
    xq, xqT, hq, hqT, ident, turned = buf
    nh = HIDDEN // P
    with nc.Fori(0, TILES) as t:
        with nc.Block() as block:

            @block.tensor
            def _(pe):
                pe.wait_ge(k.sem("xq_ready"), 1)
                for c in range(CHUNKS):
                    last = nc.tensor.transpose(turned[:, c * P:(c + 1) * P], xq[:, c * P:(c + 1) * P], ident)
                last.then_inc(k.sem("xq_turned"), 1)
                pe.wait_ge(k.sem("xqT_ready"), 1)
                for h in range(HIDDEN // BANK):
                    for c in range(CHUNKS):
                        last = nc.tensor.matmul(k.banks[:, 2 + h, :], xqT[:, c, :], w1[:, c, h * BANK:(h + 1) * BANK],
                                                start=(c == 0), stop=(c == CHUNKS - 1))
                    last.then_inc(k.sem("hidden_ready"), 1)
                pe.wait_ge(k.sem("hq_ready"), 1)
                for c in range(nh):
                    last = nc.tensor.transpose(turned[:, c * P:(c + 1) * P], hq[:, c * P:(c + 1) * P], ident)
                last.then_inc(k.sem("hq_turned"), 1)
                pe.wait_ge(k.sem("hqT_ready"), 1)
                for c in range(nh):
                    last = nc.tensor.matmul(k.banks[:, 4, 0:D], hqT[:, c, :], w2[:, c, :], start=(c == 0), stop=(c == nh - 1))
                last.then_inc(k.sem("branch_ready"), 1)

            @block.scalar
            def _(act):
                link = linker(act, k.sem("act_step"))
                prepare_x[0](act, link, t)
                act.wait_ge(k.sem("xq_turned"), 1)
                nc.scalar.copy(xqT[:, :, :], turned[:, 0:D].rearrange("p (c n) -> p c n", n=P)).then_inc(k.sem("xqT_ready"), 1)
                hidden_act(act, link)
                prepare_h[0](act, link)
                act.wait_ge(k.sem("hq_turned"), 1)
                nc.scalar.copy(hqT[:, :, :], turned[:, 0:HIDDEN].rearrange("p (c n) -> p c n", n=P)).then_inc(k.sem("hqT_ready"), 1)

            @block.vector
            def _(dve):
                link = linker(dve, k.sem("dve_step"))
                prepare_x[1](dve, link, t)
                prepare_h[1](dve, link)
                dve.wait_ge(k.sem("branch_ready"), 1)
                finish(dve, link, t)
        k.clear()


def abs_totals(k, dve, link, flat, work, tot):
    nc = k.nc
    for i in range(2):
        nc.vector.tensor_reduce(work[:, 32 * i:32 * i + 32], flat[i].rearrange("p (a b) -> p a b", a=32), AX_X, ALU.add,
                                apply_absolute_value=True).then_inc(k.sem("runs_ready"), 1)
    dve.wait_ge(k.sem("runs_ready"), 2)
    nc.vector.tensor_reduce(tot[:, :], work[:, 0:64].rearrange("p (i a) -> p i a", i=2), AX_X, ALU.add).then_inc(k.sem("abs_ready"), 1)


def layer5_ffn(k, w):
    nc = k.nc
    nh = HIDDEN // P
    with ExitStack() as ctx:
        w1 = k.sb(ctx, "w1_int", [P, CHUNKS, HIDDEN], BF16)
        w2 = k.sb(ctx, "w2_int", [P, nh, D], BF16)
        xq = k.sb(ctx, "xq", [P, D], BF16)
        xqT = k.sb(ctx, "xqT", [P, CHUNKS, P], BF16)
        hq = k.sb(ctx, "hq", [P, HIDDEN], BF16)
        hqT = k.sb(ctx, "hqT", [P, nh, P], BF16)
        ident = k.sb(ctx, "ident16", [P, P], BF16)
        work = k.sb(ctx, "quant_work", [P, HIDDEN * 2])
        hid = k.sb(ctx, "hidden", [P, HIDDEN])
        tot = k.sb(ctx, "abs_total", [P, 2])
        ws = k.sb(ctx, "w_scales", [P, 6])
        sc = k.sb(ctx, "row_scales", [P, 8])
        turned = k.banks[:, 0, :].bitcast(BF16)
        flat = [w["w1"].rearrange("p a b -> p (a b)"), w["w2"].rearrange("p a b -> p (a b)")]
        outs = [w1[:, :, :].rearrange("p a b -> p (a b)"), w2[:, :, :].rearrange("p a b -> p (a b)")]
        with nc.Block() as block:

            @block.scalar
            def _(act):
                nc.scalar.copy(ident[:, :], k.ident[:, :])

            @block.tensor
            def _(pe):
                pe.wait_ge(k.sem("abs_ready"), 1)
                nc.tensor.matmul(k.banks[:, 1, 0:2], w["ones"], tot[:, :], start=True, stop=True).then_inc(k.sem("total_ready"), 1)

            @block.vector
            def _(dve):
                link = linker(dve, k.sem("dve_step"))
                abs_totals(k, dve, link, flat, work, tot)
                dve.wait_ge(k.sem("total_ready"), 1)
                link(nc.vector.tensor_scalar(ws[:, 0:2], k.banks[:, 1, 0:2], 1.0 / (HIDDEN * D), 1e-5, ALU.mult, ALU.max))
                link(nc.vector.reciprocal(ws[:, 2:4], ws[:, 0:2]))
                link(nc.vector.tensor_scalar(ws[:, 4:6], ws[:, 0:2], 1.0 / QB, None, ALU.mult))
                for i in range(2):
                    link(nc.vector.tensor_scalar(work[:, :], flat[i], ws[:, 2 + i:3 + i], ROUND, ALU.mult, ALU.add))
                    link(nc.vector.tensor_scalar(work[:, :], work[:, :], ROUND, 1.0, ALU.subtract, ALU.min))
                    link(nc.vector.tensor_scalar(outs[i], work[:, :], -1.0, None, ALU.max))
        k.clear()

        def quantize(dve, link, src, out, n, col, ready):
            link(nc.vector.tensor_reduce(sc[:, col:col + 1], src, AX_X, ALU.max, apply_absolute_value=True))
            link(nc.vector.tensor_scalar(sc[:, col:col + 1], sc[:, col:col + 1], 1e-5, None, ALU.max))
            link(nc.vector.reciprocal(sc[:, col + 1:col + 2], sc[:, col:col + 1]))
            link(nc.vector.tensor_scalar(sc[:, col + 1:col + 2], sc[:, col + 1:col + 2], QB, None, ALU.mult))
            link(nc.vector.tensor_scalar(work[:, 0:n], src, sc[:, col + 1:col + 2], ROUND, ALU.mult, ALU.add))
            link(nc.vector.tensor_scalar(work[:, 0:n], work[:, 0:n], ROUND, QB, ALU.subtract, ALU.min))
            nc.vector.tensor_scalar(out, work[:, 0:n], -QB - 1.0, None, ALU.max).then_inc(k.sem(ready), 1)

        def x_dve(dve, link, t):
            quantize(dve, link, k.xn[:, t, :], xq[:, :], D, 0, "xq_ready")
            link(nc.vector.tensor_tensor(sc[:, 2:3], sc[:, 0:1], ws[:, 4:5], ALU.mult))

        def h_dve(dve, link):
            dve.wait_ge(k.sem("hidden_ready"), 2)
            nc.vector.scalar_tensor_tensor(hid[:, :], k.banks[:, 2:4, :].rearrange("p h n -> p (h n)"), sc[:, 2:3], w["b1"],
                                           ALU.mult, ALU.add).then_inc(k.sem("pre_ready"), 1)
            dve.wait_ge(k.sem("gelu_ready"), 1)
            quantize(dve, link, hid[:, :], hq[:, :], HIDDEN, 4, "hq_ready")
            link(nc.vector.tensor_tensor(sc[:, 6:7], sc[:, 4:5], ws[:, 5:6], ALU.mult))

        def gelu(act, link):
            act.wait_ge(k.sem("pre_ready"), 1)
            nc.scalar.activation(hid[:, :], hid[:, :], ACT.Gelu).then_inc(k.sem("gelu_ready"), 1)

        def finish(dve, link, t):
            link(nc.vector.scalar_tensor_tensor(work[:, 0:D], k.banks[:, 4, 0:D], sc[:, 6:7], w["b2"], ALU.mult, ALU.add))
            link(nc.vector.tensor_tensor(k.x[:, t, :], k.x[:, t, :], work[:, 0:D], ALU.add))

        two_layers(k, BF16, (lambda *_: None, x_dve), gelu, (lambda *_: None, h_dve), finish, w1, w2,
                   (xq, xqT, hq, hqT, ident[:, :], turned))


def layer11_ffn(k, w):
    nc = k.nc
    nh = HIDDEN // P
    with ExitStack() as ctx:
        w1 = k.sb(ctx, "w1_tern", [P, CHUNKS, HIDDEN])
        w2 = k.sb(ctx, "w2_tern", [P, nh, D])
        xq = k.sb(ctx, "x_unit", [P, D])
        xqT = k.sb(ctx, "x_unitT", [P, CHUNKS, P])
        hq = k.sb(ctx, "h_unit", [P, HIDDEN])
        hqT = k.sb(ctx, "h_unitT", [P, nh, P])
        work = k.sb(ctx, "work", [P, HIDDEN * 2])
        hid = k.sb(ctx, "hidden", [P, HIDDEN])
        tot = k.sb(ctx, "abs_total", [P, 2])
        th = k.sb(ctx, "thresholds", [P, 4])
        sc = k.sb(ctx, "row_scales", [P, 4])
        flat = [w["w1"].rearrange("p a b -> p (a b)"), w["w2"].rearrange("p a b -> p (a b)")]
        outs = [w1[:, :, :].rearrange("p a b -> p (a b)"), w2[:, :, :].rearrange("p a b -> p (a b)")]
        with nc.Block() as block:


            @block.tensor
            def _(pe):
                pe.wait_ge(k.sem("abs_ready"), 1)
                nc.tensor.matmul(k.banks[:, 1, 0:2], w["ones"], tot[:, :], start=True, stop=True).then_inc(k.sem("total_ready"), 1)

            @block.vector
            def _(dve):
                link = linker(dve, k.sem("dve_step"))
                abs_totals(k, dve, link, flat, work, tot)
                dve.wait_ge(k.sem("total_ready"), 1)
                nc.vector.tensor_scalar(th[:, 0:2], k.banks[:, 1, 0:2], 0.5 / (HIDDEN * D), None, ALU.mult)
                link(nc.vector.tensor_scalar(th[:, 2:4], k.banks[:, 1, 0:2], -0.5 / (HIDDEN * D), None, ALU.mult))
                for i in range(2):
                    link(nc.vector.tensor_scalar(work[:, :], flat[i], th[:, 2 + i:3 + i], None, ALU.is_lt))
                    link(nc.vector.scalar_tensor_tensor(outs[i], flat[i], th[:, i:i + 1], work[:, :], ALU.is_gt, ALU.subtract))
        k.clear()

        def unit(dve, link, src, out, n, col, ready):
            link(nc.vector.tensor_scalar(sc[:, col:col + 1], sc[:, col:col + 1], 1e-8, None, ALU.add))
            link(nc.vector.reciprocal(sc[:, col:col + 1], sc[:, col:col + 1]))
            nc.vector.tensor_scalar(out, src, sc[:, col:col + 1], None, ALU.mult).then_inc(k.sem(ready), 1)

        def x_act(act, link, t):
            link(nc.scalar.activation(work[:, 0:D], k.xn[:, t, :], ACT.Square, accum_out=sc[:, 0:1]))
            nc.scalar.activation(sc[:, 0:1], sc[:, 0:1], ACT.Sqrt, scale=1.0 / D).then_inc(k.sem("x_rms"), 1)

        def x_dve(dve, link, t):
            dve.wait_ge(k.sem("x_rms"), 1)
            unit(dve, link, k.xn[:, t, :], xq[:, :], D, 0, "xq_ready")

        def gelu(act, link):
            act.wait_ge(k.sem("hidden_ready"), 2)
            link(nc.scalar.activation(hid[:, :], k.banks[:, 2:4, :].rearrange("p h n -> p (h n)"), ACT.Gelu))

        def h_act(act, link):
            link(nc.scalar.activation(work[:, HIDDEN:], hid[:, :], ACT.Square, accum_out=sc[:, 1:2]))
            nc.scalar.activation(sc[:, 1:2], sc[:, 1:2], ACT.Sqrt, scale=1.0 / HIDDEN).then_inc(k.sem("h_rms"), 1)

        def h_dve(dve, link):
            dve.wait_ge(k.sem("h_rms"), 1)
            unit(dve, link, hid[:, :], hq[:, :], HIDDEN, 1, "hq_ready")

        def finish(dve, link, t):
            link(nc.vector.tensor_tensor(k.x[:, t, :], k.x[:, t, :], k.banks[:, 4, 0:D], ALU.add))

        two_layers(k, F32, (x_act, x_dve), gelu, (h_act, h_dve), finish, w1, w2,
                   (xq, xqT, hq, hqT, k.ident[:, :], k.banks[:, 0:2, :].rearrange("p b n -> p (b n)")))


PROTOS, RANK = 32, 16


def layer8_ffn(k, w):
    nc = k.nc
    pr = PROTOS * RANK
    nr = pr // P
    with ExitStack() as ctx:
        rows = k.sb(ctx, "x_rows", [P, CHUNKS, P])
        psq = k.sb(ctx, "proto_squares", [P, CHUNKS, PROTOS])
        p2 = k.sb(ctx, "proto_norms", [P, PROTOS])
        temp = k.sb(ctx, "temp_inverse", [P, 2])
        dist = k.sb(ctx, "dist", [P, PROTOS])
        wt = k.sb(ctx, "proto_weights", [P, PROTOS])
        pick = k.sb(ctx, "picked_two", [P, 2, PROTOS])
        best = k.sb(ctx, "best8", [P, 8])
        where = k.sb(ctx, "best8_at", [P, 8], mybir.dt.uint32)
        wheref = k.sb(ctx, "best8_at_float", [P, 8])
        cols = k.sb(ctx, "columns", [P, 8])
        junk = k.sb(ctx, "x_squares", [P, D])
        low = k.sb(ctx, "low_rank", [P, pr])
        lowT = k.sb(ctx, "low_rankT", [P, nr, P])
        wtT = k.sb(ctx, "proto_weightsT", [PROTOS, P])
        with nc.Block() as block:

            @block.scalar
            def _(act):
                nc.scalar.activation(psq[:, :, :], w["protos"], ACT.Square).then_inc(k.sem("squares_ready"), 1)
                nc.scalar.activation(temp[:, 0:1], w["temp"], ACT.Abs).then_inc(k.sem("temp_ready"), 1)

            @block.tensor
            def _(pe):
                pe.wait_ge(k.sem("squares_ready"), 1)
                for c in range(CHUNKS):
                    last = nc.tensor.matmul(k.banks[:, 0, 0:PROTOS], w["ones"], psq[:, c, :], start=(c == 0), stop=(c == CHUNKS - 1))
                last.then_inc(k.sem("norms_ready"), 1)

            @block.vector
            def _(dve):
                link = linker(dve, k.sem("dve_step"))
                dve.wait_ge(k.sem("temp_ready"), 1)
                link(nc.vector.tensor_scalar(temp[:, 0:1], temp[:, 0:1], 0.1, None, ALU.max))
                link(nc.vector.reciprocal(temp[:, 0:1], temp[:, 0:1]))
                nc.vector.tensor_scalar(temp[:, 1:2], temp[:, 0:1], -1.0, None, ALU.mult)
                dve.wait_ge(k.sem("norms_ready"), 1)
                nc.vector.tensor_copy(p2[:, :], k.banks[:, 0, 0:PROTOS])
        k.clear()
        with nc.Fori(0, TILES) as t:
            with nc.Block() as block:

                @block.tensor
                def _(pe):
                    pe.wait_ge(k.sem("rows_ready"), 1)
                    for c in range(CHUNKS):
                        last = nc.tensor.matmul(k.banks[:, 0, 0:PROTOS], rows[:, c, :], w["protos"][:, c, :],
                                                start=(c == 0), stop=(c == CHUNKS - 1))
                    last.then_inc(k.sem("cross_ready"), 1)
                    for c in range(CHUNKS):
                        last = nc.tensor.matmul(k.banks[:, 1, :], rows[:, c, :], w["B"][:, c, :], start=(c == 0), stop=(c == CHUNKS - 1))
                    last.then_inc(k.sem("low_ready"), 1)
                    pe.wait_ge(k.sem("weights_ready"), 1)
                    nc.tensor.transpose(k.banks[0:PROTOS, 3, 0:P], wt[:, :], k.ident[:, :])
                    pe.wait_ge(k.sem("weighted_ready"), 1)
                    for c in range(nr):
                        last = nc.tensor.transpose(k.banks[:, 2, c * P:(c + 1) * P], low[:, c * P:(c + 1) * P], k.ident[:, :])
                    last.then_inc(k.sem("turned"), 1)
                    pe.wait_ge(k.sem("turned_ready"), 2)
                    for c in range(nr):
                        nc.tensor.matmul(k.banks[:, 4, 0:D], lowT[:, c, :], w["A"][:, c, :], start=(c == 0), stop=False)
                    nc.tensor.matmul(k.banks[:, 4, 0:D], wtT[:, :], w["bias"][0:PROTOS, :], start=False,
                                     stop=True).then_inc(k.sem("branch_ready"), 1)

                @block.scalar
                def _(act):
                    nc.scalar.copy(rows[:, :, :], k.xnT[:, :, bass.ds(t * P, P)]).then_inc(k.sem("rows_ready"), 1)
                    nc.scalar.activation(junk[:, :], k.xn[:, t, :], ACT.Square, accum_out=cols[:, 0:1]).then_inc(k.sem("x2_ready"), 1)
                    act.wait_ge(k.sem("d2_ready"), 1)
                    nc.scalar.activation(dist[:, :], dist[:, :], ACT.Sqrt).then_inc(k.sem("dist_ready"), 1)
                    act.wait_ge(k.sem("shift_ready"), 1)
                    nc.scalar.activation(wt[:, :], dist[:, :], ACT.Exp, scale=temp[:, 1:2], bias=cols[:, 1:2],
                                         accum_out=cols[:, 2:3]).then_inc(k.sem("exp_ready"), 1)
                    act.wait_ge(k.sem("turned"), 1)
                    nc.scalar.copy(lowT[:, :, :], k.banks[:, 2, :].rearrange("p (c n) -> p c n", n=P)).then_inc(k.sem("turned_ready"), 1)
                    nc.scalar.copy(wtT[:, :], k.banks[0:PROTOS, 3, 0:P]).then_inc(k.sem("turned_ready"), 1)

                @block.vector
                def _(dve):
                    link = linker(dve, k.sem("dve_step"))
                    dve.wait_ge(k.sem("cross_ready"), 1)
                    dve.wait_ge(k.sem("x2_ready"), 1)
                    link(nc.vector.scalar_tensor_tensor(dist[:, :], k.banks[:, 0, 0:PROTOS], -2.0, p2[:, :], ALU.mult, ALU.add))
                    nc.vector.tensor_scalar(dist[:, :], dist[:, :], cols[:, 0:1], 0.0, ALU.add, ALU.max).then_inc(k.sem("d2_ready"), 1)
                    dve.wait_ge(k.sem("dist_ready"), 1)
                    link(nc.vector.tensor_reduce(cols[:, 1:2], dist[:, :], AX_X, ALU.min))
                    nc.vector.tensor_tensor(cols[:, 1:2], cols[:, 1:2], temp[:, 0:1], ALU.mult).then_inc(k.sem("shift_ready"), 1)
                    dve.wait_ge(k.sem("exp_ready"), 1)
                    link(nc.vector.reciprocal(cols[:, 2:3], cols[:, 2:3]))
                    link(nc.vector.tensor_scalar(wt[:, :], wt[:, :], cols[:, 2:3], None, ALU.mult))
                    link(nc.vector.max(best[:, :], wt[:, :]))
                    link(nc.vector.max_index(where[:, :], best[:, :], wt[:, :]))
                    link(nc.vector.tensor_copy(wheref[:, :], where[:, :]))
                    for i in range(2):
                        link(nc.vector.tensor_scalar(pick[:, i, :], w["iota"], wheref[:, i:i + 1], None, ALU.is_equal))
                    link(nc.vector.tensor_tensor(pick[:, 0, :], pick[:, 0, :], pick[:, 1, :], ALU.add))
                    link(nc.vector.tensor_tensor(wt[:, :], wt[:, :], pick[:, 0, :], ALU.mult))
                    link(nc.vector.reduce_sum(cols[:, 3:4], best[:, 0:2], AX_X))
                    link(nc.vector.reciprocal(cols[:, 3:4], cols[:, 3:4]))
                    nc.vector.tensor_scalar(wt[:, :], wt[:, :], cols[:, 3:4], None, ALU.mult).then_inc(k.sem("weights_ready"), 1)
                    dve.wait_ge(k.sem("weights_ready"), 1)
                    dve.wait_ge(k.sem("low_ready"), 1)
                    nc.vector.tensor_tensor(low[:, :].rearrange("p (a r) -> p a r", r=RANK),
                                            k.banks[:, 1, :].rearrange("p (a r) -> p a r", r=RANK),
                                            wt[:, :].unsqueeze(2).broadcast_to([P, PROTOS, RANK]), ALU.mult).then_inc(k.sem("weighted_ready"), 1)
                    dve.wait_ge(k.sem("branch_ready"), 1)
                    nc.vector.tensor_tensor(k.x[:, t, :], k.x[:, t, :], k.banks[:, 4, 0:D], ALU.add)
            k.clear()


BUILDERS |= {5: layer5_ffn, 8: layer8_ffn, 9: layer9_xattn, 11: layer11_ffn}


def layout_blocks(g, out):
    ones = np.ones((P, P), np.float32)
    a = "L1_ffn_"
    out[5] = dict(w1=_mat(g[a + "W1"].T), w2=_mat(g[a + "W2"].T), b1=_row(g[a + "b1"]), b2=_row(g[a + "b2"]), ones=ones)
    a = "L3_ffn_"
    out[11] = dict(w1=_mat(g[a + "w_up"].T), w2=_mat(g[a + "w_down"].T), ones=ones)
    a = "L2_ffn_"
    out[8] = dict(protos=_mat(g[a + "prototypes"].T), B=_mat(g[a + "B"].reshape(-1, D).T),
                  A=_mat(g[a + "A"].transpose(0, 2, 1).reshape(-1, D)), bias=g[a + "bias"],
                  temp=_row(g[a + "temp"].reshape(1)), iota=_row(np.arange(PROTOS, dtype=np.float32)), ones=ones)
    a = "L3_xattn_"
    hd = 64
    q = g[a + "q_w"].transpose(1, 0, 2)
    kv = g[a + "kv_w"][:, 0]
    swap = np.concatenate([np.arange(hd // 2, hd), np.arange(hd // 2)])
    timescale = np.float32(10000.0) ** (np.float32(2.0 / hd) * np.arange(hd // 2, dtype=np.float32))

    def table(fn, positions, signed):
        radians = positions.astype(np.float32)[:, None] / timescale
        t = fn(radians).T.astype(np.float32)
        both = np.concatenate([-t if signed else t, t])
        return np.ascontiguousarray(np.concatenate([both, both]))

    qpos, kpos = np.arange(CTX, CTX + SEQ), np.arange(CTX)
    out[9] = dict(wq=_mat(q.reshape(D, -1)), wqs=_mat(q[:, :, swap].reshape(D, -1)),
                  wk=_mat(np.concatenate([kv[0], kv[0], kv[0][:, swap], kv[0][:, swap]], 1)),
                  wv=_mat(np.concatenate([kv[1], kv[1]], 1)), wo=_mat(g[a + "out_w"].reshape(-1, D)), rms=_col(g[a + "rms_scale"]),
                  cosq=table(np.cos, qpos, False), sinq=table(np.sin, qpos, True),
                  cosk=table(np.cos, kpos, False), sink=table(np.sin, kpos, True), ones=ones)



STATES = 16


def token_product(k, src, w, chunks, evacuate):
    nc = k.nc
    with nc.Block() as block:

        @block.tensor
        def _(pe):
            for t in range(TILES):
                if t >= 2:
                    pe.wait_ge(k.sem("tile_used"), t - 1)
                for c in range(chunks):
                    last = nc.tensor.matmul(k.banks[:, t % 2, 0:D], src[:, c, t * P:(t + 1) * P], w[:, c, :],
                                            start=(c == 0), stop=(c == chunks - 1))
                last.then_inc(k.sem("tile_ready"), 1)

        @block.vector
        def _(dve):
            link = linker(dve, k.sem("dve_step"))
            for t in range(TILES):
                dve.wait_ge(k.sem("tile_ready"), t + 1)
                evacuate(dve, link, t, k.banks[:, t % 2, 0:D])
    k.clear()


def short_conv(k, items):
    nc = k.nc
    n = len(items)
    ntaps = items[0][2].shape[1]
    with nc.Block() as block:

        @block.vector
        def _(dve):
            for x, _, taps, bias, tmp in items:
                if bias is None:
                    last = nc.vector.tensor_scalar(tmp, x, taps[:, ntaps - 1:ntaps], None, ALU.mult)
                else:
                    last = nc.vector.tensor_scalar(tmp, x, taps[:, ntaps - 1:ntaps], bias, ALU.mult, ALU.add)
                last.then_inc(k.sem("taps_done"), 1)
            for j in range(ntaps - 1):
                back = ntaps - 1 - j
                for c, (x, _, taps, _, tmp) in enumerate(items):
                    dve.wait_ge(k.sem("taps_done"), n * j + c + 1)
                    o = tmp.rearrange("p (b s) -> p b s", s=SEQ)
                    v = x.rearrange("p (b s) -> p b s", s=SEQ)
                    nc.vector.scalar_tensor_tensor(o[:, :, back:], v[:, :, :SEQ - back], taps[:, j:j + 1], o[:, :, back:],
                                                   ALU.mult, ALU.add).then_inc(k.sem("taps_done"), 1)

        @block.scalar
        def _(act):
            for c, (_, out, _, _, tmp) in enumerate(items):
                act.wait_ge(k.sem("taps_done"), n * (ntaps - 1) + c + 1)
                nc.scalar.activation(out, tmp, ACT.Silu)
    k.clear()


def selective_scan(k, ctx, chunks, u, delta, bc, a_log, skip, y):
    nc = k.nc
    NB, ND, NS, NP = 4, 3, 3, 3
    b_banks = 1 if chunks == 4 else 2
    c_banks = 8 - chunks - b_banks
    AHEAD = 3
    neg_a = k.sb(ctx, "neg_a", [P, chunks, STATES])
    decay = k.sb(ctx, "decay", [P, NB, BANK])
    drive = k.sb(ctx, "drive", [P, ND, BANK])
    brow = k.xn[:, :, :].rearrange("p t d -> p (t d)").rearrange("p (i n) -> p i n", i=AHEAD + 1)
    state = k.sb(ctx, "state", [P, NS, BANK])
    part = k.sb(ctx, "state_out", [P, NP, BANK])
    du = k.sb(ctx, "delta_u", [P, chunks, TOKENS])
    rows = 2 * STATES
    split = k.sb(ctx, "bc_split", [3 * rows, TOKENS], BF16)
    pick = k.sb(ctx, "row_pick", [3 * rows, rows], BF16)
    picks = part[0:3 * rows, 0, 0:rows]
    with nc.Block() as block:

        @block.scalar
        def _(act):
            nc.scalar.activation(neg_a[:, :, :], a_log, ACT.Exp).then_inc(k.sem("a_ready"), 1)

        @block.gpsimd
        def _(pool):
            nc.gpsimd.memset(decay[:, :, :], 0.0)

        @block.vector
        def _(dve):
            nc.vector.tensor_tensor(du[:, :, :], delta, u, ALU.mult)
            dve.wait_ge(k.sem("a_ready"), 1)
            nc.vector.tensor_scalar(neg_a[:, :, :], neg_a[:, :, :], -1.0, None, ALU.mult)
            link = linker(dve, k.sem("dve_step"))
            every = slice(0, 3 * rows)
            link(nc.vector.tensor_tensor(picks, k.ident[every, 0:rows], k.ident[every, rows:2 * rows], ALU.add))
            link(nc.vector.tensor_tensor(pick[:, :], picks, k.ident[every, 2 * rows:3 * rows], ALU.add))
            link(nc.vector.tensor_copy(split[:, :], bc[:, :]))
            for first in (1, 2):
                for i in range(first, 3):
                    at = slice(rows * i, rows * (i + 1))
                    link(nc.vector.tensor_tensor(bc[at, :], bc[at, :], split[at, :], ALU.subtract))
                    link(nc.vector.tensor_copy(split[at, :], bc[at, :]))
    k.clear()
    units = [(n, c) for n in range(STATES) for c in range(chunks)]

    def b_bank(n):
        return k.banks[:, chunks + n % b_banks, :]

    def c_bank(n):
        return k.banks[:, chunks + b_banks + n % c_banks, :]

    with nc.Fori(0, TOKENS // BANK) as h:
        cols = bass.ds(h * BANK, BANK)
        with nc.Block() as block:

            @block.tensor
            def _(pe):
                def spread(n):
                    for i, bank in enumerate((b_bank(n), c_bank(n))):
                        if i == 0 and n >= b_banks:
                            pe.wait_ge(k.sem("b_copied"), n - b_banks + 1)
                        if i == 1 and n >= c_banks:
                            pe.wait_ge(k.sem("parts_ready"), chunks * (n - c_banks + 1))
                        row = STATES * i + n
                        nc.tensor.matmul(bank, pick[:, row:row + 1].broadcast_to([3 * rows, P]), split[:, cols],
                                         start=True, stop=True).then_inc(k.sem("rows_spread"), 1)

                for n in range(AHEAD):
                    spread(n)
                for i, (n, c) in enumerate(units):
                    pe.wait_ge(k.sem("parts_ready"), i + 1)
                    nc.tensor.matmul(k.banks[:, c, :], k.ident[:, :], part[:, i % NP, :], start=(n == 0),
                                     stop=(n == STATES - 1)).then_inc(k.sem("parts_used"), 1)
                    if c == chunks - 1 and n + AHEAD < STATES:
                        spread(n + AHEAD)

            @block.scalar
            def _(act):
                def copy_b(n):
                    act.wait_ge(k.sem("rows_spread"), 2 * n + 1)
                    if n > AHEAD:
                        act.wait_ge(k.sem("drive_ready"), chunks * (n - AHEAD))
                    nc.scalar.copy(brow[:, n % (AHEAD + 1), :], b_bank(n)).then_inc(k.sem("b_copied"), 1)

                copy_b(0)
                for i, (n, c) in enumerate(units):
                    if c == 0 and n + 1 < STATES:
                        copy_b(n + 1)
                    if i >= NB:
                        act.wait_ge(k.sem("scanned"), i - NB + 1)
                    nc.scalar.activation(decay[:, i % NB, :].rearrange("p (b s) -> p b s", s=SEQ)[:, :, 1:],
                                         delta[:, c, cols].rearrange("p (b s) -> p b s", s=SEQ)[:, :, 1:], ACT.Exp,
                                         scale=neg_a[:, c, n:n + 1]).then_inc(k.sem("decay_ready"), 1)

            @block.gpsimd
            def _(pool):
                for i, (n, c) in enumerate(units):
                    if c == 0:
                        pool.wait_ge(k.sem("b_copied"), n + 1)
                    if i >= ND:
                        pool.wait_ge(k.sem("scanned"), i - ND + 1)
                    nc.gpsimd.tensor_tensor(drive[:, i % ND, :], du[:, c, cols], brow[:, n % (AHEAD + 1), :], ALU.mult).then_inc(k.sem("drive_ready"), 1)

            @block.vector
            def _(dve):
                for i in range(len(units) + 1):
                    if i < len(units):
                        dve.wait_ge(k.sem("decay_ready"), i + 1)
                        dve.wait_ge(k.sem("drive_ready"), i + 1)
                        if i >= NS:
                            dve.wait_ge(k.sem("parts_ready"), i - NS + 1)
                        nc.vector.tensor_tensor_scan(state[:, i % NS, :], decay[:, i % NB, :], drive[:, i % ND, :], 0.0, ALU.mult,
                                                     ALU.add).then_inc(k.sem("scanned"), 1)
                    if i:
                        m = i - 1
                        n = units[m][0]
                        dve.wait_ge(k.sem("scanned"), m + 1)
                        dve.wait_ge(k.sem("rows_spread"), 2 * n + 2)
                        if m >= NP:
                            dve.wait_ge(k.sem("parts_used"), m - NP + 1)
                        nc.vector.tensor_tensor(part[:, m % NP, :], state[:, m % NS, :], c_bank(n),
                                                ALU.mult).then_inc(k.sem("parts_ready"), 1)
                dve.wait_ge(k.sem("parts_used"), len(units))
                for c in range(chunks):
                    nc.vector.scalar_tensor_tensor(y[:, c, cols], u[:, c, cols], skip[:, c:c + 1], k.banks[:, c, :], ALU.mult, ALU.add)
        k.clear()


def layer10_attn(k, w):
    nc = k.nc
    chunks = 4
    with ExitStack() as ctx:
        u = k.sb(ctx, "u", [P, chunks, TOKENS])
        delta = k.sb(ctx, "delta", [P, chunks, TOKENS])
        dt = k.sb(ctx, "dt_low", [STATES, 1, TOKENS])
        bc = k.sb(ctx, "bc", [6 * STATES, TOKENS])
        project(k, [(w["win"], c * P, u[:, c, :], None, ACT.Identity) for c in range(chunks)])
        short_conv(k, [(u[:, c, :], u[:, c, :], w["taps"][:, c, :], w["cbias"][:, c:c + 1], delta[:, c, :]) for c in range(chunks)])
        project(k, [(w["wdt_low"], 0, dt[:, 0, :], None, ACT.Identity), (w["wbc"], 0, bc[:, :], None, ACT.Identity)], src=u, chunks=chunks)
        project(k, [(w["wdt"], c * P, delta[:, c, :], w["dtb"][:, c:c + 1], ACT.Identity) for c in range(chunks)], src=dt, chunks=1)
        with ExitStack() as room:
            e, low = (k.sb(room, n, [P, chunks, TOKENS])[:, :, :] for n in ("softplus_e", "softplus_low"))
            softplus(k, delta[:, :, :], e, low)
        selective_scan(k, ctx, chunks, u[:, :, :], delta[:, :, :], bc, w["a_log"], w["skip"], u)

        def finish(dve, link, t, psum):
            nc.vector.tensor_tensor(k.x[:, t, :], k.x[:, t, :], psum, ALU.add).then_inc(k.sem("tile_used"), 1)

        token_product(k, u, w["wout"], chunks, finish)


def layer4_attn(k, w):
    nc = k.nc
    with ExitStack() as ctx:
        s = k.sb(ctx, "inner_stream", [P, TILES, D])
        with nc.Block() as block:

            @block.gpsimd
            def _(pool):
                nc.gpsimd.tensor_copy(s[:, :, :], k.xn[:, :, :])
        normalize(k, src=k.xn, scale=w["n1g"], shift=w["n1b"])
        with ExitStack() as inner:
            u = k.sb(inner, "u", [P, CHUNKS, TOKENS])
            z = k.sb(inner, "z", [P, CHUNKS, TOKENS])
            delta = k.sb(inner, "delta", [P, CHUNKS, TOKENS])
            dt = k.sb(inner, "dt_low", [64, 1, TOKENS])
            bc = k.sb(inner, "bc", [6 * STATES, TOKENS])
            hs = k.sb(inner, "mixed", [P, D])
            st = k.sb(inner, "mixed_stats", [P, 6])
            mv = k.sb(inner, "mixed_meanvar", [P, 2])
            project(k, [(w["win"], c * P, u[:, c, :], None, ACT.Identity) for c in range(CHUNKS)]
                    + [(w["win"], D + c * P, z[:, c, :], None, ACT.Silu) for c in range(CHUNKS)])
            short_conv(k, [(u[:, c, :], u[:, c, :], w["taps"][:, c, :], w["cbias"][:, c:c + 1], delta[:, c, :]) for c in range(CHUNKS)])
            project(k, [(w["wdt_low"], 0, dt[:, 0, :], None, ACT.Identity), (w["wbc"], 0, bc[:, :], None, ACT.Identity)], src=u)
            project(k, [(w["wdt"], c * P, delta[:, c, :], w["dtb"][:, c:c + 1], ACT.Identity) for c in range(CHUNKS)], src=dt, chunks=1)
            with ExitStack() as room:
                e, low = (k.sb(room, n, [P, CHUNKS, TOKENS])[:, :, :] for n in ("softplus_e", "softplus_low"))
                softplus(k, delta[:, :, :], e, low)
            selective_scan(k, inner, CHUNKS, u[:, :, :], delta[:, :, :], bc, w["a_log"], w["skip"], u)
            with nc.Block() as block:

                @block.vector
                def _(dve):
                    nc.vector.tensor_tensor(u[:, :, :], u[:, :, :], z[:, :, :], ALU.mult)
            h_tok = k.xn

            def keep(dve, link, t, psum):
                nc.vector.tensor_copy(h_tok[:, t, :], psum).then_inc(k.sem("tile_used"), 1)

            token_product(k, u, w["wout"], CHUNKS, keep)
        normalize(k, src=k.xn, turn=False)
        with nc.Block() as block:

            @block.vector
            def _(dve):
                link = linker(dve, k.sem("dve_step"))
                for op, row in ((ALU.mult, w["mg"]), (ALU.add, w["mb"])):
                    link(nc.vector.tensor_tensor(k.xn[:, :, :], k.xn[:, :, :], row.unsqueeze(1).broadcast_to([P, TILES, D]), op))
                nc.vector.tensor_tensor(s[:, :, :], s[:, :, :], k.xn[:, :, :], ALU.add)
        k.clear()
        normalize(k, src=s, scale=w["n2g"], shift=w["n2b"])
        hidden = k.sb(ctx, "leaky_hidden", [P, HIDDEN // P, TOKENS])
        project(k, [(w["w1"], c * P, hidden[:, c, :], None, ACT.Identity) for c in range(HIDDEN // P)])
        with nc.Block() as block:

            @block.vector
            def _(dve):
                for c in range(HIDDEN // P):
                    nc.vector.scalar_tensor_tensor(hidden[:, c, :], hidden[:, c, :], 0.01, hidden[:, c, :], ALU.mult, ALU.max)

        def add_s(dve, link, t, psum):
            nc.vector.tensor_tensor(s[:, t, :], s[:, t, :], psum, ALU.add).then_inc(k.sem("tile_used"), 1)

        token_product(k, hidden, w["w2"], HIDDEN // P, add_s)
        normalize(k, src=s, scale=w["n3g"], shift=w["n3b"])

        def last(dve, link, t, psum):
            nc.vector.tensor_tensor(s[:, t, :], s[:, t, :], psum, ALU.add).then_inc(k.sem("tile_used"), 1)
            dve.wait_ge(k.sem("tile_used"), t + 1)
            link(nc.vector.tensor_tensor(s[:, t, :], s[:, t, :], w["feb"], ALU.add))
            nc.vector.tensor_tensor(k.x[:, t, :], k.x[:, t, :], s[:, t, :], ALU.add)

        token_product(k, k.xnT, w["fe"], CHUNKS, last)


BUILDERS |= {4: layer4_attn, 10: layer10_attn}


def layout_scans(g, out):
    a = "L1_attn_"
    xp = g[a + "x_proj_w"].T
    out[4] = dict(win=_mat(g[a + "in_proj_w"].T), taps=g[a + "conv_w"].reshape(-1, P, 2).transpose(1, 0, 2), cbias=_col(g[a + "conv_b"]),
                  wdt_low=_mat(xp[:, :64]), wbc=_mat(np.tile(xp[:, 64:], (1, 3))), wdt=g[a + "dt_proj_w"].T[:, None, :], dtb=_col(g[a + "dt_proj_b"]),
                  a_log=g[a + "A_log"].reshape(-1, P, STATES).transpose(1, 0, 2), skip=_col(g[a + "Dp"]), wout=_mat(g[a + "out_proj_w"].T),
                  n1g=_col(g[a + "n1_g"]), n1b=_col(g[a + "n1_b"]), n2g=_col(g[a + "n2_g"]), n2b=_col(g[a + "n2_b"]),
                  n3g=_col(g[a + "n3_g"]), n3b=_col(g[a + "n3_b"]), mg=_row(g[a + "mnorm_g"]), mb=_row(g[a + "mnorm_b"]),
                  w1=_mat(g[a + "ffn_w1"].T), w2=_mat(g[a + "ffn_w2"].T), fe=_mat(g[a + "fe_w"].T), feb=_row(g[a + "fe_b"]))
    a = "L3_attn_"
    wx = g[a + "W_x"]
    out[10] = dict(win=_mat(g[a + "W_in"]), taps=g[a + "conv_w"].reshape(-1, P, 4).transpose(1, 0, 2), cbias=_col(g[a + "conv_b"]),
                   wdt_low=_mat(wx[:, :16]), wbc=_mat(np.tile(wx[:, 16:], (1, 3))), wdt=g[a + "W_dt"][:, None, :], dtb=_col(g[a + "b_dt"]),
                   a_log=g[a + "A_log"].reshape(-1, P, STATES).transpose(1, 0, 2), skip=_col(g[a + "D"]), wout=_mat(g[a + "W_out"]))



DH = 4
HD = D // DH
DCHUNK = 32
LEVELS = 5


def unit_heads(k, xs, sq, same64, eps):
    nc = k.nc
    parts = [(x[:, c, h * BANK:(h + 1) * BANK], sq[:, n * CHUNKS + c, h * BANK:(h + 1) * BANK])
             for n, x in enumerate(xs) for c in range(CHUNKS) for h in range(TOKENS // BANK)]
    with nc.Block() as block:

        @block.gpsimd
        def _(pool):
            nc.gpsimd.memset(eps, 1e-6).then_inc(k.sem("eps_ready"), 1)
            for n, (x, s) in enumerate(parts):
                pool.wait_ge(k.sem("inverse_ready"), n + 1)
                nc.gpsimd.tensor_tensor(x, x, s, ALU.mult)

        @block.scalar
        def _(act):
            for x, s in parts:
                nc.scalar.activation(s, x, ACT.Square).then_inc(k.sem("squares_ready"), 1)
            act.wait_ge(k.sem("eps_ready"), 1)
            for n, (x, s) in enumerate(parts):
                act.wait_ge(k.sem("sums_in_psum"), n + 1)
                nc.scalar.activation(s, k.banks[:, n, :], ACT.Sqrt, bias=eps).then_inc(k.sem("norm_ready"), 1)

        @block.tensor
        def _(pe):
            for n, (x, s) in enumerate(parts):
                pe.wait_ge(k.sem("squares_ready"), n + 1)
                nc.tensor.matmul(k.banks[:, n, :], same64, s, start=True, stop=True).then_inc(k.sem("sums_in_psum"), 1)

        @block.vector
        def _(dve):
            for n, (x, s) in enumerate(parts):
                dve.wait_ge(k.sem("norm_ready"), n + 1)
                nc.vector.reciprocal(s, s).then_inc(k.sem("inverse_ready"), 1)
    k.clear()


def layer7_attn(k, w):
    nc = k.nc
    with ExitStack() as ctx:
        q, kk, v, kb, vb = (k.sb(ctx, "delta_" + n, [P, CHUNKS, TOKENS]) for n in ("q", "k", "v", "kb", "vb"))
        mixed = k.xn[:, :, :].rearrange("p t d -> p (t d)").rearrange("p (c n) -> p c n", c=CHUNKS)
        with ExitStack() as inner:
            cat = k.sb(inner, "conv_cat", [P, 6, TOKENS])
            DIAGS = 8
            diag = k.sb(inner, "tap_diagonals", [P, DIAGS, P])
            eps = k.sb(inner, "unit_eps", [P, 1])
            project(k, [(w[n], c * P, o[:, c, :], None, f) for n, o, f in
                        (("wq", q, ACT.Identity), ("wk", kk, ACT.Identity), ("wv", v, ACT.Identity), ("wb", vb, ACT.Sigmoid))
                        for c in range(CHUNKS)])
            short_conv(k, [(x[:, c, :], x[:, c, :], taps[:, c, :], None, cat[:, 2 * i + c, :])
                           for i, (x, taps) in enumerate(((v, w["tv"]), (q, w["tq"]), (kk, w["tk"]))) for c in range(CHUNKS)])
            unit_heads(k, (q, kk), cat[:, 0:4, :], w["same64"], eps[:, 0:1])
            pe_taps = [(g, c, j) for g, n in ((0, 3), (1, 15)) for c in range(CHUNKS) for j in range(n)]
            taps_of = (w["t3"], w["t15"])
            with nc.Block() as block:

                @block.gpsimd
                def _(pool):
                    nc.gpsimd.tensor_tensor(kb[:, :, :], kk[:, :, :], vb[:, :, :], ALU.mult).then_inc(k.sem("kb_ready"), 1)
                    pool.wait_ge(k.sem("kb_ready"), 1)
                    nc.gpsimd.tensor_tensor(vb[:, :, :], v[:, :, :], vb[:, :, :], ALU.mult)

                @block.scalar
                def _(act):
                    for n, (g, c, j) in enumerate(pe_taps):
                        if n >= DIAGS:
                            act.wait_ge(k.sem("diag_used"), n - DIAGS + 1)
                        last = taps_of[g].shape[2] - 1
                        nc.scalar.activation(diag[:, n % DIAGS, :], k.ident[:, :], ACT.Copy,
                                             scale=taps_of[g][:, c, last - j:last - j + 1]).then_inc(k.sem("diag_ready"), 1)
                    for g in range(2):
                        for c in range(CHUNKS):
                            act.wait_ge(k.sem("diag_used"), sum(1 for tap in pe_taps if tap[0:2] <= (g, c)))
                            nc.scalar.copy(cat[:, 2 * g + c, :], k.banks[:, 4 * g + 2 * c:4 * g + 2 * c + 2, :].rearrange("p b n -> p (b n)"))

                @block.tensor
                def _(pe):
                    for n, (g, c, j) in enumerate(pe_taps):
                        pe.wait_ge(k.sem("diag_ready"), n + 1)
                        ntaps = taps_of[g].shape[2]
                        for h in range(TOKENS // BANK):
                            o = k.banks[:, 4 * g + 2 * c + h, :].rearrange("p (b s) -> p b s", s=SEQ)
                            x = v[:, c, h * BANK:(h + 1) * BANK].rearrange("p (b s) -> p b s", s=SEQ)
                            last = nc.tensor.matmul(o[:, :, j:], diag[:, n % DIAGS, :], x[:, :, :SEQ - j], start=(j == 0), stop=(j == ntaps - 1))
                        last.then_inc(k.sem("diag_used"), 1)

                @block.vector
                def _(dve):
                    n = w["t31"].shape[2]
                    for j in range(n):
                        for c in range(CHUNKS):
                            o = cat[:, 4 + c, :].rearrange("p (b s) -> p b s", s=SEQ)
                            x = v[:, c, :].rearrange("p (b s) -> p b s", s=SEQ)
                            tap = w["t31"][:, c, n - 1 - j:n - j]
                            done = k.sem(f"conv{c}")
                            if j == 0:
                                nc.vector.tensor_scalar(o, x, tap, None, ALU.mult).then_inc(done, 1)
                            else:
                                dve.wait_ge(done, j)
                                nc.vector.scalar_tensor_tensor(o[:, :, j:], x[:, :, :SEQ - j], tap, o[:, :, j:], ALU.mult,
                                                               ALU.add).then_inc(done, 1)
            k.clear()
            with nc.Block() as block:

                @block.tensor
                def _(pe):
                    for c in range(CHUNKS):
                        for h in range(TOKENS // BANK):
                            for g in range(3):
                                last = nc.tensor.matmul(k.banks[:, 2 * c + h, :], w["mix"][:, 3 * c + g, :], cat[:, 3 * c + g, h * BANK:(h + 1) * BANK],
                                                        start=(g == 0), stop=(g == 2))
                            last.then_inc(k.sem("mix_ready"), 1)

                @block.scalar
                def _(act):
                    for n in range(4):
                        act.wait_ge(k.sem("mix_ready"), n + 1)
                        nc.scalar.copy(mixed[:, n // 2, (n % 2) * BANK:(n % 2 + 1) * BANK], k.banks[:, n, :])
            k.clear()
        delta_tiles(k, ctx, w, (q, kk, kb, vb, v, mixed))


DELTA_COUNTS = dict(copied=4, turned=1, gram_in_psum=2, local_in_psum=2, gram_copied=2, tok_ready=2, level_ready=5, product_ready=5,
                    T_ready=4, TT_ready=5, U_ready=4, stepT_ready=4, step_ready=3, local_ready=2, two_ready=6, q_turned=1, u_in_psum=1,
                    w_in_psum=1, by_seq_copied=2, u_copied=1, state_in_psum=1, state_copied=1, ws_in_psum=1, u_final=1,
                    delta_in_psum=1, delta_read=1, late_copied=2, v_turned=1, conv_in_psum=1, conv_ready=2, means_ready=1,
                    means_turned=1, meansT_ready=1, gate_in_psum=1, gate_hidden_ready=4, logits_in_psum=1, shifted=1, gate_exp=1,
                    mean_square=1, root=1, out_ready=1, out_turned=1, outT_ready=1, branch_ready=1, added=1)


def alternate(rule, mix, unroll):
    for j in range(unroll + 1):
        for _ in zip_longest(rule(j) if j < unroll else (), mix(j - 1) if j else ()):
            pass


def delta_tiles(k, ctx, w, sources):
    nc = k.nc
    unroll = 4
    here = k.sb(ctx, "tile_feat", [P, 4, CHUNKS, P])
    late = k.sb(ctx, "tile_feat_late", [P, 2, CHUNKS, P])
    tok = k.sb(ctx, "tile_tok", [P, 4, DH, HD])
    gram = k.sb(ctx, "gramT", [P, DH, P])
    level = k.sb(ctx, "gramT_level", [P, 2, DH, P])
    local = k.sb(ctx, "localT", [P, DH, P])
    T, TT, U = (k.sb(ctx, n, [P, DH, P]) for n in ("inverse", "inverseT", "level_product"))
    two = k.sb(ctx, "by_sequence", [P, 3, DH, PER_TILE, HD])
    qT2, wT2 = gram, T
    u = k.sb(ctx, "delta_u", [P, DH, HD])
    S = k.sb(ctx, "delta_state", [P, DH, HD])
    parts = k.sb(ctx, "mix_parts", [P, 3, DH, HD])
    F = k.sb(ctx, "head_means", [P, 12])
    FT = k.sb(ctx, "head_meansT", [12, P])
    hdn = k.sb(ctx, "gate_hidden", [P, 4, P])
    lg = k.sb(ctx, "gate_logits", [P, DH, 3])
    gm = k.sb(ctx, "gate_col", [P, DH])
    o = k.sb(ctx, "mix_out", [P, DH, HD])
    o2 = k.sb(ctx, "mix_work", [P, 3, DH, HD])
    oT = k.sb(ctx, "mix_outT", [P, CHUNKS, P])
    Q, K_, KB, VB, V_, MIX = range(6)
    B = k.banks

    def heads(bank, width):
        return B[:, bank, 0:DH * width].rearrange("p (h n) -> p h n", h=DH)

    def pair(bank, i):
        return B[:, bank, 2 * P * i:2 * P * (i + 1)].rearrange("p (h n) -> p h n", h=2)

    def waiter(eng, j):
        def wait(name, n):
            eng.wait_ge(k.sem(name), DELTA_COUNTS[name] * j + n)

        def before(name):
            if j:
                eng.wait_ge(k.sem(name), DELTA_COUNTS[name] * j)
        return wait, before

    with nc.Fori(0, TILES // unroll) as t:

        def cols(j):
            return bass.ds((t * unroll + j) * P, P)

        with nc.Block() as block:

            @block.gpsimd
            def _(pool):
                def rule(j):
                    wait, before = waiter(pool, j)
                    yield
                    wait("gram_copied", 2)
                    before("product_ready")
                    for s in range(LEVELS):
                        if s >= 2:
                            wait("product_ready", s - 1)
                        if s == 2:
                            wait("TT_ready", 1)
                        nc.gpsimd.tensor_tensor(level[:, s % 2, :, :], gram[:, :, :], w["levels"][:, s, :].unsqueeze(1).broadcast_to([P, DH, P]),
                                                ALU.mult).then_inc(k.sem("level_ready"), 1)
                        if s == 1:
                            wait("tok_ready", 2)
                            before("state_in_psum")
                            for i, (src, ind) in enumerate(((Q, "second"), (KB, "second"), (K_, "first"))):
                                for b in range(PER_TILE):
                                    nc.gpsimd.tensor_scalar(two[:, i, :, b, :], tok[:, src, :, :], w[ind][:, b:b + 1], None,
                                                            ALU.mult).then_inc(k.sem("two_ready"), 1)
                        yield

                def mix(j):
                    wait, before = waiter(pool, j)
                    before("conv_in_psum")
                    for i in range(2):
                        nc.gpsimd.tensor_copy(late[:, i, :, :], sources[V_ + i][:, :, cols(j)]).then_inc(k.sem("late_copied"), 1)
                    yield

                alternate(rule, mix, unroll)

            @block.tensor
            def _(pe):
                def rule(j):
                    wait, before = waiter(pe, j)
                    wait("copied", 4)
                    for i in range(4):
                        for c in range(CHUNKS):
                            last = nc.tensor.transpose(B[:, i // 2, ((i % 2) * 2 + c) * P:((i % 2) * 2 + c + 1) * P], here[:, i, c, :], k.ident[:, :])
                    last.then_inc(k.sem("turned"), 1)
                    for half, rhs, ready in ((0, KB, "gram_in_psum"), (1, Q, "local_in_psum")):
                        for h in range(DH):
                            part = slice(HD * (h % 2), HD * (h % 2) + HD)
                            last = nc.tensor.matmul(pair(3 + 2 * (h % 2), half)[:, h // 2, :], here[part, K_, h // 2, :],
                                                    here[part, rhs, h // 2, :], start=True, stop=True)
                            if h >= DH - 2:
                                last.then_inc(k.sem(ready), 1)
                    yield
                    before("delta_read")
                    for s in range(LEVELS):
                        wait("level_ready", s + 1)
                        if s:
                            wait("T_ready", s)
                            wait("local_ready", 2)
                        for h in range(DH):
                            last = nc.tensor.matmul(B[:, 5 if s else 6, h * P:(h + 1) * P], level[:, s % 2, h, :],
                                                    T[:, h, :] if s else k.ident[:, :], start=True, stop=True)
                        last.then_inc(k.sem("product_ready"), 1)
                        if s:
                            wait("U_ready", s)
                            wait("TT_ready", s)
                            if s < LEVELS - 1:
                                for h in range(DH):
                                    last = nc.tensor.matmul(B[:, 6, h * P:(h + 1) * P], TT[:, h, :], U[:, h, :], start=True, stop=True)
                                last.then_inc(k.sem("step_ready"), 1)
                            for h in range(DH):
                                last = nc.tensor.matmul(B[:, 7, h * P:(h + 1) * P], U[:, h, :], TT[:, h, :], start=True, stop=True)
                            last.then_inc(k.sem("stepT_ready"), 1)
                        yield
                    wait("two_ready", 6)
                    for h in range(DH):
                        last = nc.tensor.transpose(B[:, 0, h * P:(h + 1) * P], two[:, 0, h, :, :].rearrange("p b n -> p (b n)"), k.ident[:, :])
                    last.then_inc(k.sem("q_turned"), 1)
                    wait("TT_ready", LEVELS)
                    for h in range(DH):
                        last = nc.tensor.matmul(B[:, 3, h * HD:(h + 1) * HD], TT[:, h, :], tok[:, VB, h, :], start=True, stop=True)
                    last.then_inc(k.sem("u_in_psum"), 1)
                    for h in range(DH):
                        last = nc.tensor.matmul(B[:, 1, h * P:(h + 1) * P], two[:, 1, h, :, :].rearrange("p b n -> p (b n)"), TT[:, h, :],
                                                start=True, stop=True)
                    last.then_inc(k.sem("w_in_psum"), 1)
                    wait("u_copied", 1)
                    for h in range(DH):
                        last = nc.tensor.matmul(B[:, 3, h * HD:(h + 1) * HD], two[:, 2, h, :, :].rearrange("p b n -> p (b n)"), u[:, h, :],
                                                start=True, stop=True)
                    last.then_inc(k.sem("state_in_psum"), 1)
                    yield
                    wait("state_copied", 1)
                    wait("by_seq_copied", 2)
                    for h in range(DH):
                        last = nc.tensor.matmul(B[:, 5, h * HD:(h + 1) * HD], wT2[:, h, :], S[:, h, :], start=True, stop=True)
                    last.then_inc(k.sem("ws_in_psum"), 1)
                    yield
                    wait("u_final", 1)
                    for h in range(DH):
                        nc.tensor.matmul(B[:, 6, h * HD:(h + 1) * HD], qT2[:, h, :], S[:, h, :], start=True, stop=False)
                        last = nc.tensor.matmul(B[:, 6, h * HD:(h + 1) * HD], local[:, h, :], u[:, h, :], start=False, stop=True)
                    last.then_inc(k.sem("delta_in_psum"), 1)
                    yield

                def mix(j):
                    wait, before = waiter(pe, j)
                    wait("late_copied", 2)
                    before("added")
                    for c in range(CHUNKS):
                        last = nc.tensor.transpose(B[:, 2, c * P:(c + 1) * P], late[:, 0, c, :], k.ident[:, :])
                    last.then_inc(k.sem("v_turned"), 1)
                    for c in range(CHUNKS):
                        last = nc.tensor.matmul(B[:, 4, 0:D], late[:, 1, c, :], w["mixer"][:, c, :], start=(c == 0), stop=(c == CHUNKS - 1))
                    last.then_inc(k.sem("conv_in_psum"), 1)
                    yield
                    yield
                    wait("means_ready", 1)
                    wait("conv_ready", 2)
                    nc.tensor.transpose(B[0:12, 2, 0:P], F[:, :], k.ident[:, :]).then_inc(k.sem("means_turned"), 1)
                    yield
                    wait("meansT_ready", 1)
                    for m in range(4):
                        for c in range(CHUNKS):
                            nc.tensor.matmul(B[:, 4, m * P:(m + 1) * P], w["f1"][:, c, m * P:(m + 1) * P], k.xnT[:, c, cols(j)],
                                             start=(c == 0), stop=False)
                        last = nc.tensor.matmul(B[:, 4, m * P:(m + 1) * P], w["f1m"][:, m * P:(m + 1) * P], FT[:, :], start=False, stop=True)
                    last.then_inc(k.sem("gate_in_psum"), 1)
                    yield
                    wait("gate_hidden_ready", 4)
                    for m in range(4):
                        last = nc.tensor.matmul(B[:, 2, 0:12], hdn[:, m, :], w["f2"][:, m, :], start=(m == 0), stop=(m == 3))
                    last.then_inc(k.sem("logits_in_psum"), 1)
                    yield
                    yield
                    yield
                    wait("out_ready", 1)
                    for c in range(CHUNKS):
                        last = nc.tensor.transpose(B[:, 4, c * P:(c + 1) * P], o[:, 2 * c:2 * c + 2, :].rearrange("p h n -> p (h n)"), k.ident[:, :])
                    last.then_inc(k.sem("out_turned"), 1)
                    yield
                    wait("outT_ready", 1)
                    for c in range(CHUNKS):
                        last = nc.tensor.matmul(B[:, 2, 0:D], oT[:, c, :], w["wo"][:, c, :], start=(c == 0), stop=(c == CHUNKS - 1))
                    last.then_inc(k.sem("branch_ready"), 1)
                    yield

                alternate(rule, mix, unroll)

            @block.scalar
            def _(act):
                def rule(j):
                    wait, before = waiter(act, j)
                    before("delta_in_psum")
                    for i in range(4):
                        nc.scalar.copy(here[:, i, :, :], sources[i][:, :, cols(j)]).then_inc(k.sem("copied"), 1)
                    yield
                    wait("local_in_psum", 2)
                    for r in range(2):
                        nc.scalar.copy(gram[:, r::2, :], pair(3 + 2 * r, 0)).then_inc(k.sem("gram_copied"), 1)
                    for i in range(2):
                        nc.scalar.copy(tok[:, 2 * i:2 * i + 2, :, :].rearrange("p a h n -> p (a h n)"), B[:, i, :]).then_inc(k.sem("tok_ready"), 1)
                    yield
                    for s in range(1, LEVELS):
                        wait("product_ready", s + 1)
                        nc.scalar.copy(U[:, :, :], heads(5, P)).then_inc(k.sem("U_ready"), 1)
                        yield
                    wait("q_turned", 1)
                    nc.scalar.copy(qT2[:, :, :], heads(0, P)).then_inc(k.sem("by_seq_copied"), 1)
                    wait("w_in_psum", 1)
                    nc.scalar.copy(wT2[:, :, :], heads(1, P)).then_inc(k.sem("by_seq_copied"), 1)
                    wait("state_in_psum", 1)
                    nc.scalar.copy(S[:, :, :], heads(3, HD)).then_inc(k.sem("state_copied"), 1)
                    yield

                def mix(j):
                    wait, before = waiter(act, j)
                    wait("v_turned", 1)
                    nc.scalar.copy(parts[:, 2, :, :], heads(2, HD)).then_inc(k.sem("conv_ready"), 1)
                    wait("conv_in_psum", 1)
                    nc.scalar.copy(parts[:, 0, :, :], heads(4, HD)).then_inc(k.sem("conv_ready"), 1)
                    yield
                    yield
                    wait("means_turned", 1)
                    nc.scalar.copy(FT[:, :], B[0:12, 2, 0:P]).then_inc(k.sem("meansT_ready"), 1)
                    yield
                    wait("gate_in_psum", 1)
                    for m in range(4):
                        nc.scalar.activation(hdn[:, m, :], B[:, 4, m * P:(m + 1) * P], ACT.Gelu,
                                             bias=w["f1b"][:, m:m + 1]).then_inc(k.sem("gate_hidden_ready"), 1)
                    yield
                    wait("shifted", 1)
                    nc.scalar.activation(lg[:, :, :], lg[:, :, :], ACT.Exp).then_inc(k.sem("gate_exp"), 1)
                    yield
                    yield
                    wait("mean_square", 1)
                    nc.scalar.activation(gm[:, :], gm[:, :], ACT.Sqrt).then_inc(k.sem("root"), 1)
                    yield
                    wait("out_turned", 1)
                    before("branch_ready")
                    nc.scalar.copy(oT[:, :, :], B[:, 4, 0:D].rearrange("p (c n) -> p c n", n=P)).then_inc(k.sem("outT_ready"), 1)
                    yield

                alternate(rule, mix, unroll)

            @block.vector
            def _(dve):
                link = linker(dve, k.sem("dve_step"))
                eye = k.ident[:, :].unsqueeze(1).broadcast_to([P, DH, P])

                def rule(j):
                    wait, before = waiter(dve, j)
                    yield
                    wait("level_ready", 1)
                    nc.vector.tensor_tensor(TT[:, :, :], eye, level[:, 0, :, :], ALU.subtract).then_inc(k.sem("TT_ready"), 1)
                    wait("product_ready", 1)
                    nc.vector.tensor_tensor(T[:, :, :], eye, heads(6, P), ALU.subtract).then_inc(k.sem("T_ready"), 1)
                    wait("local_in_psum", 2)
                    wait("gram_copied", 2)
                    for r in range(2):
                        nc.vector.tensor_tensor(local[:, r::2, :], pair(3 + 2 * r, 1),
                                                w["inclusive"].unsqueeze(1).broadcast_to([P, 2, P]), ALU.mult).then_inc(k.sem("local_ready"), 1)
                    yield
                    for s in range(1, LEVELS):
                        if s < LEVELS - 1:
                            wait("step_ready", s)
                            wait("T_ready", s)
                            nc.vector.tensor_tensor(T[:, :, :], T[:, :, :], heads(6, P), ALU.subtract).then_inc(k.sem("T_ready"), 1)
                        wait("stepT_ready", s)
                        wait("TT_ready", s)
                        nc.vector.tensor_tensor(TT[:, :, :], TT[:, :, :], heads(7, P), ALU.subtract).then_inc(k.sem("TT_ready"), 1)
                        yield
                    wait("u_in_psum", 1)
                    nc.vector.tensor_copy(u[:, :, :], heads(3, HD)).then_inc(k.sem("u_copied"), 1)
                    yield
                    wait("u_copied", 1)
                    wait("ws_in_psum", 1)
                    nc.vector.tensor_tensor(u[:, :, :], u[:, :, :], heads(5, HD), ALU.subtract).then_inc(k.sem("u_final"), 1)
                    yield
                    wait("delta_in_psum", 1)
                    nc.vector.tensor_copy(parts[:, 1, :, :], heads(6, HD)).then_inc(k.sem("delta_read"), 1)
                    yield

                def mix(j):
                    wait, before = waiter(dve, j)
                    yield
                    wait("delta_read", 1)
                    wait("conv_ready", 2)
                    link(nc.vector.tensor_reduce(F[:, :], parts[:, :, :, :].rearrange("p i h n -> p (i h) n"), AX_X, ALU.add,
                                                 apply_absolute_value=True))
                    nc.vector.tensor_scalar(F[:, :], F[:, :], 1.0 / HD, None, ALU.mult).then_inc(k.sem("means_ready"), 1)
                    yield
                    yield
                    yield
                    wait("logits_in_psum", 1)
                    link(nc.vector.tensor_tensor(lg[:, :, :].rearrange("p h n -> p (h n)"), B[:, 2, 0:12], w["f2b"], ALU.add))
                    link(nc.vector.reduce_max(gm[:, :], lg[:, :, :], AX_X))
                    nc.vector.tensor_tensor(lg[:, :, :], lg[:, :, :], gm[:, :].unsqueeze(2).broadcast_to([P, DH, 3]),
                                            ALU.subtract).then_inc(k.sem("shifted"), 1)
                    yield
                    wait("gate_exp", 1)
                    link(nc.vector.reduce_sum(gm[:, :], lg[:, :, :], AX_X))
                    link(nc.vector.reciprocal(gm[:, :], gm[:, :]))
                    link(nc.vector.tensor_tensor(lg[:, :, :], lg[:, :, :], gm[:, :].unsqueeze(2).broadcast_to([P, DH, 3]), ALU.mult))
                    link(nc.vector.tensor_tensor(o2[:, :, :, :], parts[:, :, :, :],
                                                 lg[:, :, :].rearrange("p h i -> p i h").unsqueeze(3).broadcast_to([P, 3, DH, HD]), ALU.mult))
                    yield
                    link(nc.vector.tensor_tensor(o[:, :, :], o2[:, 0, :, :], o2[:, 1, :, :], ALU.add))
                    link(nc.vector.tensor_tensor(o[:, :, :], o[:, :, :], o2[:, 2, :, :], ALU.add))
                    link(nc.vector.tensor_tensor(o2[:, 0, :, :], o[:, :, :], o[:, :, :], ALU.mult))
                    link(nc.vector.reduce_sum(gm[:, :], o2[:, 0, :, :], AX_X))
                    nc.vector.tensor_scalar(gm[:, :], gm[:, :], 1.0 / HD, 1e-5, ALU.mult, ALU.add).then_inc(k.sem("mean_square"), 1)
                    yield
                    wait("root", 1)
                    link(nc.vector.reciprocal(gm[:, :], gm[:, :]))
                    link(nc.vector.tensor_tensor(o[:, :, :], o[:, :, :], gm[:, :].unsqueeze(2).broadcast_to([P, DH, HD]), ALU.mult))
                    nc.vector.tensor_tensor(o[:, :, :], o[:, :, :], w["onorm"].unsqueeze(1).broadcast_to([P, DH, HD]),
                                            ALU.mult).then_inc(k.sem("out_ready"), 1)
                    yield
                    wait("branch_ready", 1)
                    dst = k.x[:, t * unroll + j, :]
                    nc.vector.tensor_tensor(dst, dst, B[:, 2, 0:D], ALU.add).then_inc(k.sem("added"), 1)
                    yield

                alternate(rule, mix, unroll)
        k.clear()


BUILDERS |= {7: layer7_attn}


def layout_delta(g, out):
    a = "L2_attn_"
    i = np.arange(P)
    same = i[:, None] // DCHUNK == i[None, :] // DCHUNK
    levels = []
    for s in range(LEVELS):
        r = 2 ** s
        levels.append((i[None, :] > i[:, None]) & (i[:, None] // (2 * r) == i[None, :] // (2 * r)) & (i[:, None] // r != i[None, :] // r))
    levels = np.stack(levels, 1).astype(np.float32)
    inclusive = ((i[None, :] >= i[:, None]) & same).astype(np.float32)
    seqs, second = i // SEQ, (i % SEQ) // DCHUNK
    ind = {n: np.stack([((seqs == b) & (second == s)) for b in range(PER_TILE)], 1).astype(np.float32) for n, s in (("first", 0), ("second", 1))}
    mix = np.zeros((6, P, P), np.float32)
    km = g[a + "kernel_mix_w"]
    for h in range(DH):
        for r0 in range(0, 192, 64):
            row = 192 * h + r0
            mix[row // P, row % P:row % P + 64, HD * (h % 2):HD * (h % 2) + HD] = km[r0:r0 + 64]

    def taps(n):
        wt = g[a + n]
        return wt.reshape(-1, P, wt.shape[1]).transpose(1, 0, 2)

    f1 = g[a + "fusion_w1"]
    out[7] = dict(wq=_mat(g[a + "Wq"]), wk=_mat(g[a + "Wk"]), wv=_mat(g[a + "Wv"]), wb=_mat(np.repeat(g[a + "Wb"], HD, axis=1)),
                  tq=taps("conv_q_w"), tk=taps("conv_k_w"), tv=taps("conv_v_w"), t3=taps("ms_w3"), t15=taps("ms_w15"), t31=taps("ms_w31"),
                  mix=mix.transpose(1, 0, 2), mixer=_mat(g[a + "channel_mixer_w"]), f1=_mat(f1[:D]), f1m=f1[D:], f1b=_col(g[a + "fusion_b1"]),
                  f2=_mat(g[a + "fusion_w2"]), f2b=_row(g[a + "fusion_b2"]), onorm=_row(g[a + "o_norm_w"]), wo=_mat(g[a + "Wo"]),
                  same64=(i[:, None] // HD == i[None, :] // HD).astype(np.float32), levels=levels, inclusive=inclusive, **ind)


def build(nc, dram, places, layers):
    with ExitStack() as ctx:
        k = Core(nc, ctx, dram)
        loaded = ctx.enter_context(nc.semaphore("weights_loaded"))
        first = ctx.enter_context(nc.semaphore("first_loads"))
        stored = ctx.enter_context(nc.semaphore("out_stored"))
        with nc.Block() as block:

            @block.sync
            def _(sp):
                sp.dma_start(k.x[:, :, :], dram["x"].rearrange("(t c) s d -> (c s) t d", c=PER_TILE)).then_inc(first, 16)
                sp.dma_start(k.ident[:, :], dram["ident"]).then_inc(first, 16)
                sp.dma_start(k.hmask16[:, :], dram["hmask16"]).then_inc(first, 16)
                sp.dma_start(k.hmask64[:, :], dram["hmask64"]).then_inc(first, 16)
                sp.dma_start(k.ctxT[:, :, :], dram["ctxT"].rearrange("(c p) n -> p c n", p=P)).then_inc(first, 16)
                n = dram[f"w{layers[0]}"].shape[1]
                sp.dma_start(k.weights[0][:, 0:n], dram[f"w{layers[0]}"]).then_inc(loaded, 16)
                sp.dma_start(k.fold[:, :], dram["fold"]).then_inc(first, 16)
                sp.wait_ge(first, 6 * 16)
        for i, layer in enumerate(layers):
            with nc.Block() as block:

                @block.sync
                def _(sp):
                    sp.wait_ge(loaded, 16 * (i + 1))
                    if i + 1 < len(layers):
                        n = dram[f"w{layers[i + 1]}"].shape[1]
                        sp.dma_start(k.weights[(i + 1) % 2][:, 0:n], dram[f"w{layers[i + 1]}"]).then_inc(loaded, 16)
            w = {}
            for name, (at, shape) in places[layer].items():
                size = int(np.prod(shape[1:]))
                v = k.weights[i % 2][0:shape[0], at:at + size]
                if len(shape) == 3:
                    v = v.rearrange("p (a b) -> p a b", a=shape[1])
                w[name] = v
            k.prefix = f"sub{layer}_"
            normalize(k)
            BUILDERS[layer](k, w)
        with nc.Block() as block:

            @block.sync
            def _(sp):
                sp.dma_start(dram["out"].rearrange("(t c) s d -> (c s) t d", c=PER_TILE), k.x[:, :, :]).then_inc(stored, 16)
                sp.wait_ge(stored, 16)


def _mat(w):
    w = np.asarray(w)
    return np.ascontiguousarray(w.reshape(-1, P, w.shape[1]).transpose(1, 0, 2)) if w.shape[0] >= P else w[:, None, :]


def _col(v):
    return np.ascontiguousarray(np.asarray(v).reshape(-1, P).T)


def _row(v):
    v = np.asarray(v).reshape(1, -1)
    return np.broadcast_to(v, (P, v.shape[1]))


def layout(inp):
    g = {n: np.asarray(v) for n, v in inp.items()}
    out = {}
    a = "L0_xattn_"
    out[0] = dict(wq=_mat(g[a + "wq_w"].T), wk=_mat(g[a + "wk_w"].T), wv=_mat(g[a + "wv_w"].T), wo=_mat(g[a + "wo_w"].T),
                  bq=_col(g[a + "wq_b"]), bk=_col(g[a + "wk_b"]), bv=_col(g[a + "wv_b"]), bo=_row(g[a + "wo_b"]))
    a = "L2_xattn_"
    out[6] = dict(wq=_mat(g[a + "Wq"]), wk=_mat(g[a + "Wk"]), wv=_mat(g[a + "Wv"]), wo=_mat(g[a + "Wo"]),
                  bq=_col(g[a + "bq"]), bk=_col(g[a + "bk"]), bv=_col(g[a + "bv"]), bo=_row(g[a + "bo"]))
    more_layout(g, out)
    return out


def more_layout(g, out):
    layout_attention(g, out)
    layout_blocks(g, out)
    layout_scans(g, out)
    layout_delta(g, out)


def kernel(**inputs):
    import concourse.bacc as bacc
    from concourse.bass_utils import run_bass_kernel_spmd

    arrays = {}
    arrays["x"] = np.ascontiguousarray(inputs["x"])
    arrays["ctxT"] = np.ascontiguousarray(np.asarray(inputs["ctx_1024"]).reshape(BATCH * CTX, D).T)
    arrays["ident"] = np.eye(P, dtype=np.float32)
    arrays["hmask16"] = (np.arange(P)[:, None] // 16 == np.arange(8)[None, :]).astype(np.float32)
    arrays["fold"] = (np.arange(P)[:, None] % SEQ == np.arange(SEQ)[None, :]).astype(np.float32)
    arrays["hmask64"] = (np.arange(P)[:, None] // 64 == np.arange(2)[None, :]).astype(np.float32)
    for name, src in (("mask_xattn", "mask_BxS2_bf1"), ("mask_last", "mask_BxS2_bk0")):
        m = np.asarray(inputs[src]).reshape(1, BATCH * CTX)
        arrays[name] = np.ascontiguousarray(np.broadcast_to(m, (P, BATCH * CTX)))
    places = {}
    for layer, pieces in layout(inputs).items():
        if layer not in LAYERS:
            continue
        at, place, flat = 0, {}, []
        for name, piece in pieces.items():
            rows = piece.shape[0]
            size = int(np.prod(piece.shape[1:]))
            block = np.zeros((P, size), piece.dtype)
            block[:rows] = piece.reshape(rows, size)
            flat.append(block)
            place[name] = (at, piece.shape)
            at += size
        assert at <= WMAX, (layer, at)
        arrays[f"w{layer}"] = np.ascontiguousarray(np.concatenate(flat, axis=1))
        places[layer] = place

    nc = bacc.Bacc("TRN2", target_bir_lowering=False, num_devices=1)
    dram = {name: nc.dram_tensor(f"in_{name}", a.shape, mybir.dt.from_np(a.dtype), kind="ExternalInput").ap()
            for name, a in arrays.items()}
    dram["out"] = nc.dram_tensor("out_x", (BATCH, SEQ, D), F32, kind="ExternalOutput").ap()
    build(nc, dram, places, LAYERS)
    r = run_bass_kernel_spmd(nc, [{f"in_{n}": a for n, a in arrays.items()}], core_ids=[0])
    return r.results[0]["out_x"]
```

```python
from contextlib import ExitStack
from itertools import zip_longest

import numpy as np
import concourse.bass as bass
from concourse import mybir

F32 = mybir.dt.float32
BF16 = mybir.dt.bfloat16
U8 = mybir.dt.uint8
ALU = mybir.AluOpType
ACT = mybir.ActivationFunctionType
AX_X = mybir.AxisListType.X

P = 128
BATCH, SEQ, D = 16, 64, 256
TOKENS = BATCH * SEQ
TILES = TOKENS // P
PER_TILE = P // SEQ
CTX = 256
CTX_TILE = PER_TILE * CTX
CHUNKS = D // P
BANK = 512
LN_EPS = 1e-5
NEG = float(np.finfo(np.float32).min)
WMAX = (7552, 8464)

LAYERS = [0, 1, 2, 3, 4, 5, 6, 7, 8, 9, 10, 11]


class Core:

    def __init__(self, nc, ctx, dram):
        self.nc, self.ctx, self.dram = nc, ctx, dram
        self.sems, self.used = {}, set()
        self.prefix = ""
        self.x = self.sb(ctx, "x_tok", [P, TILES, D])
        self.xn = self.sb(ctx, "xn_tok", [P, TILES, D])
        self.xnT = self.sb(ctx, "xn_feat", [P, CHUNKS, TOKENS])
        self.ctxT = self.sb(ctx, "ctx_feat", [P, CHUNKS, BATCH * CTX])
        self.ident = self.sb(ctx, "ident", [P, P])
        self.hmask16 = self.sb(ctx, "hmask16", [P, 8])
        self.fold = self.sb(ctx, "fold", [P, SEQ])
        self.hmask64 = self.sb(ctx, "hmask64", [P, 2])
        self.stats = self.sb(ctx, "ln_stats", [P, TILES, 6])
        self.meanvar = self.sb(ctx, "ln_meanvar", [P, TILES, 2])
        self.rstd = self.sb(ctx, "ln_rstd", [P, TILES])
        self.weights = [self.sb(ctx, f"weights{i}", [P, WMAX[i]]) for i in range(2)]
        self.banks = ctx.enter_context(nc.psum_tensor("banks", [P, 8, BANK], F32))

    def sb(self, ctx, name, shape, dt=F32):
        return ctx.enter_context(self.nc.sbuf_tensor(f"{self.prefix}{name}", shape, dt))

    def sem(self, name):
        if name not in self.sems:
            self.sems[name] = self.ctx.enter_context(self.nc.semaphore(name))
        self.used.add(name)
        return self.sems[name]

    def clear(self):
        names = sorted(self.used)
        self.used = set()
        with self.nc.Block() as block:

            @block.sync
            def _(sp):
                for name in names:
                    sp.sem_clear(self.sems[name])


def linker(eng, sem, start=0):
    count = [start]

    def link(ins):
        count[0] += 1
        ins.then_inc(sem, 1)
        eng.wait_ge(sem, count[0])

    return link


def normalize(k, src=None, turn=True, scale=None, shift=None):
    src = k.x if src is None else src
    nc = k.nc
    with nc.Block() as block:

        @block.vector
        def _(dve):
            link = linker(dve, k.sem("dve_step"))
            for h in range(2):
                half = slice(4 * h, 4 * h + 4)
                for t in range(4 * h, 4 * h + 4):
                    last = nc.vector.bn_stats(k.stats[:, t, :], src[:, t, :])
                link(last)
                for t in range(4 * h, 4 * h + 4):
                    last = nc.vector.bn_aggr(k.meanvar[:, t, :], k.stats[:, t, :])
                link(last)
                nc.vector.tensor_scalar(k.rstd[:, half], k.meanvar[:, half, 1], LN_EPS, None, ALU.add).then_inc(k.sem("var_ready"), 1)
            for h in range(2):
                half = slice(4 * h, 4 * h + 4)
                dve.wait_ge(k.sem("std_ready"), h + 1)
                link(nc.vector.reciprocal(k.rstd[:, half], k.rstd[:, half]))
                for t in range(4 * h, 4 * h + 4):
                    nc.vector.tensor_scalar(k.xn[:, t, :], src[:, t, :], k.meanvar[:, t, 0:1], k.rstd[:, t:t + 1],
                                            ALU.subtract, ALU.mult).then_inc(k.sem("xn_ready"), 1)

        @block.scalar
        def _(act):
            for h in range(2):
                act.wait_ge(k.sem("var_ready"), h + 1)
                half = slice(4 * h, 4 * h + 4)
                nc.scalar.activation(k.rstd[:, half], k.rstd[:, half], ACT.Sqrt).then_inc(k.sem("std_ready"), 1)
            for h in range(TILES // 4 if turn else 0):
                for c in range(CHUNKS):
                    act.wait_ge(k.sem("xnT_in_psum"), CHUNKS * h + c + 1)
                    out, raw = k.xnT[:, c, h * BANK:(h + 1) * BANK], k.banks[:, CHUNKS * h + c, :]
                    if scale is None:
                        nc.scalar.copy(out, raw)
                    else:
                        nc.scalar.activation(out, raw, ACT.Identity, bias=shift[:, c:c + 1], scale=scale[:, c:c + 1])

        @block.tensor
        def _(pe):
            for h in range(TILES // 4 if turn else 0):
                for t in range(4):
                    pe.wait_ge(k.sem("xn_ready"), 4 * h + t + 1)
                    for c in range(CHUNKS):
                        last = nc.tensor.transpose(k.banks[:, CHUNKS * h + c, t * P:(t + 1) * P],
                                                   k.xn[:, 4 * h + t, c * P:(c + 1) * P], k.ident[:, :])
                        if t == 3:
                            last.then_inc(k.sem("xnT_in_psum"), 1)
    k.clear()


def project(k, jobs, src=None, chunks=CHUNKS, tokens=TOKENS, then=None):
    nc = k.nc
    src = k.xnT if src is None else src
    halves = [(j, h) for j in range(len(jobs)) for h in range(tokens // BANK)]
    with nc.Block() as block:

        @block.tensor
        def _(pe):
            for n, (j, h) in enumerate(halves):
                w, col, out, _, _ = jobs[j]
                m = out.shape[0]
                if n >= 4:
                    pe.wait_ge(k.sem("product_used"), n - 3)
                for c in range(chunks):
                    last = nc.tensor.matmul(k.banks[0:m, n % 4, :], w[:, c, col:col + m], src[:, c, h * BANK:(h + 1) * BANK],
                                            start=(c == 0), stop=(c == chunks - 1))
                last.then_inc(k.sem("product_ready"), 1)

        @block.scalar
        def _(act):
            for n, (j, h) in enumerate(halves):
                _, _, out, bias, func = jobs[j]
                m = out.shape[0]
                act.wait_ge(k.sem("product_ready"), n + 1)
                nc.scalar.activation(out[:, h * BANK:(h + 1) * BANK], k.banks[0:m, n % 4, :], func,
                                     bias=0.0 if bias is None else bias).then_inc(k.sem("product_used"), 1)

        if then:
            @block.vector
            def _(dve):
                for n, (j, h) in enumerate(halves):
                    dve.wait_ge(k.sem("product_used"), n + 1)
                    then(jobs[j][2][:, h * BANK:(h + 1) * BANK])
    k.clear()


def softplus(k, parts):
    nc = k.nc
    with nc.Block() as block:

        @block.scalar
        def _(act):
            for x, e, low in parts:
                nc.scalar.activation(e, x, ACT.Abs).then_inc(k.sem("abs_ready"), 1)
            for n, (x, e, low) in enumerate(parts):
                act.wait_ge(k.sem("abs_ready"), n + 1)
                nc.scalar.activation(e, e, ACT.Exp, scale=-1.0).then_inc(k.sem("exp_ready"), 1)
            for n, (x, e, low) in enumerate(parts):
                act.wait_ge(k.sem("low_ready"), n + 1)
                nc.scalar.activation(e, e, ACT.Ln, bias=1.0).then_inc(k.sem("log_ready"), 1)

        @block.gpsimd
        def _(pool):
            for n, (x, e, low) in enumerate(parts):
                pool.wait_ge(k.sem("rounded_ready"), n + 1)
                nc.gpsimd.tensor_tensor(low, e, low, ALU.subtract).then_inc(k.sem("low_ready"), 1)

        @block.vector
        def _(dve):
            for n, (x, e, low) in enumerate(parts):
                dve.wait_ge(k.sem("exp_ready"), n + 1)
                nc.vector.tensor_scalar(low, e, 1.0, 1.0, ALU.add, ALU.subtract).then_inc(k.sem("rounded_ready"), 1)
            for n, (x, e, low) in enumerate(parts):
                dve.wait_ge(k.sem("log_ready"), n + 1)
                nc.vector.tensor_tensor(low, low, e, ALU.add).then_inc(k.sem("log1p_ready"), 1)
                dve.wait_ge(k.sem("log1p_ready"), n + 1)
                nc.vector.scalar_tensor_tensor(x, x, 0.0, low, ALU.max, ALU.add)
    k.clear()




class Attention:

    SLOTS = 4

    def __init__(self, k, ctx, keys, qchunks, kchunks, vfeat, head, pairs, scale, unroll, jobs, copied=False, topk=False, gated=False,
                 split=False):
        self.keys, self.qchunks, self.kchunks, self.head, self.scale = keys, qchunks, kchunks, head, scale
        self.vfeat, self.copied, self.topk, self.unroll, self.split = vfeat, copied, topk, unroll, split
        self.per_seq = len(pairs)
        self.per_tile = PER_TILE * self.per_seq
        self.seqs = 1 if split else PER_TILE
        self.per_unit = self.seqs * self.per_seq
        self.units = unroll * PER_TILE // self.seqs
        self.groups = [(j, b, (j * PER_TILE + b) // self.seqs, b % self.seqs, g)
                       for j in range(unroll) for b in range(PER_TILE) for g in pairs]
        self.kparts = (keys + P - 1) // P
        self.krows = min(keys, P)
        self.rows = 2 * head
        self.exp_lag = 1 if topk else 0
        self.turn_lag, self.out_lag, self.fold_lag = (3, 4, 5) if topk else (2, 3, 4)
        n = len(self.groups)
        self.first = [(kind, 0, i, h) for kind, i, h in jobs if kind != "v"]
        self.at = [[] for _ in range(n + self.fold_lag + 3)]
        early = [job for job in jobs if job[0] != "v"]
        late = [job for job in jobs if job[0] == "v"]
        for m, (kind, i, h) in enumerate(late):
            self.at[1 + m * 2 // len(late)].append((kind, 0, i, h))
        for u in range(1, self.units):
            for m, (kind, i, h) in enumerate(early):
                if kind != "q" or not split:
                    self.at[self.per_unit * (u - 1) + m * self.per_unit // len(early)].append((kind, u, i, h))
                elif u % PER_TILE == 0:
                    self.at[self.per_unit * (u - 1) - 1].append((kind, u // PER_TILE, i, h))
            for m, (kind, i, h) in enumerate(late):
                self.at[self.per_unit * (u - 1) + self.out_lag + m * self.per_unit // len(late)].append((kind, u, i, h))
        for j in range(unroll):
            folded = self.per_tile * (j + 1) + self.fold_lag
            if gated:
                self.at[folded].append(("g", j, 0, 0))
            self.at[folded + gated].append(("o", j, 0, 0))
        self.order = self.first + [job for step in self.at for job in step]
        self.steps = len(self.at)
        self.place = {job: (s, i, m) for s in range(self.steps) for i in range(self.SLOTS) for m, job in enumerate(self.slot(s, i))}
        self.nk = sum(kind == "k" for kind, _, _ in jobs)
        self.nv = sum(kind == "v" for kind, _, _ in jobs)
        bufs = min(2, self.units)
        self.q_heads = k.sb(ctx, "q_heads", [P, bufs, qchunks, self.seqs, P // head * SEQ])
        self.kT = k.sb(ctx, "kT", [P, bufs, kchunks, self.seqs * keys]) if kchunks else None
        self.v = k.sb(ctx, "v", [P, bufs, self.seqs * self.kparts, vfeat])
        self.moving = k.sb(ctx, "unit_rows", [P, bufs, CHUNKS, self.seqs * keys])
        self.probs = k.sb(ctx, "probs", [P, 2, 4, keys])
        self.probsT = k.sb(ctx, "probsT", [P, 2, self.kparts, BANK])
        self.own = k.sb(ctx, "own_out", [P, 2, 4 * self.rows])
        self.factor = k.sb(ctx, "own_factor", [P, n, 4, 2])
        self.oT = k.sb(ctx, "oT", [P, min(2, unroll), qchunks, P])
        self.rowmax = k.sb(ctx, "rowmax", [P, n, 4])
        self.rowsum = k.sb(ctx, "rowsum", [P, n, 4])
        self.sum = k.sb(ctx, "branch", [P, D])
        self.keys_of = None
        self.oT_scale = self.oT_bias = None

    def score(self, k, g):
        flat = k.banks[:, 2 * (g % 2):2 * (g % 2) + 2, :].rearrange("p b n -> p (b n)")
        return flat[:, 0:4 * self.keys].rearrange("p (i n) -> p i n", i=4)

    def turned(self, k):
        return k.banks[:, 4:4 + self.kparts, :]

    def products(self, k, g):
        return k.banks[:, 6, 0:len(self.groups[g][4]) * self.rows]

    def folded(self, k, g):
        return k.banks[:, 6, 0:len(self.groups[g][4]) * self.rows // P * SEQ]

    def bank_of(self, n):
        if n < len(self.first):
            return 7 if n % 4 == 0 else n % 4
        s, i, m = self.place[self.order[n]]
        return 5 if i == 0 and m == 0 else 4 if i == 3 and m == 1 else 7

    def bank(self, k, kind, j, i, h):
        return k.banks[:, self.bank_of(self.order.index((kind, j, i, h))), :]

    def wait_job(self, k, eng, kind, j, i, h):
        eng.wait_ge(k.sem("job_ready"), self.order.index((kind, j, i, h)) + 1)

    def wait_read(self, k, eng, n):
        kind = self.order[n][0]
        count = sum(1 for job in self.order[:n + 1] if job[0] == kind)
        eng.wait_ge(k.sem({"q": "queries_ready", "k": "keys_ready", "v": "values_ready", "g": "gates_read", "o": "branch_read"}[kind]), count)

    def wait_bank(self, k, eng, kind, j, i, h):
        n = self.order.index((kind, j, i, h))
        before = [m for m in range(n) if self.bank_of(m) == self.bank_of(n)]
        if before:
            self.wait_read(k, eng, before[-1])
        if n >= len(self.first) and self.bank_of(n) != 7:
            s, i, _ = self.place[self.order[n]]
            turned = min(s - self.turn_lag + (i > 1), len(self.groups))
            if turned > 0:
                eng.wait_ge(k.sem("probsT_ready"), turned)

    def wait_turned_banks(self, k, eng, s):
        for bank in (4, 5):
            before = [n for n in range(len(self.first), len(self.order))
                      if self.bank_of(n) == bank and self.place[self.order[n]][0:2] <= (s, 1)]
            if before:
                self.wait_read(k, eng, before[-1])

    def slot(self, s, i):
        jobs = self.at[s]
        if self.split:
            return jobs[-(-len(jobs) * i // self.SLOTS):-(-len(jobs) * (i + 1) // self.SLOTS)]
        return jobs[len(jobs) * i // self.SLOTS:len(jobs) * (i + 1) // self.SLOTS]

    def wait_unit(self, k, eng, sem, u):
        if u >= 2:
            eng.wait_ge(k.sem(sem), self.per_unit * (u - 1))


def attend_pe(k, a, pe, job):
    nc, n = k.nc, len(a.groups)

    def run(jobs):
        for one in jobs:
            a.wait_bank(k, pe, *one)
            job(pe, *one).then_inc(k.sem("job_ready"), 1)

    run(a.first)
    for s in range(a.steps):
        run(a.slot(s, 0))
        g = s - a.fold_lag
        if 0 <= g < n:
            pe.wait_ge(k.sem("own_ready"), g + 1)
            w = len(a.groups[g][4]) * a.rows // P
            for c in range(w):
                last = nc.tensor.matmul(a.folded(k, g)[:, c * SEQ:(c + 1) * SEQ], a.own[:, g % 2, c * P:(c + 1) * P], k.fold[:, :],
                                        start=True, stop=True)
            last.then_inc(k.sem("folded_ready"), 1)
        run(a.slot(s, 1))
        g = s - a.turn_lag
        if 0 <= g < n:
            pairs = a.groups[g][4]
            pe.wait_ge(k.sem("picked_ready" if a.topk else "exp_ready"), g + 1)
            if g >= 1:
                pe.wait_ge(k.sem("probsT_ready"), g)
            a.wait_turned_banks(k, pe, s)
            for part in range(a.kparts):
                for i in range(len(pairs)):
                    last = nc.tensor.transpose(a.turned(k)[0:a.krows, part, i * P:(i + 1) * P],
                                               a.probs[:, g % 2, i, part * P:part * P + a.krows], k.ident[:, :])
            last.then_inc(k.sem("probs_turned"), 1)
        run(a.slot(s, 2))
        if s < n:
            j, b, u, ub, pairs = a.groups[s]
            if s < 2:
                for m in range(max(0, len(a.first) - 4), len(a.first)):
                    if a.bank_of(m) // 2 == s:
                        a.wait_read(k, pe, m)
            pe.wait_ge(k.sem("q_heads_ready"), (u * a.seqs + ub) * a.qchunks + max(pair[0] for pair in pairs) + 1)
            if a.nk:
                pe.wait_ge(k.sem("keys_ready"), u * a.nk + max(pair[1] for pair in pairs) * a.nk // a.kchunks + 1)
            if s >= 2:
                pe.wait_ge(k.sem("scores_copied" if a.copied else "exp_ready"), s - 1)
            for i, (qc, kc, vc, row) in enumerate(pairs):
                head = row // a.head
                keys = a.keys_of(j, kc, b) if a.keys_of else a.kT[:, u % 2, kc, ub * a.keys:(ub + 1) * a.keys]
                last = nc.tensor.matmul(a.score(k, s)[:, i, :], a.q_heads[:, u % 2, qc, ub, head * SEQ:(head + 2) * SEQ], keys,
                                        start=True, stop=True)
            last.then_inc(k.sem("scores_ready"), 1)
        run(a.slot(s, 3))
        g = s - a.out_lag
        if 0 <= g < n:
            j, b, u, ub, pairs = a.groups[g]
            if g % a.per_unit == 0:
                pe.wait_ge(k.sem("values_ready"), (u + 1) * a.nv)
            pe.wait_ge(k.sem("probsT_ready"), g + 1)
            if g >= 1:
                pe.wait_ge(k.sem("oT_chunks"), g)
            for i, (_, _, vc, row) in enumerate(pairs):
                for part in range(a.kparts):
                    last = nc.tensor.matmul(a.products(k, g)[:, i * a.rows:(i + 1) * a.rows],
                                            a.probsT[0:a.krows, g % 2, part, i * P:(i + 1) * P],
                                            a.v[0:a.krows, u % 2, ub * a.kparts + part, vc * P + row:vc * P + row + a.rows],
                                            start=(part == 0), stop=(part == a.kparts - 1))
            last.then_inc(k.sem("out_ready"), 1)


def attend_act(k, a, act, job):
    nc, n = k.nc, len(a.groups)

    def run(jobs):
        for one in jobs:
            job(act, *one)

    run(a.first)
    for s in range(a.steps):
        run(a.slot(s, 0))
        g = s - a.fold_lag
        if 0 <= g < n:
            j, b, _, _, pairs = a.groups[g]
            act.wait_ge(k.sem("folded_ready"), g + 1)
            if j >= 2 and g % a.per_tile == 0:
                act.wait_ge(k.sem("branch_read"), j - 1)
            w, c0 = len(pairs) * a.rows // P, pairs[0][0]
            out, src = a.oT[:, j % 2, c0:c0 + w, b * SEQ:(b + 1) * SEQ], a.folded(k, g).rearrange("p (c q) -> p c q", q=SEQ)
            if a.oT_scale is None and a.oT_bias is None:
                nc.scalar.copy(out, src).then_inc(k.sem("oT_chunks"), 1)
            else:
                nc.scalar.activation(out, src, ACT.Identity, scale=1.0 if a.oT_scale is None else a.oT_scale[:, c0:c0 + 1],
                                     bias=0.0 if a.oT_bias is None else a.oT_bias[:, c0:c0 + 1]).then_inc(k.sem("oT_chunks"), 1)
        run(a.slot(s, 1))
        g = s - a.turn_lag
        if 0 <= g < n:
            act.wait_ge(k.sem("probs_turned"), g + 1)
            if g >= 2:
                act.wait_ge(k.sem("out_ready"), g - 1)
            w = len(a.groups[g][4]) * P
            nc.scalar.copy(a.probsT[0:a.krows, g % 2, :, 0:w], a.turned(k)[0:a.krows, :, 0:w]).then_inc(k.sem("probsT_ready"), 1)
        run(a.slot(s, 2))
        if a.topk and s < n:
            act.wait_ge(k.sem("scores_ready"), s + 1)
            if s >= 2:
                act.wait_ge(k.sem("outside_ready"), s - 1)
            nc.scalar.copy(a.masked[:, s % 2, :, :], a.score(k, s)).then_inc(k.sem("scores_copied"), 1)
        g = s - a.exp_lag
        if 0 <= g < n:
            act.wait_ge(k.sem("rowmax_ready"), g + 1)
            if g >= 2:
                act.wait_ge(k.sem("probs_turned"), g - 1)
            for i in range(len(a.groups[g][4])):
                src = a.masked[:, g % 2, i, :] if a.topk else a.probs[:, g % 2, i, :] if a.copied else a.score(k, g)[:, i, :]
                last = nc.scalar.activation(a.probs[:, g % 2, i, :], src, ACT.Exp, bias=a.rowmax[:, g, i:i + 1], scale=a.scale,
                                            accum_out=None if a.topk else a.rowsum[:, g, i:i + 1])
            last.then_inc(k.sem("exp_ready"), 1)
        run(a.slot(s, 3))


def attend_dve(k, a, dve, link, job, mask=None):
    nc, n = k.nc, len(a.groups)

    def run(jobs):
        for one in jobs:
            job(dve, *one)

    run(a.first)
    for s in range(a.steps):
        for i in range(3):
            run(a.slot(s, i))
        g = s - a.exp_lag
        if 0 <= g < n:
            j, b, _, _, pairs = a.groups[g]
            w = len(pairs)
            if a.topk:
                mask(dve, g)
            else:
                dve.wait_ge(k.sem("scores_ready"), g + 1)
                if mask is not None:
                    if g >= 2:
                        dve.wait_ge(k.sem("probs_turned"), g - 1)
                    mask(dve, g, j, b, w)
                else:
                    link(nc.vector.reduce_max(a.rowmax[:, g, 0:w], a.score(k, g)[:, 0:w, :], AX_X))
                nc.vector.tensor_scalar(a.rowmax[:, g, 0:w], a.rowmax[:, g, 0:w], -a.scale, None,
                                        ALU.mult).then_inc(k.sem("rowmax_ready"), 1)
        g = s - 2
        if a.topk and 0 <= g < n:
            mask.pick(dve, g)
        run(a.slot(s, 3))
        g = s - a.out_lag
        if 0 <= g < n:
            w = len(a.groups[g][4])
            dve.wait_ge(k.sem("picked_ready" if a.topk else "exp_ready"), g + 1)
            link(nc.vector.reciprocal(a.rowsum[:, g, 0:w], a.rowsum[:, g, 0:w]))
            link(nc.vector.tensor_tensor(a.factor[:, g, 0:w, :], a.rowsum[:, g, 0:w].unsqueeze(2).broadcast_to([P, w, 2]),
                                         k.hmask64[:, :].unsqueeze(1).broadcast_to([P, w, 2]), ALU.mult))
            dve.wait_ge(k.sem("out_ready"), g + 1)
            if g >= 2:
                dve.wait_ge(k.sem("folded_ready"), g - 1)
            nc.vector.tensor_tensor(a.own[:, g % 2, 0:w * a.rows].rearrange("p (i h d) -> p i h d", i=w, h=2),
                                    a.products(k, g).rearrange("p (i h d) -> p i h d", i=w, h=2),
                                    a.factor[:, g, 0:w, :].unsqueeze(3).broadcast_to([P, w, 2, a.head]),
                                    ALU.mult).then_inc(k.sem("own_ready"), 1)


def mask_queries(k, a, pool, u, q_of):
    nc = k.nc
    m = k.hmask16 if a.head == 16 else k.hmask64
    n = P // a.head
    a.wait_unit(k, pool, "scores_ready", u)
    for b in range(a.seqs):
        for c in range(a.qchunks):
            nc.gpsimd.tensor_tensor(a.q_heads[:, u % 2, c, b, :].rearrange("p (h q) -> p h q", q=SEQ),
                                    q_of(c, b).unsqueeze(1).broadcast_to([P, n, SEQ]),
                                    m[:, :].unsqueeze(2).broadcast_to([P, n, SEQ]), ALU.mult).then_inc(k.sem("q_heads_ready"), 1)


def copy_rows(k, a, pool, u, src):
    if u >= 2:
        a.wait_job(k, pool, *[job for job in a.order if job[0] == "v" and job[1] == u - 2][-1])
    k.nc.gpsimd.tensor_copy(a.moving[:, u % 2, :, :], src).then_inc(k.sem("rows_copied"), 1)


def context_jobs(kchunks, vfeat, seqs=PER_TILE, queries=0):
    per = BANK // (seqs * CTX)
    jobs = [("q", c, 0) for c in range(0, queries, 4)] + [("k", c, 0) for c in range(0, kchunks, per)]
    rows = seqs * CTX // P
    if vfeat >= BANK:
        return jobs + [("v", j, n) for j in range(rows) for n in range(vfeat // BANK)]
    return jobs + [("v", j, 0) for j in range(0, rows, BANK // vfeat)]


def projections(k, a, w, t, ctx_keys, x_moving=None, gates=None):
    nc = k.nc

    def job(pe, kind, j, i, h):
        bank = a.bank(k, kind, j, i, h)
        if kind == "q":
            for m in range(4):
                for c in range(CHUNKS):
                    last = nc.tensor.matmul(bank[:, m * P:(m + 1) * P], w["wq"][:, c, (i + m) * P:(i + m + 1) * P], x_moving(j, c),
                                            start=(c == 0), stop=(c == CHUNKS - 1))
        elif kind == "k":
            n = a.seqs * CTX
            for m in range(BANK // n):
                for c in range(CHUNKS):
                    last = nc.tensor.matmul(bank[:, m * n:(m + 1) * n], w["wk"][:, c, (i + m) * P:(i + m + 1) * P], ctx_keys(j, c),
                                            start=(c == 0), stop=(c == CHUNKS - 1))
        elif kind == "v":
            pe.wait_ge(k.sem("rows_copied"), j + 1)
            if a.keys == CTX:
                width = min(a.vfeat, BANK)
                for m in range(BANK // width):
                    for c in range(CHUNKS):
                        last = nc.tensor.matmul(bank[:, m * width:(m + 1) * width], a.moving[:, j % 2, c, (i + m) * P:(i + m + 1) * P],
                                                w["wv"][:, c, h * BANK:h * BANK + width], start=(c == 0), stop=(c == CHUNKS - 1))
            else:
                for b in range(PER_TILE):
                    for c in range(CHUNKS):
                        last = nc.tensor.matmul(bank[0:SEQ, b * D:(b + 1) * D], a.moving[:, j % 2, c, b * SEQ:(b + 1) * SEQ],
                                                w["wv"][:, c, :], start=(c == 0), stop=(c == CHUNKS - 1))
        elif kind == "g":
            pe.wait_ge(k.sem("oT_chunks"), a.per_tile * (j + 1))
            for c in range(CHUNKS):
                last = nc.tensor.matmul(bank[:, 0:17], a.oT[:, j % 2, c, :], w["wgate"][:, c, :], start=(c == 0), stop=(c == CHUNKS - 1))
        else:
            pe.wait_ge(k.sem("oT_chunks"), a.per_tile * (j + 1))
            for c in range(a.qchunks):
                last = nc.tensor.matmul(bank[:, 0:D], a.oT[:, j % 2, c, :], w["wo"][:, c, :], start=(c == 0), stop=(c == a.qchunks - 1))
        return last

    return job


def values_out(k, a, eng, copy, j, i, h):
    a.wait_job(k, eng, "v", j, i, h)
    a.wait_unit(k, eng, "out_ready", j)
    if a.keys == CTX:
        width = min(a.vfeat, BANK)
        rows, out = P, a.v[:, j % 2, i:i + BANK // width, h * BANK:h * BANK + width]
    else:
        width, rows = D, SEQ
        out = a.v[0:SEQ, j % 2, :, :]
    copy(out, a.bank(k, "v", j, i, h)[0:rows, :].rearrange("p (i w) -> p i w", w=width)).then_inc(k.sem("values_ready"), 1)


def act_jobs(k, a, bk, gate=None, values=False):
    nc = k.nc

    def job(act, kind, j, i, h):
        if kind == "q":
            a.wait_job(k, act, kind, j, i, h)
            if j >= 1:
                act.wait_ge(k.sem("q_heads_ready"), j * PER_TILE * a.qchunks)
            nc.scalar.copy(a.q_tile[:, i:i + 4, :], a.bank(k, kind, j, i, h).rearrange("p (i n) -> p i n", i=4)).then_inc(k.sem("queries_ready"), 1)
        elif kind == "k":
            a.wait_job(k, act, kind, j, i, h)
            a.wait_unit(k, act, "scores_ready", j)
            n = a.seqs * CTX
            nc.scalar.activation(a.kT[:, j % 2, i:i + BANK // n, :], a.bank(k, kind, j, i, h).rearrange("p (i n) -> p i n", n=n), ACT.Identity,
                                 bias=0.0 if bk is None else bk[:, i:i + 1]).then_inc(k.sem("keys_ready"), 1)
        elif kind == "v" and values:
            values_out(k, a, act, nc.scalar.copy, j, i, h)
        elif kind == "g":
            gate(act, j)

    return job


def dve_jobs(k, a, link, t, bo=None, factor=None, gate=None, factor_of=None, values=True):
    nc = k.nc

    def job(dve, kind, j, i, h):
        if kind == "v" and values:
            values_out(k, a, dve, nc.vector.tensor_copy, j, i, h)
        elif kind == "g":
            gate(dve, j)
        elif kind == "o":
            if factor_of:
                factor_of(dve, j)
            a.wait_job(k, dve, kind, j, i, h)
            dst = k.x[:, t * a.unroll + j, :]
            src = a.bank(k, kind, j, i, h)[:, 0:D]
            if bo is not None:
                nc.vector.tensor_tensor(a.sum[:, :], src, bo, ALU.add).then_inc(k.sem("branch_read"), 1)
                dve.wait_ge(k.sem("branch_read"), j + 1)
                src = a.sum[:, :]
            if factor is not None:
                last = nc.vector.scalar_tensor_tensor(dst, src, factor, dst, ALU.mult, ALU.add)
            else:
                last = nc.vector.tensor_tensor(dst, src, dst, ALU.add)
            if bo is None:
                last.then_inc(k.sem("branch_read"), 1)

    return job


def pairs16():
    return [[(fc, fc, fc, 32 * j) for j in range(4)] for fc in range(CHUNKS)]


def pairs64(qchunks, shared):
    n = min(4, qchunks)
    return [[(c, 0 if shared else c, 0 if shared else c, 0) for c in range(g, g + n)] for g in range(0, qchunks, n)]


def load_mask(k, mask8, name):
    with k.nc.Block() as block:

        @block.sync
        def _(sp):
            sp.dma_start(mask8[:, :], k.dram[name]).then_inc(k.sem("mask_loaded"), 16)
            sp.wait_ge(k.sem("mask_loaded"), 16)
    k.clear()


def context_attention(k, w, topk):
    nc = k.nc
    unroll = 4
    with ExitStack() as ctx:
        a = Attention(k, ctx, CTX, CHUNKS, CHUNKS, D, 16, pairs16(), 0.25, unroll, context_jobs(CHUNKS, D), copied=topk, topk=topk)
        a.oT_bias = w["bv"]
        qT = k.xn[:, :, :].rearrange("p t d -> p (t d)").rearrange("p (c n) -> p c n", c=CHUNKS)
        if topk:
            low = k.sb(ctx, "key_low", [P, PER_TILE, CTX])
            mask8 = k.sb(ctx, "key_mask", [P, BATCH * CTX], U8)
            work = k.sb(ctx, "topk_work", [P, 2, 4, CTX])
            best = k.sb(ctx, "topk_best", [P, 4, 8])
            allout = k.sb(ctx, "all_masked", [P, 2, 4])
            a.masked = k.sb(ctx, "masked_scores", [P, 2, 4, CTX])
            load_mask(k, mask8, "mask_xattn")
        project(k, [(w["wq"], c * P, qT[:, c, :], w["bq"][:, c:c + 1], ACT.Identity) for c in range(CHUNKS)])
        with nc.Fori(0, TILES // unroll) as t:

            def ctx_cols(j):
                return bass.ds((t * unroll + j) * CTX_TILE, CTX_TILE)

            def best_keys(dve, g):
                sc = a.masked[:, g % 2]
                dve.wait_ge(k.sem("masked_ready"), g + 1)
                if g >= 2:
                    dve.wait_ge(k.sem("picked_ready"), g - 1)

                def step(ins):
                    best_keys.done += 1
                    ins.then_inc(k.sem("topk_step"), 1)

                def settled(back):
                    dve.wait_ge(k.sem("topk_step"), best_keys.done - back)

                for r in range(8):
                    src = work[:, g % 2] if r else sc
                    for i in range(4):
                        if g or r:
                            settled(3)
                        step(nc.vector.max(best[:, i, :], src[:, i, :]))
                    if r == 0:
                        settled(0)
                        nc.vector.tensor_scalar(allout[:, g % 2, :], best[:, :, 0], NEG, -1.0, ALU.is_equal, ALU.mult)
                        nc.vector.tensor_scalar(a.rowmax[:, g, :], best[:, :, 0], -a.scale, None, ALU.mult).then_inc(k.sem("rowmax_ready"), 1)
                    for i in range(4):
                        settled(3)
                        step(nc.vector.match_replace(work[:, g % 2, i, :], best[:, i, :], src[:, i, :], NEG))

            def pick(dve, g):
                dve.wait_ge(k.sem("outside_ready"), g + 1)
                dve.wait_ge(k.sem("exp_ready"), g + 1)
                for i in range(4):
                    last = nc.vector.scalar_tensor_tensor(a.probs[:, g % 2, i, :], work[:, g % 2, i, :], allout[:, g % 2, i:i + 1],
                                                          a.probs[:, g % 2, i, :], ALU.is_gt, ALU.mult, accum_out=a.rowsum[:, g, i:i + 1])
                last.then_inc(k.sem("picked_ready"), 1)

            best_keys.pick = pick

            with nc.Block() as block:

                @block.gpsimd
                def _(pool):
                    def rows(j):
                        copy_rows(k, a, pool, j, k.ctxT[:, :, ctx_cols(j)])

                    def tile(j):
                        mask_queries(k, a, pool, j, lambda c, b: qT[:, c, bass.ds((t * unroll + j) * P + b * SEQ, SEQ)])
                    if not topk:
                        for j in range(unroll):
                            tile(j)
                            rows(j)
                        return
                    tile(0)
                    for s in range(len(a.groups) + 1):
                        if s < len(a.groups):
                            j, b = a.groups[s][0:2]
                            if s % CHUNKS == 0:
                                seq = s // CHUNKS
                                nc.gpsimd.tensor_copy(low[:, b, :], mask8[:, bass.ds((t * unroll * PER_TILE + seq) * CTX, CTX)]
                                                      ).then_inc(k.sem("low_step"), 1)
                                pool.wait_ge(k.sem("low_step"), 2 * seq + 1)
                                nc.gpsimd.tensor_scalar(low[:, b, :], low[:, b, :], -NEG, NEG, ALU.mult, ALU.add).then_inc(k.sem("low_step"), 1)
                                pool.wait_ge(k.sem("low_step"), 2 * seq + 2)
                            sc = a.masked[:, s % 2, :, :]
                            pool.wait_ge(k.sem("scores_copied"), s + 1)
                            nc.gpsimd.tensor_tensor(sc, sc, low[:, b, :].unsqueeze(1).broadcast_to([P, 4, CTX]),
                                                    ALU.add).then_inc(k.sem("masked_ready"), 1)
                            if s == 0:
                                rows(0)
                            if s % a.per_tile == 1 and j + 1 < unroll:
                                rows(j + 1)
                                tile(j + 1)
                        if s >= 1:
                            g = s - 1
                            pool.wait_ge(k.sem("topk_step"), 64 * (g + 1))
                            pool.wait_ge(k.sem("exp_ready"), g + 1)
                            nc.gpsimd.tensor_tensor(work[:, g % 2], a.masked[:, g % 2], work[:, g % 2],
                                                    ALU.subtract).then_inc(k.sem("outside_ready"), 1)

                @block.tensor
                def _(pe):
                    attend_pe(k, a, pe, projections(k, a, w, t, lambda j, c: k.ctxT[:, c, ctx_cols(j)]))

                @block.scalar
                def _(act):
                    attend_act(k, a, act, act_jobs(k, a, w["bk"], values=topk))

                @block.vector
                def _(dve):
                    link = linker(dve, k.sem("dve_step"))
                    best_keys.done = 0
                    attend_dve(k, a, dve, link, dve_jobs(k, a, link, t, w["bo"], values=not topk), best_keys if topk else None)
            k.clear()


def layer0_xattn(k, w):
    context_attention(k, w, True)


def layer6_xattn(k, w):
    context_attention(k, w, False)


BUILDERS = {0: layer0_xattn, 6: layer6_xattn}


def self_attention(k, w, a, qT, kT, mask=None, gates=None, factor_of=None, factor=None, bo=None):
    nc = k.nc
    unroll = a.unroll
    with nc.Fori(0, TILES // unroll) as t:

        def keys_of(j, c, b):
            return kT[:, c, bass.ds((t * unroll + j) * P + b * SEQ, SEQ)]

        a.keys_of = keys_of
        with nc.Block() as block:

            @block.gpsimd
            def _(pool):
                for j in range(unroll):
                    mask_queries(k, a, pool, j, lambda c, b: qT[:, c, bass.ds((t * unroll + j) * P + b * SEQ, SEQ)])
                    copy_rows(k, a, pool, j, k.xnT[:, :, bass.ds((t * unroll + j) * P, P)])

            @block.tensor
            def _(pe):
                attend_pe(k, a, pe, projections(k, a, w, t, None))

            @block.scalar
            def _(act):
                attend_act(k, a, act, act_jobs(k, a, None, gate=gates and gates[0]))

            @block.vector
            def _(dve):
                link = linker(dve, k.sem("dve_step"))
                jobs = dve_jobs(k, a, link, t, bo=bo, factor=factor,
                                gate=gates and (lambda dve, j: gates[1](dve, link, j)),
                                factor_of=factor_of and (lambda dve, j: factor_of(dve, link, j)))
                attend_dve(k, a, dve, link, jobs, mask and mask(link))
        k.clear()


def layer1_attn(k, w):
    nc = k.nc
    with ExitStack() as ctx:
        a = Attention(k, ctx, SEQ, CHUNKS, 0, D, 16, pairs16(), 0.25, 4, [("v", 0, 0)], copied=True)
        qT = k.sb(ctx, "qT", [P, CHUNKS, TOKENS])
        kT = k.sb(ctx, "kT_all", [P, CHUNKS, TOKENS])
        a.oT_scale = share = k.sb(ctx, "dot_share", [P, CHUNKS])
        project(k, [(w[n], c * P, o[:, c, :], None, ACT.Identity) for n, o in (("wq", qT), ("wk", kT)) for c in range(CHUNKS)])
        with nc.Block() as block:

            @block.scalar
            def _(act):
                nc.scalar.activation(share[:, :], w["beta"], ACT.Sigmoid, scale=-1.0)
        k.clear()

        def mask(link):
            def causal(dve, g, j, b, n):
                pr = a.probs[:, g % 2, 0:n, :]
                nc.vector.tensor_tensor(pr, a.score(k, g)[:, 0:n, :], w["causal"].unsqueeze(1).broadcast_to([P, n, SEQ]),
                                        ALU.add).then_inc(k.sem("scores_copied"), 1)
                dve.wait_ge(k.sem("scores_copied"), g + 1)
                link(nc.vector.reduce_max(a.rowmax[:, g, 0:n], pr, AX_X))
            return causal

        self_attention(k, w, a, qT, kT, mask)


def layer2_ffn(k, w):
    nc = k.nc
    with ExitStack() as ctx:
        a = Attention(k, ctx, SEQ, CHUNKS, 0, D, 16, pairs16(), 0.25, 4, [("v", 0, 0)], gated=True)
        qT = k.sb(ctx, "qT", [P, CHUNKS, TOKENS])
        kT = k.sb(ctx, "kT_all", [P, CHUNKS, TOKENS])
        sq = k.sb(ctx, "q_squares", [P, CHUNKS, TOKENS])
        a.oT_bias = w["bv"]
        heat = k.sb(ctx, "heat", [P, 2, CHUNKS])
        softplus(k, [(w["temp"], heat[:, 0, :], heat[:, 1, :])])
        gate = k.sb(ctx, "gates", [P, 17])
        best = k.sb(ctx, "gates_best", [P, 8])
        cols = k.sb(ctx, "gate_cols", [P, 10])
        factor = k.sb(ctx, "gate_factor", [P, 1])
        project(k, [(w[n], c * P, o[:, c, :], w[bn][:, c:c + 1], ACT.Identity)
                    for n, bn, o in (("wq", "bq", qT), ("wk", "bk", kT)) for c in range(CHUNKS)])
        parts = [(c, h) for c in range(CHUNKS) for h in range(TOKENS // BANK)]
        with nc.Block() as block:

            @block.scalar
            def _(act):
                for c in range(CHUNKS):
                    nc.scalar.activation(sq[:, c, :], qT[:, c, :], ACT.Square).then_inc(k.sem("squares_ready"), 1)
                for n, (c, h) in enumerate(parts):
                    act.wait_ge(k.sem("norm_in_psum"), n + 1)
                    nc.scalar.activation(sq[:, c, h * BANK:(h + 1) * BANK], k.banks[:, n, :], ACT.Sqrt).then_inc(k.sem("norm_ready"), 1)

            @block.tensor
            def _(pe):
                pe.wait_ge(k.sem("squares_ready"), CHUNKS)
                for n, (c, h) in enumerate(parts):
                    nc.tensor.matmul(k.banks[:, n, :], w["same16"], sq[:, c, h * BANK:(h + 1) * BANK],
                                     start=True, stop=True).then_inc(k.sem("norm_in_psum"), 1)

            @block.vector
            def _(dve):
                link = linker(dve, k.sem("dve_step"))
                dve.wait_ge(k.sem("norm_ready"), len(parts))
                link(nc.vector.reciprocal(sq[:, :, :], sq[:, :, :]))
                link(nc.vector.tensor_tensor(qT[:, :, :], qT[:, :, :], sq[:, :, :], ALU.mult))
                for c in range(CHUNKS):
                    nc.vector.tensor_scalar(qT[:, c, :], qT[:, c, :], w["qe"][:, c:c + 1], w["temp"][:, c:c + 1], ALU.add, ALU.mult)
        k.clear()

        def gate_act(act, j):
            act.wait_ge(k.sem("gate_max_ready"), j + 1)
            nc.scalar.activation(gate[:, 0:15], gate[:, 0:15], ACT.Exp, bias=cols[:, 0:1], accum_out=cols[:, 2:3])
            nc.scalar.activation(gate[:, 15:17], gate[:, 15:17], ACT.Exp, bias=cols[:, 1:2],
                                 accum_out=cols[:, 3:4]).then_inc(k.sem("gate_exp_ready"), 1)

        def gate_dve(dve, link, j):
            a.wait_job(k, dve, "g", j, 0, 0)
            nc.vector.tensor_tensor(gate[:, :], a.bank(k, "g", j, 0, 0)[:, 0:17], w["bgate"], ALU.add).then_inc(k.sem("gates_read"), 1)
            dve.wait_ge(k.sem("gates_read"), j + 1)
            nc.vector.reduce_max(cols[:, 0:1], gate[:, 0:15], AX_X)
            link(nc.vector.reduce_max(cols[:, 1:2], gate[:, 15:17], AX_X))
            nc.vector.tensor_scalar(cols[:, 0:2], cols[:, 0:2], -1.0, None, ALU.mult).then_inc(k.sem("gate_max_ready"), 1)

        def gate_factor(dve, link, j):
            dve.wait_ge(k.sem("gate_exp_ready"), j + 1)
            link(nc.vector.reciprocal(cols[:, 2:4], cols[:, 2:4]))
            link(nc.vector.max(best[:, :], gate[:, 0:15]))
            link(nc.vector.reduce_sum(cols[:, 4:5], best[:, 0:3], AX_X))
            link(nc.vector.tensor_tensor(cols[:, 4:5], cols[:, 4:5], cols[:, 2:3], ALU.mult))
            link(nc.vector.tensor_scalar(cols[:, 5:7], gate[:, 15:17], cols[:, 3:4], None, ALU.mult))
            link(nc.vector.reduce_sum(cols[:, 7:8], cols[:, 5:7], AX_X))
            link(nc.vector.scalar_tensor_tensor(cols[:, 7:8], cols[:, 7:8], 2.0, cols[:, 5:6], ALU.mult, ALU.mult))
            link(nc.vector.scalar_tensor_tensor(cols[:, 8:9], cols[:, 4:5], 6.0, cols[:, 6:7], ALU.mult, ALU.mult))
            link(nc.vector.tensor_tensor(factor[:, :], cols[:, 7:8], cols[:, 8:9], ALU.add))

        self_attention(k, w, a, qT, kT, gates=(gate_act, gate_dve), factor_of=gate_factor, factor=factor[:, 0:1])
        with nc.Block() as block:

            @block.vector
            def _(dve):
                nc.vector.tensor_tensor(k.x[:, :, :], k.x[:, :, :], w["bo"].unsqueeze(1).broadcast_to([P, TILES, D]), ALU.add)


def layer3_xattn(k, w):
    nc = k.nc
    inner = 1024
    unroll = 4
    normalize(k, src=k.xn, scale=w["gamma"], shift=w["beta"])
    with ExitStack() as ctx:
        a = Attention(k, ctx, CTX, inner // P, inner // P, inner, 64, pairs64(inner // P, False), 0.125, unroll,
                      context_jobs(inner // P, inner, seqs=1, queries=inner // P), split=True)
        a.q_tile = k.sb(ctx, "q_tile", [P, inner // P, P])
        opening = k.sb(ctx, "gate_tanh", [P, 1])
        with nc.Block() as block:

            @block.scalar
            def _(act):
                nc.scalar.activation(opening[:, :], w["gate"], ACT.Tanh)
        with nc.Fori(0, TILES // unroll) as t:

            def ctx_cols(u):
                return bass.ds((t * a.units + u) * CTX, CTX)

            with nc.Block() as block:

                @block.gpsimd
                def _(pool):
                    for u in range(a.units):
                        if u:
                            copy_rows(k, a, pool, u, k.ctxT[:, :, ctx_cols(u)])
                        pool.wait_ge(k.sem("queries_ready"), 2 * (u // PER_TILE + 1))
                        mask_queries(k, a, pool, u, lambda c, b: a.q_tile[:, c, (u % PER_TILE) * SEQ:(u % PER_TILE + 1) * SEQ])
                        if not u:
                            copy_rows(k, a, pool, u, k.ctxT[:, :, ctx_cols(u)])

                @block.tensor
                def _(pe):
                    attend_pe(k, a, pe, projections(k, a, w, t, lambda u, c: k.ctxT[:, c, ctx_cols(u)],
                                                    lambda j, c: k.xnT[:, c, bass.ds((t * unroll + j) * P, P)]))

                @block.scalar
                def _(act):
                    attend_act(k, a, act, act_jobs(k, a, None))

                @block.vector
                def _(dve):
                    link = linker(dve, k.sem("dve_step"))
                    attend_dve(k, a, dve, link, dve_jobs(k, a, link, t, w["bo"], factor=opening[:, 0:1]))
            k.clear()


BUILDERS |= {1: layer1_attn, 2: layer2_ffn, 3: layer3_xattn}


def layout_attention(g, out):
    a = "L0_attn_"
    later = (np.arange(SEQ)[None, :] > (np.arange(P) % SEQ)[:, None]) * np.float32(NEG)
    out[1] = dict(wq=_mat(g[a + "W_q"].T), wk=_mat(g[a + "W_k"].T), wv=_mat(g[a + "W_v"].T), wo=_mat(g[a + "W_o"].T),
                  beta=_col(np.repeat(g[a + "beta_param"], 16)), causal=later.astype(np.float32))
    a = "L0_ffn_"
    same = (np.arange(P)[:, None] // 16 == np.arange(P)[None, :] // 16).astype(np.float32)
    out[2] = dict(wq=_mat(g[a + "Wq"].T), wk=_mat(g[a + "Wk"].T), wv=_mat(g[a + "Wv"].T), wo=_mat(g[a + "Wp"].T),
                  bq=_col(g[a + "bq"]), bk=_col(g[a + "bk"]), bv=_col(g[a + "bv"]), bo=_row(g[a + "bp"]),
                  temp=_col(np.repeat(g[a + "temperature"].reshape(-1), 16)), qe=_col(g[a + "query_embedding"].reshape(-1)),
                  wgate=_mat(np.concatenate([g[a + "Wr"], g[a + "Ws"]]).T),
                  bgate=_row(np.concatenate([g[a + "br"], g[a + "bs"]])), same16=same)
    a = "L1_xattn_"
    kv = g[a + "w_kv"]
    out[3] = dict(wq=_mat(g[a + "w_q"]), wk=_mat(kv[:, :1024]), wv=_mat(kv[:, 1024:]), wo=_mat(g[a + "w_out"]),
                  gamma=_col(g[a + "ln_gamma"]), beta=_col(g[a + "ln_beta"]), bo=_row(g[a + "b_out"]), gate=_row(g[a + "gate"]))


def rms_inverse(k, ones, src, squares, inv, chunks, scale_rows):
    nc = k.nc
    with nc.Block() as block:

        @block.gpsimd
        def _(pool):
            for n in range(chunks):
                if n >= 2:
                    pool.wait_ge(k.sem("sumsq_ready"), n - 1)
                cols = src[:, :, n * BANK:(n + 1) * BANK]
                nc.gpsimd.tensor_tensor(squares[:, n % 2, :, :], cols, cols, ALU.mult).then_inc(k.sem("squares_ready"), 1)

        @block.scalar
        def _(act):
            for n in range(chunks):
                act.wait_ge(k.sem("sumsq_ready"), n + 1)
                nc.scalar.activation(inv[:, n * BANK:(n + 1) * BANK], k.banks[:, n % 4, :], ACT.Sqrt, bias=scale_rows["eps"],
                                     scale=1.0 / D).then_inc(k.sem("rms_ready"), 1)

        @block.tensor
        def _(pe):
            for n in range(chunks):
                pe.wait_ge(k.sem("squares_ready"), n + 1)
                if n >= 4:
                    pe.wait_ge(k.sem("rms_ready"), n - 3)
                for c in range(CHUNKS):
                    last = nc.tensor.matmul(k.banks[:, n % 4, :], ones, squares[:, n % 2, c, :], start=(c == 0), stop=(c == CHUNKS - 1))
                last.then_inc(k.sem("sumsq_ready"), 1)

        @block.vector
        def _(dve):
            for n in range(chunks):
                cols = slice(n * BANK, (n + 1) * BANK)
                dve.wait_ge(k.sem("rms_ready"), n + 1)
                nc.vector.reciprocal(inv[:, cols], inv[:, cols]).then_inc(k.sem("inverse_ready"), 1)
                dve.wait_ge(k.sem("inverse_ready"), n + 1)
                for c in range(CHUNKS):
                    nc.vector.scalar_tensor_tensor(src[:, c, cols], src[:, c, cols], scale_rows["gain"][:, c:c + 1], inv[:, cols],
                                                   ALU.mult, ALU.mult)
    k.clear()


def rotate(k, straight, swapped, cos, sin, batch, n):
    nc = k.nc
    with nc.Block() as block:

        @block.gpsimd
        def _(pool):
            for c in range(straight.shape[1]):
                v = swapped[:, c, :].rearrange("p (b q) -> p b q", q=n)
                nc.gpsimd.tensor_tensor(v, v, sin.unsqueeze(1).broadcast_to([P, batch, n]), ALU.mult).then_inc(k.sem("sine_ready"), 1)

        @block.vector
        def _(dve):
            for c in range(straight.shape[1]):
                v = straight[:, c, :].rearrange("p (b q) -> p b q", q=n)
                nc.vector.tensor_tensor(v, v, cos.unsqueeze(1).broadcast_to([P, batch, n]), ALU.mult).then_inc(k.sem("cosine_ready"), 1)
            for c in range(straight.shape[1]):
                dve.wait_ge(k.sem("cosine_ready"), c + 1)
                dve.wait_ge(k.sem("sine_ready"), c + 1)
                nc.vector.tensor_tensor(straight[:, c, :], straight[:, c, :], swapped[:, c, :], ALU.add)
    k.clear()


def layer9_xattn(k, w):
    nc = k.nc
    keys_all = BATCH * CTX
    unroll = 4
    with ExitStack() as ctx:
        a = Attention(k, ctx, CTX, CHUNKS, 0, P, 64, pairs64(CHUNKS, True), 0.125, unroll, context_jobs(0, P), copied=True)
        qT = k.xn[:, :, :].rearrange("p t d -> p (t d)").rearrange("p (c n) -> p c n", c=CHUNKS)
        kT = k.sb(ctx, "kT_all", [P, 1, keys_all])
        low = k.sb(ctx, "key_low", [P, 2, CTX_TILE])
        mask8 = k.sb(ctx, "key_mask", [P, keys_all], U8)
        gain = k.sb(ctx, "rms_gain", [P, CHUNKS])
        eps = k.sb(ctx, "rms_eps", [P, 1])
        with nc.Block() as block:

            @block.sync
            def _(sp):
                sp.dma_start(mask8[:, :], k.dram["mask_last"]).then_inc(k.sem("mask_loaded"), 16)
                sp.wait_ge(k.sem("mask_loaded"), 16)

            @block.vector
            def _(dve):
                nc.vector.memset(eps[:, :], 1e-6)
                nc.vector.tensor_scalar(gain[:, :], w["rms"], 1.0, None, ALU.add)
        k.clear()
        with ExitStack() as early:
            swapped = k.sb(early, "k_swapped", [P, 1, keys_all])
            squares = swapped[:, 0, 0:2 * CHUNKS * BANK].rearrange("p (i c n) -> p i c n", i=2, c=CHUNKS)
            inv = kT[:, 0, :]
            rows = dict(eps=eps[:, 0:1], gain=gain)
            rms_inverse(k, w["ones"], k.ctxT, squares, inv, keys_all // BANK, rows)
            rms_inverse(k, w["ones"], k.xnT, squares, inv, TOKENS // BANK, rows)
            qswap = swapped[:, 0, 0:CHUNKS * TOKENS].rearrange("p (c n) -> p c n", c=CHUNKS)
            project(k, [(w[n], c * P, o[:, c, :], None, ACT.Identity) for n, o in (("wq", qT), ("wqs", qswap)) for c in range(CHUNKS)])
            rotate(k, qT, qswap, w["cosq"], w["sinq"], BATCH, SEQ)
            project(k, [(w["wk"], 0, kT[:, 0, :], None, ACT.Identity), (w["wk"], P, swapped[:, 0, :], None, ACT.Identity)],
                    src=k.ctxT, tokens=keys_all)
            rotate(k, kT, swapped, w["cosk"], w["sink"], BATCH, CTX)
        with nc.Fori(0, TILES // unroll) as t:

            def cols(j, b=0):
                return bass.ds((t * unroll + j) * CTX_TILE + b * CTX, CTX)

            def mask(link):
                def hide(dve, g, j, b, n):
                    pr = a.probs[:, g % 2, 0:n, :]
                    dve.wait_ge(k.sem("low_ready"), 2 * j + 2)
                    nc.vector.tensor_tensor(pr, a.score(k, g)[:, 0:n, :],
                                            low[:, j % 2, b * CTX:(b + 1) * CTX].unsqueeze(1).broadcast_to([P, n, CTX]),
                                            ALU.add).then_inc(k.sem("scores_copied"), 1)
                    dve.wait_ge(k.sem("scores_copied"), g + 1)
                    link(nc.vector.reduce_max(a.rowmax[:, g, 0:n], pr, AX_X))
                return hide

            a.keys_of = lambda j, c, b: kT[:, 0, cols(j, b)]
            with nc.Block() as block:

                @block.gpsimd
                def _(pool):
                    for j in range(unroll):
                        tile = bass.ds((t * unroll + j) * CTX_TILE, CTX_TILE)
                        mask_queries(k, a, pool, j, lambda c, b: qT[:, c, bass.ds((t * unroll + j) * P + b * SEQ, SEQ)])
                        if j >= 2:
                            pool.wait_ge(k.sem("scores_copied"), a.per_tile * (j - 1))
                        nc.gpsimd.tensor_copy(low[:, j % 2, :], mask8[:, tile]).then_inc(k.sem("low_ready"), 1)
                        pool.wait_ge(k.sem("low_ready"), 2 * j + 1)
                        nc.gpsimd.tensor_scalar(low[:, j % 2, :], low[:, j % 2, :], -NEG, NEG, ALU.mult, ALU.add).then_inc(k.sem("low_ready"), 1)
                        copy_rows(k, a, pool, j, k.ctxT[:, :, tile])

                @block.tensor
                def _(pe):
                    attend_pe(k, a, pe, projections(k, a, w, t, None))

                @block.scalar
                def _(act):
                    attend_act(k, a, act, act_jobs(k, a, None))

                @block.vector
                def _(dve):
                    link = linker(dve, k.sem("dve_step"))
                    attend_dve(k, a, dve, link, dve_jobs(k, a, link, t), mask(link))
            k.clear()


HIDDEN = 1024
ROUND = 1.5 * 2.0 ** 23
QB = 127.0


def after(k, eng, name, n):
    if n > 0:
        eng.wait_ge(k.sem(name), n)


def two_layers(k, dt, unroll, act_x, dve_x, act_h, dve_pre, dve_h, finish, w1, w2, buf):
    nc = k.nc
    xq, xqT, hq, hqT, ident, x_turned, h_turned = buf
    nh = HIDDEN // P
    steps = [(s + 1 if s + 1 < unroll else None, s if 0 <= s < unroll else None, s - 1 if s >= 1 else None)
             for s in range(-1, unroll + 1)]
    with nc.Fori(0, TILES // unroll) as t:
        with nc.Block() as block:

            @block.tensor
            def _(pe):
                for enter, _, leave in steps:
                    if leave is not None:
                        j = leave
                        after(k, pe, "hq_ready", j + 1)
                        after(k, pe, "hqT_ready", j)
                        for c in range(nh):
                            last = nc.tensor.transpose(h_turned[:, c * P:(c + 1) * P], hq[:, c * P:(c + 1) * P], ident)
                        last.then_inc(k.sem("hq_turned"), 1)
                    if enter is not None:
                        j = enter
                        after(k, pe, "xq_ready", j + 1)
                        after(k, pe, "xqT_ready", j)
                        for c in range(CHUNKS):
                            last = nc.tensor.transpose(x_turned[:, c * P:(c + 1) * P], xq[:, c * P:(c + 1) * P], ident)
                        last.then_inc(k.sem("xq_turned"), 1)
                    if leave is not None:
                        j = leave
                        after(k, pe, "hqT_ready", j + 1)
                        after(k, pe, "added", j)
                        for c in range(nh):
                            last = nc.tensor.matmul(k.banks[:, 4, 0:D], hqT[:, c, :], w2[:, c, :], start=(c == 0), stop=(c == nh - 1))
                        last.then_inc(k.sem("branch_ready"), 1)
                    if enter is not None:
                        j = enter
                        after(k, pe, "xqT_ready", j + 1)
                        after(k, pe, "hidden_read", j)
                        for h in range(HIDDEN // BANK):
                            for c in range(CHUNKS):
                                last = nc.tensor.matmul(k.banks[:, 2 + h, :], xqT[:, c, :], w1[:, c, h * BANK:(h + 1) * BANK],
                                                        start=(c == 0), stop=(c == CHUNKS - 1))
                            last.then_inc(k.sem("hidden_ready"), 1)

            @block.scalar
            def _(act):
                link = linker(act, k.sem("act_step"))
                for enter, inner, leave in steps:
                    if leave is not None:
                        after(k, act, "hq_turned", leave + 1)
                        after(k, act, "branch_ready", leave)
                        nc.scalar.copy(hqT[:, :, :], h_turned[:, 0:HIDDEN].rearrange("p (c n) -> p c n", n=P)).then_inc(k.sem("hqT_ready"), 1)
                    if enter is not None:
                        act_x(act, link, t * unroll + enter, enter)
                    if inner is not None:
                        act_h(act, link, inner)
                    if enter is not None:
                        after(k, act, "xq_turned", enter + 1)
                        after(k, act, "hidden_ready", 2 * enter)
                        nc.scalar.copy(xqT[:, :, :], x_turned[:, 0:D].rearrange("p (c n) -> p c n", n=P)).then_inc(k.sem("xqT_ready"), 1)

            @block.vector
            def _(dve):
                link = linker(dve, k.sem("dve_step"))
                for enter, inner, leave in steps:
                    if inner is not None:
                        dve_pre(dve, link, inner)
                    if enter is not None:
                        after(k, dve, "xq_turned", enter)
                        dve_x(dve, link, t * unroll + enter, enter)
                    if inner is not None:
                        after(k, dve, "hq_turned", inner)
                        dve_h(dve, link, inner)
                    if leave is not None:
                        after(k, dve, "branch_ready", leave + 1)
                        finish(dve, link, t * unroll + leave, leave)
        k.clear()


def abs_totals(k, dve, link, flat, work, tot):
    nc = k.nc
    for i in range(2):
        nc.vector.tensor_reduce(work[:, 32 * i:32 * i + 32], flat[i].rearrange("p (a b) -> p a b", a=32), AX_X, ALU.add,
                                apply_absolute_value=True).then_inc(k.sem("runs_ready"), 1)
    dve.wait_ge(k.sem("runs_ready"), 2)
    nc.vector.tensor_reduce(tot[:, :], work[:, 0:64].rearrange("p (i a) -> p i a", i=2), AX_X, ALU.add).then_inc(k.sem("abs_ready"), 1)


def layer5_ffn(k, w):
    nc = k.nc
    nh = HIDDEN // P
    with ExitStack() as ctx:
        w1 = k.sb(ctx, "w1_int", [P, CHUNKS, HIDDEN], BF16)
        w2 = k.sb(ctx, "w2_int", [P, nh, D], BF16)
        xq = k.sb(ctx, "xq", [P, D], BF16)
        xqT = k.sb(ctx, "xqT", [P, CHUNKS, P], BF16)
        hq = k.sb(ctx, "hq", [P, HIDDEN], BF16)
        hqT = k.sb(ctx, "hqT", [P, nh, P], BF16)
        ident = k.sb(ctx, "ident16", [P, P], BF16)
        work = k.sb(ctx, "quant_work", [P, HIDDEN * 2])
        hid = k.sb(ctx, "hidden", [P, HIDDEN])
        tot = k.sb(ctx, "abs_total", [P, 2])
        ws = k.sb(ctx, "w_scales", [P, 6])
        sc = k.sb(ctx, "row_scales", [P, 2, 8])
        turned = k.banks[:, 0, :].bitcast(BF16)
        flat = [w["w1"].rearrange("p a b -> p (a b)"), w["w2"].rearrange("p a b -> p (a b)")]
        outs = [w1[:, :, :].rearrange("p a b -> p (a b)"), w2[:, :, :].rearrange("p a b -> p (a b)")]
        with nc.Block() as block:

            @block.scalar
            def _(act):
                nc.scalar.copy(ident[:, :], k.ident[:, :])

            @block.tensor
            def _(pe):
                pe.wait_ge(k.sem("abs_ready"), 1)
                nc.tensor.matmul(k.banks[:, 1, 0:2], w["ones"], tot[:, :], start=True, stop=True).then_inc(k.sem("total_ready"), 1)

            @block.vector
            def _(dve):
                link = linker(dve, k.sem("dve_step"))
                abs_totals(k, dve, link, flat, work, tot)
                dve.wait_ge(k.sem("total_ready"), 1)
                link(nc.vector.tensor_scalar(ws[:, 0:2], k.banks[:, 1, 0:2], 1.0 / (HIDDEN * D), 1e-5, ALU.mult, ALU.max))
                link(nc.vector.reciprocal(ws[:, 2:4], ws[:, 0:2]))
                link(nc.vector.tensor_scalar(ws[:, 4:6], ws[:, 0:2], 1.0 / QB, None, ALU.mult))
                for i in range(2):
                    link(nc.vector.tensor_scalar(work[:, :], flat[i], ws[:, 2 + i:3 + i], ROUND, ALU.mult, ALU.add))
                    link(nc.vector.tensor_scalar(work[:, :], work[:, :], ROUND, 1.0, ALU.subtract, ALU.min))
                    link(nc.vector.tensor_scalar(outs[i], work[:, :], -1.0, None, ALU.max))
        k.clear()

        def quantize(dve, link, src, out, n, s, ready):
            scale, inverse = s[:, 0:1], s[:, 1:2]
            link(nc.vector.tensor_reduce(scale, src, AX_X, ALU.max, apply_absolute_value=True))
            link(nc.vector.tensor_scalar(scale, scale, 1e-5, None, ALU.max))
            link(nc.vector.reciprocal(inverse, scale))
            link(nc.vector.tensor_scalar(inverse, inverse, QB, None, ALU.mult))
            link(nc.vector.tensor_scalar(work[:, 0:n], src, inverse, ROUND, ALU.mult, ALU.add))
            link(nc.vector.tensor_scalar(work[:, 0:n], work[:, 0:n], ROUND, QB, ALU.subtract, ALU.min))
            nc.vector.tensor_scalar(out, work[:, 0:n], -QB - 1.0, None, ALU.max).then_inc(k.sem(ready), 1)

        def x_dve(dve, link, t, j):
            quantize(dve, link, k.xn[:, t, :], xq[:, :], D, sc[:, j % 2, 0:2], "xq_ready")
            link(nc.vector.tensor_tensor(sc[:, j % 2, 2:3], sc[:, j % 2, 0:1], ws[:, 4:5], ALU.mult))

        def pre(dve, link, j):
            dve.wait_ge(k.sem("hidden_ready"), 2 * (j + 1))
            nc.vector.scalar_tensor_tensor(hid[:, :], k.banks[:, 2:4, :].rearrange("p h n -> p (h n)"), sc[:, j % 2, 2:3], w["b1"],
                                           ALU.mult, ALU.add).then_inc(k.sem("hidden_read"), 1)

        def h_dve(dve, link, j):
            dve.wait_ge(k.sem("gelu_ready"), j + 1)
            quantize(dve, link, hid[:, :], hq[:, :], HIDDEN, sc[:, j % 2, 4:6], "hq_ready")
            link(nc.vector.tensor_tensor(sc[:, j % 2, 6:7], sc[:, j % 2, 4:5], ws[:, 5:6], ALU.mult))

        def gelu(act, link, j):
            act.wait_ge(k.sem("hidden_read"), j + 1)
            nc.scalar.activation(hid[:, :], hid[:, :], ACT.Gelu).then_inc(k.sem("gelu_ready"), 1)

        def finish(dve, link, t, j):
            nc.vector.scalar_tensor_tensor(work[:, 0:D], k.banks[:, 4, 0:D], sc[:, j % 2, 6:7], w["b2"], ALU.mult, ALU.add).then_inc(k.sem("added"), 1)
            dve.wait_ge(k.sem("added"), j + 1)
            link(nc.vector.tensor_tensor(k.x[:, t, :], k.x[:, t, :], work[:, 0:D], ALU.add))

        two_layers(k, BF16, 4, lambda *_: None, x_dve, gelu, pre, h_dve, finish, w1, w2,
                   (xq, xqT, hq, hqT, ident[:, :], k.banks[:, 5, :].bitcast(BF16), turned))


def layer11_ffn(k, w):
    nc = k.nc
    nh = HIDDEN // P
    with ExitStack() as ctx:
        w1 = k.sb(ctx, "w1_tern", [P, CHUNKS, HIDDEN])
        w2 = k.sb(ctx, "w2_tern", [P, nh, D])
        xq = k.sb(ctx, "x_unit", [P, D])
        xqT = k.sb(ctx, "x_unitT", [P, CHUNKS, P])
        hq = k.sb(ctx, "h_unit", [P, HIDDEN])
        hqT = k.sb(ctx, "h_unitT", [P, nh, P])
        work = k.sb(ctx, "work", [P, HIDDEN * 2])
        hid = k.sb(ctx, "hidden", [P, HIDDEN])
        tot = k.sb(ctx, "abs_total", [P, 2])
        th = k.sb(ctx, "thresholds", [P, 4])
        sc = k.sb(ctx, "row_scales", [P, 2, 2])
        flat = [w["w1"].rearrange("p a b -> p (a b)"), w["w2"].rearrange("p a b -> p (a b)")]
        outs = [w1[:, :, :].rearrange("p a b -> p (a b)"), w2[:, :, :].rearrange("p a b -> p (a b)")]
        with nc.Block() as block:


            @block.tensor
            def _(pe):
                pe.wait_ge(k.sem("abs_ready"), 1)
                nc.tensor.matmul(k.banks[:, 1, 0:2], w["ones"], tot[:, :], start=True, stop=True).then_inc(k.sem("total_ready"), 1)

            @block.vector
            def _(dve):
                link = linker(dve, k.sem("dve_step"))
                abs_totals(k, dve, link, flat, work, tot)
                dve.wait_ge(k.sem("total_ready"), 1)
                nc.vector.tensor_scalar(th[:, 0:2], k.banks[:, 1, 0:2], 0.5 / (HIDDEN * D), None, ALU.mult)
                link(nc.vector.tensor_scalar(th[:, 2:4], k.banks[:, 1, 0:2], -0.5 / (HIDDEN * D), None, ALU.mult))
                for i in range(2):
                    link(nc.vector.tensor_scalar(work[:, :], flat[i], th[:, 2 + i:3 + i], None, ALU.is_lt))
                    link(nc.vector.scalar_tensor_tensor(outs[i], flat[i], th[:, i:i + 1], work[:, :], ALU.is_gt, ALU.subtract))
        k.clear()

        def unit(dve, link, src, out, s, ready):
            link(nc.vector.tensor_scalar(s, s, 1e-8, None, ALU.add))
            link(nc.vector.reciprocal(s, s))
            nc.vector.tensor_scalar(out, src, s, None, ALU.mult).then_inc(k.sem(ready), 1)

        def x_act(act, link, t, j):
            s = sc[:, j % 2, 0:1]
            link(nc.scalar.activation(work[:, 0:D], k.xn[:, t, :], ACT.Square, accum_out=s))
            nc.scalar.activation(s, s, ACT.Sqrt, scale=1.0 / D).then_inc(k.sem("x_rms"), 1)

        def x_dve(dve, link, t, j):
            dve.wait_ge(k.sem("x_rms"), j + 1)
            unit(dve, link, k.xn[:, t, :], xq[:, :], sc[:, j % 2, 0:1], "xq_ready")

        def h_act(act, link, j):
            s = sc[:, j % 2, 1:2]
            act.wait_ge(k.sem("hidden_ready"), 2 * (j + 1))
            after(k, act, "hq_ready", j)
            nc.scalar.activation(hid[:, :], k.banks[:, 2:4, :].rearrange("p h n -> p (h n)"), ACT.Gelu).then_inc(k.sem("hidden_read"), 1)
            act.wait_ge(k.sem("hidden_read"), j + 1)
            link(nc.scalar.activation(work[:, HIDDEN:], hid[:, :], ACT.Square, accum_out=s))
            nc.scalar.activation(s, s, ACT.Sqrt, scale=1.0 / HIDDEN).then_inc(k.sem("h_rms"), 1)

        def h_dve(dve, link, j):
            dve.wait_ge(k.sem("h_rms"), j + 1)
            unit(dve, link, hid[:, :], hq[:, :], sc[:, j % 2, 1:2], "hq_ready")

        def finish(dve, link, t, j):
            nc.vector.tensor_tensor(k.x[:, t, :], k.x[:, t, :], k.banks[:, 4, 0:D], ALU.add).then_inc(k.sem("added"), 1)

        two_layers(k, F32, 4, x_act, x_dve, h_act, lambda *_: None, h_dve, finish, w1, w2,
                   (xq, xqT, hq, hqT, k.ident[:, :], k.banks[:, 5, :], k.banks[:, 0:2, :].rearrange("p b n -> p (b n)")))


PROTOS, RANK = 32, 16


def layer8_ffn(k, w):
    nc = k.nc
    pr = PROTOS * RANK
    nr = pr // P
    unroll = 4
    with ExitStack() as ctx:
        psq = k.sb(ctx, "proto_squares", [P, CHUNKS, PROTOS])
        p2 = k.sb(ctx, "proto_norms", [P, PROTOS])
        temp = k.sb(ctx, "temp_inverse", [P, 2])
        dist = k.sb(ctx, "dist", [P, TILES, PROTOS])
        wt = k.sb(ctx, "proto_weights", [P, TILES, PROTOS])
        pick = k.sb(ctx, "picked_two", [P, 2, TILES, PROTOS])
        best = k.sb(ctx, "best8", [P, TILES, 8])
        where = k.sb(ctx, "best8_at", [P, TILES, 8], mybir.dt.uint32)
        wheref = k.sb(ctx, "best8_at_float", [P, TILES, 8])
        x2 = k.sb(ctx, "x_norms", [P, TILES])
        nearest = k.sb(ctx, "nearest", [P, TILES])
        total = k.sb(ctx, "weight_total", [P, TILES])
        junk = k.sb(ctx, "x_squares", [P, TILES, D])
        rows = k.sb(ctx, "x_rows", [P, 2, CHUNKS, P])
        mine = k.sb(ctx, "tile_weights", [P, 2, PROTOS])
        low = k.sb(ctx, "low_rank", [P, 2, pr])
        lowT = k.sb(ctx, "low_rankT", [P, 2, nr, P])
        wtT = k.sb(ctx, "proto_weightsT", [PROTOS, 2, P])
        cross = k.banks[:, 1, 0:TILES * PROTOS].rearrange("p (t a) -> p t a", t=TILES)

        def all_tiles(col):
            return col[:, :].unsqueeze(2).broadcast_to([P, TILES, PROTOS])

        with nc.Block() as block:

            @block.scalar
            def _(act):
                nc.scalar.activation(psq[:, :, :], w["protos"], ACT.Square).then_inc(k.sem("squares_ready"), 1)
                nc.scalar.activation(temp[:, 0:1], w["temp"], ACT.Abs).then_inc(k.sem("temp_ready"), 1)
                for t in range(TILES):
                    nc.scalar.activation(junk[:, t, :], k.xn[:, t, :], ACT.Square, accum_out=x2[:, t:t + 1]).then_inc(k.sem("x2_ready"), 1)
                act.wait_ge(k.sem("d2_ready"), 1)
                nc.scalar.activation(dist[:, :, :], dist[:, :, :], ACT.Sqrt).then_inc(k.sem("dist_ready"), 1)
                act.wait_ge(k.sem("shifted"), 1)
                nc.scalar.activation(wt[:, :, :], dist[:, :, :], ACT.Exp, scale=temp[:, 1:2]).then_inc(k.sem("exp_ready"), 1)

            @block.tensor
            def _(pe):
                pe.wait_ge(k.sem("squares_ready"), 1)
                for c in range(CHUNKS):
                    last = nc.tensor.matmul(k.banks[:, 0, 0:PROTOS], w["ones"], psq[:, c, :], start=(c == 0), stop=(c == CHUNKS - 1))
                last.then_inc(k.sem("norms_ready"), 1)
                for t in range(TILES):
                    for c in range(CHUNKS):
                        last = nc.tensor.matmul(cross[:, t, :], k.xnT[:, c, t * P:(t + 1) * P], w["protos"][:, c, :],
                                                start=(c == 0), stop=(c == CHUNKS - 1))
                last.then_inc(k.sem("cross_ready"), 1)

            @block.vector
            def _(dve):
                link = linker(dve, k.sem("dve_step"))
                dve.wait_ge(k.sem("temp_ready"), 1)
                link(nc.vector.tensor_scalar(temp[:, 0:1], temp[:, 0:1], 0.1, None, ALU.max))
                link(nc.vector.reciprocal(temp[:, 0:1], temp[:, 0:1]))
                link(nc.vector.tensor_scalar(temp[:, 1:2], temp[:, 0:1], -1.0, None, ALU.mult))
                dve.wait_ge(k.sem("norms_ready"), 1)
                link(nc.vector.tensor_copy(p2[:, :], k.banks[:, 0, 0:PROTOS]))
                dve.wait_ge(k.sem("cross_ready"), 1)
                dve.wait_ge(k.sem("x2_ready"), TILES)
                link(nc.vector.scalar_tensor_tensor(dist[:, :, :], cross, -2.0, p2[:, :].unsqueeze(1).broadcast_to([P, TILES, PROTOS]),
                                                    ALU.mult, ALU.add))
                link(nc.vector.tensor_tensor(dist[:, :, :], dist[:, :, :], all_tiles(x2), ALU.add))
                nc.vector.tensor_scalar(dist[:, :, :], dist[:, :, :], 0.0, None, ALU.max).then_inc(k.sem("d2_ready"), 1)
                dve.wait_ge(k.sem("dist_ready"), 1)
                link(nc.vector.tensor_reduce(nearest[:, :], dist[:, :, :], AX_X, ALU.min))
                nc.vector.tensor_tensor(dist[:, :, :], dist[:, :, :], all_tiles(nearest), ALU.subtract).then_inc(k.sem("shifted"), 1)
                dve.wait_ge(k.sem("exp_ready"), 1)
                link(nc.vector.reduce_sum(total[:, :], wt[:, :, :], AX_X))
                link(nc.vector.reciprocal(total[:, :], total[:, :]))
                link(nc.vector.tensor_tensor(wt[:, :, :], wt[:, :, :], all_tiles(total), ALU.mult))
                for t in range(TILES):
                    last = nc.vector.max(best[:, t, :], wt[:, t, :])
                link(last)
                for t in range(TILES):
                    last = nc.vector.max_index(where[:, t, :], best[:, t, :], wt[:, t, :])
                link(last)
                link(nc.vector.tensor_copy(wheref[:, :, :], where[:, :, :]))
                for i in range(2):
                    for t in range(TILES):
                        last = nc.vector.tensor_scalar(pick[:, i, t, :], w["iota"], wheref[:, t, i:i + 1], None, ALU.is_equal)
                link(last)
                link(nc.vector.tensor_tensor(pick[:, 0, :, :], pick[:, 0, :, :], pick[:, 1, :, :], ALU.add))
                link(nc.vector.tensor_tensor(wt[:, :, :], wt[:, :, :], pick[:, 0, :, :], ALU.mult))
                link(nc.vector.reduce_sum(total[:, :], best[:, :, 0:2], AX_X))
                link(nc.vector.reciprocal(total[:, :], total[:, :]))
                link(nc.vector.tensor_tensor(wt[:, :, :], wt[:, :, :], all_tiles(total), ALU.mult))
        k.clear()
        steps = [(s + 1 if s + 1 < unroll else None, s if 0 <= s < unroll else None, s - 1 if s >= 1 else None)
                 for s in range(-1, unroll + 1)]
        with nc.Fori(0, TILES // unroll) as g:
            with nc.Block() as block:

                @block.gpsimd
                def _(pool):
                    for j in range(unroll):
                        after(k, pool, "turned", j - 1)
                        nc.gpsimd.tensor_copy(rows[:, j % 2, :, :], k.xnT[:, :, bass.ds((g * unroll + j) * P, P)]).then_inc(k.sem("rows_ready"), 1)
                        nc.gpsimd.tensor_copy(mine[:, j % 2, :], wt[:, g * unroll + j, :]).then_inc(k.sem("rows_ready"), 1)

                @block.tensor
                def _(pe):
                    for enter, inner, leave in steps:
                        if inner is not None:
                            j = inner
                            after(k, pe, "weighted_ready", j + 1)
                            after(k, pe, "turned_ready", 2 * j)
                            nc.tensor.transpose(k.banks[0:PROTOS, 3, 0:P], mine[:, j % 2, :], k.ident[:, :])
                            for c in range(nr):
                                last = nc.tensor.transpose(k.banks[:, 2, c * P:(c + 1) * P], low[:, j % 2, c * P:(c + 1) * P], k.ident[:, :])
                            last.then_inc(k.sem("turned"), 1)
                        if enter is not None:
                            j = enter
                            after(k, pe, "rows_ready", 2 * (j + 1))
                            after(k, pe, "weighted_ready", j)
                            for c in range(CHUNKS):
                                last = nc.tensor.matmul(k.banks[:, 1, :], rows[:, j % 2, c, :], w["B"][:, c, :], start=(c == 0), stop=(c == CHUNKS - 1))
                            last.then_inc(k.sem("low_ready"), 1)
                        if leave is not None:
                            j = leave
                            after(k, pe, "turned_ready", 2 * (j + 1))
                            after(k, pe, "added", j)
                            for c in range(nr):
                                nc.tensor.matmul(k.banks[:, 4, 0:D], lowT[:, j % 2, c, :], w["A"][:, c, :], start=(c == 0), stop=False)
                            nc.tensor.matmul(k.banks[:, 4, 0:D], wtT[:, j % 2, :], w["bias"][0:PROTOS, :], start=False,
                                             stop=True).then_inc(k.sem("branch_ready"), 1)

                @block.scalar
                def _(act):
                    for j in range(unroll):
                        after(k, act, "turned", j + 1)
                        after(k, act, "branch_ready", j - 1)
                        nc.scalar.copy(lowT[:, j % 2, :, :], k.banks[:, 2, :].rearrange("p (c n) -> p c n", n=P)).then_inc(k.sem("turned_ready"), 1)
                        nc.scalar.copy(wtT[:, j % 2, :], k.banks[0:PROTOS, 3, 0:P]).then_inc(k.sem("turned_ready"), 1)

                @block.vector
                def _(dve):
                    for enter, _, leave in steps:
                        if enter is not None:
                            j = enter
                            after(k, dve, "low_ready", j + 1)
                            after(k, dve, "turned", j - 1)
                            nc.vector.tensor_tensor(low[:, j % 2, :].rearrange("p (a r) -> p a r", r=RANK),
                                                    k.banks[:, 1, :].rearrange("p (a r) -> p a r", r=RANK),
                                                    wt[:, g * unroll + j, :].unsqueeze(2).broadcast_to([P, PROTOS, RANK]),
                                                    ALU.mult).then_inc(k.sem("weighted_ready"), 1)
                        if leave is not None:
                            j = leave
                            after(k, dve, "branch_ready", j + 1)
                            dst = k.x[:, g * unroll + j, :]
                            nc.vector.tensor_tensor(dst, dst, k.banks[:, 4, 0:D], ALU.add).then_inc(k.sem("added"), 1)
            k.clear()


BUILDERS |= {5: layer5_ffn, 8: layer8_ffn, 9: layer9_xattn, 11: layer11_ffn}


def layout_blocks(g, out):
    ones = np.ones((P, P), np.float32)
    a = "L1_ffn_"
    out[5] = dict(w1=_mat(g[a + "W1"].T), w2=_mat(g[a + "W2"].T), b1=_row(g[a + "b1"]), b2=_row(g[a + "b2"]), ones=ones)
    a = "L3_ffn_"
    out[11] = dict(w1=_mat(g[a + "w_up"].T), w2=_mat(g[a + "w_down"].T), ones=ones)
    a = "L2_ffn_"
    out[8] = dict(protos=_mat(g[a + "prototypes"].T), B=_mat(g[a + "B"].reshape(-1, D).T),
                  A=_mat(g[a + "A"].transpose(0, 2, 1).reshape(-1, D)), bias=g[a + "bias"],
                  temp=_row(g[a + "temp"].reshape(1)), iota=_row(np.arange(PROTOS, dtype=np.float32)), ones=ones)
    a = "L3_xattn_"
    hd = 64
    q = g[a + "q_w"].transpose(1, 0, 2)
    kv = g[a + "kv_w"][:, 0]
    swap = np.concatenate([np.arange(hd // 2, hd), np.arange(hd // 2)])
    timescale = np.float32(10000.0) ** (np.float32(2.0 / hd) * np.arange(hd // 2, dtype=np.float32))

    def table(fn, positions, signed):
        radians = positions.astype(np.float32)[:, None] / timescale
        t = fn(radians).T.astype(np.float32)
        both = np.concatenate([-t if signed else t, t])
        return np.ascontiguousarray(np.concatenate([both, both]))

    qpos, kpos = np.arange(CTX, CTX + SEQ), np.arange(CTX)
    out[9] = dict(wq=_mat(q.reshape(D, -1)), wqs=_mat(q[:, :, swap].reshape(D, -1)),
                  wk=_mat(np.concatenate([kv[0], kv[0], kv[0][:, swap], kv[0][:, swap]], 1)),
                  wv=_mat(np.concatenate([kv[1], kv[1]], 1)), wo=_mat(g[a + "out_w"].reshape(-1, D)), rms=_col(g[a + "rms_scale"]),
                  cosq=table(np.cos, qpos, False), sinq=table(np.sin, qpos, True),
                  cosk=table(np.cos, kpos, False), sink=table(np.sin, kpos, True), ones=ones)



STATES = 16


def token_product(k, src, w, chunks, evacuate):
    nc = k.nc
    with nc.Block() as block:

        @block.tensor
        def _(pe):
            for t in range(TILES):
                if t >= 2:
                    pe.wait_ge(k.sem("tile_used"), t - 1)
                for c in range(chunks):
                    last = nc.tensor.matmul(k.banks[:, t % 2, 0:D], src[:, c, t * P:(t + 1) * P], w[:, c, :],
                                            start=(c == 0), stop=(c == chunks - 1))
                last.then_inc(k.sem("tile_ready"), 1)

        @block.vector
        def _(dve):
            link = linker(dve, k.sem("dve_step"))
            for t in range(TILES):
                dve.wait_ge(k.sem("tile_ready"), t + 1)
                evacuate(dve, link, t, k.banks[:, t % 2, 0:D])
    k.clear()


def short_conv(k, items):
    nc = k.nc
    n = len(items)
    ntaps = items[0][2].shape[1]
    with nc.Block() as block:

        @block.vector
        def _(dve):
            for x, _, taps, bias, tmp in items:
                if bias is None:
                    last = nc.vector.tensor_scalar(tmp, x, taps[:, ntaps - 1:ntaps], None, ALU.mult)
                else:
                    last = nc.vector.tensor_scalar(tmp, x, taps[:, ntaps - 1:ntaps], bias, ALU.mult, ALU.add)
                last.then_inc(k.sem("taps_done"), 1)
            for j in range(ntaps - 1):
                back = ntaps - 1 - j
                for c, (x, _, taps, _, tmp) in enumerate(items):
                    dve.wait_ge(k.sem("taps_done"), n * j + c + 1)
                    o = tmp.rearrange("p (b s) -> p b s", s=SEQ)
                    v = x.rearrange("p (b s) -> p b s", s=SEQ)
                    nc.vector.scalar_tensor_tensor(o[:, :, back:], v[:, :, :SEQ - back], taps[:, j:j + 1], o[:, :, back:],
                                                   ALU.mult, ALU.add).then_inc(k.sem("taps_done"), 1)

        @block.scalar
        def _(act):
            for c, (_, out, _, _, tmp) in enumerate(items):
                act.wait_ge(k.sem("taps_done"), n * (ntaps - 1) + c + 1)
                nc.scalar.activation(out, tmp, ACT.Silu)
    k.clear()


def selective_scan(k, ctx, chunks, u, delta, bc, a_log, skip, y):
    nc = k.nc
    NB, ND, NS, NP = 4, 3, 3, 3
    b_banks = 1 if chunks == 4 else 2
    c_banks = 8 - chunks - b_banks
    AHEAD = 3
    neg_a = k.sb(ctx, "neg_a", [P, chunks, STATES])
    decay = k.sb(ctx, "decay", [P, NB, BANK])
    drive = k.sb(ctx, "drive", [P, ND, BANK])
    brow = k.xn[:, :, :].rearrange("p t d -> p (t d)").rearrange("p (i n) -> p i n", i=AHEAD + 1)
    state = k.sb(ctx, "state", [P, NS, BANK])
    part = k.sb(ctx, "state_out", [P, NP, BANK])
    du = k.sb(ctx, "delta_u", [P, chunks, TOKENS])
    rows = 2 * STATES
    split = k.sb(ctx, "bc_split", [3 * rows, TOKENS], BF16)
    pick = k.sb(ctx, "row_pick", [3 * rows, rows], BF16)
    picks = part[0:3 * rows, 0, 0:rows]
    with nc.Block() as block:

        @block.scalar
        def _(act):
            nc.scalar.activation(neg_a[:, :, :], a_log, ACT.Exp).then_inc(k.sem("a_ready"), 1)

        @block.gpsimd
        def _(pool):
            nc.gpsimd.memset(decay[:, :, :], 0.0)

        @block.vector
        def _(dve):
            nc.vector.tensor_tensor(du[:, :, :], delta, u, ALU.mult)
            dve.wait_ge(k.sem("a_ready"), 1)
            nc.vector.tensor_scalar(neg_a[:, :, :], neg_a[:, :, :], -1.0, None, ALU.mult)
            link = linker(dve, k.sem("dve_step"))
            every = slice(0, 3 * rows)
            link(nc.vector.tensor_tensor(picks, k.ident[every, 0:rows], k.ident[every, rows:2 * rows], ALU.add))
            link(nc.vector.tensor_tensor(pick[:, :], picks, k.ident[every, 2 * rows:3 * rows], ALU.add))
            link(nc.vector.tensor_copy(split[:, :], bc[:, :]))
            for first in (1, 2):
                for i in range(first, 3):
                    at = slice(rows * i, rows * (i + 1))
                    link(nc.vector.tensor_tensor(bc[at, :], bc[at, :], split[at, :], ALU.subtract))
                    link(nc.vector.tensor_copy(split[at, :], bc[at, :]))
    k.clear()
    units = [(n, c) for n in range(STATES) for c in range(chunks)]

    def b_bank(n):
        return k.banks[:, chunks + n % b_banks, :]

    def c_bank(n):
        return k.banks[:, chunks + b_banks + n % c_banks, :]

    with nc.Fori(0, TOKENS // BANK) as h:
        cols = bass.ds(h * BANK, BANK)
        with nc.Block() as block:

            @block.tensor
            def _(pe):
                def spread(n):
                    for i, bank in enumerate((b_bank(n), c_bank(n))):
                        if i == 0 and n >= b_banks:
                            pe.wait_ge(k.sem("b_copied"), n - b_banks + 1)
                        if i == 1 and n >= c_banks:
                            pe.wait_ge(k.sem("parts_ready"), chunks * (n - c_banks + 1))
                        row = STATES * i + n
                        nc.tensor.matmul(bank, pick[:, row:row + 1].broadcast_to([3 * rows, P]), split[:, cols],
                                         start=True, stop=True).then_inc(k.sem("rows_spread"), 1)

                for n in range(AHEAD):
                    spread(n)
                for i, (n, c) in enumerate(units):
                    pe.wait_ge(k.sem("parts_ready"), i + 1)
                    nc.tensor.matmul(k.banks[:, c, :], k.ident[:, :], part[:, i % NP, :], start=(n == 0),
                                     stop=(n == STATES - 1)).then_inc(k.sem("parts_used"), 1)
                    if c == chunks - 1 and n + AHEAD < STATES:
                        spread(n + AHEAD)

            @block.scalar
            def _(act):
                def copy_b(n):
                    act.wait_ge(k.sem("rows_spread"), 2 * n + 1)
                    if n > AHEAD:
                        act.wait_ge(k.sem("drive_ready"), chunks * (n - AHEAD))
                    nc.scalar.copy(brow[:, n % (AHEAD + 1), :], b_bank(n)).then_inc(k.sem("b_copied"), 1)

                copy_b(0)
                for i, (n, c) in enumerate(units):
                    if c == 0 and n + 1 < STATES:
                        copy_b(n + 1)
                    if i >= NB:
                        act.wait_ge(k.sem("scanned"), i - NB + 1)
                    nc.scalar.activation(decay[:, i % NB, :].rearrange("p (b s) -> p b s", s=SEQ)[:, :, 1:],
                                         delta[:, c, cols].rearrange("p (b s) -> p b s", s=SEQ)[:, :, 1:], ACT.Exp,
                                         scale=neg_a[:, c, n:n + 1]).then_inc(k.sem("decay_ready"), 1)

            @block.gpsimd
            def _(pool):
                for i, (n, c) in enumerate(units):
                    if c == 0:
                        pool.wait_ge(k.sem("b_copied"), n + 1)
                    if i >= ND:
                        pool.wait_ge(k.sem("scanned"), i - ND + 1)
                    nc.gpsimd.tensor_tensor(drive[:, i % ND, :], du[:, c, cols], brow[:, n % (AHEAD + 1), :], ALU.mult).then_inc(k.sem("drive_ready"), 1)

            @block.vector
            def _(dve):
                for i in range(len(units) + 1):
                    if i < len(units):
                        dve.wait_ge(k.sem("decay_ready"), i + 1)
                        dve.wait_ge(k.sem("drive_ready"), i + 1)
                        if i >= NS:
                            dve.wait_ge(k.sem("parts_ready"), i - NS + 1)
                        nc.vector.tensor_tensor_scan(state[:, i % NS, :], decay[:, i % NB, :], drive[:, i % ND, :], 0.0, ALU.mult,
                                                     ALU.add).then_inc(k.sem("scanned"), 1)
                    if i:
                        m = i - 1
                        n = units[m][0]
                        dve.wait_ge(k.sem("scanned"), m + 1)
                        dve.wait_ge(k.sem("rows_spread"), 2 * n + 2)
                        if m >= NP:
                            dve.wait_ge(k.sem("parts_used"), m - NP + 1)
                        nc.vector.tensor_tensor(part[:, m % NP, :], state[:, m % NS, :], c_bank(n),
                                                ALU.mult).then_inc(k.sem("parts_ready"), 1)
                dve.wait_ge(k.sem("parts_used"), len(units))
                for c in range(chunks):
                    nc.vector.scalar_tensor_tensor(y[:, c, cols], u[:, c, cols], skip[:, c:c + 1], k.banks[:, c, :], ALU.mult, ALU.add)
        k.clear()


def layer10_attn(k, w):
    nc = k.nc
    chunks = 4
    with ExitStack() as ctx:
        u = k.sb(ctx, "u", [P, chunks, TOKENS])
        delta = k.sb(ctx, "delta", [P, chunks, TOKENS])
        dt = k.sb(ctx, "dt_low", [STATES, 1, TOKENS])
        bc = k.sb(ctx, "bc", [6 * STATES, TOKENS])
        project(k, [(w["win"], c * P, u[:, c, :], None, ACT.Identity) for c in range(chunks)])
        short_conv(k, [(u[:, c, :], u[:, c, :], w["taps"][:, c, :], w["cbias"][:, c:c + 1], delta[:, c, :]) for c in range(chunks)])
        project(k, [(w["wdt_low"], 0, dt[:, 0, :], None, ACT.Identity), (w["wbc"], 0, bc[:, :], None, ACT.Identity)], src=u, chunks=chunks)
        project(k, [(w["wdt"], c * P, delta[:, c, :], w["dtb"][:, c:c + 1], ACT.Identity) for c in range(chunks)], src=dt, chunks=1)
        with ExitStack() as room:
            e, low = (k.sb(room, n, [P, chunks, TOKENS]) for n in ("softplus_e", "softplus_low"))
            softplus(k, [(delta[:, c, :], e[:, c, :], low[:, c, :]) for c in range(chunks)])
        selective_scan(k, ctx, chunks, u[:, :, :], delta[:, :, :], bc, w["a_log"], w["skip"], u)

        def finish(dve, link, t, psum):
            nc.vector.tensor_tensor(k.x[:, t, :], k.x[:, t, :], psum, ALU.add).then_inc(k.sem("tile_used"), 1)

        token_product(k, u, w["wout"], chunks, finish)


def layer4_attn(k, w):
    nc = k.nc
    with ExitStack() as ctx:
        s = k.sb(ctx, "inner_stream", [P, TILES, D])
        with nc.Block() as block:

            @block.gpsimd
            def _(pool):
                nc.gpsimd.tensor_copy(s[:, :, :], k.xn[:, :, :])
        normalize(k, src=k.xn, scale=w["n1g"], shift=w["n1b"])
        with ExitStack() as inner:
            u = k.sb(inner, "u", [P, CHUNKS, TOKENS])
            z = k.sb(inner, "z", [P, CHUNKS, TOKENS])
            delta = k.sb(inner, "delta", [P, CHUNKS, TOKENS])
            dt = k.sb(inner, "dt_low", [64, 1, TOKENS])
            bc = k.sb(inner, "bc", [6 * STATES, TOKENS])
            hs = k.sb(inner, "mixed", [P, D])
            st = k.sb(inner, "mixed_stats", [P, 6])
            mv = k.sb(inner, "mixed_meanvar", [P, 2])
            project(k, [(w["win"], c * P, u[:, c, :], None, ACT.Identity) for c in range(CHUNKS)]
                    + [(w["win"], D + c * P, z[:, c, :], None, ACT.Silu) for c in range(CHUNKS)])
            short_conv(k, [(u[:, c, :], u[:, c, :], w["taps"][:, c, :], w["cbias"][:, c:c + 1], delta[:, c, :]) for c in range(CHUNKS)])
            project(k, [(w["wdt_low"], 0, dt[:, 0, :], None, ACT.Identity), (w["wbc"], 0, bc[:, :], None, ACT.Identity)], src=u)
            project(k, [(w["wdt"], c * P, delta[:, c, :], w["dtb"][:, c:c + 1], ACT.Identity) for c in range(CHUNKS)], src=dt, chunks=1)
            with ExitStack() as room:
                e, low = (k.sb(room, n, [P, CHUNKS, TOKENS]) for n in ("softplus_e", "softplus_low"))
                softplus(k, [(delta[:, c, :], e[:, c, :], low[:, c, :]) for c in range(CHUNKS)])
            selective_scan(k, inner, CHUNKS, u[:, :, :], delta[:, :, :], bc, w["a_log"], w["skip"], u)
            with nc.Block() as block:

                @block.vector
                def _(dve):
                    nc.vector.tensor_tensor(u[:, :, :], u[:, :, :], z[:, :, :], ALU.mult)
            h_tok = k.xn

            def keep(dve, link, t, psum):
                nc.vector.tensor_copy(h_tok[:, t, :], psum).then_inc(k.sem("tile_used"), 1)

            token_product(k, u, w["wout"], CHUNKS, keep)
        normalize(k, src=k.xn, turn=False)
        with nc.Block() as block:

            @block.vector
            def _(dve):
                link = linker(dve, k.sem("dve_step"))
                for op, row in ((ALU.mult, w["mg"]), (ALU.add, w["mb"])):
                    link(nc.vector.tensor_tensor(k.xn[:, :, :], k.xn[:, :, :], row.unsqueeze(1).broadcast_to([P, TILES, D]), op))
                nc.vector.tensor_tensor(s[:, :, :], s[:, :, :], k.xn[:, :, :], ALU.add)
        k.clear()
        normalize(k, src=s, scale=w["n2g"], shift=w["n2b"])
        hidden = k.sb(ctx, "leaky_hidden", [P, HIDDEN // P, TOKENS])
        project(k, [(w["w1"], c * P, hidden[:, c, :], None, ACT.Identity) for c in range(HIDDEN // P)],
                then=lambda part: nc.vector.scalar_tensor_tensor(part, part, 0.01, part, ALU.mult, ALU.max))

        def add_s(dve, link, t, psum):
            nc.vector.tensor_tensor(s[:, t, :], s[:, t, :], psum, ALU.add).then_inc(k.sem("tile_used"), 1)

        token_product(k, hidden, w["w2"], HIDDEN // P, add_s)
        normalize(k, src=s, scale=w["n3g"], shift=w["n3b"])

        def last(dve, link, t, psum):
            nc.vector.tensor_tensor(s[:, t, :], s[:, t, :], psum, ALU.add).then_inc(k.sem("tile_used"), 1)
            dve.wait_ge(k.sem("tile_used"), t + 1)
            link(nc.vector.tensor_tensor(s[:, t, :], s[:, t, :], w["feb"], ALU.add))
            nc.vector.tensor_tensor(k.x[:, t, :], k.x[:, t, :], s[:, t, :], ALU.add)

        token_product(k, k.xnT, w["fe"], CHUNKS, last)


BUILDERS |= {4: layer4_attn, 10: layer10_attn}


def layout_scans(g, out):
    a = "L1_attn_"
    xp = g[a + "x_proj_w"].T
    out[4] = dict(win=_mat(g[a + "in_proj_w"].T), taps=g[a + "conv_w"].reshape(-1, P, 2).transpose(1, 0, 2), cbias=_col(g[a + "conv_b"]),
                  wdt_low=_mat(xp[:, :64]), wbc=_mat(np.tile(xp[:, 64:], (1, 3))), wdt=g[a + "dt_proj_w"].T[:, None, :], dtb=_col(g[a + "dt_proj_b"]),
                  a_log=g[a + "A_log"].reshape(-1, P, STATES).transpose(1, 0, 2), skip=_col(g[a + "Dp"]), wout=_mat(g[a + "out_proj_w"].T),
                  n1g=_col(g[a + "n1_g"]), n1b=_col(g[a + "n1_b"]), n2g=_col(g[a + "n2_g"]), n2b=_col(g[a + "n2_b"]),
                  n3g=_col(g[a + "n3_g"]), n3b=_col(g[a + "n3_b"]), mg=_row(g[a + "mnorm_g"]), mb=_row(g[a + "mnorm_b"]),
                  w1=_mat(g[a + "ffn_w1"].T), w2=_mat(g[a + "ffn_w2"].T), fe=_mat(g[a + "fe_w"].T), feb=_row(g[a + "fe_b"]))
    a = "L3_attn_"
    wx = g[a + "W_x"]
    out[10] = dict(win=_mat(g[a + "W_in"]), taps=g[a + "conv_w"].reshape(-1, P, 4).transpose(1, 0, 2), cbias=_col(g[a + "conv_b"]),
                   wdt_low=_mat(wx[:, :16]), wbc=_mat(np.tile(wx[:, 16:], (1, 3))), wdt=g[a + "W_dt"][:, None, :], dtb=_col(g[a + "b_dt"]),
                   a_log=g[a + "A_log"].reshape(-1, P, STATES).transpose(1, 0, 2), skip=_col(g[a + "D"]), wout=_mat(g[a + "W_out"]))



DH = 4
HD = D // DH
DCHUNK = 32
LEVELS = 5


def unit_heads(k, xs, sq, same64, eps):
    nc = k.nc
    parts = [(x[:, c, h * BANK:(h + 1) * BANK], sq[:, n * CHUNKS + c, h * BANK:(h + 1) * BANK])
             for n, x in enumerate(xs) for c in range(CHUNKS) for h in range(TOKENS // BANK)]
    with nc.Block() as block:

        @block.gpsimd
        def _(pool):
            nc.gpsimd.memset(eps, 1e-6).then_inc(k.sem("eps_ready"), 1)
            for n, (x, s) in enumerate(parts):
                pool.wait_ge(k.sem("inverse_ready"), n + 1)
                nc.gpsimd.tensor_tensor(x, x, s, ALU.mult)

        @block.scalar
        def _(act):
            for x, s in parts:
                nc.scalar.activation(s, x, ACT.Square).then_inc(k.sem("squares_ready"), 1)
            act.wait_ge(k.sem("eps_ready"), 1)
            for n, (x, s) in enumerate(parts):
                act.wait_ge(k.sem("sums_in_psum"), n + 1)
                nc.scalar.activation(s, k.banks[:, n, :], ACT.Sqrt, bias=eps).then_inc(k.sem("norm_ready"), 1)

        @block.tensor
        def _(pe):
            for n, (x, s) in enumerate(parts):
                pe.wait_ge(k.sem("squares_ready"), n + 1)
                nc.tensor.matmul(k.banks[:, n, :], same64, s, start=True, stop=True).then_inc(k.sem("sums_in_psum"), 1)

        @block.vector
        def _(dve):
            for n, (x, s) in enumerate(parts):
                dve.wait_ge(k.sem("norm_ready"), n + 1)
                nc.vector.reciprocal(s, s).then_inc(k.sem("inverse_ready"), 1)
    k.clear()


def layer7_attn(k, w):
    nc = k.nc
    with ExitStack() as ctx:
        q, kk, v, kb, vb = (k.sb(ctx, "delta_" + n, [P, CHUNKS, TOKENS]) for n in ("q", "k", "v", "kb", "vb"))
        mixed = k.xn[:, :, :].rearrange("p t d -> p (t d)").rearrange("p (c n) -> p c n", c=CHUNKS)
        with ExitStack() as inner:
            cat = k.sb(inner, "conv_cat", [P, 6, TOKENS])
            DIAGS = 8
            diag = k.sb(inner, "tap_diagonals", [P, DIAGS, P])
            eps = k.sb(inner, "unit_eps", [P, 1])
            project(k, [(w[n], c * P, o[:, c, :], None, f) for n, o, f in
                        (("wq", q, ACT.Identity), ("wk", kk, ACT.Identity), ("wv", v, ACT.Identity), ("wb", vb, ACT.Sigmoid))
                        for c in range(CHUNKS)])
            short_conv(k, [(x[:, c, :], x[:, c, :], taps[:, c, :], None, cat[:, 2 * i + c, :])
                           for i, (x, taps) in enumerate(((v, w["tv"]), (q, w["tq"]), (kk, w["tk"]))) for c in range(CHUNKS)])
            unit_heads(k, (q, kk), cat[:, 0:4, :], w["same64"], eps[:, 0:1])
            pe_taps = [(g, c, j) for g, n in ((0, 3), (1, 15)) for c in range(CHUNKS) for j in range(n)]
            taps_of = (w["t3"], w["t15"])
            with nc.Block() as block:

                @block.gpsimd
                def _(pool):
                    nc.gpsimd.tensor_tensor(kb[:, :, :], kk[:, :, :], vb[:, :, :], ALU.mult).then_inc(k.sem("kb_ready"), 1)
                    pool.wait_ge(k.sem("kb_ready"), 1)
                    nc.gpsimd.tensor_tensor(vb[:, :, :], v[:, :, :], vb[:, :, :], ALU.mult)

                @block.scalar
                def _(act):
                    for n, (g, c, j) in enumerate(pe_taps):
                        if n >= DIAGS:
                            act.wait_ge(k.sem("diag_used"), n - DIAGS + 1)
                        last = taps_of[g].shape[2] - 1
                        nc.scalar.activation(diag[:, n % DIAGS, :], k.ident[:, :], ACT.Copy,
                                             scale=taps_of[g][:, c, last - j:last - j + 1]).then_inc(k.sem("diag_ready"), 1)
                    for g in range(2):
                        for c in range(CHUNKS):
                            act.wait_ge(k.sem("diag_used"), sum(1 for tap in pe_taps if tap[0:2] <= (g, c)))
                            nc.scalar.copy(cat[:, 2 * g + c, :], k.banks[:, 4 * g + 2 * c:4 * g + 2 * c + 2, :].rearrange("p b n -> p (b n)"))

                @block.tensor
                def _(pe):
                    for n, (g, c, j) in enumerate(pe_taps):
                        pe.wait_ge(k.sem("diag_ready"), n + 1)
                        ntaps = taps_of[g].shape[2]
                        for h in range(TOKENS // BANK):
                            o = k.banks[:, 4 * g + 2 * c + h, :].rearrange("p (b s) -> p b s", s=SEQ)
                            x = v[:, c, h * BANK:(h + 1) * BANK].rearrange("p (b s) -> p b s", s=SEQ)
                            last = nc.tensor.matmul(o[:, :, j:], diag[:, n % DIAGS, :], x[:, :, :SEQ - j], start=(j == 0), stop=(j == ntaps - 1))
                        last.then_inc(k.sem("diag_used"), 1)

                @block.vector
                def _(dve):
                    n = w["t31"].shape[2]
                    for j in range(n):
                        for c in range(CHUNKS):
                            o = cat[:, 4 + c, :].rearrange("p (b s) -> p b s", s=SEQ)
                            x = v[:, c, :].rearrange("p (b s) -> p b s", s=SEQ)
                            tap = w["t31"][:, c, n - 1 - j:n - j]
                            done = k.sem(f"conv{c}")
                            if j == 0:
                                nc.vector.tensor_scalar(o, x, tap, None, ALU.mult).then_inc(done, 1)
                            else:
                                dve.wait_ge(done, j)
                                nc.vector.scalar_tensor_tensor(o[:, :, j:], x[:, :, :SEQ - j], tap, o[:, :, j:], ALU.mult,
                                                               ALU.add).then_inc(done, 1)
            k.clear()
            with nc.Block() as block:

                @block.tensor
                def _(pe):
                    for c in range(CHUNKS):
                        for h in range(TOKENS // BANK):
                            for g in range(3):
                                last = nc.tensor.matmul(k.banks[:, 2 * c + h, :], w["mix"][:, 3 * c + g, :], cat[:, 3 * c + g, h * BANK:(h + 1) * BANK],
                                                        start=(g == 0), stop=(g == 2))
                            last.then_inc(k.sem("mix_ready"), 1)

                @block.scalar
                def _(act):
                    for n in range(4):
                        act.wait_ge(k.sem("mix_ready"), n + 1)
                        nc.scalar.copy(mixed[:, n // 2, (n % 2) * BANK:(n % 2 + 1) * BANK], k.banks[:, n, :])
            k.clear()
        delta_tiles(k, ctx, w, (q, kk, kb, vb, v, mixed))


DELTA_COUNTS = dict(copied=4, turned=1, gram_in_psum=2, local_in_psum=2, gram_copied=2, tok_ready=2, level_ready=5, product_ready=5,
                    T_ready=4, TT_ready=5, U_ready=4, stepT_ready=4, step_ready=3, local_ready=2, two_ready=6, q_turned=1, u_in_psum=1,
                    w_in_psum=1, by_seq_copied=2, u_copied=1, state_in_psum=1, state_copied=1, ws_in_psum=1, u_final=1,
                    delta_in_psum=1, delta_read=1, late_copied=2, v_turned=1, conv_in_psum=1, conv_ready=2, means_ready=1,
                    means_turned=1, meansT_ready=1, gate_in_psum=1, gate_hidden_ready=4, logits_in_psum=1, shifted=1, gate_exp=1,
                    mean_square=1, root=1, out_ready=1, out_turned=1, outT_ready=1, branch_ready=1, added=1)


def alternate(rule, mix, unroll):
    for j in range(unroll + 1):
        for _ in zip_longest(rule(j) if j < unroll else (), mix(j - 1) if j else ()):
            pass


def delta_tiles(k, ctx, w, sources):
    nc = k.nc
    unroll = 4
    here = k.sb(ctx, "tile_feat", [P, 4, CHUNKS, P])
    late = k.sb(ctx, "tile_feat_late", [P, 2, CHUNKS, P])
    tok = k.sb(ctx, "tile_tok", [P, 4, DH, HD])
    gram = k.sb(ctx, "gramT", [P, DH, P])
    level = k.sb(ctx, "gramT_level", [P, 2, DH, P])
    local = k.sb(ctx, "localT", [P, DH, P])
    T, TT, U = (k.sb(ctx, n, [P, DH, P]) for n in ("inverse", "inverseT", "level_product"))
    two = k.sb(ctx, "by_sequence", [P, 3, DH, PER_TILE, HD])
    qT2, wT2 = gram, T
    u = k.sb(ctx, "delta_u", [P, DH, HD])
    S = k.sb(ctx, "delta_state", [P, DH, HD])
    parts = k.sb(ctx, "mix_parts", [P, 3, DH, HD])
    F = k.sb(ctx, "head_means", [P, 12])
    FT = k.sb(ctx, "head_meansT", [12, P])
    hdn = k.sb(ctx, "gate_hidden", [P, 4, P])
    lg = k.sb(ctx, "gate_logits", [P, DH, 3])
    gm = k.sb(ctx, "gate_col", [P, DH])
    o = k.sb(ctx, "mix_out", [P, DH, HD])
    o2 = k.sb(ctx, "mix_work", [P, 3, DH, HD])
    oT = k.sb(ctx, "mix_outT", [P, CHUNKS, P])
    Q, K_, KB, VB, V_, MIX = range(6)
    B = k.banks

    def heads(bank, width):
        return B[:, bank, 0:DH * width].rearrange("p (h n) -> p h n", h=DH)

    def pair(bank, i):
        return B[:, bank, 2 * P * i:2 * P * (i + 1)].rearrange("p (h n) -> p h n", h=2)

    def waiter(eng, j):
        def wait(name, n):
            eng.wait_ge(k.sem(name), DELTA_COUNTS[name] * j + n)

        def before(name):
            if j:
                eng.wait_ge(k.sem(name), DELTA_COUNTS[name] * j)
        return wait, before

    with nc.Fori(0, TILES // unroll) as t:

        def cols(j):
            return bass.ds((t * unroll + j) * P, P)

        with nc.Block() as block:

            @block.gpsimd
            def _(pool):
                def rule(j):
                    wait, before = waiter(pool, j)
                    yield
                    wait("gram_copied", 2)
                    before("product_ready")
                    for s in range(LEVELS):
                        if s >= 2:
                            wait("product_ready", s - 1)
                        if s == 2:
                            wait("TT_ready", 1)
                        nc.gpsimd.tensor_tensor(level[:, s % 2, :, :], gram[:, :, :], w["levels"][:, s, :].unsqueeze(1).broadcast_to([P, DH, P]),
                                                ALU.mult).then_inc(k.sem("level_ready"), 1)
                        if s == 1:
                            wait("tok_ready", 2)
                            before("state_in_psum")
                            for i, (src, ind) in enumerate(((Q, "second"), (KB, "second"), (K_, "first"))):
                                for b in range(PER_TILE):
                                    nc.gpsimd.tensor_scalar(two[:, i, :, b, :], tok[:, src, :, :], w[ind][:, b:b + 1], None,
                                                            ALU.mult).then_inc(k.sem("two_ready"), 1)
                        yield

                def mix(j):
                    wait, before = waiter(pool, j)
                    before("conv_in_psum")
                    for i in range(2):
                        nc.gpsimd.tensor_copy(late[:, i, :, :], sources[V_ + i][:, :, cols(j)]).then_inc(k.sem("late_copied"), 1)
                    yield

                alternate(rule, mix, unroll)

            @block.tensor
            def _(pe):
                def rule(j):
                    wait, before = waiter(pe, j)
                    wait("copied", 4)
                    for i in range(4):
                        for c in range(CHUNKS):
                            last = nc.tensor.transpose(B[:, i // 2, ((i % 2) * 2 + c) * P:((i % 2) * 2 + c + 1) * P], here[:, i, c, :], k.ident[:, :])
                    last.then_inc(k.sem("turned"), 1)
                    for half, rhs, ready in ((0, KB, "gram_in_psum"), (1, Q, "local_in_psum")):
                        for h in range(DH):
                            part = slice(HD * (h % 2), HD * (h % 2) + HD)
                            last = nc.tensor.matmul(pair(3 + 2 * (h % 2), half)[:, h // 2, :], here[part, K_, h // 2, :],
                                                    here[part, rhs, h // 2, :], start=True, stop=True)
                            if h >= DH - 2:
                                last.then_inc(k.sem(ready), 1)
                    yield
                    before("delta_read")
                    for s in range(LEVELS):
                        wait("level_ready", s + 1)
                        if s:
                            wait("T_ready", s)
                            wait("local_ready", 2)
                        for h in range(DH):
                            last = nc.tensor.matmul(B[:, 5 if s else 6, h * P:(h + 1) * P], level[:, s % 2, h, :],
                                                    T[:, h, :] if s else k.ident[:, :], start=True, stop=True)
                        last.then_inc(k.sem("product_ready"), 1)
                        if s:
                            wait("U_ready", s)
                            wait("TT_ready", s)
                            if s < LEVELS - 1:
                                for h in range(DH):
                                    last = nc.tensor.matmul(B[:, 6, h * P:(h + 1) * P], TT[:, h, :], U[:, h, :], start=True, stop=True)
                                last.then_inc(k.sem("step_ready"), 1)
                            for h in range(DH):
                                last = nc.tensor.matmul(B[:, 7, h * P:(h + 1) * P], U[:, h, :], TT[:, h, :], start=True, stop=True)
                            last.then_inc(k.sem("stepT_ready"), 1)
                        yield
                    wait("two_ready", 6)
                    for h in range(DH):
                        last = nc.tensor.transpose(B[:, 0, h * P:(h + 1) * P], two[:, 0, h, :, :].rearrange("p b n -> p (b n)"), k.ident[:, :])
                    last.then_inc(k.sem("q_turned"), 1)
                    wait("TT_ready", LEVELS)
                    for h in range(DH):
                        last = nc.tensor.matmul(B[:, 3, h * HD:(h + 1) * HD], TT[:, h, :], tok[:, VB, h, :], start=True, stop=True)
                    last.then_inc(k.sem("u_in_psum"), 1)
                    for h in range(DH):
                        last = nc.tensor.matmul(B[:, 1, h * P:(h + 1) * P], two[:, 1, h, :, :].rearrange("p b n -> p (b n)"), TT[:, h, :],
                                                start=True, stop=True)
                    last.then_inc(k.sem("w_in_psum"), 1)
                    wait("u_copied", 1)
                    for h in range(DH):
                        last = nc.tensor.matmul(B[:, 3, h * HD:(h + 1) * HD], two[:, 2, h, :, :].rearrange("p b n -> p (b n)"), u[:, h, :],
                                                start=True, stop=True)
                    last.then_inc(k.sem("state_in_psum"), 1)
                    yield
                    wait("state_copied", 1)
                    wait("by_seq_copied", 2)
                    for h in range(DH):
                        last = nc.tensor.matmul(B[:, 5, h * HD:(h + 1) * HD], wT2[:, h, :], S[:, h, :], start=True, stop=True)
                    last.then_inc(k.sem("ws_in_psum"), 1)
                    yield
                    wait("u_final", 1)
                    for h in range(DH):
                        nc.tensor.matmul(B[:, 6, h * HD:(h + 1) * HD], qT2[:, h, :], S[:, h, :], start=True, stop=False)
                        last = nc.tensor.matmul(B[:, 6, h * HD:(h + 1) * HD], local[:, h, :], u[:, h, :], start=False, stop=True)
                    last.then_inc(k.sem("delta_in_psum"), 1)
                    yield

                def mix(j):
                    wait, before = waiter(pe, j)
                    wait("late_copied", 2)
                    before("added")
                    for c in range(CHUNKS):
                        last = nc.tensor.transpose(B[:, 2, c * P:(c + 1) * P], late[:, 0, c, :], k.ident[:, :])
                    last.then_inc(k.sem("v_turned"), 1)
                    for c in range(CHUNKS):
                        last = nc.tensor.matmul(B[:, 4, 0:D], late[:, 1, c, :], w["mixer"][:, c, :], start=(c == 0), stop=(c == CHUNKS - 1))
                    last.then_inc(k.sem("conv_in_psum"), 1)
                    yield
                    yield
                    wait("means_ready", 1)
                    wait("conv_ready", 2)
                    nc.tensor.transpose(B[0:12, 2, 0:P], F[:, :], k.ident[:, :]).then_inc(k.sem("means_turned"), 1)
                    yield
                    wait("meansT_ready", 1)
                    for m in range(4):
                        for c in range(CHUNKS):
                            nc.tensor.matmul(B[:, 4, m * P:(m + 1) * P], w["f1"][:, c, m * P:(m + 1) * P], k.xnT[:, c, cols(j)],
                                             start=(c == 0), stop=False)
                        last = nc.tensor.matmul(B[:, 4, m * P:(m + 1) * P], w["f1m"][:, m * P:(m + 1) * P], FT[:, :], start=False, stop=True)
                    last.then_inc(k.sem("gate_in_psum"), 1)
                    yield
                    wait("gate_hidden_ready", 4)
                    for m in range(4):
                        last = nc.tensor.matmul(B[:, 2, 0:12], hdn[:, m, :], w["f2"][:, m, :], start=(m == 0), stop=(m == 3))
                    last.then_inc(k.sem("logits_in_psum"), 1)
                    yield
                    yield
                    yield
                    wait("out_ready", 1)
                    for c in range(CHUNKS):
                        last = nc.tensor.transpose(B[:, 4, c * P:(c + 1) * P], o[:, 2 * c:2 * c + 2, :].rearrange("p h n -> p (h n)"), k.ident[:, :])
                    last.then_inc(k.sem("out_turned"), 1)
                    yield
                    wait("outT_ready", 1)
                    for c in range(CHUNKS):
                        last = nc.tensor.matmul(B[:, 2, 0:D], oT[:, c, :], w["wo"][:, c, :], start=(c == 0), stop=(c == CHUNKS - 1))
                    last.then_inc(k.sem("branch_ready"), 1)
                    yield

                alternate(rule, mix, unroll)

            @block.scalar
            def _(act):
                def rule(j):
                    wait, before = waiter(act, j)
                    before("delta_in_psum")
                    for i in range(4):
                        nc.scalar.copy(here[:, i, :, :], sources[i][:, :, cols(j)]).then_inc(k.sem("copied"), 1)
                    yield
                    wait("local_in_psum", 2)
                    for r in range(2):
                        nc.scalar.copy(gram[:, r::2, :], pair(3 + 2 * r, 0)).then_inc(k.sem("gram_copied"), 1)
                    for i in range(2):
                        nc.scalar.copy(tok[:, 2 * i:2 * i + 2, :, :].rearrange("p a h n -> p (a h n)"), B[:, i, :]).then_inc(k.sem("tok_ready"), 1)
                    yield
                    for s in range(1, LEVELS):
                        wait("product_ready", s + 1)
                        nc.scalar.copy(U[:, :, :], heads(5, P)).then_inc(k.sem("U_ready"), 1)
                        yield
                    wait("q_turned", 1)
                    nc.scalar.copy(qT2[:, :, :], heads(0, P)).then_inc(k.sem("by_seq_copied"), 1)
                    wait("w_in_psum", 1)
                    nc.scalar.copy(wT2[:, :, :], heads(1, P)).then_inc(k.sem("by_seq_copied"), 1)
                    wait("state_in_psum", 1)
                    nc.scalar.copy(S[:, :, :], heads(3, HD)).then_inc(k.sem("state_copied"), 1)
                    yield

                def mix(j):
                    wait, before = waiter(act, j)
                    wait("v_turned", 1)
                    nc.scalar.copy(parts[:, 2, :, :], heads(2, HD)).then_inc(k.sem("conv_ready"), 1)
                    wait("conv_in_psum", 1)
                    nc.scalar.copy(parts[:, 0, :, :], heads(4, HD)).then_inc(k.sem("conv_ready"), 1)
                    yield
                    yield
                    wait("means_turned", 1)
                    nc.scalar.copy(FT[:, :], B[0:12, 2, 0:P]).then_inc(k.sem("meansT_ready"), 1)
                    yield
                    wait("gate_in_psum", 1)
                    for m in range(4):
                        nc.scalar.activation(hdn[:, m, :], B[:, 4, m * P:(m + 1) * P], ACT.Gelu,
                                             bias=w["f1b"][:, m:m + 1]).then_inc(k.sem("gate_hidden_ready"), 1)
                    yield
                    wait("shifted", 1)
                    nc.scalar.activation(lg[:, :, :], lg[:, :, :], ACT.Exp).then_inc(k.sem("gate_exp"), 1)
                    yield
                    yield
                    wait("mean_square", 1)
                    nc.scalar.activation(gm[:, :], gm[:, :], ACT.Sqrt).then_inc(k.sem("root"), 1)
                    yield
                    wait("out_turned", 1)
                    before("branch_ready")
                    nc.scalar.copy(oT[:, :, :], B[:, 4, 0:D].rearrange("p (c n) -> p c n", n=P)).then_inc(k.sem("outT_ready"), 1)
                    yield

                alternate(rule, mix, unroll)

            @block.vector
            def _(dve):
                link = linker(dve, k.sem("dve_step"))
                eye = k.ident[:, :].unsqueeze(1).broadcast_to([P, DH, P])

                def rule(j):
                    wait, before = waiter(dve, j)
                    yield
                    wait("level_ready", 1)
                    nc.vector.tensor_tensor(TT[:, :, :], eye, level[:, 0, :, :], ALU.subtract).then_inc(k.sem("TT_ready"), 1)
                    wait("product_ready", 1)
                    nc.vector.tensor_tensor(T[:, :, :], eye, heads(6, P), ALU.subtract).then_inc(k.sem("T_ready"), 1)
                    wait("local_in_psum", 2)
                    wait("gram_copied", 2)
                    for r in range(2):
                        nc.vector.tensor_tensor(local[:, r::2, :], pair(3 + 2 * r, 1),
                                                w["inclusive"].unsqueeze(1).broadcast_to([P, 2, P]), ALU.mult).then_inc(k.sem("local_ready"), 1)
                    yield
                    for s in range(1, LEVELS):
                        if s < LEVELS - 1:
                            wait("step_ready", s)
                            wait("T_ready", s)
                            nc.vector.tensor_tensor(T[:, :, :], T[:, :, :], heads(6, P), ALU.subtract).then_inc(k.sem("T_ready"), 1)
                        wait("stepT_ready", s)
                        wait("TT_ready", s)
                        nc.vector.tensor_tensor(TT[:, :, :], TT[:, :, :], heads(7, P), ALU.subtract).then_inc(k.sem("TT_ready"), 1)
                        yield
                    wait("u_in_psum", 1)
                    nc.vector.tensor_copy(u[:, :, :], heads(3, HD)).then_inc(k.sem("u_copied"), 1)
                    yield
                    wait("u_copied", 1)
                    wait("ws_in_psum", 1)
                    nc.vector.tensor_tensor(u[:, :, :], u[:, :, :], heads(5, HD), ALU.subtract).then_inc(k.sem("u_final"), 1)
                    yield
                    wait("delta_in_psum", 1)
                    nc.vector.tensor_copy(parts[:, 1, :, :], heads(6, HD)).then_inc(k.sem("delta_read"), 1)
                    yield

                def mix(j):
                    wait, before = waiter(dve, j)
                    yield
                    wait("delta_read", 1)
                    wait("conv_ready", 2)
                    link(nc.vector.tensor_reduce(F[:, :], parts[:, :, :, :].rearrange("p i h n -> p (i h) n"), AX_X, ALU.add,
                                                 apply_absolute_value=True))
                    nc.vector.tensor_scalar(F[:, :], F[:, :], 1.0 / HD, None, ALU.mult).then_inc(k.sem("means_ready"), 1)
                    yield
                    yield
                    yield
                    wait("logits_in_psum", 1)
                    link(nc.vector.tensor_tensor(lg[:, :, :].rearrange("p h n -> p (h n)"), B[:, 2, 0:12], w["f2b"], ALU.add))
                    link(nc.vector.reduce_max(gm[:, :], lg[:, :, :], AX_X))
                    nc.vector.tensor_tensor(lg[:, :, :], lg[:, :, :], gm[:, :].unsqueeze(2).broadcast_to([P, DH, 3]),
                                            ALU.subtract).then_inc(k.sem("shifted"), 1)
                    yield
                    wait("gate_exp", 1)
                    link(nc.vector.reduce_sum(gm[:, :], lg[:, :, :], AX_X))
                    link(nc.vector.reciprocal(gm[:, :], gm[:, :]))
                    link(nc.vector.tensor_tensor(lg[:, :, :], lg[:, :, :], gm[:, :].unsqueeze(2).broadcast_to([P, DH, 3]), ALU.mult))
                    link(nc.vector.tensor_tensor(o2[:, :, :, :], parts[:, :, :, :],
                                                 lg[:, :, :].rearrange("p h i -> p i h").unsqueeze(3).broadcast_to([P, 3, DH, HD]), ALU.mult))
                    yield
                    link(nc.vector.tensor_tensor(o[:, :, :], o2[:, 0, :, :], o2[:, 1, :, :], ALU.add))
                    link(nc.vector.tensor_tensor(o[:, :, :], o[:, :, :], o2[:, 2, :, :], ALU.add))
                    link(nc.vector.tensor_tensor(o2[:, 0, :, :], o[:, :, :], o[:, :, :], ALU.mult))
                    link(nc.vector.reduce_sum(gm[:, :], o2[:, 0, :, :], AX_X))
                    nc.vector.tensor_scalar(gm[:, :], gm[:, :], 1.0 / HD, 1e-5, ALU.mult, ALU.add).then_inc(k.sem("mean_square"), 1)
                    yield
                    wait("root", 1)
                    link(nc.vector.reciprocal(gm[:, :], gm[:, :]))
                    link(nc.vector.tensor_tensor(o[:, :, :], o[:, :, :], gm[:, :].unsqueeze(2).broadcast_to([P, DH, HD]), ALU.mult))
                    nc.vector.tensor_tensor(o[:, :, :], o[:, :, :], w["onorm"].unsqueeze(1).broadcast_to([P, DH, HD]),
                                            ALU.mult).then_inc(k.sem("out_ready"), 1)
                    yield
                    wait("branch_ready", 1)
                    dst = k.x[:, t * unroll + j, :]
                    nc.vector.tensor_tensor(dst, dst, B[:, 2, 0:D], ALU.add).then_inc(k.sem("added"), 1)
                    yield

                alternate(rule, mix, unroll)
        k.clear()


BUILDERS |= {7: layer7_attn}


def layout_delta(g, out):
    a = "L2_attn_"
    i = np.arange(P)
    same = i[:, None] // DCHUNK == i[None, :] // DCHUNK
    levels = []
    for s in range(LEVELS):
        r = 2 ** s
        levels.append((i[None, :] > i[:, None]) & (i[:, None] // (2 * r) == i[None, :] // (2 * r)) & (i[:, None] // r != i[None, :] // r))
    levels = np.stack(levels, 1).astype(np.float32)
    inclusive = ((i[None, :] >= i[:, None]) & same).astype(np.float32)
    seqs, second = i // SEQ, (i % SEQ) // DCHUNK
    ind = {n: np.stack([((seqs == b) & (second == s)) for b in range(PER_TILE)], 1).astype(np.float32) for n, s in (("first", 0), ("second", 1))}
    mix = np.zeros((6, P, P), np.float32)
    km = g[a + "kernel_mix_w"]
    for h in range(DH):
        for r0 in range(0, 192, 64):
            row = 192 * h + r0
            mix[row // P, row % P:row % P + 64, HD * (h % 2):HD * (h % 2) + HD] = km[r0:r0 + 64]

    def taps(n):
        wt = g[a + n]
        return wt.reshape(-1, P, wt.shape[1]).transpose(1, 0, 2)

    f1 = g[a + "fusion_w1"]
    out[7] = dict(wq=_mat(g[a + "Wq"]), wk=_mat(g[a + "Wk"]), wv=_mat(g[a + "Wv"]), wb=_mat(np.repeat(g[a + "Wb"], HD, axis=1)),
                  tq=taps("conv_q_w"), tk=taps("conv_k_w"), tv=taps("conv_v_w"), t3=taps("ms_w3"), t15=taps("ms_w15"), t31=taps("ms_w31"),
                  mix=mix.transpose(1, 0, 2), mixer=_mat(g[a + "channel_mixer_w"]), f1=_mat(f1[:D]), f1m=f1[D:], f1b=_col(g[a + "fusion_b1"]),
                  f2=_mat(g[a + "fusion_w2"]), f2b=_row(g[a + "fusion_b2"]), onorm=_row(g[a + "o_norm_w"]), wo=_mat(g[a + "Wo"]),
                  same64=(i[:, None] // HD == i[None, :] // HD).astype(np.float32), levels=levels, inclusive=inclusive, **ind)


def build(nc, dram, places, layers):
    with ExitStack() as ctx:
        k = Core(nc, ctx, dram)
        loaded = ctx.enter_context(nc.semaphore("weights_loaded"))
        first = ctx.enter_context(nc.semaphore("first_loads"))
        rest = ctx.enter_context(nc.semaphore("rest_loads"))
        stored = ctx.enter_context(nc.semaphore("out_stored"))
        with nc.Block() as block:

            @block.sync
            def _(sp):
                sp.dma_start(k.x[:, :, :], dram["x"].rearrange("(t c) s d -> (c s) t d", c=PER_TILE)).then_inc(first, 16)
                sp.dma_start(k.ident[:, :], dram["ident"]).then_inc(first, 16)
                for name, table in (("hmask16", k.hmask16), ("hmask64", k.hmask64), ("fold", k.fold)):
                    sp.dma_start(table[:, :], dram[name]).then_inc(rest, 16)
                n = dram[f"w{layers[0]}"].shape[1]
                sp.dma_start(k.weights[layers[0] % 2][:, 0:n], dram[f"w{layers[0]}"]).then_inc(loaded, 16)
                sp.dma_start(k.ctxT[:, :, :], dram["ctxT"].rearrange("(c p) n -> p c n", p=P)).then_inc(rest, 16)
                sp.wait_ge(first, 2 * 16)
        for i, layer in enumerate(layers):
            k.prefix = f"sub{layer}_"
            normalize(k)
            with nc.Block() as block:

                @block.sync
                def _(sp):
                    sp.wait_ge(loaded, 16 * (i + 1))
                    if i == 0:
                        sp.wait_ge(rest, 4 * 16)
                    if i + 1 < len(layers):
                        n = dram[f"w{layers[i + 1]}"].shape[1]
                        sp.dma_start(k.weights[layers[i + 1] % 2][:, 0:n], dram[f"w{layers[i + 1]}"]).then_inc(loaded, 16)
            w = {}
            for name, (at, shape) in places[layer].items():
                size = int(np.prod(shape[1:]))
                v = k.weights[layer % 2][0:shape[0], at:at + size]
                if len(shape) == 3:
                    v = v.rearrange("p (a b) -> p a b", a=shape[1])
                w[name] = v
            BUILDERS[layer](k, w)
        with nc.Block() as block:

            @block.sync
            def _(sp):
                sp.dma_start(dram["out"].rearrange("(t c) s d -> (c s) t d", c=PER_TILE), k.x[:, :, :]).then_inc(stored, 16)
                sp.wait_ge(stored, 16)


def _mat(w):
    w = np.asarray(w)
    return np.ascontiguousarray(w.reshape(-1, P, w.shape[1]).transpose(1, 0, 2)) if w.shape[0] >= P else w[:, None, :]


def _col(v):
    return np.ascontiguousarray(np.asarray(v).reshape(-1, P).T)


def _row(v):
    v = np.asarray(v).reshape(1, -1)
    return np.broadcast_to(v, (P, v.shape[1]))


def layout(inp):
    g = {n: np.asarray(v) for n, v in inp.items()}
    out = {}
    a = "L0_xattn_"
    out[0] = dict(wq=_mat(g[a + "wq_w"].T), wk=_mat(g[a + "wk_w"].T), wv=_mat(g[a + "wv_w"].T), wo=_mat(g[a + "wo_w"].T),
                  bq=_col(g[a + "wq_b"]), bk=_col(g[a + "wk_b"]), bv=_col(g[a + "wv_b"]), bo=_row(g[a + "wo_b"]))
    a = "L2_xattn_"
    out[6] = dict(wq=_mat(g[a + "Wq"]), wk=_mat(g[a + "Wk"]), wv=_mat(g[a + "Wv"]), wo=_mat(g[a + "Wo"]),
                  bq=_col(g[a + "bq"]), bk=_col(g[a + "bk"]), bv=_col(g[a + "bv"]), bo=_row(g[a + "bo"]))
    more_layout(g, out)
    return out


def more_layout(g, out):
    layout_attention(g, out)
    layout_blocks(g, out)
    layout_scans(g, out)
    layout_delta(g, out)


def kernel(**inputs):
    import concourse.bacc as bacc
    from concourse.bass_utils import run_bass_kernel_spmd

    arrays = {}
    arrays["x"] = np.ascontiguousarray(inputs["x"])
    arrays["ctxT"] = np.ascontiguousarray(np.asarray(inputs["ctx_1024"]).reshape(BATCH * CTX, D).T)
    arrays["ident"] = np.eye(P, dtype=np.float32)
    arrays["hmask16"] = (np.arange(P)[:, None] // 16 == np.arange(8)[None, :]).astype(np.float32)
    arrays["fold"] = (np.arange(P)[:, None] % SEQ == np.arange(SEQ)[None, :]).astype(np.float32)
    arrays["hmask64"] = (np.arange(P)[:, None] // 64 == np.arange(2)[None, :]).astype(np.float32)
    for name, src in (("mask_xattn", "mask_BxS2_bf1"), ("mask_last", "mask_BxS2_bk0")):
        m = np.asarray(inputs[src]).reshape(1, BATCH * CTX)
        arrays[name] = np.ascontiguousarray(np.broadcast_to(m, (P, BATCH * CTX)))
    places = {}
    for layer, pieces in layout(inputs).items():
        if layer not in LAYERS:
            continue
        at, place, flat = 0, {}, []
        for name, piece in pieces.items():
            rows = piece.shape[0]
            size = int(np.prod(piece.shape[1:]))
            block = np.zeros((P, size), piece.dtype)
            block[:rows] = piece.reshape(rows, size)
            flat.append(block)
            place[name] = (at, piece.shape)
            at += size
        assert at <= WMAX[layer % 2], (layer, at)
        arrays[f"w{layer}"] = np.ascontiguousarray(np.concatenate(flat, axis=1))
        places[layer] = place

    nc = bacc.Bacc("TRN2", target_bir_lowering=False, num_devices=1)
    dram = {name: nc.dram_tensor(f"in_{name}", a.shape, mybir.dt.from_np(a.dtype), kind="ExternalInput").ap()
            for name, a in arrays.items()}
    dram["out"] = nc.dram_tensor("out_x", (BATCH, SEQ, D), F32, kind="ExternalOutput").ap()
    build(nc, dram, places, LAYERS)
    r = run_bass_kernel_spmd(nc, [{f"in_{n}": a for n, a in arrays.items()}], core_ids=[0])
    return r.results[0]["out_x"]
```
